# Optimizing a Trainium2 kernel written in Bass

```python
import numpy as np
import jax
import jax.numpy as jnp

def _softmax(x, axis=-1):
    return jax.nn.softmax(x, axis=axis)

def _gelu(x):
    return jax.nn.gelu(x, approximate=True)

def _silu(x):
    return jax.nn.silu(x)

def _sigmoid(x):
    return jax.nn.sigmoid(x)

def _layernorm(x, axis=-1, eps=1e-05):
    m = jnp.mean(x, axis=axis, keepdims=True)
    v = jnp.var(x, axis=axis, keepdims=True)
    return (x - m) / jnp.sqrt(v + eps)

def _scatter_add(tgt, idx, src, axis=0):
    return tgt.at[idx].add(src)

def _segment_sum(src, seg, n):
    return jax.ops.segment_sum(src, seg, n)
kernel_name = 'mk_audio_tower_d4_tok_aud1d512_r4_723a42'

def setup_inputs(seed: int=0):
    np.random.seed(seed)
    _w = jnp.asarray

    def _rec_inputs():
        import jax
        import jax.numpy as jnp
        _rk = jax.random.key(seed)
        x = -0.00238186 + 1.00146 * jax.random.normal(jax.random.fold_in(_rk, 1), (64, 5000), jnp.float32)
        return x
    x = _rec_inputs()

    def _L0_tok_setup():
        import jax, jax.numpy as jnp
        import numpy as np
        B, E, G, P = (8, 16, 5000, 128)
        MASK_DENSITY = 0.1
        key = jax.random.key(seed)
        k_x, k_w, k_m = jax.random.split(key, 3)
        x = jax.random.normal(k_x, (B, G), dtype=jnp.float32)
        weight = jax.random.normal(k_w, (E, G, P), dtype=jnp.float32) * 0.01
        bias = jnp.zeros((E, P), dtype=jnp.float32)
        mask = (jax.random.uniform(k_m, (G, P)) < MASK_DENSITY).astype(jnp.float32)
        return {'x': x, 'weight': weight, 'bias': bias, 'mask': mask}
    _L0_tok_all = _L0_tok_setup()
    _L0_tok_in = {k: v for k, v in _L0_tok_all.items() if k in ('weight', 'bias', 'mask')}
    del _L0_tok_all

    def _L0_attn_setup():
        import jax, jax.numpy as jnp
        import numpy as np
        B, T, D = (8, 128, 128)
        key = jax.random.key(seed)
        ks = jax.random.split(key, 13)
        s = 1.0 / np.sqrt(D)
        inp = {'x': jax.random.normal(ks[0], (B, T, D), dtype=jnp.float32)}
        names = ['qf', 'kf', 'vf', 'qt', 'kt', 'vt']
        for i, n in enumerate(names):
            inp[f'W_{n}'] = jax.random.uniform(ks[1 + 2 * i], (D, D), dtype=jnp.float32, minval=-s, maxval=s)
            inp[f'b_{n}'] = jax.random.uniform(ks[2 + 2 * i], (D,), dtype=jnp.float32, minval=-s, maxval=s)
        return inp
    _L0_attn_all = _L0_attn_setup()
    _L0_attn_in = {k: v for k, v in _L0_attn_all.items() if k in ('W_qf', 'b_qf', 'W_kf', 'b_kf', 'W_vf', 'b_vf', 'W_qt', 'b_qt', 'W_kt', 'b_kt', 'W_vt', 'b_vt')}
    del _L0_attn_all

    def _L0_ffn_setup():
        import jax, jax.numpy as jnp
        import numpy as np
        K = 2
        EPS = 1e-06

        def _layernorm(x, gamma, beta):
            mu = jnp.mean(x, axis=-1, keepdims=True)
            var = jnp.mean(jnp.square(x - mu), axis=-1, keepdims=True)
            return (x - mu) * jax.lax.rsqrt(var + EPS) * gamma + beta
        key = jax.random.key(seed)
        ks = jax.random.split(key, 5)
        B, S, D, F, E = (8, 512, 128, 512, 8)
        x = jax.random.normal(ks[0], (B, S, D), dtype=jnp.float32)
        router_w = jax.random.normal(ks[1], (D, E), dtype=jnp.float32) * 0.02
        w1 = jax.random.normal(ks[2], (E, D, F), dtype=jnp.float32) * 0.02
        b1 = jnp.zeros((E, F), dtype=jnp.float32)
        w2 = jax.random.normal(ks[3], (E, F, D), dtype=jnp.float32) * 0.02
        b2 = jnp.zeros((E, D), dtype=jnp.float32)
        gamma = jnp.ones((E, D), dtype=jnp.float32)
        beta = jnp.zeros((E, D), dtype=jnp.float32)
        return {'x': x, 'router_w': router_w, 'w1': w1, 'b1': b1, 'w2': w2, 'b2': b2, 'gamma': gamma, 'beta': beta}
    _L0_ffn_all = _L0_ffn_setup()
    _L0_ffn_in = {k: v for k, v in _L0_ffn_all.items() if k in ('router_w', 'w1', 'b1', 'w2', 'b2', 'gamma', 'beta')}
    del _L0_ffn_all

    def _L1_attn_setup():
        import jax, jax.numpy as jnp
        import numpy as np
        D = 128
        M = 64
        SE = 32
        SS = 64
        H = 4
        B, L = (2, 256)
        BOT = max(D // 4, 32)

        def _layernorm(x, g, b, eps=1e-05):
            mu = jnp.mean(x, axis=-1, keepdims=True)
            var = jnp.var(x, axis=-1, keepdims=True)
            return (x - mu) * jax.lax.rsqrt(var + eps) * g + b

        def _forward(x, Wq, Wk, Wv, Wf, bf, Wo, ln_g, ln_b, eslots, Eq, Ek, Ev, Eo, know, Sin, Sg_w, Sg_b, So, C1w, C1b, C2w, C2b):
            b, l, d = x.shape
            scale = M ** (-0.5)
            q = (jax.nn.elu(x @ Wq) + 1.0) * scale
            k = jax.nn.elu(x @ Wk) + 1.0
            v = x @ Wv
            forget = jax.nn.sigmoid(x @ Wf + bf)
            log_f_cum = jnp.clip(jnp.cumsum(jnp.log(jnp.clip(forget, 1e-06, None)), axis=1), -20.0, 20.0)
            exp_neg = jnp.exp(-log_f_cum)
            exp_pos = jnp.exp(log_f_cum)
            kv = k[..., :, None] * v[..., None, :]
            cum_kv = jnp.cumsum(exp_neg[..., None] * kv, axis=1)
            Mstate = exp_pos[..., None] * cum_kv
            z = exp_pos * jnp.cumsum(exp_neg * k, axis=1)
            num = jnp.einsum('blm,blmd->bld', q, Mstate)
            den = jnp.einsum('blm,blm->bl', q, z)[..., None] + 1e-06
            w_out = _layernorm(num / den, ln_g, ln_b) @ Wo
            hd = D // H
            mem = jnp.broadcast_to(eslots, (b, SE, D))
            qh = (x @ Eq).reshape(b, l, H, hd)
            kh = (mem @ Ek).reshape(b, SE, H, hd)
            vh = (mem @ Ev).reshape(b, SE, H, hd)
            scores = jnp.einsum('blhe,bshe->bhls', qh, kh) / jnp.sqrt(jnp.float32(hd))
            attn = jax.nn.softmax(scores, axis=-1)
            e_out = jnp.einsum('bhls,bshe->blhe', attn, vh).reshape(b, l, D) @ Eo
            kb = jnp.broadcast_to(know, (b, SS, D))
            qs = x @ Sin
            s_scores = jnp.einsum('bld,bsd->bls', qs, kb) / jnp.sqrt(jnp.float32(D))
            s_attn = jax.nn.softmax(s_scores, axis=-1)
            retrieved = jnp.einsum('bls,bsd->bld', s_attn, kb)
            gate = jax.nn.sigmoid(x @ Sg_w + Sg_b)
            s_out = (gate * retrieved + (1.0 - gate) * x) @ So
            wts = jax.nn.softmax(jax.nn.silu(x @ C1w + C1b) @ C2w + C2b, axis=-1)
            fused = wts[..., 0:1] * w_out + wts[..., 1:2] * e_out + wts[..., 2:3] * s_out
            return fused
        key = jax.random.key(seed)
        ks = jax.random.split(key, 24)
        r = lambda i, shape, s=0.02: jax.random.normal(ks[i], shape, dtype=jnp.float32) * s
        return {'x': jax.random.normal(ks[0], (B, L, D), dtype=jnp.float32), 'Wq': r(1, (D, M)), 'Wk': r(2, (D, M)), 'Wv': r(3, (D, D)), 'Wf': r(4, (D, M)), 'bf': jnp.zeros((M,), jnp.float32), 'Wo': r(5, (D, D)), 'ln_g': jnp.ones((D,), jnp.float32), 'ln_b': jnp.zeros((D,), jnp.float32), 'eslots': r(6, (1, SE, D)), 'Eq': r(7, (D, D)), 'Ek': r(8, (D, D)), 'Ev': r(9, (D, D)), 'Eo': r(10, (D, D)), 'know': r(11, (1, SS, D)), 'Sin': r(12, (D, D)), 'Sg_w': r(13, (D, D)), 'Sg_b': jnp.zeros((D,), jnp.float32), 'So': r(14, (D, D)), 'C1w': r(15, (D, BOT)), 'C1b': jnp.zeros((BOT,), jnp.float32), 'C2w': r(16, (BOT, 3)), 'C2b': jnp.zeros((3,), jnp.float32)}
    _L1_attn_all = _L1_attn_setup()
    _L1_attn_in = {k: v for k, v in _L1_attn_all.items() if k in ('Wq', 'Wk', 'Wv', 'Wf', 'bf', 'Wo', 'ln_g', 'ln_b', 'eslots', 'Eq', 'Ek', 'Ev', 'Eo', 'know', 'Sin', 'Sg_w', 'Sg_b', 'So', 'C1w', 'C1b', 'C2w', 'C2b')}
    del _L1_attn_all

    def _L1_ffn_setup():
        import jax, jax.numpy as jnp
        import numpy as np
        DIM = 128
        HID = 256
        E = 8
        K = 2
        B, S = (4, 512)
        key = jax.random.key(seed)
        ks = jax.random.split(key, 10)
        sd = DIM ** (-0.5)
        sh = HID ** (-0.5)
        return {'x': jax.random.normal(ks[0], (B, S, DIM), dtype=jnp.float32), 'gate_w': jax.random.normal(ks[1], (E, DIM), dtype=jnp.float32) * sd, 'biases': jnp.zeros((E,), dtype=jnp.float32), 'w1': jax.random.normal(ks[2], (E, DIM, HID), dtype=jnp.float32) * sd, 'w3': jax.random.normal(ks[3], (E, DIM, HID), dtype=jnp.float32) * sd, 'w2': jax.random.normal(ks[4], (E, HID, DIM), dtype=jnp.float32) * sh, 'sw1': jax.random.normal(ks[5], (DIM, HID), dtype=jnp.float32) * sd, 'sw3': jax.random.normal(ks[6], (DIM, HID), dtype=jnp.float32) * sd, 'sw2': jax.random.normal(ks[7], (HID, DIM), dtype=jnp.float32) * sh}
    _L1_ffn_all = _L1_ffn_setup()
    _L1_ffn_in = {k: v for k, v in _L1_ffn_all.items() if k in ('gate_w', 'biases', 'w1', 'w3', 'w2', 'sw1', 'sw3', 'sw2')}
    del _L1_ffn_all

    def _L2_attn_setup():
        import jax, jax.numpy as jnp
        import numpy as np
        import math
        D_MODEL = 128
        D_STATE = 16
        D_CONV = 4
        EXPAND = 2
        D_INNER = EXPAND * D_MODEL
        DT_RANK = math.ceil(D_MODEL / 16)
        B, N = (4, 512)
        DIM_K = 128
        DIM_V = 128
        OUT_DIM = 128
        NORM_FACT = 1.0 / math.sqrt(DIM_K)

        def _mamba(x, in_proj_w, conv_w, conv_b, x_proj_w, dt_proj_w, dt_proj_b, A_log, D_param, out_proj_w):
            xz = jnp.einsum('bld,ed->ble', x, in_proj_w)
            xi, z = jnp.split(xz, 2, axis=-1)
            xc = jax.lax.conv_general_dilated(xi.transpose(0, 2, 1), conv_w[:, None, :], (1,), [(D_CONV - 1, 0)], feature_group_count=D_INNER, dimension_numbers=('NCH', 'OIH', 'NCH'))
            xc = jax.nn.silu(xc.transpose(0, 2, 1) + conv_b)
            x_dbl = jnp.einsum('blc,ec->ble', xc, x_proj_w)
            dt, Bp, Cp = jnp.split(x_dbl, [DT_RANK, DT_RANK + D_STATE], axis=-1)
            dt = jax.nn.softplus(jnp.einsum('blr,cr->blc', dt, dt_proj_w) + dt_proj_b)
            A = -jnp.exp(A_log)
            dA = jnp.exp(dt[..., None] * A)
            dBx = dt[..., None] * Bp[:, :, None, :] * xc[..., None]

            def step(h, inp):
                dA_t, dBx_t, C_t = inp
                h = dA_t * h + dBx_t
                return (h, jnp.einsum('bcs,bs->bc', h, C_t))
            h0 = jnp.zeros((x.shape[0], D_INNER, D_STATE), xc.dtype)
            _, ys = jax.lax.scan(step, h0, (dA.transpose(1, 0, 2, 3), dBx.transpose(1, 0, 2, 3), Cp.transpose(1, 0, 2)))
            y = ys.transpose(1, 0, 2) + xc * D_param
            y = y * jax.nn.silu(z)
            return jnp.einsum('blc,dc->bld', y, out_proj_w)
        key = jax.random.key(seed)
        ks = jax.random.split(key, 16)
        w = lambda i, shape: jax.random.normal(ks[i], shape, jnp.float32) * 0.02
        dt_bias = math.log(math.expm1(0.01))
        return {'x': jax.random.normal(ks[0], (B, N, D_MODEL), jnp.float32), 'in_proj_w': w(1, (2 * D_INNER, D_MODEL)), 'conv_w': w(2, (D_INNER, D_CONV)), 'conv_b': jnp.zeros((D_INNER,), jnp.float32), 'x_proj_w': w(3, (DT_RANK + 2 * D_STATE, D_INNER)), 'dt_proj_w': w(4, (D_INNER, DT_RANK)), 'dt_proj_b': jnp.full((D_INNER,), dt_bias, jnp.float32), 'A_log': jnp.broadcast_to(jnp.log(jnp.arange(1, D_STATE + 1, dtype=jnp.float32)), (D_INNER, D_STATE)).copy(), 'D_param': jnp.ones((D_INNER,), jnp.float32), 'out_proj_w': w(5, (D_MODEL, D_INNER)), 'wq': w(6, (DIM_K, D_MODEL)), 'wk': w(7, (DIM_K, D_MODEL)), 'wv': w(8, (DIM_V, D_MODEL)), 'fc_w': w(9, (OUT_DIM, DIM_V)), 'fc_b': jnp.zeros((OUT_DIM,), jnp.float32)}
    _L2_attn_all = _L2_attn_setup()
    _L2_attn_in = {k: v for k, v in _L2_attn_all.items() if k in ('in_proj_w', 'conv_w', 'conv_b', 'x_proj_w', 'dt_proj_w', 'dt_proj_b', 'A_log', 'D_param', 'out_proj_w', 'wq', 'wk', 'wv', 'fc_w', 'fc_b')}
    del _L2_attn_all

    def _L2_ffn_setup():
        import jax, jax.numpy as jnp
        import numpy as np
        D_IN, D_HID, E, K = (128, 512, 10, 2)
        KS = (9, 1)

        def conv1d_same(x, w, b):
            y = jax.lax.conv_general_dilated(x, w, window_strides=(1,), padding='SAME', dimension_numbers=('NCH', 'OIH', 'NCH'))
            return y + b[None, :, None]
        key = jax.random.key(seed)
        ks = jax.random.split(key, 16)
        s = 0.02
        B, T = (2, 512)
        return {'x': jax.random.normal(ks[0], (B, T, D_IN), jnp.float32), 'rc_w1': jax.random.normal(ks[1], (D_IN, D_IN, 3), jnp.float32) * s, 'rc_b1': jnp.zeros((D_IN,), jnp.float32), 'rc_w2': jax.random.normal(ks[2], (E, D_IN, 3), jnp.float32) * s, 'rc_b2': jnp.zeros((E,), jnp.float32), 'sh_w1': jax.random.normal(ks[3], (D_HID, D_IN, KS[0]), jnp.float32) * s, 'sh_b1': jnp.zeros((D_HID,), jnp.float32), 'sh_w2': jax.random.normal(ks[4], (D_IN, D_HID, KS[1]), jnp.float32) * s, 'sh_b2': jnp.zeros((D_IN,), jnp.float32), 'e_w1': jax.random.normal(ks[5], (E, D_IN, D_HID), jnp.float32) * s, 'e_b1': jnp.zeros((E, D_HID), jnp.float32), 'e_w2': jax.random.normal(ks[6], (E, D_HID, D_IN), jnp.float32) * s, 'e_b2': jnp.zeros((E, D_IN), jnp.float32), 'ln_g': jnp.ones((D_IN,), jnp.float32), 'ln_b': jnp.zeros((D_IN,), jnp.float32)}
    _L2_ffn_all = _L2_ffn_setup()
    _L2_ffn_in = {k: v for k, v in _L2_ffn_all.items() if k in ('rc_w1', 'rc_b1', 'rc_w2', 'rc_b2', 'sh_w1', 'sh_b1', 'sh_w2', 'sh_b2', 'e_w1', 'e_b1', 'e_w2', 'e_b2', 'ln_g', 'ln_b')}
    del _L2_ffn_all

    def _L3_attn_setup():
        import jax, jax.numpy as jnp
        import numpy as np
        from jax import lax
        B, S, D = (4, 512, 128)
        H, DK, DV, DH = (8, 64, 64, 64)
        KCONV = 4
        LN_EPS = 1e-05

        def _mlp(x, W2, W1, residual):
            h = jax.nn.silu(x @ W2.T) @ W1.T
            return x + h if residual else h

        def _ln(x, g, b):
            mu = jnp.mean(x, axis=-1, keepdims=True)
            var = jnp.mean(jnp.square(x - mu), axis=-1, keepdims=True)
            return (x - mu) * jax.lax.rsqrt(var + LN_EPS) * g + b
        key = jax.random.key(seed)
        ks = jax.random.split(key, 20)
        sc = 0.02
        return {'x': jax.random.normal(ks[0], (B, S, D), jnp.float32), 'conv_w': jax.random.normal(ks[1], (D, 1, KCONV), jnp.float32) * sc, 'conv_b': jnp.zeros((D,), jnp.float32), 'Wq': jax.random.normal(ks[2], (H * DK, D), jnp.float32) * sc, 'Mk_W2': jax.random.normal(ks[3], (DH, D), jnp.float32) * sc, 'Mk_W1': jax.random.normal(ks[4], (H * DK, DH), jnp.float32) * sc, 'Mv_W2': jax.random.normal(ks[5], (DH, D), jnp.float32) * sc, 'Mv_W1': jax.random.normal(ks[6], (H * DV, DH), jnp.float32) * sc, 'Meta_W2': jax.random.normal(ks[7], (DH, D), jnp.float32) * sc, 'Meta_W1': jax.random.normal(ks[8], (H, DH), jnp.float32) * sc, 'Malpha_W2': jax.random.normal(ks[9], (DH, D), jnp.float32) * sc, 'Malpha_W1': jax.random.normal(ks[10], (H, DH), jnp.float32) * sc, 'Mvh_W2': jax.random.normal(ks[11], (DH, H * DV), jnp.float32) * sc, 'Mvh_W1': jax.random.normal(ks[12], (H * DV, DH), jnp.float32) * sc, 'normk_g': jnp.ones((H * DK,), jnp.float32), 'normk_b': jnp.zeros((H * DK,), jnp.float32), 'normq_g': jnp.ones((H * DK,), jnp.float32), 'normq_b': jnp.zeros((H * DK,), jnp.float32), 'out_W': jax.random.normal(ks[13], (D, H * DV), jnp.float32) * sc, 'out_b': jnp.zeros((D,), jnp.float32)}
    _L3_attn_all = _L3_attn_setup()
    _L3_attn_in = {k: v for k, v in _L3_attn_all.items() if k in ('conv_w', 'conv_b', 'Wq', 'Mk_W2', 'Mk_W1', 'Mv_W2', 'Mv_W1', 'Meta_W2', 'Meta_W1', 'Malpha_W2', 'Malpha_W1', 'Mvh_W2', 'Mvh_W1', 'normk_g', 'normk_b', 'normq_g', 'normq_b', 'out_W', 'out_b')}
    del _L3_attn_all

    def _L3_ffn_setup():
        import jax, jax.numpy as jnp
        import numpy as np
        H = 128
        F = 512
        E = 16
        SHARED = 2
        TOP_K = 4
        B, S = (2, 512)

        def _mlp(x, w1, b1, w2, b2):
            return jax.nn.gelu(x @ w1 + b1, approximate=False) @ w2 + b2
        key = jax.random.key(seed)
        ks = jax.random.split(key, 10)
        sc = 0.02
        return {'hidden_states': jax.random.normal(ks[0], (B, S, H), dtype=jnp.float32), 'gate_w': jax.random.normal(ks[1], (E, H), dtype=jnp.float32) * sc, 're_w1': jax.random.normal(ks[2], (E, H, F), dtype=jnp.float32) * sc, 're_b1': jnp.zeros((E, F), dtype=jnp.float32), 're_w2': jax.random.normal(ks[3], (E, F, H), dtype=jnp.float32) * sc, 're_b2': jnp.zeros((E, H), dtype=jnp.float32), 'se_w1': jax.random.normal(ks[4], (SHARED, H, F), dtype=jnp.float32) * sc, 'se_b1': jnp.zeros((SHARED, F), dtype=jnp.float32), 'se_w2': jax.random.normal(ks[5], (SHARED, F, H), dtype=jnp.float32) * sc, 'se_b2': jnp.zeros((SHARED, H), dtype=jnp.float32)}
    _L3_ffn_all = _L3_ffn_setup()
    _L3_ffn_in = {k: v for k, v in _L3_ffn_all.items() if k in ('gate_w', 're_w1', 're_b1', 're_w2', 're_b2', 'se_w1', 'se_b1', 'se_w2', 'se_b2')}
    del _L3_ffn_all
    return {'x': x, 'L0_tok_weight': _L0_tok_in['weight'], 'L0_tok_bias': _L0_tok_in['bias'], 'L0_tok_mask': _L0_tok_in['mask'], 'L0_attn_W_qf': _L0_attn_in['W_qf'], 'L0_attn_b_qf': _L0_attn_in['b_qf'], 'L0_attn_W_kf': _L0_attn_in['W_kf'], 'L0_attn_b_kf': _L0_attn_in['b_kf'], 'L0_attn_W_vf': _L0_attn_in['W_vf'], 'L0_attn_b_vf': _L0_attn_in['b_vf'], 'L0_attn_W_qt': _L0_attn_in['W_qt'], 'L0_attn_b_qt': _L0_attn_in['b_qt'], 'L0_attn_W_kt': _L0_attn_in['W_kt'], 'L0_attn_b_kt': _L0_attn_in['b_kt'], 'L0_attn_W_vt': _L0_attn_in['W_vt'], 'L0_attn_b_vt': _L0_attn_in['b_vt'], 'L0_ffn_router_w': _L0_ffn_in['router_w'], 'L0_ffn_w1': _L0_ffn_in['w1'], 'L0_ffn_b1': _L0_ffn_in['b1'], 'L0_ffn_w2': _L0_ffn_in['w2'], 'L0_ffn_b2': _L0_ffn_in['b2'], 'L0_ffn_gamma': _L0_ffn_in['gamma'], 'L0_ffn_beta': _L0_ffn_in['beta'], 'L1_attn_Wq': _L1_attn_in['Wq'], 'L1_attn_Wk': _L1_attn_in['Wk'], 'L1_attn_Wv': _L1_attn_in['Wv'], 'L1_attn_Wf': _L1_attn_in['Wf'], 'L1_attn_bf': _L1_attn_in['bf'], 'L1_attn_Wo': _L1_attn_in['Wo'], 'L1_attn_ln_g': _L1_attn_in['ln_g'], 'L1_attn_ln_b': _L1_attn_in['ln_b'], 'L1_attn_eslots': _L1_attn_in['eslots'], 'L1_attn_Eq': _L1_attn_in['Eq'], 'L1_attn_Ek': _L1_attn_in['Ek'], 'L1_attn_Ev': _L1_attn_in['Ev'], 'L1_attn_Eo': _L1_attn_in['Eo'], 'L1_attn_know': _L1_attn_in['know'], 'L1_attn_Sin': _L1_attn_in['Sin'], 'L1_attn_Sg_w': _L1_attn_in['Sg_w'], 'L1_attn_Sg_b': _L1_attn_in['Sg_b'], 'L1_attn_So': _L1_attn_in['So'], 'L1_attn_C1w': _L1_attn_in['C1w'], 'L1_attn_C1b': _L1_attn_in['C1b'], 'L1_attn_C2w': _L1_attn_in['C2w'], 'L1_attn_C2b': _L1_attn_in['C2b'], 'L1_ffn_gate_w': _L1_ffn_in['gate_w'], 'L1_ffn_biases': _L1_ffn_in['biases'], 'L1_ffn_w1': _L1_ffn_in['w1'], 'L1_ffn_w3': _L1_ffn_in['w3'], 'L1_ffn_w2': _L1_ffn_in['w2'], 'L1_ffn_sw1': _L1_ffn_in['sw1'], 'L1_ffn_sw3': _L1_ffn_in['sw3'], 'L1_ffn_sw2': _L1_ffn_in['sw2'], 'L2_attn_in_proj_w': _L2_attn_in['in_proj_w'], 'L2_attn_conv_w': _L2_attn_in['conv_w'], 'L2_attn_conv_b': _L2_attn_in['conv_b'], 'L2_attn_x_proj_w': _L2_attn_in['x_proj_w'], 'L2_attn_dt_proj_w': _L2_attn_in['dt_proj_w'], 'L2_attn_dt_proj_b': _L2_attn_in['dt_proj_b'], 'L2_attn_A_log': _L2_attn_in['A_log'], 'L2_attn_D_param': _L2_attn_in['D_param'], 'L2_attn_out_proj_w': _L2_attn_in['out_proj_w'], 'L2_attn_wq': _L2_attn_in['wq'], 'L2_attn_wk': _L2_attn_in['wk'], 'L2_attn_wv': _L2_attn_in['wv'], 'L2_attn_fc_w': _L2_attn_in['fc_w'], 'L2_attn_fc_b': _L2_attn_in['fc_b'], 'L2_ffn_rc_w1': _L2_ffn_in['rc_w1'], 'L2_ffn_rc_b1': _L2_ffn_in['rc_b1'], 'L2_ffn_rc_w2': _L2_ffn_in['rc_w2'], 'L2_ffn_rc_b2': _L2_ffn_in['rc_b2'], 'L2_ffn_sh_w1': _L2_ffn_in['sh_w1'], 'L2_ffn_sh_b1': _L2_ffn_in['sh_b1'], 'L2_ffn_sh_w2': _L2_ffn_in['sh_w2'], 'L2_ffn_sh_b2': _L2_ffn_in['sh_b2'], 'L2_ffn_e_w1': _L2_ffn_in['e_w1'], 'L2_ffn_e_b1': _L2_ffn_in['e_b1'], 'L2_ffn_e_w2': _L2_ffn_in['e_w2'], 'L2_ffn_e_b2': _L2_ffn_in['e_b2'], 'L2_ffn_ln_g': _L2_ffn_in['ln_g'], 'L2_ffn_ln_b': _L2_ffn_in['ln_b'], 'L3_attn_conv_w': _L3_attn_in['conv_w'], 'L3_attn_conv_b': _L3_attn_in['conv_b'], 'L3_attn_Wq': _L3_attn_in['Wq'], 'L3_attn_Mk_W2': _L3_attn_in['Mk_W2'], 'L3_attn_Mk_W1': _L3_attn_in['Mk_W1'], 'L3_attn_Mv_W2': _L3_attn_in['Mv_W2'], 'L3_attn_Mv_W1': _L3_attn_in['Mv_W1'], 'L3_attn_Meta_W2': _L3_attn_in['Meta_W2'], 'L3_attn_Meta_W1': _L3_attn_in['Meta_W1'], 'L3_attn_Malpha_W2': _L3_attn_in['Malpha_W2'], 'L3_attn_Malpha_W1': _L3_attn_in['Malpha_W1'], 'L3_attn_Mvh_W2': _L3_attn_in['Mvh_W2'], 'L3_attn_Mvh_W1': _L3_attn_in['Mvh_W1'], 'L3_attn_normk_g': _L3_attn_in['normk_g'], 'L3_attn_normk_b': _L3_attn_in['normk_b'], 'L3_attn_normq_g': _L3_attn_in['normq_g'], 'L3_attn_normq_b': _L3_attn_in['normq_b'], 'L3_attn_out_W': _L3_attn_in['out_W'], 'L3_attn_out_b': _L3_attn_in['out_b'], 'L3_ffn_gate_w': _L3_ffn_in['gate_w'], 'L3_ffn_re_w1': _L3_ffn_in['re_w1'], 'L3_ffn_re_b1': _L3_ffn_in['re_b1'], 'L3_ffn_re_w2': _L3_ffn_in['re_w2'], 'L3_ffn_re_b2': _L3_ffn_in['re_b2'], 'L3_ffn_se_w1': _L3_ffn_in['se_w1'], 'L3_ffn_se_b1': _L3_ffn_in['se_b1'], 'L3_ffn_se_w2': _L3_ffn_in['se_w2'], 'L3_ffn_se_b2': _L3_ffn_in['se_b2']}

def reference(x, L0_tok_weight, L0_tok_bias, L0_tok_mask, L0_attn_W_qf, L0_attn_b_qf, L0_attn_W_kf, L0_attn_b_kf, L0_attn_W_vf, L0_attn_b_vf, L0_attn_W_qt, L0_attn_b_qt, L0_attn_W_kt, L0_attn_b_kt, L0_attn_W_vt, L0_attn_b_vt, L0_ffn_router_w, L0_ffn_w1, L0_ffn_b1, L0_ffn_w2, L0_ffn_b2, L0_ffn_gamma, L0_ffn_beta, L1_attn_Wq, L1_attn_Wk, L1_attn_Wv, L1_attn_Wf, L1_attn_bf, L1_attn_Wo, L1_attn_ln_g, L1_attn_ln_b, L1_attn_eslots, L1_attn_Eq, L1_attn_Ek, L1_attn_Ev, L1_attn_Eo, L1_attn_know, L1_attn_Sin, L1_attn_Sg_w, L1_attn_Sg_b, L1_attn_So, L1_attn_C1w, L1_attn_C1b, L1_attn_C2w, L1_attn_C2b, L1_ffn_gate_w, L1_ffn_biases, L1_ffn_w1, L1_ffn_w3, L1_ffn_w2, L1_ffn_sw1, L1_ffn_sw3, L1_ffn_sw2, L2_attn_in_proj_w, L2_attn_conv_w, L2_attn_conv_b, L2_attn_x_proj_w, L2_attn_dt_proj_w, L2_attn_dt_proj_b, L2_attn_A_log, L2_attn_D_param, L2_attn_out_proj_w, L2_attn_wq, L2_attn_wk, L2_attn_wv, L2_attn_fc_w, L2_attn_fc_b, L2_ffn_rc_w1, L2_ffn_rc_b1, L2_ffn_rc_w2, L2_ffn_rc_b2, L2_ffn_sh_w1, L2_ffn_sh_b1, L2_ffn_sh_w2, L2_ffn_sh_b2, L2_ffn_e_w1, L2_ffn_e_b1, L2_ffn_e_w2, L2_ffn_e_b2, L2_ffn_ln_g, L2_ffn_ln_b, L3_attn_conv_w, L3_attn_conv_b, L3_attn_Wq, L3_attn_Mk_W2, L3_attn_Mk_W1, L3_attn_Mv_W2, L3_attn_Mv_W1, L3_attn_Meta_W2, L3_attn_Meta_W1, L3_attn_Malpha_W2, L3_attn_Malpha_W1, L3_attn_Mvh_W2, L3_attn_Mvh_W1, L3_attn_normk_g, L3_attn_normk_b, L3_attn_normq_g, L3_attn_normq_b, L3_attn_out_W, L3_attn_out_b, L3_ffn_gate_w, L3_ffn_re_w1, L3_ffn_re_b1, L3_ffn_re_w2, L3_ffn_re_b2, L3_ffn_se_w1, L3_ffn_se_b1, L3_ffn_se_w2, L3_ffn_se_b2):
    import jax
    import jax.numpy as jnp

    def _L0_tok_ref(x, weight, bias, mask):
        import jax, jax.numpy as jnp
        import numpy as np
        B, E, G, P = (8, 16, 5000, 128)
        MASK_DENSITY = 0.1
        W = weight * mask[None, :, :]
        out = jnp.einsum('bg,egp->bep', x, W)
        return out + bias[None, :, :]

    def _L0_attn_ref(x, W_qf, b_qf, W_kf, b_kf, W_vf, b_vf, W_qt, b_qt, W_kt, b_kt, W_vt, b_vt):
        import jax, jax.numpy as jnp
        import numpy as np
        B, T, D = (8, 128, 128)
        lin = lambda h, W, b: jnp.einsum('bti,oi->bto', h, W) + b
        Q_f = lin(x, W_qf, b_qf)
        K_f = lin(x, W_kf, b_kf)
        V_f = lin(x, W_vf, b_vf)
        ctx_f = jax.nn.softmax(Q_f * K_f, axis=-1) * V_f
        Q_t = lin(x, W_qt, b_qt)
        K_t = lin(x, W_kt, b_kt)
        V_t = lin(x, W_vt, b_vt)
        scores_t = jnp.einsum('bti,btj->btij', Q_t, K_t)
        probs_t = jax.nn.softmax(scores_t, axis=-1)
        ctx_t = jnp.einsum('btij,btj->bti', probs_t, V_t)
        return ctx_f + ctx_t

    def _L0_ffn_ref(x, router_w, w1, b1, w2, b2, gamma, beta):
        import jax, jax.numpy as jnp
        import numpy as np
        K = 2
        EPS = 1e-06

        def _layernorm(x, gamma, beta):
            mu = jnp.mean(x, axis=-1, keepdims=True)
            var = jnp.mean(jnp.square(x - mu), axis=-1, keepdims=True)
            return (x - mu) * jax.lax.rsqrt(var + EPS) * gamma + beta
        B, S, D = x.shape
        E = w1.shape[0]
        xf = x.reshape(-1, D)
        logits = xf @ router_w
        gate_vals, idx = jax.lax.top_k(logits, K)
        gates = jax.nn.softmax(gate_vals, axis=-1)
        out = jnp.zeros_like(xf)
        for e in range(E):
            h = jax.nn.relu(xf @ w1[e] + b1[e]) @ w2[e] + b2[e]
            y = _layernorm(xf + h, gamma[e], beta[e])
            w = jnp.sum(jnp.where(idx == e, gates, 0.0), axis=-1)
            out = out + w[:, None] * y
        return out.reshape(B, S, D)

    def _L1_attn_ref(x, Wq, Wk, Wv, Wf, bf, Wo, ln_g, ln_b, eslots, Eq, Ek, Ev, Eo, know, Sin, Sg_w, Sg_b, So, C1w, C1b, C2w, C2b):
        import jax, jax.numpy as jnp
        import numpy as np
        D = 128
        M = 64
        SE = 32
        SS = 64
        H = 4
        B, L = (2, 256)
        BOT = max(D // 4, 32)

        def _layernorm(x, g, b, eps=1e-05):
            mu = jnp.mean(x, axis=-1, keepdims=True)
            var = jnp.var(x, axis=-1, keepdims=True)
            return (x - mu) * jax.lax.rsqrt(var + eps) * g + b

        def _forward(x, Wq, Wk, Wv, Wf, bf, Wo, ln_g, ln_b, eslots, Eq, Ek, Ev, Eo, know, Sin, Sg_w, Sg_b, So, C1w, C1b, C2w, C2b):
            b, l, d = x.shape
            scale = M ** (-0.5)
            q = (jax.nn.elu(x @ Wq) + 1.0) * scale
            k = jax.nn.elu(x @ Wk) + 1.0
            v = x @ Wv
            forget = jax.nn.sigmoid(x @ Wf + bf)
            log_f_cum = jnp.clip(jnp.cumsum(jnp.log(jnp.clip(forget, 1e-06, None)), axis=1), -20.0, 20.0)
            exp_neg = jnp.exp(-log_f_cum)
            exp_pos = jnp.exp(log_f_cum)
            kv = k[..., :, None] * v[..., None, :]
            cum_kv = jnp.cumsum(exp_neg[..., None] * kv, axis=1)
            Mstate = exp_pos[..., None] * cum_kv
            z = exp_pos * jnp.cumsum(exp_neg * k, axis=1)
            num = jnp.einsum('blm,blmd->bld', q, Mstate)
            den = jnp.einsum('blm,blm->bl', q, z)[..., None] + 1e-06
            w_out = _layernorm(num / den, ln_g, ln_b) @ Wo
            hd = D // H
            mem = jnp.broadcast_to(eslots, (b, SE, D))
            qh = (x @ Eq).reshape(b, l, H, hd)
            kh = (mem @ Ek).reshape(b, SE, H, hd)
            vh = (mem @ Ev).reshape(b, SE, H, hd)
            scores = jnp.einsum('blhe,bshe->bhls', qh, kh) / jnp.sqrt(jnp.float32(hd))
            attn = jax.nn.softmax(scores, axis=-1)
            e_out = jnp.einsum('bhls,bshe->blhe', attn, vh).reshape(b, l, D) @ Eo
            kb = jnp.broadcast_to(know, (b, SS, D))
            qs = x @ Sin
            s_scores = jnp.einsum('bld,bsd->bls', qs, kb) / jnp.sqrt(jnp.float32(D))
            s_attn = jax.nn.softmax(s_scores, axis=-1)
            retrieved = jnp.einsum('bls,bsd->bld', s_attn, kb)
            gate = jax.nn.sigmoid(x @ Sg_w + Sg_b)
            s_out = (gate * retrieved + (1.0 - gate) * x) @ So
            wts = jax.nn.softmax(jax.nn.silu(x @ C1w + C1b) @ C2w + C2b, axis=-1)
            fused = wts[..., 0:1] * w_out + wts[..., 1:2] * e_out + wts[..., 2:3] * s_out
            return fused
        return _forward(x, Wq, Wk, Wv, Wf, bf, Wo, ln_g, ln_b, eslots, Eq, Ek, Ev, Eo, know, Sin, Sg_w, Sg_b, So, C1w, C1b, C2w, C2b)

    def _L1_ffn_ref(x, gate_w, biases, w1, w3, w2, sw1, sw3, sw2):
        import jax, jax.numpy as jnp
        import numpy as np
        DIM = 128
        HID = 256
        E = 8
        K = 2
        B, S = (4, 512)
        Bb, Ss, D = x.shape
        xt = x.reshape(Bb * Ss, D)
        shared = jax.nn.silu(xt @ sw1) * (xt @ sw3) @ sw2
        scores = xt @ gate_w.T
        _, idx = jax.lax.top_k(scores + biases, K)
        topv, _ = jax.lax.top_k(scores, K)
        p = jax.nn.sigmoid(topv)
        p = p / jnp.sum(p, axis=-1, keepdims=True)
        h = jax.nn.silu(jnp.einsum('td,edh->eth', xt, w1)) * jnp.einsum('td,edh->eth', xt, w3)
        y = jnp.einsum('eth,ehd->etd', h, w2)
        onehot = jax.nn.one_hot(idx, E, dtype=xt.dtype)
        comb = jnp.einsum('tk,tke->te', p, onehot)
        out = jnp.einsum('te,etd->td', comb, y) + shared
        return out.reshape(Bb, Ss, D)

    def _L2_attn_ref(x, in_proj_w, conv_w, conv_b, x_proj_w, dt_proj_w, dt_proj_b, A_log, D_param, out_proj_w, wq, wk, wv, fc_w, fc_b):
        import jax, jax.numpy as jnp
        import numpy as np
        import math
        D_MODEL = 128
        D_STATE = 16
        D_CONV = 4
        EXPAND = 2
        D_INNER = EXPAND * D_MODEL
        DT_RANK = math.ceil(D_MODEL / 16)
        B, N = (4, 512)
        DIM_K = 128
        DIM_V = 128
        OUT_DIM = 128
        NORM_FACT = 1.0 / math.sqrt(DIM_K)

        def _mamba(x, in_proj_w, conv_w, conv_b, x_proj_w, dt_proj_w, dt_proj_b, A_log, D_param, out_proj_w):
            xz = jnp.einsum('bld,ed->ble', x, in_proj_w)
            xi, z = jnp.split(xz, 2, axis=-1)
            xc = jax.lax.conv_general_dilated(xi.transpose(0, 2, 1), conv_w[:, None, :], (1,), [(D_CONV - 1, 0)], feature_group_count=D_INNER, dimension_numbers=('NCH', 'OIH', 'NCH'))
            xc = jax.nn.silu(xc.transpose(0, 2, 1) + conv_b)
            x_dbl = jnp.einsum('blc,ec->ble', xc, x_proj_w)
            dt, Bp, Cp = jnp.split(x_dbl, [DT_RANK, DT_RANK + D_STATE], axis=-1)
            dt = jax.nn.softplus(jnp.einsum('blr,cr->blc', dt, dt_proj_w) + dt_proj_b)
            A = -jnp.exp(A_log)
            dA = jnp.exp(dt[..., None] * A)
            dBx = dt[..., None] * Bp[:, :, None, :] * xc[..., None]

            def step(h, inp):
                dA_t, dBx_t, C_t = inp
                h = dA_t * h + dBx_t
                return (h, jnp.einsum('bcs,bs->bc', h, C_t))
            h0 = jnp.zeros((x.shape[0], D_INNER, D_STATE), xc.dtype)
            _, ys = jax.lax.scan(step, h0, (dA.transpose(1, 0, 2, 3), dBx.transpose(1, 0, 2, 3), Cp.transpose(1, 0, 2)))
            y = ys.transpose(1, 0, 2) + xc * D_param
            y = y * jax.nn.silu(z)
            return jnp.einsum('blc,dc->bld', y, out_proj_w)
        xm = _mamba(x, in_proj_w, conv_w, conv_b, x_proj_w, dt_proj_w, dt_proj_b, A_log, D_param, out_proj_w)
        q = jnp.einsum('bnd,kd->bnk', xm, wq)
        k = jnp.einsum('bnd,kd->bnk', xm, wk)
        v = jnp.einsum('bnd,vd->bnv', xm, wv)
        scores = jnp.einsum('bik,bjk->bij', q, k) * NORM_FACT
        mask = jnp.tril(jnp.ones((xm.shape[1], xm.shape[1]), bool))
        att = jax.nn.softmax(jnp.where(mask, scores, -jnp.inf), axis=-1)
        out = jnp.einsum('bij,bjv->biv', att, v)
        return jnp.einsum('biv,ov->bio', out, fc_w) + fc_b

    def _L2_ffn_ref(x, rc_w1, rc_b1, rc_w2, rc_b2, sh_w1, sh_b1, sh_w2, sh_b2, e_w1, e_b1, e_w2, e_b2, ln_g, ln_b):
        import jax, jax.numpy as jnp
        import numpy as np
        D_IN, D_HID, E, K = (128, 512, 10, 2)
        KS = (9, 1)

        def conv1d_same(x, w, b):
            y = jax.lax.conv_general_dilated(x, w, window_strides=(1,), padding='SAME', dimension_numbers=('NCH', 'OIH', 'NCH'))
            return y + b[None, :, None]
        B, T, d = x.shape
        residual = x
        xt = jnp.transpose(x, (0, 2, 1))
        rc = conv1d_same(xt, rc_w1, rc_b1)
        rc = jax.nn.gelu(rc, approximate=False)
        rc = conv1d_same(rc, rc_w2, rc_b2)
        logits = jnp.transpose(rc, (0, 2, 1)).reshape(-1, E)
        vals, idx = jax.lax.top_k(logits, K)
        gv = jax.nn.softmax(vals, axis=-1)
        N = logits.shape[0]
        gates = jnp.zeros((N, E), x.dtype).at[jnp.arange(N)[:, None], idx].set(gv)
        x2 = x.reshape(-1, d)
        h = jnp.einsum('nd,edh->enh', x2, e_w1) + e_b1[:, None, :]
        h = jax.nn.elu(h)
        eo = jnp.einsum('enh,ehd->end', h, e_w2) + e_b2[:, None, :]
        y = jnp.einsum('end,ne->nd', eo, gates).reshape(B, T, d)
        sh = conv1d_same(xt, sh_w1, sh_b1)
        sh = jax.nn.silu(sh)
        sh = conv1d_same(sh, sh_w2, sh_b2)
        sh = jnp.transpose(sh, (0, 2, 1))
        z = residual + y + sh
        mu = jnp.mean(z, axis=-1, keepdims=True)
        var = jnp.mean(jnp.square(z - mu), axis=-1, keepdims=True)
        return (z - mu) * jax.lax.rsqrt(var + 1e-05) * ln_g + ln_b

    def _L3_attn_ref(x, conv_w, conv_b, Wq, Mk_W2, Mk_W1, Mv_W2, Mv_W1, Meta_W2, Meta_W1, Malpha_W2, Malpha_W1, Mvh_W2, Mvh_W1, normk_g, normk_b, normq_g, normq_b, out_W, out_b):
        import jax, jax.numpy as jnp
        import numpy as np
        from jax import lax
        B, S, D = (4, 512, 128)
        H, DK, DV, DH = (8, 64, 64, 64)
        KCONV = 4
        LN_EPS = 1e-05

        def _mlp(x, W2, W1, residual):
            h = jax.nn.silu(x @ W2.T) @ W1.T
            return x + h if residual else h

        def _ln(x, g, b):
            mu = jnp.mean(x, axis=-1, keepdims=True)
            var = jnp.mean(jnp.square(x - mu), axis=-1, keepdims=True)
            return (x - mu) * jax.lax.rsqrt(var + LN_EPS) * g + b
        b, s, d = x.shape
        xc = jnp.transpose(x, (0, 2, 1))
        yc = lax.conv_general_dilated(xc, conv_w, (1,), [(KCONV - 1, 0)], feature_group_count=d)
        x = x + jnp.transpose(yc + conv_b[None, :, None], (0, 2, 1))
        k = _ln(_mlp(x, Mk_W2, Mk_W1, False), normk_g, normk_b)
        v = _mlp(x, Mv_W2, Mv_W1, False)
        q = _ln(x @ Wq.T, normq_g, normq_b)
        eta = jax.nn.softplus(_mlp(x, Meta_W2, Meta_W1, False)) * 0.1
        alpha = jax.nn.sigmoid(_mlp(x, Malpha_W2, Malpha_W1, False))
        v_hat = _mlp(v, Mvh_W2, Mvh_W1, True)
        to_s = lambda t, dd: jnp.transpose(t.reshape(b, s, H, dd), (1, 0, 2, 3))
        q_s, k_s = (to_s(q, DK), to_s(k, DK))
        vh_s = to_s(v_hat, DV)
        eta_s = jnp.transpose(eta, (1, 0, 2))
        al_s = jnp.transpose(alpha, (1, 0, 2))
        eye = jnp.eye(DK, dtype=x.dtype)

        def step(mem, inp):
            q_t, k_t, vh_t, e_t, a_t = inp
            y_t = jnp.einsum('bhvk,bhk->bhv', mem, q_t)
            kn = k_t / jnp.maximum(jnp.linalg.norm(k_t, axis=-1, keepdims=True), 1e-12)
            err = jnp.einsum('bhvk,bhk->bhv', mem, kn) - vh_t
            e4 = e_t[:, :, None, None]
            a4 = a_t[:, :, None, None]
            decay = a4 * eye - e4 * (kn[:, :, :, None] * kn[:, :, None, :])
            mem = jnp.einsum('bhvk,bhkl->bhvl', mem, decay) - e4 * (err[:, :, :, None] * kn[:, :, None, :])
            return (mem, y_t)
        mem0 = jnp.zeros((b, H, DV, DK), x.dtype)
        _, ys = lax.scan(step, mem0, (q_s, k_s, vh_s, eta_s, al_s))
        out = jnp.transpose(ys, (1, 0, 2, 3)).reshape(b, s, H * DV)
        return out @ out_W.T + out_b

    def _L3_ffn_ref(hidden_states, gate_w, re_w1, re_b1, re_w2, re_b2, se_w1, se_b1, se_w2, se_b2):
        import jax, jax.numpy as jnp
        import numpy as np
        H = 128
        F = 512
        E = 16
        SHARED = 2
        TOP_K = 4
        B, S = (2, 512)

        def _mlp(x, w1, b1, w2, b2):
            return jax.nn.gelu(x @ w1 + b1, approximate=False) @ w2 + b2
        b, s, h = hidden_states.shape
        x = hidden_states.reshape(-1, h)
        gate_probs = jax.nn.softmax(x @ gate_w.T, axis=-1)
        top_v, top_i = jax.lax.top_k(gate_probs, TOP_K)
        top_v = jax.nn.softmax(top_v, axis=-1)
        combine = jnp.einsum('tk,tke->te', top_v, jax.nn.one_hot(top_i, E, dtype=x.dtype))
        routed = jnp.zeros_like(x)
        for e in range(E):
            routed = routed + combine[:, e:e + 1] * _mlp(x, re_w1[e], re_b1[e], re_w2[e], re_b2[e])
        shared = jnp.zeros_like(x)
        for j in range(SHARED):
            shared = shared + _mlp(x, se_w1[j], se_b1[j], se_w2[j], se_b2[j])
        shared = shared / SHARED
        return (routed + shared).reshape(b, s, h)
    h = _L0_tok_ref(x, L0_tok_weight, L0_tok_bias, L0_tok_mask)
    h = h + _L0_attn_ref(_layernorm(h, axis=-1), L0_attn_W_qf, L0_attn_b_qf, L0_attn_W_kf, L0_attn_b_kf, L0_attn_W_vf, L0_attn_b_vf, L0_attn_W_qt, L0_attn_b_qt, L0_attn_W_kt, L0_attn_b_kt, L0_attn_W_vt, L0_attn_b_vt)
    h = h + _L0_ffn_ref(_layernorm(h, axis=-1), L0_ffn_router_w, L0_ffn_w1, L0_ffn_b1, L0_ffn_w2, L0_ffn_b2, L0_ffn_gamma, L0_ffn_beta)
    h = h + _L1_attn_ref(_layernorm(h, axis=-1), L1_attn_Wq, L1_attn_Wk, L1_attn_Wv, L1_attn_Wf, L1_attn_bf, L1_attn_Wo, L1_attn_ln_g, L1_attn_ln_b, L1_attn_eslots, L1_attn_Eq, L1_attn_Ek, L1_attn_Ev, L1_attn_Eo, L1_attn_know, L1_attn_Sin, L1_attn_Sg_w, L1_attn_Sg_b, L1_attn_So, L1_attn_C1w, L1_attn_C1b, L1_attn_C2w, L1_attn_C2b)
    h = h + _L1_ffn_ref(_layernorm(h, axis=-1), L1_ffn_gate_w, L1_ffn_biases, L1_ffn_w1, L1_ffn_w3, L1_ffn_w2, L1_ffn_sw1, L1_ffn_sw3, L1_ffn_sw2)
    h = h + _L2_attn_ref(_layernorm(h, axis=-1), L2_attn_in_proj_w, L2_attn_conv_w, L2_attn_conv_b, L2_attn_x_proj_w, L2_attn_dt_proj_w, L2_attn_dt_proj_b, L2_attn_A_log, L2_attn_D_param, L2_attn_out_proj_w, L2_attn_wq, L2_attn_wk, L2_attn_wv, L2_attn_fc_w, L2_attn_fc_b)
    h = h + _L2_ffn_ref(_layernorm(h, axis=-1), L2_ffn_rc_w1, L2_ffn_rc_b1, L2_ffn_rc_w2, L2_ffn_rc_b2, L2_ffn_sh_w1, L2_ffn_sh_b1, L2_ffn_sh_w2, L2_ffn_sh_b2, L2_ffn_e_w1, L2_ffn_e_b1, L2_ffn_e_w2, L2_ffn_e_b2, L2_ffn_ln_g, L2_ffn_ln_b)
    h = h + _L3_attn_ref(_layernorm(h, axis=-1), L3_attn_conv_w, L3_attn_conv_b, L3_attn_Wq, L3_attn_Mk_W2, L3_attn_Mk_W1, L3_attn_Mv_W2, L3_attn_Mv_W1, L3_attn_Meta_W2, L3_attn_Meta_W1, L3_attn_Malpha_W2, L3_attn_Malpha_W1, L3_attn_Mvh_W2, L3_attn_Mvh_W1, L3_attn_normk_g, L3_attn_normk_b, L3_attn_normq_g, L3_attn_normq_b, L3_attn_out_W, L3_attn_out_b)
    h = h + _L3_ffn_ref(_layernorm(h, axis=-1), L3_ffn_gate_w, L3_ffn_re_w1, L3_ffn_re_b1, L3_ffn_re_w2, L3_ffn_re_b2, L3_ffn_se_w1, L3_ffn_se_b1, L3_ffn_se_w2, L3_ffn_se_b2)
    return h

_drawn_inputs = setup_inputs


def setup_inputs(seed=0):
    import zlib

    import numpy as np

    out = dict(_drawn_inputs(seed))
    spreads = {'L0_tok_bias': (0.0, 0.1),
     'L0_ffn_b1': (0.0, 0.1),
     'L0_ffn_b2': (0.0, 0.1),
     'L0_ffn_gamma': (1.0, 0.2),
     'L0_ffn_beta': (0.0, 0.1),
     'L1_attn_bf': (0.0, 2.0),
     'L1_attn_ln_g': (1.0, 0.2),
     'L1_attn_ln_b': (0.0, 0.387),
     'L1_attn_Sg_b': (0.0, 0.8),
     'L1_attn_C1b': (0.0, 0.8),
     'L1_attn_C2b': (0.0, 0.292),
     'L1_ffn_biases': (0.0, 0.1),
     'L2_attn_conv_b': (0.0, 0.8),
     'L2_attn_dt_proj_b': (-4.600165843963623, 0.6),
     'L2_attn_D_param': (1.0, 0.6),
     'L2_attn_fc_b': (0.0, 0.439),
     'L2_ffn_rc_b1': (0.0, 1.525),
     'L2_ffn_rc_b2': (0.0, 0.526),
     'L2_ffn_sh_b1': (0.0, 2.0),
     'L2_ffn_sh_b2': (0.0, 0.638),
     'L2_ffn_e_b1': (0.0, 2.0),
     'L2_ffn_e_b2': (0.0, 0.954),
     'L2_ffn_ln_g': (1.0, 0.6),
     'L2_ffn_ln_b': (0.0, 0.628),
     'L3_attn_conv_b': (0.0, 0.8),
     'L3_attn_normk_g': (1.0, 0.6),
     'L3_attn_normk_b': (0.0, 0.8),
     'L3_attn_normq_g': (1.0, 0.6),
     'L3_attn_normq_b': (0.0, 0.8),
     'L3_attn_out_b': (0.0, 0.76),
     'L3_ffn_re_b1': (0.0, 0.8),
     'L3_ffn_re_b2': (0.0, 2.0),
     'L3_ffn_se_b1': (0.0, 0.8),
     'L3_ffn_se_b2': (0.0, 1.682)}
    factors = {'L0_attn_b_qf': 6.845,
     'L0_attn_b_kf': 8.0,
     'L0_attn_b_vf': 4.468,
     'L0_attn_b_vt': 2.677,
     'L1_attn_Wq': 7.685,
     'L1_attn_Wk': 5.128,
     'L1_attn_Wf': 33.651,
     'L1_attn_eslots': 8.0,
     'L1_attn_Eq': 8.0,
     'L1_attn_Ek': 8.0,
     'L1_attn_Ev': 8.0,
     'L1_attn_Eo': 8.0,
     'L1_attn_know': 8.0,
     'L1_attn_Sin': 24.917,
     'L1_attn_Sg_w': 4.079,
     'L1_attn_C1w': 8.0,
     'L1_attn_C2w': 8.0,
     'L2_attn_in_proj_w': 8.0,
     'L2_attn_conv_w': 8.0,
     'L2_attn_x_proj_w': 8.0,
     'L2_attn_dt_proj_w': 8.0,
     'L2_attn_A_log': 8.0,
     'L2_attn_out_proj_w': 8.0,
     'L2_attn_wq': 8.0,
     'L2_attn_wk': 8.0,
     'L2_attn_wv': 8.0,
     'L2_attn_fc_w': 8.0,
     'L3_attn_conv_w': 8.0,
     'L3_attn_Wq': 8.0,
     'L3_attn_Mk_W2': 8.0,
     'L3_attn_Mk_W1': 8.0,
     'L3_attn_Mv_W2': 8.0,
     'L3_attn_Mv_W1': 8.0,
     'L3_attn_Meta_W2': 8.0,
     'L3_attn_Meta_W1': 8.0,
     'L3_attn_Malpha_W2': 8.0,
     'L3_attn_Malpha_W1': 8.0,
     'L3_attn_Mvh_W2': 8.0,
     'L3_attn_Mvh_W1': 8.0,
     'L3_attn_out_W': 8.0,
     'L3_ffn_gate_w': 2.868,
     'L3_ffn_re_w1': 5.343,
     'L3_ffn_re_w2': 4.825,
     'L3_ffn_se_w1': 3.814,
     'L3_ffn_se_w2': 3.405,
     'L2_ffn_rc_w1': 3.822,
     'L2_ffn_rc_w2': 3.328,
     'L2_ffn_sh_w1': 3.203,
     'L2_ffn_e_w1': 7.415,
     'L2_ffn_e_w2': 3.245}
    for name, (base, spread) in spreads.items():
        noise = np.random.default_rng([zlib.crc32(name.encode()), seed]).standard_normal(out[name].shape)
        drawn = base * np.exp(spread * noise) if base else spread * noise
        out[name] = jnp.asarray(drawn.astype(out[name].dtype))
    for name, factor in factors.items():
        out[name] = (out[name] * factor).astype(out[name].dtype)
    return out
```

```python
from contextlib import ExitStack

import numpy as np

import concourse.bass as bass
from concourse import mybir

F32 = mybir.dt.float32
BF16 = mybir.dt.bfloat16
ALU = mybir.AluOpType
ACT = mybir.ActivationFunctionType
AX_X = mybir.AxisListType.X

STAGES = 9
D = 128
B, T = 64, 16
N = B * T
HALF = 512
NT = N // 128
G, GP = 5000, 125
GC = G // GP
NEG = -1.0e30


def pack_columns():
    first = [("ident", 128, 128), ("mean", 128, 128), ("tok_bias", 16, 128)]
    l0 = [("a0_nat", 128, 768), ("a0_natb", 128, 768), ("a0_vt", 128, 128), ("a0_vtb", 128, 1),
          ("f0_router", 128, 8), ("f0_beta", 8, 128), ("rank", 128, 16)]
    l1 = [("causal_sl", 128, 128), ("ones", 128, 128), ("a1_wq", 128, 64), ("a1_wk", 128, 64), ("a1_wf", 128, 64),
          ("a1_bf", 64, 1), ("a1_wv", 128, 128), ("a1_wo", 128, 128), ("a1_g", 128, 1), ("a1_b", 128, 1),
          ("a1_slots", 128, 32), ("a1_slots4", 128, 128), ("a1_eq", 128, 128), ("a1_ek", 128, 128),
          ("a1_ev", 128, 128), ("a1_eo", 128, 128), ("heads4", 128, 128), ("a1_sin", 128, 128),
          ("a1_knowT", 128, 64), ("a1_know", 64, 128), ("a1_sgw", 128, 128), ("a1_sgb", 128, 1),
          ("a1_so", 128, 128), ("a1_c1w", 128, 32), ("a1_c1b", 32, 1), ("a1_c2w", 32, 3), ("a1_c2b", 128, 3),
          ("sel3", 3, 384), ("f1_gate", 128, 8), ("f1_bias", 128, 8), ("f1_zero", 9, 128)]
    l2 = [("a2_in", 128, 512), ("a2_cw", 128, 8), ("a2_cb", 128, 2), ("a2_xp", 128, 80), ("a2_dtw", 8, 256),
          ("a2_dtb", 128, 2), ("a2_alog", 128, 32), ("a2_d", 128, 2), ("a2_out", 128, 256), ("a2_wq", 128, 128),
          ("a2_wk", 128, 128), ("a2_wv", 128, 128), ("a2_fc", 128, 128), ("a2_fcb", 128, 1), ("causal_add", 128, 128),
          ("f2_rc1", 128, 384), ("f2_rcb1", 128, 1), ("f2_rc2", 128, 30), ("f2_rcb2", 128, 10),
          ("f2_sh1", 128, 9 * 512), ("f2_shb1", 128, 4), ("f2_sh2", 128, 512), ("f2_shb2", 128, 1),
          ("f2_eb2", 10, 128), ("f2_g", 128, 1), ("f2_b", 128, 1)]
    l3 = [("a3_cw", 128, 4), ("a3_cb", 128, 1), ("a3_wq", 128, 512), ("a3_k2", 128, 64), ("a3_k1", 64, 512),
          ("a3_v2", 128, 64), ("a3_v1", 64, 512), ("a3_e2", 128, 64), ("a3_e1", 64, 8), ("a3_a2", 128, 64),
          ("a3_a1", 64, 8), ("a3_h2", 128, 256), ("a3_h1", 64, 512), ("a3_kg", 128, 512), ("a3_kb", 128, 512),
          ("a3_qg", 128, 512), ("a3_qb", 128, 512), ("a3_ow", 128, 512), ("a3_ob", 128, 1),
          ("strict_add", 128, 128), ("strict01", 128, 128), ("incl01", 128, 128),
          ("a3_one", 128, 1), ("f3_gate", 128, 16), ("f3_b2", 18, 128)]
    return [first, l0, l1, l2, l3]


FFN_COLUMNS = [512 + 512 + 4 + 3, 768, 512 + 512 + 4, 512 + 512 + 4]
FFN_EXPERTS = [8, 9, 10, 18]


LINES = {
    "a0_tensor": [
        ("a0_vps", 2), ("a0_proj", 8), ("a0_ctxfT", 1),
    ],
    "a1_tensor": [
        ("a1_qkf", 3), ("a1_v", 1), ("a1_c1", 1), ("a1_qh", 1), ("a1_qs", 1), ("a1_kv", 1), ("a1_se", 1),
        ("a1_ss", 1), ("a1_sc", 1), ("a1_sl", 1), ("a1_num", 1), ("a1_peT", 1), ("a1_psT", 1), ("a1_oh", 1),
        ("a1_eo", 1), ("a1_ret", 1), ("a1_sg", 1), ("a1_wo", 1), ("a1_pcT", 1), ("a1_so", 1), ("a1_bw", 3),
    ],
    "a2_tensor": [
        ("a2_xz", 4), ("a2_xp", 2), ("a2_dt", 2), ("a2_out", 1), ("a2_qk", 2), ("a2_v", 1), ("a2_s", 1),
        ("a2_atT", 1), ("a2_o", 1), ("a2_fc", 2),
    ],
    "a3_tensor": [
        ("a3_s", 4), ("a3_vps", 4), ("a3_h", 1), ("a3_ea", 1), ("a3_cum", 1), ("a3_o", 2),
    ],
    "a0_scalar": [
        ("a0_v", 2), ("a0_fexp", 1),
    ],
    "a1_scalar": [
        ("a1_sig", 1), ("a1_vcopy", 1), ("a1_exp2", 2), ("a1_qhcopy", 1), ("a1_silu", 1), ("a1_qscopy", 1),
        ("a1_ln", 1), ("a1_en", 1), ("a1_ep", 1), ("a1_eexp", 1), ("a1_sexp", 1), ("a1_cexp", 1),
        ("a1_peTcopy", 1), ("a1_psTcopy", 1), ("a1_ohcopy", 1), ("a1_gate", 1), ("a1_pcTcopy", 1),
    ],
    "a2_scalar": [
        ("a2_zg", 2), ("a2_xc", 2), ("a2_dtl", 1), ("a2_bcT", 1), ("a2_A", 1), ("a2_e", 2), ("a2_l", 2),
        ("a2_xm", 1), ("a2_qkcopy", 2), ("a2_vcopy", 1), ("a2_aexp", 1), ("a2_atTcopy", 1), ("a2_ocopy", 1),
    ],
    "a3_scalar": [
        ("a3_silu", 4), ("a3_vT", 4), ("a3_hsilu", 1), ("a3_e", 1), ("a3_l", 1),
    ],
    "a0_vector": [
        ("a0_nat", 8), ("a0_split", 9), ("a0_fshift", 1), ("a0_ctxf", 1),
    ],
    "a1_vector": [
        ("a1_min", 2), ("a1_sgmax", 1), ("a1_qk", 2), ("a1_kvm", 2), ("a1_cum", 1), ("a1_hat", 2),
        ("a1_eshift", 1), ("a1_sshift", 1), ("a1_cshift", 1), ("a1_slm", 1), ("a1_pe", 1), ("a1_ps", 1),
        ("a1_pc", 1), ("a1_w", 2), ("a1_sin_", 2), ("a1_mixed", 3),
    ],
    "a2_vector": [
        ("a2_conv", 2), ("a2_negA", 1), ("a2_nabs", 2), ("a2_dtx", 2), ("a2_ym", 2), ("a2_shift", 1),
        ("a2_att", 1),
    ],
    "a3_vector": [
        ("a3_x", 1), ("a3_nabs", 1), ("a3_la", 1), ("a3_negc", 1),
    ],
}


class Sems(dict):

    def __init__(self, make):
        super().__init__()
        self.make, self.log = make, []
        self.line = {name: line for line, results in LINES.items() for name, _ in results}

    def __missing__(self, name):
        line = self.line.get(name)
        self[name] = self[line] if line else self.make(name)
        return self[name]

    def base(self, name):
        base = 0
        for other, times in LINES.get(self.line.get(name), ()):
            if other == name:
                return base
            base += times
        return 0


class Order:

    def __init__(self, eng, sem, sems):
        self.eng, self.sem, self.sems, self.n = eng, sem, sems, 0
        self.told = {}
        self.i = None

    def loop(self, i, per):
        self.i, self.per, self.base, self.n = i, per, self.n, 0

    def end(self, times):
        assert self.n == self.per, (self.n, self.per)
        self.n, self.i = self.base + times * self.per, None

    def step(self, ins):
        self.n += 1
        ins.then_inc(self.sem, 1)
        if self.i is None:
            self.eng.wait_ge(self.sem, self.n)
        else:
            self.eng.wait_ge(self.sem, self.i * self.per + (self.base + self.n))

    def tell(self, ins, name):
        ins.then_inc(self.sems[name], 1)
        self.told[name] = self.told.get(name, 0) + 1

    def tell_step(self, ins, name):
        self.tell(ins, name)
        self.eng.wait_ge(self.sems[name], self.told[name] + self.sems.base(name))


def build(nc, a, out):
    ctx = ExitStack()
    with ctx:
        S = Sems(lambda name: ctx.enter_context(nc.semaphore("s_" + name)))

        def done(name, n):
            return S[name], n + S.base(name)

        def sb(name, shape, dt=F32):
            return ctx.enter_context(nc.sbuf_tensor(name, shape, dt))

        PS = ctx.enter_context(nc.psum_tensor("banks", [128, 8 * 512], F32))

        def bank(b, n=1, rows=128):
            return PS[0:rows, b * 512:(b + n) * 512]

        packs = pack_columns()
        width = [sum(c for _, _, c in p) for p in packs]
        WP = [sb(f"weights{k}", [128, w]) for k, w in enumerate(width)]
        where = {}
        for k, p in enumerate(packs):
            at = 0
            for name, rows, cols in p:
                where[name] = (k, rows, at, cols)
                at += cols

        def W(name, c0=0, c1=None):
            k, rows, at, cols = where[name]
            return WP[k][0:rows, at + c0:at + (cols if c1 is None else c1)]

        hT = sb("hT", [128, N])
        xT = sb("xT", [128, N])
        xc = sb("ln_xc", [128, N])
        sq = sb("ln_sq", [128, N])
        eps5 = sb("eps5", [128, 1])
        eps6 = sb("eps6", [128, 1])
        epsd = sb("epsd", [128, 1])
        BIG = sb("big", [128, 16 * N])
        POOLB = sb("bigb", [128, 6 * N])

        def big(k, n=1, rows=128):
            return BIG[0:rows, k * N:(k + n) * N]

        def bigb(k, n=1, rows=128):
            return POOLB[0:rows, k * N:(k + n) * N]

        spl_dram = nc.dram_tensor("spl_dram", [9, N, 128], BF16).ap()
        gates_dram = nc.dram_tensor("gates_dram", [4, 18, N], F32).ap()
        bc_dram = nc.dram_tensor("bc_dram", [32, N], F32).ap()

        def h(x, k):
            return x[:, k * HALF:(k + 1) * HALF]

        def mm(o, l, r, start=True, stop=True):
            return nc.tensor.matmul(o, l, r, start=start, stop=stop, skip_group_check=True)

        def tile(x, t):
            return x[:, t * 128:(t + 1) * 128]

        TQ, TSLOTS = 2, 4
        TGROUPS = GC // TQ
        tokw = BIG[0:GP, 0:TSLOTS * 16 * TQ * 128].rearrange("p (s e q d) -> p s e q d", s=TSLOTS, e=16, q=TQ)
        tokm = POOLB[0:GP, 0:TSLOTS * TQ * 128].rearrange("p (s q d) -> p s q d", s=TSLOTS, q=TQ)
        xg = POOLB[0:GP, N:N + GC * 64]
        wtok = a["tok_w"].rearrange("e (p c) d -> p e (c d)", p=GP)
        mtok = a["tok_m"].rearrange("(p c) d -> p (c d)", p=GP)

        def tok_load(sp, s, at):
            sp.dma_start(tokw[:, s].rearrange("p e q d -> p e (q d)"),
                         wtok[:, :, at]).then_inc(S[f"tok_loaded{s}"], 16)
            sp.dma_start(tokm[:, s].rearrange("p q d -> p (q d)"), mtok[:, at]).then_inc(S[f"tok_loaded{s}"], 16)

        def tok_sp(sp):
            sp.dma_start(xg, a["tok_x"]).then_inc(S["x_loaded"], 16)
            sp.dma_start(WP[0][:, :], a["pack0"]).then_inc(S["pack0"], 16)
            for s in range(TSLOTS):
                tok_load(sp, s, slice(s * TQ * 128, (s + 1) * TQ * 128))
            with sp.Fori(1, TGROUPS // TSLOTS) as i:
                for s in range(TSLOTS):
                    sp.wait_ge(*done("tok_used", i * TSLOTS + (s + 1 - TSLOTS)))
                    tok_load(sp, s, bass.ds(i * (TSLOTS * TQ * 128) + s * TQ * 128, TQ * 128))

        def tok_dve(dve, o):
            with dve.Fori(0, TGROUPS // TSLOTS) as i:
                for s in range(TSLOTS):
                    dve.wait_ge(*done(f"tok_loaded{s}", i * 32 + 32))
                    m = tokm[:, s].unsqueeze(1).to_broadcast([GP, 16, TQ, 128])
                    nc.vector.tensor_tensor(
                        tokw[:, s].rearrange("p e q d -> p e (q d)"), tokw[:, s].rearrange("p e q d -> p e (q d)"),
                        m.rearrange("p e q d -> p e (q d)"), ALU.mult).then_inc(S["tok_masked"], 1)
            dve.wait_ge(*done("tok_used", TGROUPS))
            hv = hT[:, :].rearrange("p (b e) -> p e b", e=16)
            for k in range(2):
                o.tell_step(nc.vector.tensor_copy(hv[:, 8 * k:8 * k + 8, :],
                                                  bank(k).rearrange("p (e b) -> p e b", b=64)), "h_ready")

        def tok_pe(pe):
            pe.wait_ge(*done("pack0", 16))
            pe.wait_ge(*done("x_loaded", 16))
            for k in range(2):
                r = W("ident")[0:16, 8 * k:8 * k + 8].unsqueeze(2).to_broadcast([16, 8, 64])
                mm(bank(k), W("tok_bias"), r, True, False)
            with pe.Fori(0, TGROUPS // TSLOTS) as i:
                for s in range(TSLOTS):
                    pe.wait_ge(*done("tok_masked", i * TSLOTS + (s + 1)))
                    for q in range(TQ):
                        x = xg[:, bass.ds(i * (TSLOTS * TQ * 64) + (s * TQ + q) * 64, 64)]
                        for e in range(16):
                            last = mm(PS[:, e * 64:(e + 1) * 64], tokw[:, s, e, q, :], x, False, False)
                    last.then_inc(S["tok_used"], 1)

        def ln_pe(pe, c, src, ready, rows=None):
            for k in range(2):
                pe.wait_ge(*done(ready[0], ready[1 + k]))
                mm(bank(6 + k), W("mean"), h(src, k)).then_inc(S["ln_mean"], 1)
            for k in range(2):
                pe.wait_ge(*done("ln_sq", 2 * c + k + 1))
                mm(bank(6 + k), W("mean"), h(sq, k)).then_inc(S["ln_var"], 1)

        def ln_act(act, c, eps):
            for k in range(2):
                act.wait_ge(*done("ln_xc", 2 * c + k + 1))
                nc.scalar.activation(h(sq, k), h(xc, k), ACT.Square).then_inc(S["ln_sq"], 1)
            for k in range(2):
                act.wait_ge(*done("ln_var", 2 * c + k + 1))
                nc.scalar.activation(h(sq, k), bank(6 + k), ACT.Sqrt, bias=eps[:, 0:1]).then_inc(S["ln_std"], 1)

        def ln_dve(dve, o, c, src, dst, gain=None, shift=None):
            for k in range(2):
                dve.wait_ge(*done("ln_mean", 2 * c + k + 1))
                o.tell_step(nc.vector.tensor_tensor(h(xc, k), h(src, k), bank(6 + k), ALU.subtract), "ln_xc")
            for k in range(2):
                dve.wait_ge(*done("ln_std", 2 * c + k + 1))
                o.step(nc.vector.reciprocal(h(sq, k), h(sq, k)))
                if gain is not None:
                    o.step(nc.vector.tensor_tensor(h(xc, k), h(xc, k), h(sq, k), ALU.mult))
                    o.tell_step(nc.vector.tensor_scalar(h(dst, k), h(xc, k), gain, shift, ALU.mult, ALU.add), "ln_out")
                else:
                    o.tell_step(nc.vector.tensor_tensor(h(dst, k), h(xc, k), h(sq, k), ALU.mult), "ln_out")

        nat = BIG[:, 0:8 * 768].rearrange("p (t c) -> p t c", c=768)
        neg_max = big(6)
        rest = big(7)
        spl = BIG[:, 8 * N:8 * N + 9 * 512].bitcast(BF16).rearrange("p (x t d) -> p x t d", x=9, d=128)
        expf = big(13)
        ctxf = big(14)
        ctxt = big(15)
        small = sb("small", [128, 96])
        v1 = bigb(0, 2).rearrange("p (n two) -> p n two", two=2)
        AG = 32
        BG = AG // 8
        v1s = sb("v1s", [128, 2, AG, 2])
        krows = BIG[0:12, 8 * N:12 * N].bitcast(BF16).rearrange("r (s c) -> r s c", s=2)
        qrows = [POOLB[0:12, 4 * N:6 * N].bitcast(BF16), BIG[0:12, 6 * N:8 * N].bitcast(BF16)]
        Ex = bigb(2, 2).rearrange("p (s c) -> p s c", s=2)
        rden = sb("rden", [128, 2, AG])
        AGROUPS = N // AG

        def a0_rows_load(sp, s, at):
            sl = S[f"a0_rows{s}"]
            k = spl_dram[3:6].rearrange("a n d -> a (n d)")[:, at]
            q = spl_dram[0:3].rearrange("a n d -> a (n d)")[:, at]
            m = spl_dram[6:9].rearrange("a n d -> a (n d)")[:, at]
            for j in range(3):
                sp.dma_start(krows[3 + 3 * j:6 + 3 * j, s, :], k).then_inc(sl, 16)
                sp.dma_start(qrows[s][3 + 3 * j:6 + 3 * j, :],
                             q[j:j + 1].to_broadcast([3, AG * 128])).then_inc(sl, 16)
            sp.dma_start(qrows[s][0:3, :], m).then_inc(sl, 16)

        def a0_sp(sp):
            sp.dma_start(WP[1][:, :], a["pack1"]).then_inc(S["pack1"], 16)
            for x in range(3):
                sp.wait_ge(*done("a0_split", 3 * x + 3))
                sp.dma_start(spl_dram[3 * x:3 * x + 3].rearrange("x (t p) d -> p x t d", p=128),
                             spl[:, 3 * x:3 * x + 3]).then_inc(S["a0_spl_out"], 16)
            sp.wait_ge(*done("a0_spl_out", 48))
            sp.wait_ge(*done("a0_ones", 2))
            for s in range(2):
                a0_rows_load(sp, s, slice(s * AG * 128, (s + 1) * AG * 128))
            with sp.Fori(1, AGROUPS // 2) as i:
                for s in range(2):
                    sp.wait_ge(*done("a0_arg", i * (2 * BG) + (BG * s + BG - 2 * BG)))
                    a0_rows_load(sp, s, bass.ds(i * (2 * AG * 128) + s * AG * 128, AG * 128))

        def a0_pool(pool):
            nc.gpsimd.memset(eps5[:, :], 1e-5).then_inc(S["eps"], 1)
            nc.gpsimd.memset(eps6[:, :], 1e-6).then_inc(S["eps"], 1)
            nc.gpsimd.memset(epsd[:, :], 1e-6).then_inc(S["eps"], 1)

        def a0_pool2(pool):
            pool.wait_ge(*done("tok_used", TGROUPS))
            nc.gpsimd.memset(v1[:, :, 1], 1.0).then_inc(S["a0_v1ones"], 1)
            pool.wait_ge(*done("a0_v1ones", 1))
            pool.wait_ge(*done("a0_spl_out", 48))
            nc.gpsimd.memset(krows[:, 0, :], 1.0).then_inc(S["a0_ones"], 1)
            nc.gpsimd.memset(krows[:, 1, :], 1.0).then_inc(S["a0_ones"], 1)
            pool.wait_ge(*done("a0_v", 2))
            for s in range(2):
                nc.gpsimd.tensor_copy(v1s[:, s], v1[:, s * AG:(s + 1) * AG, :]).then_inc(S["a0_v1s"], 1)
            with pool.Fori(1, AGROUPS // 2) as i:
                for s in range(2):
                    pool.wait_ge(*done("a0_pv", i * (2 * BG) + (BG * s + BG - 2 * BG + 2)))
                    nc.gpsimd.tensor_copy(v1s[:, s], v1[:, bass.ds(i * (2 * AG) + s * AG, AG), :]).then_inc(S["a0_v1s"], 1)

        def a0_pe(pe):
            pe.wait_ge(*done("pack1", 16))
            for k in range(2):
                pe.wait_ge(*done("ln_out", k + 1))
                mm(bank(4 + k), W("a0_vt"), h(xT, k)).then_inc(S["a0_vps"], 1)
            for t in range(NT):
                if t >= 2:
                    pe.wait_ge(*done("a0_nat", t - 1))
                b = 2 * (t % 2)
                mm(bank(b), tile(xT, t), W("a0_nat", 0, 512))
                mm(PS[:, (b + 1) * 512:(b + 1) * 512 + 256], tile(xT, t), W("a0_nat", 512, 768)).then_inc(S["a0_proj"], 1)
            pe.wait_ge(*done("a0_nat", 8))
            pe.wait_ge(*done("a0_v", 2))

            def args(i, s, j):
                b = BG * s + j
                if j == 0:
                    pe.wait_ge(*done(f"a0_rows{s}", i * 112 + 112))
                pe.wait_ge(*done("a0_exp", i * (2 * BG) + (b + 1)))
                for n in range(8):
                    t = j * 8 + n
                    last = mm(PS[:, (b % 2) * 1024 + n * 128:(b % 2) * 1024 + (n + 1) * 128],
                              krows[:, s, t * 128:(t + 1) * 128], qrows[s][:, t * 128:(t + 1) * 128])
                last.then_inc(S["a0_arg"], 1)

            def weigh(i, s, j):
                b = BG * s + j
                if j == 0:
                    pe.wait_ge(*done("a0_v1s", i * 2 + (s + 1)))
                    pe.wait_ge(*done("a0_ctx", i * 2 + (s + 1)))
                pe.wait_ge(*done("a0_exp", i * (2 * BG) + (b + 3)))
                for n in range(8):
                    t = j * 8 + n
                    last = mm(PS[:, (4 + s) * 512 + 2 * t:(4 + s) * 512 + 2 * t + 2],
                              Ex[:, b % 2, n * 128:(n + 1) * 128], v1s[:, s, t, :])
                last.then_inc(S["a0_pv"], 1)

            with pe.Fori(0, AGROUPS // 2) as i:
                args(i, 0, 0)
                for b in range(2 * BG):
                    if b < 2 * BG - 1:
                        args(i, (b + 1) // BG, (b + 1) % BG)
                    weigh(i, b // BG, b % BG)
            pe.wait_ge(*done("a0_ctxf", 1))
            for t in range(NT):
                last = nc.tensor.transpose(PS[:, t * 128:(t + 1) * 128], ctxf[:, t * 128:(t + 1) * 128], W("ident"))
            last.then_inc(S["a0_ctxfT"], 1)

        def a0_act(act, o):
            act.wait_ge(*done("tok_used", TGROUPS))
            for k in range(2):
                act.wait_ge(*done("a0_vps", k + 1))
                nc.scalar.activation(v1[:, k * HALF:(k + 1) * HALF, 0], bank(4 + k), ACT.Identity,
                                     bias=W("a0_vtb")).then_inc(S["a0_v"], 1)
            act.sem_inc(S["a0_exp"], 2)
            act.wait_ge(*done("a0_fshift", 1))
            nc.scalar.activation(expf, expf, ACT.Exp).then_inc(S["a0_fexp"], 1)
            with act.Fori(0, AGROUPS // 2) as i:
                for b in range(2 * BG):
                    act.wait_ge(*done("a0_arg", i * (2 * BG) + (b + 1)))
                    act.wait_ge(*done("a0_pv", i * (2 * BG) + (b + 1)))
                    nc.scalar.activation(Ex[:, b % 2, :], PS[:, (b % 2) * 1024:(b % 2 + 1) * 1024],
                                         ACT.Exp).then_inc(S["a0_exp"], 1)

        def a0_dve(dve, o):
            V = nc.vector
            for t in range(NT):
                dve.wait_ge(*done("a0_proj", t + 1))
                b = 2 * (t % 2)
                o.tell_step(V.tensor_tensor(nat[:, t, :], PS[:, b * 512:b * 512 + 768], W("a0_natb"), ALU.add), "a0_nat")
            qf, kf, vf, qt, kt = (nat[:, :, x * 128:(x + 1) * 128] for x in range(5))
            kmax, kmin = small[:, 0:8], small[:, 8:16]
            v3 = lambda x: x.rearrange("p (t d) -> p t d", d=128)
            bc = lambda x: x.unsqueeze(2).to_broadcast([128, 8, 128])
            o.step(V.tensor_reduce(kmax, kt, AX_X, ALU.max))
            o.step(V.tensor_reduce(kmin, kt, AX_X, ALU.min))
            o.step(V.tensor_scalar(small[:, 0:16], small[:, 0:16], -1.0, None, ALU.mult))
            o.step(V.tensor_tensor(v3(neg_max), qt, bc(kmax), ALU.mult))
            o.step(V.tensor_tensor(v3(rest), qt, bc(kmin), ALU.mult))
            o.step(V.tensor_tensor(neg_max, neg_max, rest, ALU.min))
            for x, src in enumerate((qt, kt, v3(neg_max))):
                o.tell_step(V.tensor_copy(spl[:, 3 * x], src), "a0_split")
                o.step(V.tensor_tensor(v3(rest), src, spl[:, 3 * x], ALU.subtract))
                o.tell_step(V.tensor_copy(spl[:, 3 * x + 1], v3(rest)), "a0_split")
                o.step(V.tensor_tensor(v3(rest), v3(rest), spl[:, 3 * x + 1], ALU.subtract))
                o.tell_step(V.tensor_copy(spl[:, 3 * x + 2], v3(rest)), "a0_split")
            fmax, fsum = small[:, 16:24], small[:, 24:32]
            o.step(V.tensor_tensor(v3(expf), qf, kf, ALU.mult))
            o.step(V.tensor_reduce(fmax, v3(expf), AX_X, ALU.max))
            o.tell_step(V.tensor_tensor(v3(expf), v3(expf), bc(fmax), ALU.subtract), "a0_fshift")
            dve.wait_ge(*done("a0_fexp", 1))
            o.step(V.tensor_reduce(fsum, v3(expf), AX_X, ALU.add))
            o.step(V.reciprocal(fsum, fsum))
            o.step(V.tensor_tensor(v3(ctxf), v3(expf), vf, ALU.mult))
            o.tell_step(V.tensor_tensor(v3(ctxf), v3(ctxf), bc(fsum), ALU.mult), "a0_ctxf")
            with dve.Fori(0, AGROUPS // 2) as i:
                o.loop(i, 2)
                for s in range(2):
                    dve.wait_ge(*done("a0_pv", i * (2 * BG) + (BG * s + BG + 2)))
                    pv = PS[:, (4 + s) * 512:(4 + s) * 512 + 2 * AG].rearrange("p (n two) -> p n two", two=2)
                    o.step(V.reciprocal(rden[:, s, :], pv[:, :, 1]))
                    V.tensor_tensor(ctxt[:, bass.ds(i * (2 * AG) + s * AG, AG)], pv[:, :, 0], rden[:, s, :],
                                    ALU.mult).then_inc(S["a0_ctx"], 1)
                o.end(AGROUPS // 2)
            dve.wait_ge(*done("a0_ctx", AGROUPS + 2))
            dve.wait_ge(*done("a0_ctxfT", 1))
            for k in range(2):
                o.step(V.tensor_tensor(h(hT, k), h(hT, k), h(ctxt, k), ALU.add))
                o.tell_step(V.tensor_tensor(h(hT, k), h(hT, k), bank(k), ALU.add), "h_ready")

        wslot = sb("wslot", [128, 2, max(FFN_COLUMNS)])
        gslot = sb("gslot", [128, 2, N])
        gT = sb("gT", [18, N])
        gtmp = sb("gtmp", [128, 14, 8 * 18])
        RH = 4
        hid = big(0, 2).rearrange("p (r c) -> p r c", r=RH)
        hidg = big(2, 2).rearrange("p (r c) -> p r c", r=RH)
        hid2 = big(4, 2).rearrange("p (r c) -> p r c", r=RH)
        acc = big(6)
        z0 = big(7)
        zc = big(8)
        zs = big(9)
        FC = [4, 2, 4, 4]
        RP = [4, 2, 4, 4]
        NU = [2 * c for c in FC]

        def gview(j, e):
            return gtmp[:, j, 0:8 * e].rearrange("p (t e) -> p t e", e=e)

        def gcol(j):
            return gtmp[:, j, 0:8]

        def gbc(x, e):
            return x.unsqueeze(2).to_broadcast([128, 8, e])

        def top(o, score, value, mark, idx, e, more):
            V = nc.vector
            rank = W("rank", 0, e).unsqueeze(1).to_broadcast([128, 8, e])
            o.step(V.tensor_reduce(value, score, AX_X, ALU.max))
            o.step(V.tensor_tensor(mark, score, gbc(value, e), ALU.is_equal))
            o.step(V.tensor_tensor(mark, mark, rank, ALU.mult))
            o.step(V.tensor_reduce(idx, mark, AX_X, ALU.max))
            o.step(V.tensor_tensor(mark, mark, gbc(idx, e), ALU.is_equal))
            if more:
                o.step(V.scalar_tensor_tensor(out=score, in0=mark, scalar=NEG, in1=score, op0=ALU.mult, op1=ALU.add))

        def router_pe(pe, k, lhs, wname, ready):
            e = FFN_EXPERTS[k] - {1: 1, 3: 2}.get(k, 0)
            pe.wait_ge(*done(ready[0], ready[1]))
            for t in range(NT):
                last = mm(PS[:, 1024 + t * e:1024 + (t + 1) * e], tile(lhs, t), W(wname))
            last.then_inc(S["logits"], 1)

        def gates_pe(pe, k):
            e = FFN_EXPERTS[k]
            pe.wait_ge(*done("gates", k + 1))
            for t in range(NT):
                last = nc.tensor.transpose(PS[0:e, 1024 + t * 128:1024 + (t + 1) * 128], gview(0, e)[:, t, :], W("ident"))
            last.then_inc(S["gatesT_ps"], 1)

        def gates_act(act, k):
            e = FFN_EXPERTS[k]
            act.wait_ge(*done("gatesT_ps", k + 1))
            nc.scalar.activation(gT[0:e, :], PS[0:e, 1024:2048], ACT.Copy).then_inc(S["gatesT"], 1)

        def ffn_load(sp, k, s, e):
            sp.dma_start(wslot[:, s, 0:FFN_COLUMNS[k]], a[f"ffn{k}"][e].rearrange("o p c -> (o p) c")).then_inc(S[f"f{k}_w{s}"], 16)

        def gate_load(sp, k, s, e):
            sp.dma_start(gslot[:, s, :], gates_dram[k][e].to_broadcast([128, N])).then_inc(S[f"f{k}_g{s}"], 16)

        def ffn_sp(sp, k):
            E = FFN_EXPERTS[k]
            if k == 1:
                sp.wait_ge(*done("h_ready", 6))
            if k:
                sp.wait_ge(*done(f"f{k - 1}_down", NU[k - 1] * FFN_EXPERTS[k - 1] + RH))
            for s in range(2):
                ffn_load(sp, k, s, slice(s, s + 1))
            sp.wait_ge(*done("gatesT", k + 1))
            sp.dma_start(gates_dram[k, 0:E], gT[0:E, :]).then_inc(S["gates_out"], 16)
            sp.wait_ge(*done("gates_out", 16 * (k + 1)))
            if k:
                sp.wait_ge(*done("h_ready", 4 * k + 2))
            for s in range(2):
                gate_load(sp, k, s, slice(s, s + 1))
            with sp.Fori(1, E // 2) as i:
                for s in range(2):
                    sp.wait_ge(*done(f"f{k}_down", i * (2 * NU[k]) + (NU[k] * (s - 1) + RH)))
                    if k == 0:
                        sp.wait_ge(*done("f0_sum", i * 4 + (2 * s + 2 - 4)))
                    ffn_load(sp, k, s, bass.ds(i * 2 + s, 1))
                    gate_load(sp, k, s, bass.ds(i * 2 + s, 1))
            if E % 2:
                sp.wait_ge(*done(f"f{k}_down", NU[k] * (E - 2) + RH))
                ffn_load(sp, k, 0, slice(E - 1, E))
                gate_load(sp, k, 0, slice(E - 1, E))

        def at(i, per, x):
            return i * per + x

        def w1_(k, s, f):
            return wslot[:, s, f * 128:(f + 1) * 128]

        def w2_(k, s, f):
            c = 512 + f * 128
            return wslot[:, s, c:c + 128]

        def ffn_up(pe, k, i, s, v):
            u, nu = v % NU[k], NU[k]
            if u == 0:
                pe.wait_ge(*done(f"f{k}_w{s}", i * 16 + 16))
            if k == 1:
                pe.wait_ge(*done("f1_gated", at(i, 2 * nu, v + 1 + RH - RP[1])))
                b = 2 * (v % 2)
                mm(bank(b), w1_(k, s, u // 2), h(xT, u % 2))
                mm(bank(b + 1), wslot[:, s, 256 + (u // 2) * 128:256 + (u // 2) * 128 + 128],
                   h(xT, u % 2)).then_inc(S["f1_up"], 1)
            else:
                pe.wait_ge(*done(f"f{k}_act", at(i, 2 * nu, v + 1)))
                mm(bank(v % 4), w1_(k, s, u // 2), h(xT, u % 2)).then_inc(S[f"f{k}_up"], 1)

        def ffn_down(pe, k, i, s, v):
            u, nu = v % NU[k], NU[k]
            if k == 0:
                if u < 2:
                    pe.wait_ge(*done("f0_z", at(i, 4, 2 * s + u + 1)))
                pe.wait_ge(*done("f0_act", at(i, 2 * nu, v + 1 + RP[0])))
                mm(bank(4 + u % 2), w2_(k, s, u // 2), hid[:, v % RH, :], u < 2, u >= nu - 2).then_inc(S["f0_down"], 1)
            else:
                pe.wait_ge(*done(f"f{k}_gated", at(i, 2 * nu, v + 1 + RH)))
                mm(bank(4 + u % 2), w2_(k, s, u // 2), hidg[:, v % RH, :], False, False).then_inc(S[f"f{k}_down"], 1)

        def ffn_units_pe(pe, k, i, experts):
            n = NU[k] * experts
            for v in range(n + 2):
                if v < n:
                    ffn_up(pe, k, i, v // NU[k], v)
                if v >= 2:
                    ffn_down(pe, k, i, (v - 2) // NU[k], v - 2)

        def ffn_pe(pe, k, bias):
            E = FFN_EXPERTS[k]
            pe.sem_inc(S[f"f{k}_down"], RH)
            pe.wait_ge(*done("gatesT", k + 1))
            for c in range(2):
                mm(bank(4 + c), bias, gT[0:E, c * HALF:(c + 1) * HALF], True, False)
            with pe.Fori(0, E // 2) as i:
                ffn_units_pe(pe, k, i, 2)
            if E % 2:
                ffn_units_pe(pe, k, E // 2, 1)

        def ffn_unit_act(act, k, i, s, v):
            u, nu = v % NU[k], NU[k]
            act.wait_ge(*done(f"f{k}_up", at(i, 2 * nu, v + 1)))
            if k == 0:
                act.wait_ge(*done("f0_down", at(i, 2 * nu, v + 1)))
                nc.scalar.activation(hid[:, v % RH, :], bank(v % 4), ACT.Relu,
                                     bias=wslot[:, s, 1024 + u // 2:1025 + u // 2]).then_inc(S["f0_act"], 1)
                return
            act.wait_ge(*done(f"f{k}_gated", at(i, 2 * nu, v + 1)))
            if k == 1:
                nc.scalar.activation(hid[:, v % RH, :], bank(2 * (v % 2)), ACT.Silu).then_inc(S["f1_act"], 1)
            elif k == 2:
                b1 = wslot[:, s, 1024 + u // 2:1025 + u // 2]
                nc.scalar.activation(hid[:, v % RH, :], bank(v % 4), ACT.Exp, bias=b1)
                nc.scalar.activation(hid2[:, v % RH, :], bank(v % 4), ACT.Relu, bias=b1).then_inc(S["f2_act"], 1)
            else:
                nc.scalar.activation(hid[:, v % RH, :], bank(v % 4), ACT.Gelu,
                                     bias=wslot[:, s, 1024 + u // 2:1025 + u // 2]).then_inc(S["f3_act"], 1)

        def ffn_act(act, k):
            E = FFN_EXPERTS[k]
            act.sem_inc(S[f"f{k}_act"], RP[k])
            with act.Fori(0, E // 2) as i:
                for v in range(2 * NU[k]):
                    ffn_unit_act(act, k, i, v // NU[k], v)
            if E % 2:
                for v in range(NU[k]):
                    ffn_unit_act(act, k, E // 2, 0, v)

        def ffn_unit_dve(dve, o, k, i, s, v):
            V = nc.vector
            u, nu = v % NU[k], NU[k]
            if u == 0:
                dve.wait_ge(*done(f"f{k}_g{s}", i * 16 + 16))
            dve.wait_ge(*done(f"f{k}_act", at(i, 2 * nu, v + 1 + RP[k])))
            dve.wait_ge(*done(f"f{k}_down", at(i, 2 * nu, v + 1)))
            g = gslot[:, s, (u % 2) * HALF:(u % 2 + 1) * HALF]
            hv = hid[:, v % RH, :]
            if k == 1:
                o.step(V.tensor_tensor(hv, hv, bank(2 * (v % 2) + 1), ALU.mult))
                V.tensor_tensor(hidg[:, v % RH, :], hv, g, ALU.mult).then_inc(S["f1_gated"], 1)
            elif k == 2:
                o.step(V.scalar_tensor_tensor(out=hv, in0=hv, scalar=1.0, in1=hid2[:, v % RH, :], op0=ALU.min, op1=ALU.add))
                V.scalar_tensor_tensor(out=hidg[:, v % RH, :], in0=hv, scalar=-1.0, in1=g, op0=ALU.add,
                                       op1=ALU.mult).then_inc(S["f2_gated"], 1)
            else:
                V.tensor_tensor(hidg[:, v % RH, :], hv, g, ALU.mult).then_inc(S[f"f{k}_gated"], 1)

        def ffn_dve(dve, o, k):
            E = FFN_EXPERTS[k]
            dve.sem_inc(S[f"f{k}_gated"], RH)
            steps = {1: 2 * NU[1], 2: 2 * NU[2]}.get(k, 0)
            with dve.Fori(0, E // 2) as i:
                o.loop(i, steps)
                for v in range(2 * NU[k]):
                    ffn_unit_dve(dve, o, k, i, v // NU[k], v)
                o.end(E // 2)
            if E % 2:
                for v in range(NU[k]):
                    ffn_unit_dve(dve, o, k, E // 2, 0, v)
            dve.wait_ge(*done(f"f{k}_down", NU[k] * E + RH))

        def f0_mean_pe(pe, i, s):
            for c in range(2):
                pe.wait_ge(*done("f0_z", at(i, 4, 2 * s + c + 1 + 2)))
                mm(bank(6 + c), W("mean"), h(z0, c)).then_inc(S["f0_mean"], 1)

        def f0_var_pe(pe, i, s):
            for c in range(2):
                pe.wait_ge(*done("f0_sq", at(i, 4, 2 * s + c + 1)))
                mm(bank(6 + c), W("mean"), h(zs, c)).then_inc(S["f0_var"], 1)

        def f0_pe(pe):
            pe.sem_inc(S["f0_down"], RH)
            pe.wait_ge(*done("gatesT", 1))
            n = NU[0]
            with pe.Fori(0, 4) as i:
                for v in range(2 * n + 2):
                    if v < 2 * n:
                        ffn_up(pe, 0, i, v // n, v)
                    if v >= 2:
                        ffn_down(pe, 0, i, (v - 2) // n, v - 2)
                    if v == n + 3:
                        f0_mean_pe(pe, i, 0)
                    if v == n + 5:
                        f0_var_pe(pe, i, 0)
                f0_mean_pe(pe, i, 1)
                f0_var_pe(pe, i, 1)
            pe.wait_ge(*done("f0_z", 18))
            for c in range(2):
                mm(bank(4 + c), W("f0_beta"), gT[0:8, c * HALF:(c + 1) * HALF]).then_inc(S["f0_beta"], 1)

        def f0_sq_act(act, i, s):
            for c in range(2):
                act.wait_ge(*done("f0_zc", at(i, 4, 2 * s + c + 1)))
                nc.scalar.activation(h(zs, c), h(zc, c), ACT.Square).then_inc(S["f0_sq"], 1)

        def f0_std_act(act, i, s):
            for c in range(2):
                act.wait_ge(*done("f0_var", at(i, 4, 2 * s + c + 1)))
                nc.scalar.activation(h(zs, c), bank(6 + c), ACT.Sqrt, bias=eps6[:, 0:1]).then_inc(S["f0_std"], 1)

        def f0_act(act):
            act.sem_inc(S["f0_act"], RP[0])
            n = NU[0]
            with act.Fori(0, 4) as i:
                for v in range(2 * n):
                    ffn_unit_act(act, 0, i, v // n, v)
                    if v == n + 3:
                        f0_sq_act(act, i, 0)
                    if v == n + 5:
                        f0_std_act(act, i, 0)
                f0_sq_act(act, i, 1)
                f0_std_act(act, i, 1)

        def f0_dve(dve, o):
            V = nc.vector
            dve.sem_inc(S["f0_z"], 2)
            o.step(V.memset(acc, 0.0))
            n = NU[0]
            with dve.Fori(0, 4) as i:
                o.loop(i, 12)
                for s in range(2):
                    dve.wait_ge(*done(f"f0_g{s}", i * 16 + 16))
                    for c in range(2):
                        dve.wait_ge(*done("f0_down", at(i, 2 * n, n * s + n - 1 + c + RH)))
                        V.scalar_tensor_tensor(out=h(z0, c), in0=bank(4 + c), scalar=wslot[:, s, 1028:1029],
                                               in1=h(xT, c), op0=ALU.add, op1=ALU.add).then_inc(S["f0_z"], 1)
                    for c in range(2):
                        dve.wait_ge(*done("f0_mean", at(i, 4, 2 * s + c + 1)))
                        V.tensor_tensor(h(zc, c), h(z0, c), bank(6 + c), ALU.subtract).then_inc(S["f0_zc"], 1)
                    for c in range(2):
                        dve.wait_ge(*done("f0_std", at(i, 4, 2 * s + c + 1)))
                        o.step(V.reciprocal(h(zs, c), h(zs, c)))
                        o.step(V.tensor_tensor(h(zc, c), h(zc, c), h(zs, c), ALU.mult))
                        o.step(V.scalar_tensor_tensor(out=h(zc, c), in0=h(zc, c), scalar=wslot[:, s, 1029:1030],
                                                      in1=gslot[:, s, c * HALF:(c + 1) * HALF], op0=ALU.mult, op1=ALU.mult))
                        V.tensor_tensor(h(acc, c), h(acc, c), h(zc, c), ALU.add).then_inc(S["f0_sum"], 1)
                o.end(4)
            dve.wait_ge(*done("f0_sum", 16))
            for c in range(2):
                dve.wait_ge(*done("f0_beta", c + 1))
                o.step(V.tensor_tensor(h(hT, c), h(hT, c), h(acc, c), ALU.add))
                o.tell_step(V.tensor_tensor(h(hT, c), h(hT, c), bank(4 + c), ALU.add), "h_ready")

        def softmax2(o, act_sem, k, v1_, v2_, g1, g2, d):
            V = nc.vector
            o.tell_step(V.tensor_tensor(d, v2_, v1_, ALU.subtract), f"g{k}_shift")
            o.eng.wait_ge(*done(f"g{k}_exp", 1))
            o.step(V.tensor_scalar(g1, d, 1.0, None, ALU.add))
            o.step(V.reciprocal(g1, g1))
            o.step(V.tensor_tensor(g2, d, g1, ALU.mult))

        def mix2(o, e, m1, m2, g1, g2, dst, k):
            V = nc.vector
            o.step(V.tensor_tensor(m1, m1, gbc(g1, e), ALU.mult))
            o.step(V.tensor_tensor(m2, m2, gbc(g2, e), ALU.mult))
            o.tell_step(V.tensor_tensor(dst, m1, m2, ALU.add), "gates")

        def g0_dve(dve, o):
            V = nc.vector
            dve.wait_ge(*done("logits", 1))
            lg, m1, m2, dst = gview(1, 8), gview(2, 8), gview(3, 8), gview(0, 8)
            o.step(V.tensor_copy(lg, PS[:, 1024:1024 + 64].rearrange("p (t e) -> p t e", e=8)))
            top(o, lg, gcol(4), m1, gcol(5), 8, True)
            top(o, lg, gcol(6), m2, gcol(5), 8, False)
            softmax2(o, None, 0, gcol(4), gcol(6), gcol(7), gcol(8), gcol(9))
            mix2(o, 8, m1, m2, gcol(7), gcol(8), dst, 0)

        def g_exp_act(act, k):
            act.wait_ge(*done(f"g{k}_shift", 1))
            nc.scalar.activation(gcol(9), gcol(9), ACT.Exp).then_inc(S[f"g{k}_exp"], 1)

        def g1_dve(dve, o):
            V = nc.vector
            dve.wait_ge(*done("logits", 2))
            lg, lb, m1, m2, mx = (gview(x, 8) for x in (1, 2, 3, 4, 5))
            o.step(V.tensor_copy(lg, PS[:, 1024:1024 + 64].rearrange("p (t e) -> p t e", e=8)))
            o.step(V.tensor_tensor(lb, lg, W("f1_bias").unsqueeze(1).to_broadcast([128, 8, 8]), ALU.add))
            top(o, lb, gcol(6), m1, gcol(7), 8, True)
            top(o, lb, gcol(6), m2, gcol(7), 8, False)
            v12 = gtmp[:, 8, 0:16]
            top(o, lg, gtmp[:, 8, 0:8], mx, gcol(7), 8, True)
            o.tell_step(V.tensor_reduce(gtmp[:, 8, 8:16], lg, AX_X, ALU.max), "g1_top")
            dve.wait_ge(*done("g1_sig", 1))
            o.step(V.tensor_tensor(gcol(9), gtmp[:, 8, 0:8], gtmp[:, 8, 8:16], ALU.add))
            o.step(V.reciprocal(gcol(9), gcol(9)))
            o.step(V.tensor_tensor(gcol(10), gtmp[:, 8, 0:8], gcol(9), ALU.mult))
            o.step(V.tensor_tensor(gcol(11), gtmp[:, 8, 8:16], gcol(9), ALU.mult))
            dst = gview(0, 9)
            o.step(V.memset(dst, 1.0))
            mix2(o, 8, m1, m2, gcol(10), gcol(11), dst[:, :, 0:8], 1)

        def g1_act(act):
            act.wait_ge(*done("g1_top", 1))
            nc.scalar.activation(gtmp[:, 8, 0:16], gtmp[:, 8, 0:16], ACT.Sigmoid).then_inc(S["g1_sig"], 1)

        def ffn_add_dve(dve, o, k):
            for c in range(2):
                o.tell_step(nc.vector.tensor_tensor(h(hT, c), h(hT, c), bank(4 + c), ALU.add), "h_ready")

        def a1_pe(pe):
            pe.wait_ge(*done("pack2", 16))
            pe.wait_ge(*done("ln_out", 6))
            for x, name in enumerate(("a1_wq", "a1_wk", "a1_wf")):
                for k in range(2):
                    last = mm(bank(2 * x + k, rows=64), W(name), h(xT, k))
                last.then_inc(S["a1_qkf"], 1)
            for t in range(NT):
                last = mm(PS[:, 3072 + t * 128:3072 + (t + 1) * 128], tile(xT, t), W("a1_wv"))
            last.then_inc(S["a1_v"], 1)
            pe.wait_ge(*done("a1_qk", 2))
            for k in range(2):
                last = mm(bank(k, rows=32), W("a1_c1w"), h(xT, k))
            last.then_inc(S["a1_c1"], 1)
            for k in range(2):
                last = mm(bank(2 + k), W("a1_eq"), h(xT, k))
            last.then_inc(S["a1_qh"], 1)
            pe.wait_ge(*done("a1_sig", 1))
            for k in range(2):
                last = mm(bank(4 + k), W("a1_sin"), h(xT, k))
            last.then_inc(S["a1_qs"], 1)
            pe.wait_ge(*done("a1_vcopy", 1))
            mm(PS[:, 3072:3072 + 32], W("a1_ek"), W("a1_slots"))
            mm(PS[:, 3584:3584 + 128], W("a1_slots4"), W("a1_ev")).then_inc(S["a1_kv"], 1)
            pe.wait_ge(*done("a1_kvm", 2))
            pe.wait_ge(*done("a1_qhcopy", 1))
            for t in range(NT):
                last = mm(PS[:, 1024 + t * 128:1024 + (t + 1) * 128], tile(qhT, t), khm)
            last.then_inc(S["a1_se"], 1)
            pe.wait_ge(*done("a1_qscopy", 1))
            for t in range(NT):
                last = mm(PS[:, 2048 + t * 64:2048 + (t + 1) * 64], tile(qsT, t), W("a1_knowT"))
            last.then_inc(S["a1_ss"], 1)
            pe.wait_ge(*done("a1_silu", 1))
            for t in range(NT):
                last = mm(PS[:, 2560 + t * 3:2560 + (t + 1) * 3], tile(c1, t), W("a1_c2w"))
            last.then_inc(S["a1_sc"], 1)
            pe.wait_ge(*done("a1_hat", 2))
            for t in range(NT):
                last = mm(PS[:, t * 128:(t + 1) * 128], tile(khat, t), tile(qhat, t))
            last.then_inc(S["a1_sl"], 1)
            pe.wait_ge(*done("a1_slm", 1))
            for t in range(NT):
                mm(PS[:, 3072 + t * 128:3072 + (t + 1) * 128], tile(vN, t), tile(slm, t))
            for k in range(2):
                last = mm(bank(k), W("ones"), h(slm, k))
            last.then_inc(S["a1_num"], 1)
            pe.wait_ge(*done("a1_pe", 1))
            for t in range(NT):
                last = nc.tensor.transpose(PS[:, 1024 + t * 128:1024 + (t + 1) * 128], tile(pE, t), W("ident"))
            last.then_inc(S["a1_peT"], 1)
            pe.wait_ge(*done("a1_ps", 1))
            for t in range(NT):
                last = nc.tensor.transpose(PS[0:64, 2048 + t * 128:2048 + (t + 1) * 128], pS[:, t * 64:(t + 1) * 64],
                                           W("ident"))
            last.then_inc(S["a1_psT"], 1)
            pe.wait_ge(*done("a1_peTcopy", 1))
            for k in range(2):
                last = mm(bank(2 + k), vhm, h(peT, k))
            last.then_inc(S["a1_oh"], 1)
            ln_pe(pe, 3, wn, ("a1_w", 1, 2))
            pe.wait_ge(*done("a1_ohcopy", 1))
            for k in range(2):
                last = mm(bank(2 + k), W("a1_eo"), h(ohT, k))
            last.then_inc(S["a1_eo"], 1)
            pe.wait_ge(*done("a1_psTcopy", 1))
            for k in range(2):
                last = mm(bank(k), W("a1_know"), h(psT, k))
            last.then_inc(S["a1_ret"], 1)
            for k in range(2):
                last = mm(bank(4 + k), W("a1_sgw"), h(xT, k))
            last.then_inc(S["a1_sg"], 1)
            for k in range(2):
                pe.wait_ge(*done("ln_out", 7 + k))
                last = mm(bank(6 + k), W("a1_wo"), h(wln, k))
            last.then_inc(S["a1_wo"], 1)
            pe.wait_ge(*done("a1_gate", 1))
            pe.wait_ge(*done("a1_pc", 1))
            for t in range(NT):
                last = nc.tensor.transpose(PS[0:3, 2048 + t * 128:2048 + (t + 1) * 128], pC[:, t * 3:(t + 1) * 3],
                                           W("ident"))
            last.then_inc(S["a1_pcT"], 1)
            pe.wait_ge(*done("a1_sin_", 2))
            for k in range(2):
                last = mm(bank(k), W("a1_so"), h(sIn, k))
            last.then_inc(S["a1_so"], 1)
            pe.wait_ge(*done("a1_pcTcopy", 1))
            for b in range(3):
                if b:
                    pe.wait_ge(*done("a1_mixed", b))
                for k in range(2):
                    last = mm(bank(4 + k), W("sel3", b * 128, (b + 1) * 128), wT[:, k * HALF:(k + 1) * HALF])
                last.then_inc(S["a1_bw"], 1)

        minq, mink = big(0, rows=64), big(1, rows=64)
        qhat, khat = big(2, rows=64), big(3, rows=64)
        slm, wn, vN, qhT, qsT, pE = big(4), big(5), big(10), big(11), big(12), big(13)
        logf, eneg, epos = big(6, rows=64), big(7, rows=64), big(8, rows=64)
        c1 = big(9, rows=32)
        pS = big(14)[:, 0:512]
        pC = big(14)[:, 512:536]
        pst = big(14)[:, 640:768]
        peT = big(15)
        psT, ohT, wln = bigb(0, rows=64), bigb(1), bigb(3)
        khm, vhm = bigb(4)[:, 0:128], bigb(4)[:, 128:256]
        wT = bigb(2, rows=3)
        reset = bigb(5)
        gS, sIn, rec = big(0), big(1), big(6)

        def a1_act(act, o):
            A = nc.scalar
            act.wait_ge(*done("pack2", 16))
            act.wait_ge(*done("a1_qkf", 3))
            A.activation(logf, PS[0:64, 2048:3072], ACT.Sigmoid, bias=W("a1_bf")).then_inc(S["a1_sig"], 1)
            act.wait_ge(*done("a1_v", 1))
            A.activation(vN, PS[:, 3072:4096], ACT.Copy).then_inc(S["a1_vcopy"], 1)
            for x, m in enumerate((minq, mink)):
                act.wait_ge(*done("a1_min", x + 1))
                A.activation(m, m, ACT.Exp).then_inc(S["a1_exp2"], 1)
            act.wait_ge(*done("a1_qh", 1))
            A.activation(qhT, PS[:, 1024:2048], ACT.Copy).then_inc(S["a1_qhcopy"], 1)
            act.wait_ge(*done("a1_c1", 1))
            A.activation(c1, PS[0:32, 0:1024], ACT.Silu, bias=W("a1_c1b")).then_inc(S["a1_silu"], 1)
            act.wait_ge(*done("a1_qs", 1))
            A.activation(qsT, PS[:, 2048:3072], ACT.Copy).then_inc(S["a1_qscopy"], 1)
            act.wait_ge(*done("a1_sgmax", 1))
            A.activation(logf, logf, ACT.Ln).then_inc(S["a1_ln"], 1)
            act.wait_ge(*done("a1_cum", 1))
            A.activation(eneg, logf, ACT.Exp, scale=-1.0).then_inc(S["a1_en"], 1)
            A.activation(epos, logf, ACT.Exp).then_inc(S["a1_ep"], 1)
            act.wait_ge(*done("a1_eshift", 1))
            A.activation(pE, pE, ACT.Exp, scale=32.0 ** -0.5).then_inc(S["a1_eexp"], 1)
            act.wait_ge(*done("a1_sshift", 1))
            A.activation(pS, pS, ACT.Exp, scale=128.0 ** -0.5).then_inc(S["a1_sexp"], 1)
            act.wait_ge(*done("a1_cshift", 1))
            A.activation(pC, pC, ACT.Exp).then_inc(S["a1_cexp"], 1)
            act.wait_ge(*done("a1_peT", 1))
            A.activation(peT, PS[:, 1024:2048], ACT.Copy).then_inc(S["a1_peTcopy"], 1)
            act.wait_ge(*done("a1_psT", 1))
            A.activation(psT, PS[0:64, 2048:3072], ACT.Copy).then_inc(S["a1_psTcopy"], 1)
            act.wait_ge(*done("a1_oh", 1))
            A.activation(ohT, PS[:, 1024:2048], ACT.Copy).then_inc(S["a1_ohcopy"], 1)
            ln_act(act, 3, eps5)
            act.wait_ge(*done("a1_sg", 1))
            A.activation(gS, PS[:, 2048:3072], ACT.Sigmoid, bias=W("a1_sgb")).then_inc(S["a1_gate"], 1)
            act.wait_ge(*done("a1_pcT", 1))
            A.activation(wT, PS[0:3, 2048:3072], ACT.Copy).then_inc(S["a1_pcTcopy"], 1)

        def a1_pool(pool):
            pool.wait_ge(*done("h_ready", 4))
            nc.gpsimd.memset(reset, 1.0).then_inc(S["reset"], 1)
            pool.wait_ge(*done("reset", 1))
            nc.gpsimd.memset(reset.rearrange("p (b t) -> p b t", t=T)[:, :, 0], 0.0).then_inc(S["reset"], 1)

        def soft_shift(o, dst, src, top_, grp, width, name, extra=None):
            V = nc.vector
            d3 = dst.rearrange("p (g w) -> p g w", w=width)
            s3 = src.rearrange("p (g w) -> p g w", w=width)
            if extra is not None:
                o.step(V.tensor_tensor(d3, s3, extra, ALU.add))
                s3 = d3
            o.step(V.tensor_reduce(top_, s3, AX_X, ALU.max))
            o.tell_step(V.tensor_tensor(d3, s3, top_.unsqueeze(2).to_broadcast([128, grp, width]), ALU.subtract), name)

        def soft_norm(o, x, sum_, grp, width, name):
            V = nc.vector
            x3 = x.rearrange("p (g w) -> p g w", w=width)
            o.step(V.tensor_reduce(sum_, x3, AX_X, ALU.add))
            o.step(V.reciprocal(sum_, sum_))
            o.tell_step(V.tensor_tensor(x3, x3, sum_.unsqueeze(2).to_broadcast([128, grp, width]), ALU.mult), name)

        def a1_dve(dve, o):
            V = nc.vector
            dve.wait_ge(*done("pack2", 16))
            for x, m in enumerate((minq, mink)):
                dve.wait_ge(*done("a1_qkf", x + 1))
                o.tell(V.tensor_scalar(m, PS[0:64, x * 1024:(x + 1) * 1024], 0.0, None, ALU.min), "a1_min")
            dve.wait_ge(*done("a1_sig", 1))
            o.tell(V.tensor_scalar(logf, logf, 1e-6, None, ALU.max), "a1_sgmax")
            for x, (m, dst) in enumerate(((minq, qhat), (mink, khat))):
                dve.wait_ge(*done("a1_exp2", x + 1))
                o.tell_step(V.scalar_tensor_tensor(out=dst, in0=PS[0:64, x * 1024:(x + 1) * 1024], scalar=0.0, in1=m,
                                                   op0=ALU.max, op1=ALU.add), "a1_qk")
            dve.wait_ge(*done("a1_kv", 1))
            hv = W("heads4")
            o.tell(V.tensor_tensor(khm.rearrange("p (h s) -> p h s", s=32),
                                   PS[:, 3072:3104].unsqueeze(1).to_broadcast([128, 4, 32]),
                                   hv.rearrange("p (h s) -> p h s", s=32), ALU.mult), "a1_kvm")
            o.tell(V.tensor_tensor(vhm, PS[:, 3584:3712], hv, ALU.mult), "a1_kvm")
            dve.wait_ge(*done("a1_ln", 1))
            dve.wait_ge(*done("reset", 2))
            o.step(V.tensor_tensor_scan(eneg, reset[0:64, :], logf, 0.0, ALU.mult, ALU.add))
            o.tell_step(V.tensor_scalar(logf, eneg, -20.0, 20.0, ALU.max, ALU.min), "a1_cum")
            dve.wait_ge(*done("a1_ep", 1))
            o.tell(V.scalar_tensor_tensor(out=qhat, in0=qhat, scalar=0.125, in1=epos, op0=ALU.mult, op1=ALU.mult), "a1_hat")
            o.tell(V.tensor_tensor(khat, khat, eneg, ALU.mult), "a1_hat")
            dve.wait_ge(*done("a1_se", 1))
            soft_shift(o, pE, PS[:, 1024:2048], pst[:, 0:32], 32, 32, "a1_eshift")
            dve.wait_ge(*done("a1_ss", 1))
            soft_shift(o, pS, PS[:, 2048:2560], pst[:, 32:40], 8, 64, "a1_sshift")
            dve.wait_ge(*done("a1_sc", 1))
            soft_shift(o, pC, PS[:, 2560:2584], pst[:, 40:48], 8, 3, "a1_cshift",
                       extra=W("a1_c2b").unsqueeze(1).to_broadcast([128, 8, 3]))
            dve.wait_ge(*done("a1_sl", 1))
            o.tell(V.tensor_tensor(slm.rearrange("p (t l) -> p t l", l=128), PS[:, 0:1024].rearrange("p (t l) -> p t l", l=128),
                                   W("causal_sl").unsqueeze(1).to_broadcast([128, 8, 128]), ALU.mult), "a1_slm")
            dve.wait_ge(*done("a1_eexp", 1))
            soft_norm(o, pE, pst[:, 0:32], 32, 32, "a1_pe")
            dve.wait_ge(*done("a1_sexp", 1))
            soft_norm(o, pS, pst[:, 32:40], 8, 64, "a1_ps")
            dve.wait_ge(*done("a1_cexp", 1))
            soft_norm(o, pC, pst[:, 40:48], 8, 3, "a1_pc")
            dve.wait_ge(*done("a1_num", 1))
            for k in range(2):
                o.step(V.tensor_scalar(h(rec, k), bank(k), 1e-6, None, ALU.add))
                o.step(V.reciprocal(h(rec, k), h(rec, k)))
                o.tell_step(V.tensor_tensor(h(wn, k), bank(6 + k), h(rec, k), ALU.mult), "a1_w")
            ln_dve(dve, o, 3, wn, wln, W("a1_g"), W("a1_b"))
            dve.wait_ge(*done("a1_ret", 1))
            dve.wait_ge(*done("a1_gate", 1))
            for k in range(2):
                o.step(V.tensor_tensor(h(sIn, k), bank(k), h(xT, k), ALU.subtract))
                o.step(V.tensor_tensor(h(sIn, k), h(sIn, k), h(gS, k), ALU.mult))
                o.tell_step(V.tensor_tensor(h(sIn, k), h(sIn, k), h(xT, k), ALU.add), "a1_sin_")
            for b, (ready, where_) in enumerate((("a1_wo", 6), ("a1_eo", 2), ("a1_so", 0))):
                dve.wait_ge(*done(ready, 1))
                o.step(V.tensor_copy(rec, PS[:, where_ * 512:(where_ + 2) * 512]))
                dve.wait_ge(*done("a1_bw", b + 1))
                o.tell_step(V.tensor_tensor(rec, rec, PS[:, 2048:3072], ALU.mult), "a1_mixed")
                for k in range(2):
                    ins = V.tensor_tensor(h(hT, k), h(hT, k), h(rec, k), ALU.add)
                    if b == 2:
                        o.tell_step(ins, "h_ready")
                    else:
                        o.step(ins)

        xcv = [big(0), big(1)]
        zg = [big(2), big(3)]
        dt = [big(4), big(5)]
        dtx = [big(6), big(7)]
        dA = [big(8), big(9)]
        dB = [big(10), big(11)]
        hs = [big(12), big(13)]
        hc = [big(14), big(15)]
        bcs = [[bigb(0), bigb(1)], [bigb(2), bigb(3)]]
        bcT = bigb(4, rows=32)
        dtl = gslot[0:8, 0, :]
        negA = sb("negA", [128, 32])
        ym = [big(8), big(9)]
        xm, q2, k2, v2, at2, atT, o2 = big(10), big(11), big(12), big(13), big(14), big(15), big(0)

        def bt(x):
            return x.rearrange("p (b t) -> p b t", t=T)

        def a2_pe(pe):
            pe.wait_ge(*done("pack3", 16))
            pe.wait_ge(*done("ln_out", 12))
            for x in range(4):
                for k in range(2):
                    last = mm(bank(2 * x + k), W("a2_in", x * 128, (x + 1) * 128), h(xT, k))
                last.then_inc(S["a2_xz"], 1)
            pe.wait_ge(*done("a2_xc", 2))
            for r0, r1, b0 in ((0, 8, 0), (8, 40, 2)):
                for k in range(2):
                    for c in range(2):
                        last = mm(bank(b0 + k, rows=r1 - r0), W("a2_xp", c * 40 + r0, c * 40 + r1), h(xcv[c], k), c == 0, c == 1)
                last.then_inc(S["a2_xp"], 1)
            pe.wait_ge(*done("a2_dtl", 1))
            for c in range(2):
                for k in range(2):
                    last = mm(bank(4 + 2 * c + k), W("a2_dtw", c * 128, (c + 1) * 128), h(dtl, k))
                last.then_inc(S["a2_dt"], 1)
            pe.wait_ge(*done("a2_bcT", 1))
            for b in range(4):
                mm(bank(b), W("f1_zero"), xT[0:9, 0:HALF], True, False)
            with pe.Fori(0, 8) as i:
                for s in range(2):
                    for c in range(2):
                        pe.wait_ge(*done("a2_hc", i * 4 + (2 * s + c + 1)))
                        for k in range(2):
                            last = mm(bank(2 * c + k), W("ident"), h(hc[c], k), False, False)
                        last.then_inc(S["a2_ysum"], 1)
            pe.wait_ge(*done("a2_ym", 2))
            for k in range(2):
                for c in range(2):
                    last = mm(bank(4 + k), W("a2_out", c * 128, (c + 1) * 128), h(ym[c], k), c == 0, c == 1)
            last.then_inc(S["a2_out"], 1)
            pe.wait_ge(*done("a2_xm", 1))
            for x, name in enumerate(("a2_wq", "a2_wk")):
                for k in range(2):
                    last = mm(bank(2 * x + k), W(name), h(xm, k))
                last.then_inc(S["a2_qk"], 1)
            for t in range(NT):
                last = mm(PS[:, 3072 + t * 128:3072 + (t + 1) * 128], tile(xm, t), W("a2_wv"))
            last.then_inc(S["a2_v"], 1)
            pe.wait_ge(*done("a2_qkcopy", 2))
            for t in range(NT):
                last = mm(PS[:, 2048 + t * 128:2048 + (t + 1) * 128], tile(q2, t), tile(k2, t))
            last.then_inc(S["a2_s"], 1)
            pe.wait_ge(*done("a2_att", 1))
            for t in range(NT):
                last = nc.tensor.transpose(PS[:, t * 128:(t + 1) * 128], tile(at2, t), W("ident"))
            last.then_inc(S["a2_atT"], 1)
            pe.wait_ge(*done("a2_atTcopy", 1))
            pe.wait_ge(*done("a2_vcopy", 1))
            for t in range(NT):
                last = mm(PS[:, 1024 + t * 128:1024 + (t + 1) * 128], tile(v2, t), tile(atT, t))
            last.then_inc(S["a2_o"], 1)
            pe.wait_ge(*done("a2_ocopy", 1))
            for k in range(2):
                mm(bank(4 + k), W("a2_fc"), h(o2, k)).then_inc(S["a2_fc"], 1)

        def a2_sp(sp):
            sp.wait_ge(*done("a2_bcT", 1))
            sp.dma_start(bc_dram, bcT).then_inc(S["a2_bcout"], 16)
            sp.wait_ge(*done("a2_bcout", 16))

            def load(s, b, c):
                sp.dma_start(bcs[s][0], b.to_broadcast([128, N])).then_inc(S[f"a2_bc{s}"], 16)
                sp.dma_start(bcs[s][1], c.to_broadcast([128, N])).then_inc(S[f"a2_bc{s}"], 16)

            for s in range(2):
                load(s, bc_dram[s:s + 1], bc_dram[16 + s:17 + s])
            with sp.Fori(1, 8) as i:
                for s in range(2):
                    sp.wait_ge(*done("a2_hc", i * 4 + (2 * s + 2 - 4)))
                    load(s, bc_dram[bass.ds(i * 2 + s, 1)], bc_dram[bass.ds(i * 2 + (s + 16), 1)])

        def a2_pool(pool):
            pool.wait_ge(*done("h_ready", 10))
            for c in range(2):
                nc.gpsimd.memset(bt(dA[c])[:, :, 0], 0.0).then_inc(S["a2_dA0"], 1)
            with pool.Fori(0, 8) as i:
                for s in range(2):
                    pool.wait_ge(*done(f"a2_bc{s}", i * 32 + 32))
                    for c in range(2):
                        if s == 0:
                            pool.wait_ge(*done("a2_dtx", 2))
                        pool.wait_ge(*done("a2_scan", i * 4 + (2 * s + c + 1)))
                        nc.gpsimd.tensor_tensor(dB[c], dtx[c], bcs[s][0], ALU.mult).then_inc(S["a2_dB"], 1)

        def a2_act(act, o):
            A = nc.scalar
            act.wait_ge(*done("pack3", 16))
            for c in range(2):
                act.wait_ge(*done("a2_xz", 3 + c))
                A.activation(zg[c], PS[:, (4 + 2 * c) * 512:(6 + 2 * c) * 512], ACT.Silu).then_inc(S["a2_zg"], 1)
            for c in range(2):
                act.wait_ge(*done("a2_conv", c + 1))
                A.activation(xcv[c], xcv[c], ACT.Silu, bias=W("a2_cb", c, c + 1)).then_inc(S["a2_xc"], 1)
            act.wait_ge(*done("a2_xp", 1))
            A.activation(dtl, PS[0:8, 0:1024], ACT.Copy).then_inc(S["a2_dtl"], 1)
            act.wait_ge(*done("a2_xp", 2))
            A.activation(bcT, PS[0:32, 1024:2048], ACT.Copy).then_inc(S["a2_bcT"], 1)
            A.activation(negA[:, :], W("a2_alog"), ACT.Exp).then_inc(S["a2_A"], 1)
            for c in range(2):
                act.wait_ge(*done("a2_nabs", c + 1))
                A.activation(hs[c], hs[c], ACT.Exp).then_inc(S["a2_e"], 1)
            for c in range(2):
                act.wait_ge(*done("a2_e", c + 1))
                A.activation(hs[c], hs[c], ACT.Ln, bias=W("ones", 0, 1)).then_inc(S["a2_l"], 1)
            act.wait_ge(*done("a2_negA", 1))
            act.wait_ge(*done("a2_dtx", 2))
            act.wait_ge(*done("a2_dA0", 2))
            with act.Fori(0, 8) as i:
                for s in range(2):
                    for c in range(2):
                        act.wait_ge(*done("a2_scan", i * 4 + (2 * s + c + 1)))
                        A.activation(bt(dA[c])[:, :, 1:], bt(dt[c])[:, :, 1:], ACT.Exp,
                                     scale=negA[:, bass.ds(i * 2 + (c * 16 + s), 1)]).then_inc(S["a2_dA"], 1)
            act.wait_ge(*done("a2_out", 1))
            A.activation(xm, PS[:, 2048:3072], ACT.Copy).then_inc(S["a2_xm"], 1)
            for x, dst in enumerate((q2, k2)):
                act.wait_ge(*done("a2_qk", x + 1))
                A.activation(dst, PS[:, x * 1024:(x + 1) * 1024], ACT.Copy).then_inc(S["a2_qkcopy"], 1)
            act.wait_ge(*done("a2_v", 1))
            A.activation(v2, PS[:, 3072:4096], ACT.Copy).then_inc(S["a2_vcopy"], 1)
            act.wait_ge(*done("a2_shift", 1))
            A.activation(at2, at2, ACT.Exp).then_inc(S["a2_aexp"], 1)
            act.wait_ge(*done("a2_atT", 1))
            A.activation(atT, PS[:, 0:1024], ACT.Copy).then_inc(S["a2_atTcopy"], 1)
            act.wait_ge(*done("a2_o", 1))
            A.activation(o2, PS[:, 1024:2048], ACT.Copy).then_inc(S["a2_ocopy"], 1)

        def a2_dve(dve, o):
            V = nc.vector
            dve.wait_ge(*done("pack3", 16))
            for c in range(2):
                dve.wait_ge(*done("a2_xz", c + 1))
                xi = bt(PS[:, c * 1024:(c + 1) * 1024])
                y = bt(xcv[c])
                o.step(V.tensor_scalar(y, xi, W("a2_cw", 4 * c + 3, 4 * c + 4), None, ALU.mult))
                for d in (1, 2, 3):
                    ins = V.scalar_tensor_tensor(out=y[:, :, d:], in0=xi[:, :, 0:T - d],
                                                 scalar=W("a2_cw", 4 * c + 3 - d, 4 * c + 4 - d), in1=y[:, :, d:],
                                                 op0=ALU.mult, op1=ALU.add)
                    if d < 3:
                        o.step(ins)
                    else:
                        o.tell_step(ins, "a2_conv")
            dve.wait_ge(*done("a2_A", 1))
            o.tell(V.tensor_scalar(negA[:, :], negA[:, :], -1.0, None, ALU.mult), "a2_negA")
            for c in range(2):
                dve.wait_ge(*done("a2_dt", c + 1))
                o.step(V.tensor_scalar(dt[c], PS[:, (4 + 2 * c) * 512:(6 + 2 * c) * 512], W("a2_dtb", c, c + 1), None, ALU.add))
                o.tell_step(V.scalar_tensor_tensor(out=hs[c], in0=dt[c], scalar=-1.0, in1=dt[c], op0=ALU.mult, op1=ALU.min),
                            "a2_nabs")
            dve.wait_ge(*done("a2_xc", 2))
            for c in range(2):
                dve.wait_ge(*done("a2_l", c + 1))
                o.step(V.scalar_tensor_tensor(out=dt[c], in0=dt[c], scalar=0.0, in1=hs[c], op0=ALU.max, op1=ALU.add))
                o.tell_step(V.tensor_tensor(dtx[c], dt[c], xcv[c], ALU.mult), "a2_dtx")
            dve.sem_inc(S["a2_scan"], 2)
            with dve.Fori(0, 8) as i:
                for s in range(2):
                    for c in range(2):
                        n = 2 * s + c
                        dve.wait_ge(*done("a2_dA", i * 4 + (n + 1)))
                        dve.wait_ge(*done("a2_dB", i * 4 + (n + 1)))
                        V.tensor_tensor_scan(hs[c], dA[c], dB[c], 0.0, ALU.mult, ALU.add).then_inc(S["a2_scan"], 1)
                        dve.wait_ge(*done("a2_scan", i * 4 + (n + 3)))
                        dve.wait_ge(*done("a2_ysum", i * 4 + (n + 1)))
                        V.tensor_tensor(hc[c], hs[c], bcs[s][1], ALU.mult).then_inc(S["a2_hc"], 1)
            dve.wait_ge(*done("a2_ysum", 34))
            for c in range(2):
                o.step(V.scalar_tensor_tensor(out=ym[c], in0=xcv[c], scalar=W("a2_d", c, c + 1),
                                              in1=PS[:, c * 1024:(c + 1) * 1024], op0=ALU.mult, op1=ALU.add))
                o.tell_step(V.tensor_tensor(ym[c], ym[c], zg[c], ALU.mult), "a2_ym")
            dve.wait_ge(*done("a2_s", 1))
            a3d = at2.rearrange("p (t l) -> p t l", l=128)
            o.step(V.scalar_tensor_tensor(out=a3d, in0=PS[:, 2048:3072].rearrange("p (t l) -> p t l", l=128),
                                          scalar=128.0 ** -0.5, in1=W("causal_add").unsqueeze(1).to_broadcast([128, 8, 128]),
                                          op0=ALU.mult, op1=ALU.add))
            soft_shift(o, at2, at2, small[:, 32:40], 8, 128, "a2_shift")
            dve.wait_ge(*done("a2_aexp", 1))
            soft_norm(o, at2, small[:, 32:40], 8, 128, "a2_att")
            for k in range(2):
                dve.wait_ge(*done("a2_fc", k + 1))
                o.tell_step(V.scalar_tensor_tensor(out=h(hT, k), in0=bank(4 + k), scalar=W("a2_fcb"), in1=h(hT, k),
                                                   op0=ALU.add, op1=ALU.add), "h_ready")

        xpad = BIG[:, 10 * N:10 * N + 64 * 24].rearrange("p (b t) -> p b t", t=24)
        rpad = BIG[:, 12 * N:12 * N + 64 * 24].rearrange("p (b t) -> p b t", t=24)
        lnz = big(7)
        lno = big(9)

        def f2_pool(pool):
            pool.wait_ge(*done("h_ready", 12))
            nc.gpsimd.memset(xpad, 0.0).then_inc(S["f2_pad0"], 1)
            nc.gpsimd.memset(rpad, 0.0).then_inc(S["f2_pad0"], 1)

        def f2_pe(pe):
            pe.wait_ge(*done("f2_xpad", 1))
            for k in range(2):
                for j in range(3):
                    last = mm(bank(k).rearrange("p (b t) -> p b t", t=T), W("f2_rc1", j * 128, (j + 1) * 128),
                              xpad[:, 32 * k:32 * k + 32, 3 + j:19 + j], j == 0, j == 2)
            last.then_inc(S["f2_rc"], 1)
            pe.wait_ge(*done("f2_rpad", 1))
            for k in range(2):
                for j in range(3):
                    last = mm(bank(2 + k, rows=10).rearrange("p (b t) -> p b t", t=T), W("f2_rc2", j * 10, (j + 1) * 10),
                              rpad[:, 32 * k:32 * k + 32, 3 + j:19 + j], j == 0, j == 2)
            last.then_inc(S["f2_lt"], 1)
            pe.wait_ge(*done("f2_ltcopy", 1))
            for t in range(NT):
                last = nc.tensor.transpose(PS[:, 1024 + t * 10:1024 + (t + 1) * 10], gT[0:10, t * 128:(t + 1) * 128],
                                           W("ident")[0:10, 0:10])
            last.then_inc(S["logits"], 1)
            ring = [0, 1, 6, 7]

            def sh_down(u):
                pe.wait_ge(*done("f2_shact", u + 1))
                mm(bank(4 + u % 2), W("f2_sh2", (u // 2) * 128, (u // 2) * 128 + 128), hid[:, u % RH, :], u < 2,
                   False).then_inc(S["f2_shdown"], 1)

            for u in range(8):
                if u >= 4:
                    pe.wait_ge(*done("f2_shact", u - 3))
                for j in range(9):
                    c0 = j * 512 + (u // 2) * 128
                    last = mm(bank(ring[u % 4]).rearrange("p (b t) -> p b t", t=T), W("f2_sh1", c0, c0 + 128),
                              xpad[:, 32 * (u % 2):32 * (u % 2) + 32, j:j + T], j == 0, j == 8)
                last.then_inc(S["f2_shup"], 1)
                if u >= 1:
                    sh_down(u - 1)
            sh_down(7)
            gates_pe(pe, 2)

        def f2_loop_pe(pe):
            pe.sem_inc(S["f2_down"], RH)
            pe.wait_ge(*done("gatesT", 3))
            for c in range(2):
                mm(bank(4 + c), W("f2_eb2"), gT[0:10, c * HALF:(c + 1) * HALF], False, False)
            with pe.Fori(0, 5) as i:
                ffn_units_pe(pe, 2, i, 2)

        def f2_act(act, o):
            A = nc.scalar
            act.wait_ge(*done("f2_pad0", 2))
            act.wait_ge(*done("ln_out", 14))
            A.activation(xpad[:, :, 4:20], bt(xT[:, :]), ACT.Copy).then_inc(S["f2_xpad"], 1)
            act.wait_ge(*done("f2_rc", 1))
            A.activation(rpad[:, :, 4:20], bt(PS[:, 0:1024]), ACT.Gelu, bias=W("f2_rcb1")).then_inc(S["f2_rpad"], 1)
            act.wait_ge(*done("f2_lt", 1))
            A.activation(gT[0:10, :], PS[0:10, 1024:2048], ACT.Copy).then_inc(S["f2_ltcopy"], 1)
            for u in range(8):
                act.wait_ge(*done("f2_shup", u + 1))
                if u >= RH:
                    act.wait_ge(*done("f2_shdown", u - RH + 1))
                A.activation(hid[:, u % RH, :], bank([0, 1, 6, 7][u % 4]), ACT.Silu,
                             bias=W("f2_shb1", u // 2, u // 2 + 1)).then_inc(S["f2_shact"], 1)
            g_exp_act(act, 2)
            gates_act(act, 2)
            ffn_act(act, 2)

        def f2_dve(dve, o):
            V = nc.vector
            dve.wait_ge(*done("logits", 3))
            lg, m1, m2, dst = gview(1, 10), gview(2, 10), gview(3, 10), gview(0, 10)
            o.step(V.tensor_tensor(lg, PS[:, 1024:1024 + 80].rearrange("p (t e) -> p t e", e=10),
                                   W("f2_rcb2").unsqueeze(1).to_broadcast([128, 8, 10]), ALU.add))
            top(o, lg, gcol(4), m1, gcol(5), 10, True)
            top(o, lg, gcol(6), m2, gcol(5), 10, False)
            softmax2(o, None, 2, gcol(4), gcol(6), gcol(7), gcol(8), gcol(9))
            mix2(o, 10, m1, m2, gcol(7), gcol(8), dst, 2)
            ffn_dve(dve, o, 2)
            for k in range(2):
                o.tell_step(V.scalar_tensor_tensor(out=h(lnz, k), in0=bank(4 + k), scalar=W("f2_shb2"), in1=h(xT, k),
                                                   op0=ALU.add, op1=ALU.add), "f2_z")
            ln_dve(dve, o, 7, lnz, lno, W("f2_g"), W("f2_b"))
            for k in range(2):
                o.tell_step(V.tensor_tensor(h(hT, k), h(hT, k), h(lno, k), ALU.add), "h_ready")

        x3 = big(0)
        sk3, sv3, se3, sa3 = (big(1 + j, rows=64) for j in range(4))
        vT3 = [big(5 + j) for j in range(4)]
        sh3 = big(9, rows=64)
        vh3 = big(5, 4).rearrange("p (t c) -> p t c", c=512)
        kT3 = big(10, 4).rearrange("p (g n) -> p g n", n=N)
        qT3 = bigb(0, 4).rearrange("p (g n) -> p g n", n=N)
        kw = big(14).rearrange("p (r c) -> p r c", r=2)
        qw = big(15).rearrange("p (r c) -> p r c", r=2)
        sqk = bigb(4).rearrange("p (r c) -> p r c", r=2)
        st3 = sb("st3", [128, 2, 32])
        la3 = sb("la3", [128, 5, 64])
        yT3 = big(0, 4).rearrange("p (g n) -> p g n", n=N)
        dec = [big(4), xT[:, :]]
        mt3 = [big(14), big(15)]
        pt3 = [bigb(4), bigb(5)]
        ue3 = big(9).rearrange("p (r c) -> p r c", r=2)
        uu3 = xc[:, :].rearrange("p (r c) -> p r c", r=2)
        ITERS = T - 1

        def hpos(hd):
            return slice(((hd % 2) * 4 + hd // 2) * 128, ((hd % 2) * 4 + hd // 2 + 1) * 128)

        def h8(x):
            return x.rearrange("p (h d) -> p h d", h=8)

        def a3_pe(pe):
            pe.wait_ge(*done("pack4", 16))
            pe.wait_ge(*done("a3_x", 1))
            for j, name in enumerate(("a3_k2", "a3_v2", "a3_e2", "a3_a2")):
                for k in range(2):
                    last = mm(bank(2 * j + k, rows=64), W(name), h(x3, k))
                last.then_inc(S["a3_s"], 1)
            pe.wait_ge(*done("a3_silu", 4))
            for f in range(4):
                if f >= 2:
                    pe.wait_ge(*done("a3_vT", f - 1))
                for k in range(2):
                    last = mm(bank(2 * (f % 2) + k), W("a3_v1", f * 128, (f + 1) * 128), h(sv3, k))
                last.then_inc(S["a3_vps"], 1)
            pe.wait_ge(*done("a3_vT", 4))
            for k in range(2):
                for f in range(4):
                    last = mm(bank(4 + k, rows=64), W("a3_h2", f * 64, (f + 1) * 64), h(vT3[f], k), f == 0, f == 3)
            last.then_inc(S["a3_h"], 1)
            for t in range(NT):
                mm(PS[:, 3072 + t * 8:3072 + (t + 1) * 8], tile(se3, t), W("a3_e1"))
                last = mm(PS[:, 3136 + t * 8:3136 + (t + 1) * 8], tile(sa3, t), W("a3_a1"))
            last.then_inc(S["a3_ea"], 1)
            pe.wait_ge(*done("a3_hsilu", 1))
            pe.wait_ge(*done("a3_la", 1))
            mm(PS[:, 3584:3648], W("incl01"), la3[:, 0, :]).then_inc(S["a3_cum"], 1)
            pe.wait_ge(*done("a3_negc", 1))

            def turn(t):
                j = t % 2
                pe.wait_ge(*done("a3_kn", t + 1))
                if t:
                    pe.wait_ge(*done("a3_kqT", 2 * t))
                for g in range(4):
                    last = nc.tensor.transpose(PS[:, 3072 + g * 128:3072 + (g + 1) * 128], kw[:, j, g * 128:(g + 1) * 128],
                                               W("ident"))
                last.then_inc(S["a3_turn"], 1)
                pe.wait_ge(*done("a3_qn", t + 1))
                for g in range(4):
                    last = nc.tensor.transpose(PS[:, 3584 + g * 128:3584 + (g + 1) * 128], qw[:, j, g * 128:(g + 1) * 128],
                                               W("ident"))
                last.then_inc(S["a3_turn"], 1)

            for t in range(NT):
                j = t % 2
                if t >= 2:
                    pe.wait_ge(*done("a3_kraw", t - 1))
                    pe.wait_ge(*done("a3_qraw", t - 1))
                    pe.wait_ge(*done("a3_vh", t - 1))
                mm(bank(j), tile(sk3, t), W("a3_k1")).then_inc(S["a3_kqv"], 1)
                mm(bank(2 + j), tile(x3, t), W("a3_wq")).then_inc(S["a3_kqv"], 1)
                mm(bank(4 + j), tile(sv3, t), W("a3_v1"), True, False)
                mm(bank(4 + j), tile(sh3, t), W("a3_h1"), False, True).then_inc(S["a3_kqv"], 1)
                if t >= 1:
                    turn(t - 1)
            turn(NT - 1)
            pe.wait_ge(*done("a3_kqT", 2 * NT))
            pe.wait_ge(*done("a3_vh", NT))

            for p in range(NT // 2):
                for j in range(2):
                    t = 2 * p + j
                    if t:
                        pe.wait_ge(*done("a3_m", t))
                    for hd in range(8):
                        last = mm(PS[:, hpos(hd)],
                                  la3[:, 0, t * 8 + hd:t * 8 + hd + 1].to_broadcast([128, 128]), W("strict01"))
                    last.then_inc(S["a3_cex"], 1)
                    for b0, src in ((1024, kT3), (2048, qT3)):
                        if t:
                            pe.wait_ge(*done("a3_gq", 2 * t - (1 if b0 == 1024 else 0)))
                        for hd in range(8):
                            r = slice((hd % 2) * 64, (hd % 2) * 64 + 64)
                            kk = kT3[r, hd // 2, t * 128:(t + 1) * 128]
                            last = mm(PS[:, b0:b0 + 1024][:, hpos(hd)], kk, src[r, hd // 2, t * 128:(t + 1) * 128])
                        last.then_inc(S["a3_gqps"], 1)
                    pe.wait_ge(*done("a3_dm", t + 1))
                    for hd in range(8):
                        last = mm(PS[:, hpos(hd)],
                                  la3[:, 1, t * 8 + hd:t * 8 + hd + 1].to_broadcast([128, 128]), W("ident"))
                    last.then_inc(S["a3_eb"], 1)
                pe.wait_ge(*done("a3_m", 2 * p + 2))
                with pe.Fori(0, ITERS) as i:
                    for j in range(2):
                        pe.wait_ge(*done("a3_u", i * 2 + (p * (2 * ITERS + 2) + j + 1)))
                        for hd in range(8):
                            last = mm(PS[:, (6 + j) * 512 + hd * 64:(6 + j) * 512 + (hd + 1) * 64],
                                      mt3[j][:, hpos(hd)], uu3[:, j, hd * 64:(hd + 1) * 64])
                        last.then_inc(S["a3_w"], 1)
                pe.wait_ge(*done("a3_u", (p + 1) * (2 * ITERS + 2)))
                pe.wait_ge(*done("a3_gq", 4 * p + 4))
                for j in range(2):
                    for hd in range(8):
                        c = (6 + j) * 512 + (hd // 2) * 128
                        last = mm(PS[(hd % 2) * 64:(hd % 2) * 64 + 64, c:c + 128], uu3[:, j, hd * 64:(hd + 1) * 64],
                                  pt3[j][:, hpos(hd)])
                    last.then_inc(S["a3_y"], 1)
            pe.wait_ge(*done("a3_yT", NT))
            for k in range(2):
                for g in range(4):
                    last = mm(bank(4 + k), W("a3_ow", g * 128, (g + 1) * 128), yT3[:, g, k * HALF:(k + 1) * HALF], g == 0, g == 3)
                last.then_inc(S["a3_o"], 1)

        def a3_act(act, o):
            A = nc.scalar
            act.wait_ge(*done("pack4", 16))
            for j, dst in enumerate((sk3, sv3, se3, sa3)):
                act.wait_ge(*done("a3_s", j + 1))
                A.activation(dst, PS[0:64, 2 * j * 512:(2 * j + 2) * 512], ACT.Silu).then_inc(S["a3_silu"], 1)
            for f in range(4):
                act.wait_ge(*done("a3_vps", f + 1))
                A.activation(vT3[f], PS[:, (f % 2) * 1024:(f % 2 + 1) * 1024], ACT.Copy).then_inc(S["a3_vT"], 1)
            act.wait_ge(*done("a3_h", 1))
            A.activation(sh3, PS[0:64, 2048:3072], ACT.Silu).then_inc(S["a3_hsilu"], 1)
            act.wait_ge(*done("a3_nabs", 1))
            A.activation(la3[:, 2:4, :], la3[:, 2:4, :], ACT.Exp).then_inc(S["a3_e"], 1)
            act.wait_ge(*done("a3_e", 1))
            A.activation(la3[:, 2:4, :], la3[:, 2:4, :], ACT.Ln, bias=W("a3_one")).then_inc(S["a3_l"], 1)
            for t in range(NT):
                j = t % 2
                act.wait_ge(*done("a3_kqv", 3 * t + 3))
                A.activation(vh3[:, t, :], bank(4 + j), ACT.Copy).then_inc(S["a3_vh"], 1)
                act.wait_ge(*done("a3_mv", t + 1))
                A.activation(st3[:, j, 16:18], st3[:, j, 12:16].rearrange("p (x y) -> p x y", y=2)[:, :, 1], ACT.Sqrt,
                             bias=eps5[:, 0:1]).then_inc(S["a3_sd"], 1)
                act.wait_ge(*done("a3_kk", t + 1))
                A.activation(sqk[:, j, :], kw[:, j, :], ACT.Square).then_inc(S["a3_sq"], 1)
                act.wait_ge(*done("a3_n2", t + 1))
                A.activation(st3[:, j, 18:26], st3[:, j, 18:26], ACT.Sqrt).then_inc(S["a3_nrm"], 1)
                for x, dst in enumerate((kT3, qT3)):
                    act.wait_ge(*done("a3_turn", 2 * t + x + 1))
                    A.activation(dst[:, :, t * 128:(t + 1) * 128], bank(6 + x).rearrange("p (g c) -> p g c", g=4),
                                 ACT.Copy).then_inc(S["a3_kqT"], 1)
            for p in range(NT // 2):
                for j in range(2):
                    t = 2 * p + j
                    act.wait_ge(*done("a3_dm", t + 1))
                    for hd in range(8):
                        c = hpos(hd)
                        last = A.activation(dec[j][:, c], dec[j][:, c], ACT.Exp,
                                            bias=la3[:, 4, t * 8 + hd:t * 8 + hd + 1])
                    last.then_inc(S["a3_dec"], 1)
                for j in range(2):
                    t = 2 * p + j
                    act.wait_ge(*done("a3_y", t + 1))
                    A.activation(yT3[:, :, t * 128:(t + 1) * 128], bank(6 + j).rearrange("p (g c) -> p g c", g=4),
                                 ACT.Copy).then_inc(S["a3_yT"], 1)

        def a3_dve(dve, o):
            V = nc.vector
            dve.wait_ge(*done("pack4", 16))
            x, y = bt(xT[:, :]), bt(x3)
            o.step(V.tensor_scalar(y, x, W("a3_cw", 3, 4), W("a3_cb"), ALU.mult, ALU.add))
            for d in (1, 2, 3):
                o.step(V.scalar_tensor_tensor(out=y[:, :, d:], in0=x[:, :, 0:T - d], scalar=W("a3_cw", 3 - d, 4 - d),
                                              in1=y[:, :, d:], op0=ALU.mult, op1=ALU.add))
            o.tell_step(V.tensor_tensor(x3, x3, xT[:, :], ALU.add), "a3_x")
            dve.wait_ge(*done("a3_ea", 1))
            o.step(V.tensor_copy(la3[:, 1, :], PS[:, 3072:3136]))
            o.step(V.tensor_scalar(la3[:, 0, :], PS[:, 3136:3200], -1.0, None, ALU.mult))
            o.tell_step(V.scalar_tensor_tensor(out=la3[:, 2:4, :], in0=la3[:, 0:2, :], scalar=-1.0, in1=la3[:, 0:2, :],
                                               op0=ALU.mult, op1=ALU.min), "a3_nabs")
            dve.wait_ge(*done("a3_l", 1))
            o.step(V.scalar_tensor_tensor(out=la3[:, 0:2, :], in0=la3[:, 0:2, :], scalar=0.0, in1=la3[:, 2:4, :],
                                          op0=ALU.max, op1=ALU.add))
            o.step(V.tensor_scalar(la3[:, 1, :], la3[:, 1, :], 0.1, None, ALU.mult))
            o.tell_step(V.tensor_scalar(la3[:, 0, :], la3[:, 0, :], -1.0, None, ALU.mult), "a3_la")
            dve.wait_ge(*done("a3_cum", 1))
            o.tell_step(V.tensor_scalar(la3[:, 4, :], PS[:, 3584:3648], -1.0, None, ALU.mult), "a3_negc")
            for t in range(NT):
                j = t % 2
                for x_, b in ((0, j), (1, 2 + j)):
                    dve.wait_ge(*done("a3_kqv", 3 * t + 1 + x_))
                    if t >= 2 and x_ == 0:
                        dve.wait_ge(*done("a3_turn", 2 * t - 2))
                    o.step(V.bn_stats(st3[:, j, 6 * x_:6 * x_ + 6], bank(b)))
                    ins = V.bn_aggr(st3[:, j, 12 + 2 * x_:14 + 2 * x_], st3[:, j, 6 * x_:6 * x_ + 6])
                    if x_:
                        o.tell_step(ins, "a3_mv")
                    else:
                        o.step(ins)
                dve.wait_ge(*done("a3_sd", t + 1))
                o.step(V.reciprocal(st3[:, j, 16:18], st3[:, j, 16:18]))
                for x_, (w_, g_, b_, raw, fin) in enumerate(((kw, "a3_kg", "a3_kb", "a3_kraw", "a3_kk"),
                                                             (qw, "a3_qg", "a3_qb", "a3_qraw", "a3_qn"))):
                    if x_ and t >= 2:
                        dve.wait_ge(*done("a3_turn", 2 * t - 2))
                    o.tell_step(V.tensor_scalar(w_[:, j, :], bank(2 * x_ + j), st3[:, j, 12 + 2 * x_:13 + 2 * x_],
                                                st3[:, j, 16 + x_:17 + x_], ALU.subtract, ALU.mult), raw)
                    o.step(V.tensor_tensor(w_[:, j, :], w_[:, j, :], W(g_), ALU.mult))
                    o.tell_step(V.tensor_tensor(w_[:, j, :], w_[:, j, :], W(b_), ALU.add), fin)
                dve.wait_ge(*done("a3_sq", t + 1))
                o.tell_step(V.tensor_reduce(st3[:, j, 18:26], h8(sqk[:, j, :]), AX_X, ALU.add), "a3_n2")
                dve.wait_ge(*done("a3_nrm", t + 1))
                o.step(V.tensor_scalar(st3[:, j, 18:26], st3[:, j, 18:26], 1e-12, None, ALU.max))
                o.step(V.reciprocal(st3[:, j, 18:26], st3[:, j, 18:26]))
                o.tell_step(V.tensor_tensor(h8(kw[:, j, :]), h8(kw[:, j, :]),
                                            st3[:, j, 18:26].unsqueeze(2).to_broadcast([128, 8, 64]), ALU.mult), "a3_kn")
            dve.wait_ge(*done("a3_turn", 2 * NT))
            mask = W("strict_add").unsqueeze(1).to_broadcast([128, 8, 128])
            for p in range(NT // 2):
                for j in range(2):
                    t = 2 * p + j
                    dve.wait_ge(*done("a3_cex", t + 1))
                    o.tell_step(V.tensor_tensor(h8(dec[j]), h8(PS[:, 0:1024]), mask, ALU.add), "a3_dm")
                    o.step(V.tensor_tensor(h8(ue3[:, j, :]), h8(vh3[:, t, :]),
                                           la3[:, 1, t * 8:(t + 1) * 8].unsqueeze(2).to_broadcast([128, 8, 64]), ALU.mult))
                    dve.wait_ge(*done("a3_dec", t + 1))
                    dve.wait_ge(*done("a3_gqps", 2 * t + 1))
                    o.tell_step(V.scalar_tensor_tensor(out=mt3[j], in0=dec[j], scalar=2.0, in1=PS[:, 1024:2048],
                                                       op0=ALU.mult, op1=ALU.mult), "a3_gq")
                    dve.wait_ge(*done("a3_gqps", 2 * t + 2))
                    o.tell_step(V.tensor_tensor(pt3[j], dec[j], PS[:, 2048:3072], ALU.mult), "a3_gq")
                    dve.wait_ge(*done("a3_eb", t + 1))
                    o.tell_step(V.tensor_tensor(mt3[j], mt3[j], PS[:, 0:1024], ALU.mult), "a3_m")
                for j in range(2):
                    V.tensor_copy(uu3[:, j, :], ue3[:, j, :]).then_inc(S["a3_u"], 1)
                with dve.Fori(0, ITERS) as i:
                    for j in range(2):
                        dve.wait_ge(*done("a3_w", i * 2 + (p * 2 * ITERS + j + 1)))
                        V.tensor_tensor(uu3[:, j, :], ue3[:, j, :], bank(6 + j), ALU.subtract).then_inc(S["a3_u"], 1)
                dve.wait_ge(*done("a3_y", 2 * p + 2))
            for k in range(2):
                dve.wait_ge(*done("a3_o", k + 1))
                o.tell_step(V.scalar_tensor_tensor(out=h(hT, k), in0=bank(4 + k), scalar=W("a3_ob"), in1=h(hT, k),
                                                   op0=ALU.add, op1=ALU.add), "h_ready")

        def g3_act(act):
            act.wait_ge(*done("g3_shift", 1))
            nc.scalar.activation(gview(1, 16), gview(1, 16), ACT.Exp).then_inc(S["g3_exp"], 1)
            act.wait_ge(*done("g3_shift", 2))
            nc.scalar.activation(gtmp[:, 8, 0:32], gtmp[:, 8, 0:32], ACT.Exp).then_inc(S["g3_exp"], 1)

        def g3_dve(dve, o):
            V = nc.vector
            dve.wait_ge(*done("logits", 4))
            sc = gview(1, 16)
            lg = PS[:, 1024:1152].rearrange("p (t e) -> p t e", e=16)
            o.step(V.tensor_reduce(gcol(6), lg, AX_X, ALU.max))
            o.tell_step(V.tensor_tensor(sc, lg, gbc(gcol(6), 16), ALU.subtract), "g3_shift")
            dve.wait_ge(*done("g3_exp", 1))
            o.step(V.tensor_reduce(gcol(6), sc, AX_X, ALU.add))
            o.step(V.reciprocal(gcol(6), gcol(6)))
            o.step(V.tensor_tensor(sc, sc, gbc(gcol(6), 16), ALU.mult))
            vals = gtmp[:, 8, 0:32]
            for r in range(4):
                top(o, sc, gtmp[:, 8, 8 * r:8 * r + 8], gview(2 + r, 16), gcol(7), 16, r < 3)
            v3_ = vals.rearrange("p (r t) -> p r t", r=4)
            o.step(V.tensor_copy(gcol(6), gtmp[:, 8, 0:8]))
            o.tell_step(V.tensor_tensor(v3_, v3_, gcol(6).unsqueeze(1).to_broadcast([128, 4, 8]), ALU.subtract), "g3_shift")
            dve.wait_ge(*done("g3_exp", 2))
            o.step(V.tensor_reduce(gcol(6), vals.rearrange("p (r t) -> p t r", r=4), AX_X, ALU.add))
            o.step(V.reciprocal(gcol(6), gcol(6)))
            o.step(V.tensor_tensor(v3_, v3_, gcol(6).unsqueeze(1).to_broadcast([128, 4, 8]), ALU.mult))
            dst = gview(0, 18)
            o.step(V.memset(dst, 0.5))
            for r in range(4):
                m = gview(2 + r, 16)
                o.step(V.tensor_tensor(m, m, gbc(gtmp[:, 8, 8 * r:8 * r + 8], 16), ALU.mult))
            o.step(V.tensor_tensor(gview(2, 16), gview(2, 16), gview(3, 16), ALU.add))
            o.step(V.tensor_tensor(gview(4, 16), gview(4, 16), gview(5, 16), ALU.add))
            o.tell_step(V.tensor_tensor(dst[:, :, 0:16], gview(2, 16), gview(4, 16), ALU.add), "gates")

        block = ctx.enter_context(nc.Block())

        @block.sync
        def _(sp):
            tok_sp(sp)
            if STAGES >= 2:
                a0_sp(sp)
                for k in range(2, 5):
                    sp.dma_start(WP[k][:, :], a[f"pack{k}"]).then_inc(S[f"pack{k}"], 16)
            if STAGES >= 3:
                ffn_sp(sp, 0)
            if STAGES >= 5:
                ffn_sp(sp, 1)
            if STAGES >= 6:
                a2_sp(sp)
            if STAGES >= 7:
                ffn_sp(sp, 2)
            if STAGES >= 9:
                ffn_sp(sp, 3)
            for k in range(2):
                sp.wait_ge(*done("h_ready", 2 * STAGES))
                sp.dma_start(out[:, k * HALF:(k + 1) * HALF], h(hT, k)).then_inc(S["stored"], 16)
            sp.wait_ge(*done("stored", 32))

        @block.gpsimd
        def _(pool):
            a0_pool(pool)
            if STAGES >= 2:
                a0_pool2(pool)
            if STAGES >= 4:
                a1_pool(pool)
            if STAGES >= 6:
                a2_pool(pool)
            if STAGES >= 7:
                f2_pool(pool)

        @block.tensor
        def _(pe):
            tok_pe(pe)
            if STAGES >= 2:
                ln_pe(pe, 0, hT, ("h_ready", 2, 2))
                pe.sem_inc(S["a0_pv"], 2)
                a0_pe(pe)
            if STAGES >= 3:
                ln_pe(pe, 1, hT, ("h_ready", 3, 4))
                router_pe(pe, 0, xT, "f0_router", ("ln_out", 4))
                gates_pe(pe, 0)
                f0_pe(pe)
            if STAGES >= 4:
                ln_pe(pe, 2, hT, ("h_ready", 5, 6))
                a1_pe(pe)
            if STAGES >= 5:
                ln_pe(pe, 4, hT, ("h_ready", 7, 8))
                router_pe(pe, 1, xT, "f1_gate", ("ln_out", 10))
                gates_pe(pe, 1)
                ffn_pe(pe, 1, W("f1_zero"))
            if STAGES >= 6:
                ln_pe(pe, 5, hT, ("h_ready", 9, 10))
                pe.sem_inc(S["a2_ysum"], 2)
                a2_pe(pe)
            if STAGES >= 7:
                ln_pe(pe, 6, hT, ("h_ready", 11, 12))
                f2_pe(pe)
                f2_loop_pe(pe)
                ln_pe(pe, 7, lnz, ("f2_z", 1, 2))
            if STAGES >= 8:
                ln_pe(pe, 8, hT, ("h_ready", 13, 14))
                a3_pe(pe)
            if STAGES >= 9:
                ln_pe(pe, 9, hT, ("h_ready", 15, 16))
                router_pe(pe, 3, xT, "f3_gate", ("ln_out", 20))
                gates_pe(pe, 3)
                ffn_pe(pe, 3, W("f3_b2"))

        @block.scalar
        def _(act):
            o = Order(act, S["act_step"], S)
            act.wait_ge(*done("eps", 3))
            if STAGES >= 2:
                ln_act(act, 0, eps5)
                a0_act(act, o)
            if STAGES >= 3:
                ln_act(act, 1, eps5)
                g_exp_act(act, 0)
                gates_act(act, 0)
                f0_act(act)
            if STAGES >= 4:
                ln_act(act, 2, eps5)
                a1_act(act, o)
            if STAGES >= 5:
                ln_act(act, 4, eps5)
                g1_act(act)
                gates_act(act, 1)
                ffn_act(act, 1)
            if STAGES >= 6:
                ln_act(act, 5, eps5)
                a2_act(act, o)
            if STAGES >= 7:
                ln_act(act, 6, eps5)
                f2_act(act, o)
                ln_act(act, 7, eps5)
            if STAGES >= 8:
                ln_act(act, 8, eps5)
                a3_act(act, o)
            if STAGES >= 9:
                ln_act(act, 9, eps5)
                g3_act(act)
                gates_act(act, 3)
                ffn_act(act, 3)

        @block.vector
        def _(dve):
            o = Order(dve, S["dve_step"], S)
            tok_dve(dve, o)
            if STAGES >= 2:
                ln_dve(dve, o, 0, hT, xT)
                dve.sem_inc(S["a0_ctx"], 2)
                a0_dve(dve, o)
            if STAGES >= 3:
                ln_dve(dve, o, 1, hT, xT)
                g0_dve(dve, o)
                f0_dve(dve, o)
            if STAGES >= 4:
                ln_dve(dve, o, 2, hT, xT)
                a1_dve(dve, o)
            if STAGES >= 5:
                ln_dve(dve, o, 4, hT, xT)
                g1_dve(dve, o)
                ffn_dve(dve, o, 1)
                ffn_add_dve(dve, o, 1)
            if STAGES >= 6:
                ln_dve(dve, o, 5, hT, xT)
                a2_dve(dve, o)
            if STAGES >= 7:
                ln_dve(dve, o, 6, hT, xT)
                f2_dve(dve, o)
            if STAGES >= 8:
                ln_dve(dve, o, 8, hT, xT)
                a3_dve(dve, o)
            if STAGES >= 9:
                ln_dve(dve, o, 9, hT, xT)
                g3_dve(dve, o)
                ffn_dve(dve, o, 3)
                ffn_add_dve(dve, o, 3)


def kernel(**inputs):
    import concourse.bacc as bacc
    from concourse.bass_utils import run_bass_kernel_spmd

    w = {k: np.asarray(v) for k, v in inputs.items()}
    f = np.float32

    def rows(x, cols=None):
        x = np.asarray(x).reshape(1, -1)
        return np.broadcast_to(x, (128, x.shape[1]))

    def col(x):
        return np.asarray(x).reshape(-1, 128).T

    i = np.arange(128)
    same = (i[:, None] // T) == (i[None, :] // T)
    parts = {
        "ident": np.eye(128, dtype=f), "mean": np.full((128, 128), 1.0 / 128, f), "tok_bias": w["L0_tok_bias"],
        "a0_nat": np.concatenate([w[f"L0_attn_W_{n}"].T for n in ("qf", "kf", "vf", "qt", "kt", "vt")], axis=1),
        "a0_natb": rows(np.concatenate([w[f"L0_attn_b_{n}"] for n in ("qf", "kf", "vf", "qt", "kt", "vt")])),
        "a0_vt": w["L0_attn_W_vt"].T, "a0_vtb": col(w["L0_attn_b_vt"]),
        "f0_router": w["L0_ffn_router_w"], "f0_beta": w["L0_ffn_beta"],
        "rank": rows(np.arange(16, 0, -1).astype(f)),
        "causal_sl": (same & (i[:, None] <= i[None, :])).astype(f), "ones": np.ones((128, 128), f),
        "a1_wq": w["L1_attn_Wq"], "a1_wk": w["L1_attn_Wk"], "a1_wf": w["L1_attn_Wf"],
        "a1_bf": w["L1_attn_bf"].reshape(64, 1), "a1_wv": w["L1_attn_Wv"], "a1_wo": w["L1_attn_Wo"],
        "a1_g": col(w["L1_attn_ln_g"]), "a1_b": col(w["L1_attn_ln_b"]),
        "a1_slots": w["L1_attn_eslots"][0].T, "a1_slots4": np.tile(w["L1_attn_eslots"][0].T, (1, 4)),
        "a1_eq": w["L1_attn_Eq"], "a1_ek": w["L1_attn_Ek"], "a1_ev": w["L1_attn_Ev"], "a1_eo": w["L1_attn_Eo"],
        "heads4": ((i[:, None] // 32) == (i[None, :] // 32)).astype(f),
        "a1_sin": w["L1_attn_Sin"], "a1_knowT": w["L1_attn_know"][0].T, "a1_know": w["L1_attn_know"][0],
        "a1_sgw": w["L1_attn_Sg_w"], "a1_sgb": col(w["L1_attn_Sg_b"]), "a1_so": w["L1_attn_So"],
        "a1_c1w": w["L1_attn_C1w"], "a1_c1b": w["L1_attn_C1b"].reshape(32, 1), "a1_c2w": w["L1_attn_C2w"],
        "a1_c2b": rows(w["L1_attn_C2b"]), "sel3": np.repeat(np.eye(3, dtype=f), 128, axis=1),
        "f1_gate": w["L1_ffn_gate_w"].T, "f1_bias": rows(w["L1_ffn_biases"]),
        "f1_zero": np.zeros((9, 128), f),
        "a2_in": w["L2_attn_in_proj_w"].T, "a2_cw": w["L2_attn_conv_w"].reshape(2, 128, 4).transpose(1, 0, 2).reshape(128, 8),
        "a2_cb": col(w["L2_attn_conv_b"]),
        "a2_xp": w["L2_attn_x_proj_w"].T.reshape(2, 128, 40).transpose(1, 0, 2).reshape(128, 80),
        "a2_dtw": w["L2_attn_dt_proj_w"].T, "a2_dtb": col(w["L2_attn_dt_proj_b"]),
        "a2_alog": w["L2_attn_A_log"].reshape(2, 128, 16).transpose(1, 0, 2).reshape(128, 32),
        "a2_d": col(w["L2_attn_D_param"]),
        "a2_out": w["L2_attn_out_proj_w"].T.reshape(2, 128, 128).transpose(1, 0, 2).reshape(128, 256),
        "a2_wq": w["L2_attn_wq"].T, "a2_wk": w["L2_attn_wk"].T, "a2_wv": w["L2_attn_wv"].T,
        "a2_fc": w["L2_attn_fc_w"].T, "a2_fcb": col(w["L2_attn_fc_b"]),
        "causal_add": np.where(same & (i[None, :] <= i[:, None]), 0, NEG).astype(f),
        "f2_rc1": w["L2_ffn_rc_w1"].transpose(1, 2, 0).reshape(128, 384), "f2_rcb1": col(w["L2_ffn_rc_b1"]),
        "f2_rc2": w["L2_ffn_rc_w2"].transpose(1, 2, 0).reshape(128, 30), "f2_rcb2": rows(w["L2_ffn_rc_b2"]),
        "f2_sh1": w["L2_ffn_sh_w1"].transpose(1, 2, 0).reshape(128, 9 * 512), "f2_shb1": col(w["L2_ffn_sh_b1"]),
        "f2_sh2": w["L2_ffn_sh_w2"][:, :, 0].T.reshape(4, 128, 128).transpose(1, 0, 2).reshape(128, 512),
        "f2_shb2": col(w["L2_ffn_sh_b2"]), "f2_eb2": w["L2_ffn_e_b2"], "f2_g": col(w["L2_ffn_ln_g"]),
        "f2_b": col(w["L2_ffn_ln_b"]),
        "a3_cw": w["L3_attn_conv_w"][:, 0, :], "a3_cb": col(w["L3_attn_conv_b"]), "a3_wq": w["L3_attn_Wq"].T,
        "a3_k2": w["L3_attn_Mk_W2"].T, "a3_k1": w["L3_attn_Mk_W1"].T, "a3_v2": w["L3_attn_Mv_W2"].T,
        "a3_v1": w["L3_attn_Mv_W1"].T, "a3_e2": w["L3_attn_Meta_W2"].T, "a3_e1": w["L3_attn_Meta_W1"].T,
        "a3_a2": w["L3_attn_Malpha_W2"].T, "a3_a1": w["L3_attn_Malpha_W1"].T,
        "a3_h2": w["L3_attn_Mvh_W2"].T.reshape(4, 128, 64).transpose(1, 0, 2).reshape(128, 256),
        "a3_h1": w["L3_attn_Mvh_W1"].T, "a3_kg": rows(w["L3_attn_normk_g"]), "a3_kb": rows(w["L3_attn_normk_b"]),
        "a3_qg": rows(w["L3_attn_normq_g"]), "a3_qb": rows(w["L3_attn_normq_b"]),
        "a3_ow": w["L3_attn_out_W"].T.reshape(4, 128, 128).transpose(1, 0, 2).reshape(128, 512),
        "a3_ob": col(w["L3_attn_out_b"]),
        "strict_add": np.where(same & (i[:, None] < i[None, :]), 0, NEG).astype(f),
        "strict01": (same & (i[:, None] < i[None, :])).astype(f),
        "incl01": (same & (i[:, None] <= i[None, :])).astype(f),
        "a3_one": np.ones((128, 1), f), "f3_gate": w["L3_ffn_gate_w"].T, "f3_b2": np.concatenate([w["L3_ffn_re_b2"], w["L3_ffn_se_b2"]]),
    }
    arrays = {}
    for k, p in enumerate(pack_columns()):
        pack = np.zeros((128, sum(c for _, _, c in p)), f)
        at = 0
        for name, r, c in p:
            assert parts[name].shape == (r, c), (name, parts[name].shape, r, c)
            pack[:r, at:at + c] = parts[name]
            at += c
        arrays[f"pack{k}"] = pack

    def up(x):
        return x

    def down(x):
        e, ff, d = x.shape
        return x.reshape(e, ff // 128, 128, d).transpose(0, 2, 1, 3).reshape(e, 128, ff)

    def cols(x):
        return x.reshape(x.shape[0], -1, 128).transpose(0, 2, 1)

    arrays["ffn0"] = np.concatenate([w["L0_ffn_w1"], down(w["L0_ffn_w2"]), cols(w["L0_ffn_b1"]), cols(w["L0_ffn_b2"]),
                                     cols(w["L0_ffn_gamma"]), cols(w["L0_ffn_beta"])], axis=2)
    arrays["ffn1"] = np.concatenate([
        np.concatenate([w["L1_ffn_w1"], w["L1_ffn_sw1"][None]]), np.concatenate([w["L1_ffn_w3"], w["L1_ffn_sw3"][None]]),
        down(np.concatenate([w["L1_ffn_w2"], w["L1_ffn_sw2"][None]]))], axis=2)
    arrays["ffn2"] = np.concatenate([w["L2_ffn_e_w1"], down(w["L2_ffn_e_w2"]), cols(w["L2_ffn_e_b1"])], axis=2)
    arrays["ffn3"] = np.concatenate([
        np.concatenate([w["L3_ffn_re_w1"], w["L3_ffn_se_w1"]]), down(np.concatenate([w["L3_ffn_re_w2"], w["L3_ffn_se_w2"]])),
        cols(np.concatenate([w["L3_ffn_re_b1"], w["L3_ffn_se_b1"]]))], axis=2)
    arrays["tok_w"] = w["L0_tok_weight"]
    arrays["tok_m"] = w["L0_tok_mask"]
    arrays["tok_x"] = w["x"].T.reshape(GP, GC * B)

    nc = bacc.Bacc("TRN2", target_bir_lowering=False, num_devices=1)
    arrays = {k: np.ascontiguousarray(v) for k, v in arrays.items()}
    a = {k: nc.dram_tensor(k, v.shape, F32, kind="ExternalInput").ap() for k, v in arrays.items()}
    out = nc.dram_tensor("out_dram", (128, N), F32, kind="ExternalOutput").ap()
    build(nc, a, out)
    r = run_bass_kernel_spmd(nc, [arrays], core_ids=[0])
    return np.ascontiguousarray(r.results[0]["out_dram"].T).reshape(B, T, D)
```

```python
from contextlib import ExitStack

import numpy as np

import concourse.bass as bass
from concourse import mybir

F32 = mybir.dt.float32
BF16 = mybir.dt.bfloat16
ALU = mybir.AluOpType
ACT = mybir.ActivationFunctionType
AX_X = mybir.AxisListType.X

STAGES = 9
D = 128
B, T = 64, 16
N = B * T
HALF = 512
NT = N // 128
G, GP = 5000, 125
GC = G // GP
NEG = -1.0e30


def pack_columns():
    first = [("ident", 128, 128), ("mean", 128, 128), ("tok_bias", 128, 16)]
    l0 = [("a0_nat", 128, 768), ("a0_natb", 128, 768), ("a0_vt", 128, 128), ("a0_vtb", 128, 1),
          ("f0_router", 128, 8), ("f0_beta", 8, 128), ("rank", 128, 16)]
    l1 = [("causal_sl", 128, 128), ("ones", 128, 128), ("a1_wq", 128, 64), ("a1_wk", 128, 64), ("a1_wf", 128, 64),
          ("a1_bf", 64, 1), ("a1_wv", 128, 128), ("a1_wo", 128, 128), ("a1_g", 128, 1), ("a1_b", 128, 1),
          ("a1_slots", 128, 32), ("a1_slots4", 128, 128), ("a1_eq", 128, 128), ("a1_ek", 128, 128),
          ("a1_ev", 128, 128), ("a1_eo", 128, 128), ("heads4", 128, 128), ("a1_sin", 128, 128),
          ("a1_knowT", 128, 64), ("a1_know", 64, 128), ("a1_sgw", 128, 128), ("a1_sgb", 128, 1),
          ("a1_so", 128, 128), ("a1_c1w", 128, 32), ("a1_c1b", 32, 1), ("a1_c2w", 32, 3), ("a1_c2b", 128, 3),
          ("sel3", 3, 384), ("f1_gate", 128, 8), ("f1_bias", 128, 8), ("f1_zero", 9, 128)]
    l2 = [("a2_in", 128, 512), ("a2_cw", 128, 8), ("a2_cb", 128, 2), ("a2_xp", 128, 80), ("a2_dtw", 8, 256),
          ("a2_dtb", 128, 2), ("a2_alog", 128, 32), ("a2_d", 128, 2), ("a2_out", 128, 256), ("a2_wq", 128, 128),
          ("a2_wk", 128, 128), ("a2_wv", 128, 128), ("a2_fc", 128, 128), ("a2_fcb", 128, 1), ("causal_add", 128, 128),
          ("f2_rc1", 128, 384), ("f2_rcb1", 128, 1), ("f2_rc2", 128, 30), ("f2_rcb2", 128, 10),
          ("f2_sh1", 128, 9 * 512), ("f2_shb1", 128, 4), ("f2_sh2", 128, 512), ("f2_shb2", 128, 1),
          ("f2_eb2", 10, 128), ("f2_g", 128, 1), ("f2_b", 128, 1)]
    l3 = [("a3_cw", 128, 4), ("a3_cb", 128, 1), ("a3_wq", 128, 512), ("a3_k2", 128, 64), ("a3_k1", 64, 512),
          ("a3_v2", 128, 64), ("a3_v1", 64, 512), ("a3_e2", 128, 64), ("a3_e1", 64, 8), ("a3_a2", 128, 64),
          ("a3_a1", 64, 8), ("a3_h2", 128, 256), ("a3_h1", 64, 512), ("a3_kg", 128, 512), ("a3_kb", 128, 512),
          ("a3_qg", 128, 512), ("a3_qb", 128, 512), ("a3_ow", 128, 512), ("a3_ob", 128, 1),
          ("strict_add", 128, 128), ("strict01", 128, 128), ("incl01", 128, 128),
          ("a3_one", 128, 1), ("f3_gate", 128, 16), ("f3_b2", 18, 128)]
    return [first, l0, l1, l2, l3]


FFN_COLUMNS = [512 + 512 + 4 + 3, 768, 512 + 512 + 4, 512 + 512 + 4]
FFN_EXPERTS = [8, 9, 10, 18]


LINES = {
    "a0_tensor": [
        ("a0_vps", 2), ("a0_proj", 8), ("a0_ctxT", 2),
    ],
    "a1_tensor": [
        ("a1_qkf", 3), ("a1_v", 1), ("a1_c1", 1), ("a1_qh", 1), ("a1_qs", 1), ("a1_kv", 1), ("a1_se", 1),
        ("a1_ss", 1), ("a1_sc", 1), ("a1_sl", 1), ("a1_num", 1), ("a1_peT", 1), ("a1_psT", 1), ("a1_oh", 1),
        ("a1_eo", 1), ("a1_ret", 1), ("a1_sg", 1), ("a1_wo", 1), ("a1_pcT", 1), ("a1_so", 1), ("a1_bw", 3),
    ],
    "a2_tensor": [
        ("a2_xz", 4), ("a2_xp", 2), ("a2_dt", 2), ("a2_out", 1), ("a2_qk", 2), ("a2_v", 1), ("a2_s", 1),
        ("a2_atT", 1), ("a2_o", 1), ("a2_fc", 2),
    ],
    "a3_tensor": [
        ("a3_s", 4), ("a3_vps", 4), ("a3_h", 1), ("a3_ea", 1), ("a3_cum", 1), ("a3_o", 2),
    ],
    "a0_scalar": [
        ("a0_v", 2), ("a0_fexp", 1),
    ],
    "a1_scalar": [
        ("a1_sig", 1), ("a1_vcopy", 1), ("a1_exp2", 2), ("a1_qhcopy", 1), ("a1_silu", 1), ("a1_qscopy", 1),
        ("a1_ln", 1), ("a1_en", 1), ("a1_ep", 1), ("a1_eexp", 1), ("a1_sexp", 1), ("a1_cexp", 1),
        ("a1_peTcopy", 1), ("a1_psTcopy", 1), ("a1_ohcopy", 1), ("a1_gate", 1), ("a1_pcTcopy", 1),
    ],
    "a2_scalar": [
        ("a2_zg", 2), ("a2_xc", 2), ("a2_dtl", 1), ("a2_bcT", 1), ("a2_A", 1), ("a2_e", 2), ("a2_l", 2),
        ("a2_xm", 1), ("a2_qkcopy", 2), ("a2_vcopy", 1), ("a2_aexp", 1), ("a2_atTcopy", 1), ("a2_ocopy", 1),
    ],
    "a3_scalar": [
        ("a3_silu", 4), ("a3_vT", 4), ("a3_hsilu", 1), ("a3_e", 1), ("a3_l", 1),
    ],
    "a0_vector": [
        ("a0_nat", 8), ("a0_split", 9), ("a0_fshift", 1), ("a0_ctxf", 1), ("a0_ctxsum", 2),
    ],
    "a1_vector": [
        ("a1_min", 2), ("a1_sgmax", 1), ("a1_qk", 2), ("a1_kvm", 2), ("a1_cum", 1), ("a1_hat", 2),
        ("a1_eshift", 1), ("a1_sshift", 1), ("a1_cshift", 1), ("a1_slm", 1), ("a1_pe", 1), ("a1_ps", 1),
        ("a1_pc", 1), ("a1_w", 2), ("a1_sin_", 2), ("a1_mixed", 3),
    ],
    "a2_vector": [
        ("a2_conv", 2), ("a2_negA", 1), ("a2_nabs", 2), ("a2_dtx", 2), ("a2_ym", 2), ("a2_shift", 1),
        ("a2_att", 1),
    ],
    "a3_vector": [
        ("a3_x", 1), ("a3_nabs", 1), ("a3_la", 1), ("a3_negc", 1),
    ],
}


class Sems(dict):

    def __init__(self, make):
        super().__init__()
        self.make, self.log = make, []
        self.line = {name: line for line, results in LINES.items() for name, _ in results}

    def __missing__(self, name):
        line = self.line.get(name)
        self[name] = self[line] if line else self.make(name)
        return self[name]

    def base(self, name):
        base = 0
        for other, times in LINES.get(self.line.get(name), ()):
            if other == name:
                return base
            base += times
        return 0


class Order:

    def __init__(self, eng, sem, sems):
        self.eng, self.sem, self.sems, self.n = eng, sem, sems, 0
        self.told = {}
        self.i = None

    def loop(self, i, per):
        self.i, self.per, self.base, self.n = i, per, self.n, 0

    def end(self, times):
        assert self.n == self.per, (self.n, self.per)
        self.n, self.i = self.base + times * self.per, None

    def step(self, ins):
        self.n += 1
        ins.then_inc(self.sem, 1)
        if self.i is None:
            self.eng.wait_ge(self.sem, self.n)
        else:
            self.eng.wait_ge(self.sem, self.i * self.per + (self.base + self.n))

    def tell(self, ins, name):
        ins.then_inc(self.sems[name], 1)
        self.told[name] = self.told.get(name, 0) + 1

    def tell_step(self, ins, name):
        self.tell(ins, name)
        self.eng.wait_ge(self.sems[name], self.told[name] + self.sems.base(name))


def build(nc, a, out):
    ctx = ExitStack()
    with ctx:
        S = Sems(lambda name: ctx.enter_context(nc.semaphore("s_" + name)))

        def done(name, n):
            return S[name], n + S.base(name)

        def sb(name, shape, dt=F32):
            return ctx.enter_context(nc.sbuf_tensor(name, shape, dt))

        PS = ctx.enter_context(nc.psum_tensor("banks", [128, 8 * 512], F32))

        def bank(b, n=1, rows=128):
            return PS[0:rows, b * 512:(b + n) * 512]

        packs = pack_columns()
        width = [sum(c for _, _, c in p) for p in packs]
        WP = [sb(f"weights{k}", [128, w]) for k, w in enumerate(width)]
        where = {}
        for k, p in enumerate(packs):
            at = 0
            for name, rows, cols in p:
                where[name] = (k, rows, at, cols)
                at += cols

        def W(name, c0=0, c1=None):
            k, rows, at, cols = where[name]
            return WP[k][0:rows, at + c0:at + (cols if c1 is None else c1)]

        hT = sb("hT", [128, N])
        xT = sb("xT", [128, N])
        xc = sb("ln_xc", [128, N])
        sq = sb("ln_sq", [128, N])
        eps5 = sb("eps5", [128, 1])
        eps6 = sb("eps6", [128, 1])
        epsd = sb("epsd", [128, 1])
        BIG = sb("big", [128, 16 * N])
        POOLB = sb("bigb", [128, 6 * N])

        def big(k, n=1, rows=128):
            return BIG[0:rows, k * N:(k + n) * N]

        def bigb(k, n=1, rows=128):
            return POOLB[0:rows, k * N:(k + n) * N]

        spl_dram = nc.dram_tensor("spl_dram", [9, N, 128], BF16).ap()
        raw_dram = nc.dram_tensor("raw_dram", [N // 16, 4, 5 * 512], F32).ap()
        gates_dram = nc.dram_tensor("gates_dram", [4, 18, N], F32).ap()
        bc_dram = nc.dram_tensor("bc_dram", [32, N], F32).ap()

        def h(x, k):
            return x[:, k * HALF:(k + 1) * HALF]

        def mm(o, l, r, start=True, stop=True):
            return nc.tensor.matmul(o, l, r, start=start, stop=stop, skip_group_check=True)

        def tile(x, t):
            return x[:, t * 128:(t + 1) * 128]

        TQ, TSLOTS = 2, 4
        TGROUPS = GC // TQ
        tokw = BIG[0:GP, 0:TSLOTS * 16 * TQ * 128].rearrange("p (s e q d) -> p s e q d", s=TSLOTS, e=16, q=TQ)
        tokm = POOLB[0:GP, 0:TSLOTS * TQ * 128].rearrange("p (s q d) -> p s q d", s=TSLOTS, q=TQ)
        tokx = POOLB[0:GP, N:N + TSLOTS * TQ * B].rearrange("p (s q b) -> p s q b", s=TSLOTS, q=TQ)
        wtok = a["tok_w"].rearrange("e (p c) d -> p e (c d)", p=GP)
        mtok = a["tok_m"].rearrange("(p c) d -> p (c d)", p=GP)

        def tok_load(sp, s, at, xat):
            sp.dma_start(tokx[:, s].rearrange("p q b -> p (q b)"), a["tok_x"][:, xat]).then_inc(S[f"tok_loaded{s}"], 16)
            sp.dma_start(tokw[:, s].rearrange("p e q d -> p e (q d)"),
                         wtok[:, :, at]).then_inc(S[f"tok_loaded{s}"], 16)
            sp.dma_start(tokm[:, s].rearrange("p q d -> p (q d)"), mtok[:, at]).then_inc(S[f"tok_loaded{s}"], 16)

        def tok_sp(sp):
            sp.dma_start(WP[0][:, :], a["pack0"]).then_inc(S["pack0"], 16)
            for s in range(TSLOTS):
                tok_load(sp, s, slice(s * TQ * 128, (s + 1) * TQ * 128),
                         slice(s * TQ * B, (s + 1) * TQ * B))
            with sp.Fori(1, TGROUPS // TSLOTS) as i:
                for s in range(TSLOTS):
                    sp.wait_ge(*done("tok_used", i * TSLOTS + (s + 1 - TSLOTS)))
                    tok_load(sp, s, bass.ds(i * (TSLOTS * TQ * 128) + s * TQ * 128, TQ * 128),
                             bass.ds(i * (TSLOTS * TQ * B) + s * TQ * B, TQ * B))

        def tok_dve(dve, o):
            nc.vector.memset(h(sq, 0), 0.0).then_inc(S["tok_zero"], 1)
            with dve.Fori(0, TGROUPS // TSLOTS) as i:
                for s in range(TSLOTS):
                    dve.wait_ge(*done(f"tok_loaded{s}", i * 48 + 48))
                    m = tokm[:, s].unsqueeze(1).to_broadcast([GP, 16, TQ, 128])
                    nc.vector.tensor_tensor(
                        tokw[:, s].rearrange("p e q d -> p e (q d)"), tokw[:, s].rearrange("p e q d -> p e (q d)"),
                        m.rearrange("p e q d -> p e (q d)"), ALU.mult).then_inc(S["tok_masked"], 1)
            dve.wait_ge(*done("tok_used", TGROUPS))
            for k in range(2):
                nc.vector.tensor_copy(h(xc, k), bank(k)).then_inc(S["tok_rows"], 1)
            hv = hT[:, :].rearrange("p (b g k e) -> p k e g b", g=2, k=2, e=4)
            bias = W("tok_bias").rearrange("p (g k e) -> p k e g", g=2, k=2)
            dve.wait_ge(*done("pack0", 16))
            for k in range(2):
                dve.wait_ge(*done("tok_turned", k + 1))
                o.tell_step(nc.vector.tensor_tensor(
                    hv[:, k], bank(2 + k).rearrange("p (e g b) -> p e g b", e=4, g=2),
                    bias[:, k].unsqueeze(3).to_broadcast([128, 4, 2, 64]), ALU.add), "h_ready")

        def tok_pe(pe):
            pe.wait_ge(*done("tok_zero", 1))
            for k in range(2):
                mm(bank(k), sq[:, 0:128], sq[:, 0:HALF], True, False)
            with pe.Fori(0, TGROUPS // TSLOTS) as i:
                for s in range(TSLOTS):
                    pe.wait_ge(*done("tok_masked", i * TSLOTS + (s + 1)))
                    for q in range(TQ):
                        for k in range(2):
                            for g in range(2):
                                e = 8 * g + 4 * k
                                last = nc.tensor.matmul(PS[64 * g:64 * g + 64, k * 512:(k + 1) * 512], tokx[:, s, q],
                                                        tokw[:, s, e:e + 4, q, :], start=False, stop=False,
                                                        skip_group_check=True, tile_position=(0, 64 * g))
                    last.then_inc(S["tok_used"], 1)
            pe.wait_ge(*done("pack0", 16))
            for k in range(2):
                pe.wait_ge(*done("tok_rows", k + 1))
                for e in range(4):
                    last = nc.tensor.transpose(PS[:, (2 + k) * 512 + e * 128:(2 + k) * 512 + (e + 1) * 128],
                                               xc[:, k * HALF + e * 128:k * HALF + (e + 1) * 128], W("ident"))
                last.then_inc(S["tok_turned"], 1)

        def ln_pe(pe, c, src, ready, rows=None):
            for k in range(2):
                pe.wait_ge(*done(ready[0], ready[1 + k]))
                mm(bank(6 + k), W("mean"), h(src, k)).then_inc(S["ln_mean"], 1)
            for k in range(2):
                pe.wait_ge(*done("ln_sq", 2 * c + k + 1))
                mm(bank(6 + k), W("mean"), h(sq, k)).then_inc(S["ln_var"], 1)

        def ln_act(act, c, eps):
            for k in range(2):
                act.wait_ge(*done("ln_xc", 2 * c + k + 1))
                nc.scalar.activation(h(sq, k), h(xc, k), ACT.Square).then_inc(S["ln_sq"], 1)
            for k in range(2):
                act.wait_ge(*done("ln_var", 2 * c + k + 1))
                nc.scalar.activation(h(sq, k), bank(6 + k), ACT.Sqrt, bias=eps[:, 0:1]).then_inc(S["ln_std"], 1)

        def ln_dve(dve, o, c, src, dst, gain=None, shift=None):
            for k in range(2):
                dve.wait_ge(*done("ln_mean", 2 * c + k + 1))
                o.tell_step(nc.vector.tensor_tensor(h(xc, k), h(src, k), bank(6 + k), ALU.subtract), "ln_xc")
            for k in range(2):
                dve.wait_ge(*done("ln_std", 2 * c + k + 1))
                o.step(nc.vector.reciprocal(h(sq, k), h(sq, k)))
                if gain is not None:
                    o.step(nc.vector.tensor_tensor(h(xc, k), h(xc, k), h(sq, k), ALU.mult))
                    o.tell_step(nc.vector.tensor_scalar(h(dst, k), h(xc, k), gain, shift, ALU.mult, ALU.add), "ln_out")
                else:
                    o.tell_step(nc.vector.tensor_tensor(h(dst, k), h(xc, k), h(sq, k), ALU.mult), "ln_out")

        nat = BIG[:, 0:8 * 768].rearrange("p (t c) -> p t c", c=768)
        neg_max = big(6)
        rest = big(7)
        spl = BIG[:, 8 * N:8 * N + 9 * 512].bitcast(BF16).rearrange("p (x t d) -> p x t d", x=9, d=128)
        expf = big(13)
        ctxf = big(14)
        num0 = big(0).rearrange("p (t d) -> p t d", d=128)
        den0 = big(1).rearrange("p (t d) -> p t d", d=128)
        small = sb("small", [128, 96])
        QC, MC = 5, 32
        v1 = bigb(0, 2)
        v1q = v1[:, 0:N // 4 * QC].rearrange("p (q f) -> p q f", f=QC)
        VW = N // 4 * QC + MC - QC
        AG = 32
        SW = AG // 4 * QC + MC - QC
        v1s = sb("v1s", [128, 2, SW])
        krows = BIG[:, 8 * N:12 * N].bitcast(BF16).rearrange("r (s c) -> r s c", s=2)
        qrows = [POOLB[:, 4 * N:6 * N].bitcast(BF16), BIG[:, 6 * N:8 * N].bitcast(BF16)]
        Ex = [[bigb(2), bigb(3)], [xc[:, :], sq[:, :]]]
        stg = big(2, 2).rearrange("p (s c) -> p s c", s=4)
        AGROUPS = N // AG
        ATIMES = AGROUPS // 2

        def a0_rows_load(sp, s, at):
            sl = S[f"a0_rows{s}"]
            k = spl_dram[3:6].rearrange("a n d -> a (n d)")[:, at]
            q = spl_dram[0:3].rearrange("a n d -> a (n d)")[:, at]
            m = spl_dram[6:9].rearrange("a n d -> a (n d)")[:, at]
            sp.dma_start(krows[3:12, s, :], k.unsqueeze(0).to_broadcast([3, 3, AG * 128])).then_inc(sl, 16)
            sp.dma_start(qrows[s][3:12, :], q.unsqueeze(1).to_broadcast([3, 3, AG * 128])).then_inc(sl, 16)
            sp.dma_start(qrows[s][0:3, :], m).then_inc(sl, 16)

        def a0_sp(sp):
            sp.dma_start(WP[1][:, :], a["pack1"]).then_inc(S["pack1"], 16)
            for x in range(3):
                sp.wait_ge(*done("a0_split", 3 * x + 3))
                sp.dma_start(spl_dram[3 * x:3 * x + 3].rearrange("x (t p) d -> p x t d", p=128),
                             spl[:, 3 * x:3 * x + 3]).then_inc(S["a0_spl_out"], 16)
            sp.wait_ge(*done("a0_spl_out", 48))
            sp.wait_ge(*done("a0_zero", 4))
            sp.wait_ge(*done("a0_ones", 2))
            for s in range(2):
                a0_rows_load(sp, s, slice(s * AG * 128, (s + 1) * AG * 128))

            def raw_store(i, c):
                sp.wait_ge(*done("a0_ctx", i * 4 + (c + 4)))
                for g in range(4):
                    sp.dma_start(raw_dram[bass.ds(i * 4 + c, 2), g].rearrange("b (m c) -> m b c", m=QC),
                                 stg[32 * g:32 * g + QC, c:c + 2, :]).then_inc(S[f"a0_raw{c // 2}"], 16)

            with sp.Fori(0, ATIMES - 1) as i:
                for s in range(2):
                    sp.wait_ge(*done("a0_arg", i * 8 + 4 * (s + 1)))
                    a0_rows_load(sp, s, bass.ds(i * (2 * AG * 128) + (s + 2) * AG * 128, AG * 128))
                    raw_store(i, 2 * s)
            for s in range(2):
                raw_store(ATIMES - 1, 2 * s)
            for s in range(2):
                sp.wait_ge(*done(f"a0_raw{s}", 64 * ATIMES + 64))
            for t in range(NT):
                q = raw_dram[t * 8:(t + 1) * 8].rearrange("b g c -> (b g) c")
                sp.dma_start(num0[:, t, :], q.rearrange("q (r y) -> q r y", r=4)[:, :, 0:128]).then_inc(S["a0_nums"], 16)
                sp.dma_start(den0[:, t, :], q[:, 4 * 512:].rearrange("q (r y) -> q r y", r=4)).then_inc(S["a0_nums"], 16)

        def a0_pool(pool):
            nc.gpsimd.memset(eps5[:, :], 1e-5).then_inc(S["eps"], 1)
            nc.gpsimd.memset(eps6[:, :], 1e-6).then_inc(S["eps"], 1)
            nc.gpsimd.memset(epsd[:, :], 1e-6).then_inc(S["eps"], 1)

        def a0_pool2(pool):
            pool.wait_ge(*done("tok_used", TGROUPS))
            nc.gpsimd.memset(v1q[:, :, 4], 1.0).then_inc(S["a0_v1ones"], 1)
            nc.gpsimd.memset(v1[:, N // 4 * QC:VW], 0.0).then_inc(S["a0_v1ones"], 1)
            nc.gpsimd.memset(POOLB[:, 4 * N:6 * N], 0.0).then_inc(S["a0_zero"], 1)
            pool.wait_ge(*done("a0_spl_out", 48))
            pool.wait_ge(*done("a0_zero", 4))
            nc.gpsimd.memset(krows[0:3, 0, :], 1.0).then_inc(S["a0_ones"], 1)
            nc.gpsimd.memset(krows[0:3, 1, :], 1.0).then_inc(S["a0_ones"], 1)
            pool.wait_ge(*done("a0_v", 2))
            pool.wait_ge(*done("a0_v1ones", 2))
            for s in range(2):
                nc.gpsimd.tensor_copy(v1s[:, s], v1[:, s * (SW - MC + QC):s * (SW - MC + QC) + SW]).then_inc(S["a0_v1s"], 1)
            with pool.Fori(1, ATIMES) as i:
                for s in range(2):
                    pool.wait_ge(*done("a0_pv", i * 4 + 2 * s))
                    nc.gpsimd.tensor_copy(v1s[:, s], v1[:, bass.ds(i * (2 * (SW - MC + QC)) + s * (SW - MC + QC), SW)]
                                          ).then_inc(S["a0_v1s"], 1)

        def a0_pe(pe):
            pe.wait_ge(*done("pack1", 16))
            for k in range(2):
                pe.wait_ge(*done("ln_out", k + 1))
                mm(bank(4 + k), W("a0_vt"), h(xT, k)).then_inc(S["a0_vps"], 1)
            for t in range(NT):
                if t >= 2:
                    pe.wait_ge(*done("a0_nat", t - 1))
                b = 2 * (t % 2)
                mm(bank(b), tile(xT, t), W("a0_nat", 0, 512))
                mm(PS[:, (b + 1) * 512:(b + 1) * 512 + 256], tile(xT, t), W("a0_nat", 512, 768)).then_inc(S["a0_proj"], 1)
            pe.wait_ge(*done("a0_nat", 8))
            pe.wait_ge(*done("a0_v", 2))

            def args(i, c):
                s = c // 2 % 2
                if c % 2 == 0:
                    pe.wait_ge(*done(f"a0_rows{s}", (i + c // 4) * 48 + 48))
                for f in range(2):
                    pe.wait_ge(*done("a0_exp", i * 8 + (2 * c + f + 1)))
                    for n in range(8):
                        t = (c % 2) * 16 + f * 8 + n
                        last = mm(PS[:, f * 1024 + n * 128:f * 1024 + (n + 1) * 128],
                                  krows[:, s, t * 128:(t + 1) * 128], qrows[s][:, t * 128:(t + 1) * 128])
                    last.then_inc(S["a0_arg"], 1)

            def weigh(i, c):
                s = c // 2
                if c % 2 == 0:
                    pe.wait_ge(*done("a0_v1s", i * 2 + (s + 1)))
                pe.wait_ge(*done("a0_ctx", i * 4 + (c + 1)))
                pe.wait_ge(*done("a0_exp", i * 8 + (2 * c + 4)))
                for g in range(4):
                    v = v1s[:, s, ((c % 2) * 4 + g) * QC:((c % 2) * 4 + g) * QC + MC]
                    last = nc.tensor.matmul(PS[32 * g:32 * g + 32, (4 + c % 2) * 512:(5 + c % 2) * 512], v,
                                            Ex[c % 2][g // 2][:, (g % 2) * 512:(g % 2 + 1) * 512], start=True, stop=True,
                                            skip_group_check=True, tile_position=(0, 32 * g))
                last.then_inc(S["a0_pv"], 1)

            args(0, 0)
            with pe.Fori(0, ATIMES - 1) as i:
                for c in range(4):
                    args(i, c + 1)
                    weigh(i, c)
            for c in range(4):
                if c < 3:
                    args(ATIMES - 1, c + 1)
                weigh(ATIMES - 1, c)
            for t in range(NT):
                pe.wait_ge(*done("a0_ctxsum", t // 4 + 1))
                last = nc.tensor.transpose(PS[:, t * 128:(t + 1) * 128], ctxf[:, t * 128:(t + 1) * 128], W("ident"))
                if t % 4 == 3:
                    last.then_inc(S["a0_ctxT"], 1)

        def a0_act(act, o):
            act.wait_ge(*done("tok_used", TGROUPS))
            for k in range(2):
                act.wait_ge(*done("a0_vps", k + 1))
                nc.scalar.activation(v1q[:, k * 128:(k + 1) * 128, 0:4], bank(4 + k).rearrange("p (q f) -> p q f", f=4),
                                     ACT.Identity, bias=W("a0_vtb")).then_inc(S["a0_v"], 1)
            act.sem_inc(S["a0_exp"], 2)
            act.wait_ge(*done("a0_fshift", 1))
            nc.scalar.activation(expf, expf, ACT.Exp).then_inc(S["a0_fexp"], 1)
            with act.Fori(0, ATIMES) as i:
                for c in range(4):
                    for f in range(2):
                        act.wait_ge(*done("a0_arg", i * 8 + (2 * c + f + 1)))
                        if f == 0:
                            act.wait_ge(*done("a0_pv", i * 4 + (c + 1)))
                        nc.scalar.activation(Ex[c % 2][f], PS[:, f * 1024:(f + 1) * 1024], ACT.Exp).then_inc(S["a0_exp"], 1)

        def a0_dve(dve, o):
            V = nc.vector
            for t in range(NT):
                dve.wait_ge(*done("a0_proj", t + 1))
                b = 2 * (t % 2)
                o.tell_step(V.tensor_tensor(nat[:, t, :], PS[:, b * 512:b * 512 + 768], W("a0_natb"), ALU.add), "a0_nat")
            qf, kf, vf, qt, kt = (nat[:, :, x * 128:(x + 1) * 128] for x in range(5))
            kmax, kmin = small[:, 0:8], small[:, 8:16]
            v3 = lambda x: x.rearrange("p (t d) -> p t d", d=128)
            bc = lambda x: x.unsqueeze(2).to_broadcast([128, 8, 128])
            o.step(V.tensor_reduce(kmax, kt, AX_X, ALU.max))
            o.step(V.tensor_reduce(kmin, kt, AX_X, ALU.min))
            o.step(V.tensor_scalar(small[:, 0:16], small[:, 0:16], -1.0, None, ALU.mult))
            o.step(V.tensor_tensor(v3(neg_max), qt, bc(kmax), ALU.mult))
            o.step(V.tensor_tensor(v3(rest), qt, bc(kmin), ALU.mult))
            o.step(V.tensor_tensor(neg_max, neg_max, rest, ALU.min))
            for x, src in enumerate((qt, kt, v3(neg_max))):
                o.tell_step(V.tensor_copy(spl[:, 3 * x], src), "a0_split")
                o.step(V.tensor_tensor(v3(rest), src, spl[:, 3 * x], ALU.subtract))
                o.tell_step(V.tensor_copy(spl[:, 3 * x + 1], v3(rest)), "a0_split")
                o.step(V.tensor_tensor(v3(rest), v3(rest), spl[:, 3 * x + 1], ALU.subtract))
                o.tell_step(V.tensor_copy(spl[:, 3 * x + 2], v3(rest)), "a0_split")
            dve.wait_ge(*done("a0_spl_out", 48))
            V.memset(BIG[:, 6 * N:8 * N], 0.0).then_inc(S["a0_zero"], 1)
            V.memset(BIG[:, 8 * N:10 * N], 0.0).then_inc(S["a0_zero"], 1)
            V.memset(BIG[:, 10 * N:12 * N], 0.0).then_inc(S["a0_zero"], 1)
            fmax, fsum = small[:, 16:24], small[:, 24:32]
            o.step(V.tensor_tensor(v3(expf), qf, kf, ALU.mult))
            o.step(V.tensor_reduce(fmax, v3(expf), AX_X, ALU.max))
            o.tell_step(V.tensor_tensor(v3(expf), v3(expf), bc(fmax), ALU.subtract), "a0_fshift")
            dve.wait_ge(*done("a0_fexp", 1))
            o.step(V.tensor_reduce(fsum, v3(expf), AX_X, ALU.add))
            o.step(V.reciprocal(fsum, fsum))
            o.step(V.tensor_tensor(v3(ctxf), v3(expf), vf, ALU.mult))
            o.tell_step(V.tensor_tensor(v3(ctxf), v3(ctxf), bc(fsum), ALU.mult), "a0_ctxf")
            with dve.Fori(0, ATIMES) as i:
                for c in range(4):
                    dve.wait_ge(*done("a0_pv", i * 4 + (c + 3)))
                    if c % 2 == 0:
                        dve.wait_ge(*done(f"a0_raw{c // 2}", i * 64 + 64))
                    V.tensor_copy(stg[:, c, :], bank(4 + c % 2)).then_inc(S["a0_ctx"], 1)
            for k in range(2):
                dve.wait_ge(*done("a0_nums", 256))
                o.step(V.reciprocal(h(big(1), k), h(big(1), k)))
                o.step(V.tensor_tensor(h(big(0), k), h(big(0), k), h(big(1), k), ALU.mult))
                o.tell_step(V.tensor_tensor(h(ctxf, k), h(ctxf, k), h(big(0), k), ALU.add), "a0_ctxsum")
            for k in range(2):
                dve.wait_ge(*done("a0_ctxT", k + 1))
                o.tell_step(V.tensor_tensor(h(hT, k), h(hT, k), bank(k), ALU.add), "h_ready")

        wslot = sb("wslot", [128, 2, max(FFN_COLUMNS)])
        gslot = sb("gslot", [128, 2, N])
        gT = sb("gT", [18, N])
        gtmp = sb("gtmp", [128, 14, 8 * 18])
        RH = 4
        hid = big(0, 2).rearrange("p (r c) -> p r c", r=RH)
        hidg = big(2, 2).rearrange("p (r c) -> p r c", r=RH)
        hid2 = big(4, 2).rearrange("p (r c) -> p r c", r=RH)
        acc = big(6)
        z0 = big(7)
        zc = big(8)
        zs = big(9)
        FC = [4, 2, 4, 4]
        RP = [4, 2, 4, 4]
        NU = [2 * c for c in FC]

        def gview(j, e):
            return gtmp[:, j, 0:8 * e].rearrange("p (t e) -> p t e", e=e)

        def gcol(j):
            return gtmp[:, j, 0:8]

        def gbc(x, e):
            return x.unsqueeze(2).to_broadcast([128, 8, e])

        def top(o, score, value, mark, idx, e, more):
            V = nc.vector
            rank = W("rank", 0, e).unsqueeze(1).to_broadcast([128, 8, e])
            o.step(V.tensor_reduce(value, score, AX_X, ALU.max))
            o.step(V.tensor_tensor(mark, score, gbc(value, e), ALU.is_equal))
            o.step(V.tensor_tensor(mark, mark, rank, ALU.mult))
            o.step(V.tensor_reduce(idx, mark, AX_X, ALU.max))
            o.step(V.tensor_tensor(mark, mark, gbc(idx, e), ALU.is_equal))
            if more:
                o.step(V.scalar_tensor_tensor(out=score, in0=mark, scalar=NEG, in1=score, op0=ALU.mult, op1=ALU.add))

        def router_pe(pe, k, lhs, wname, ready):
            e = FFN_EXPERTS[k] - {1: 1, 3: 2}.get(k, 0)
            pe.wait_ge(*done(ready[0], ready[1]))
            for t in range(NT):
                last = mm(PS[:, 1024 + t * e:1024 + (t + 1) * e], tile(lhs, t), W(wname))
            last.then_inc(S["logits"], 1)

        def gates_pe(pe, k):
            e = FFN_EXPERTS[k]
            pe.wait_ge(*done("gates", k + 1))
            for t in range(NT):
                last = nc.tensor.transpose(PS[0:e, 1024 + t * 128:1024 + (t + 1) * 128], gview(0, e)[:, t, :], W("ident"))
            last.then_inc(S["gatesT_ps"], 1)

        def gates_act(act, k):
            e = FFN_EXPERTS[k]
            act.wait_ge(*done("gatesT_ps", k + 1))
            nc.scalar.activation(gT[0:e, :], PS[0:e, 1024:2048], ACT.Copy).then_inc(S["gatesT"], 1)

        def ffn_load(sp, k, s, e):
            sp.dma_start(wslot[:, s, 0:FFN_COLUMNS[k]], a[f"ffn{k}"][e].rearrange("o p c -> (o p) c")).then_inc(S[f"f{k}_w{s}"], 16)

        def gate_load(sp, k, s, e):
            sp.dma_start(gslot[:, s, :], gates_dram[k][e].to_broadcast([128, N])).then_inc(S[f"f{k}_g{s}"], 16)

        def ffn_sp(sp, k):
            E = FFN_EXPERTS[k]
            if k == 1:
                sp.wait_ge(*done("h_ready", 6))
            if k:
                sp.wait_ge(*done(f"f{k - 1}_down", NU[k - 1] * FFN_EXPERTS[k - 1] + RH))
            for s in range(2):
                ffn_load(sp, k, s, slice(s, s + 1))
            sp.wait_ge(*done("gatesT", k + 1))
            sp.dma_start(gates_dram[k, 0:E], gT[0:E, :]).then_inc(S["gates_out"], 16)
            sp.wait_ge(*done("gates_out", 16 * (k + 1)))
            if k:
                sp.wait_ge(*done("h_ready", 4 * k + 2))
            for s in range(2):
                gate_load(sp, k, s, slice(s, s + 1))
            with sp.Fori(1, E // 2) as i:
                for s in range(2):
                    sp.wait_ge(*done(f"f{k}_down", i * (2 * NU[k]) + (NU[k] * (s - 1) + RH)))
                    if k == 0:
                        sp.wait_ge(*done("f0_sum", i * 4 + (2 * s + 2 - 4)))
                    ffn_load(sp, k, s, bass.ds(i * 2 + s, 1))
                    gate_load(sp, k, s, bass.ds(i * 2 + s, 1))
            if E % 2:
                sp.wait_ge(*done(f"f{k}_down", NU[k] * (E - 2) + RH))
                ffn_load(sp, k, 0, slice(E - 1, E))
                gate_load(sp, k, 0, slice(E - 1, E))

        def at(i, per, x):
            return i * per + x

        def w1_(k, s, f):
            return wslot[:, s, f * 128:(f + 1) * 128]

        def w2_(k, s, f):
            c = 512 + f * 128
            return wslot[:, s, c:c + 128]

        def ffn_up(pe, k, i, s, v):
            u, nu = v % NU[k], NU[k]
            if u == 0:
                pe.wait_ge(*done(f"f{k}_w{s}", i * 16 + 16))
            if k == 1:
                pe.wait_ge(*done("f1_gated", at(i, 2 * nu, v + 1 + RH - RP[1])))
                b = 2 * (v % 2)
                mm(bank(b), w1_(k, s, u // 2), h(xT, u % 2))
                mm(bank(b + 1), wslot[:, s, 256 + (u // 2) * 128:256 + (u // 2) * 128 + 128],
                   h(xT, u % 2)).then_inc(S["f1_up"], 1)
            else:
                pe.wait_ge(*done(f"f{k}_act", at(i, 2 * nu, v + 1)))
                mm(bank(v % 4), w1_(k, s, u // 2), h(xT, u % 2)).then_inc(S[f"f{k}_up"], 1)

        def ffn_down(pe, k, i, s, v):
            u, nu = v % NU[k], NU[k]
            if k == 0:
                if u < 2:
                    pe.wait_ge(*done("f0_z", at(i, 4, 2 * s + u + 1)))
                pe.wait_ge(*done("f0_act", at(i, 2 * nu, v + 1 + RP[0])))
                mm(bank(4 + u % 2), w2_(k, s, u // 2), hid[:, v % RH, :], u < 2, u >= nu - 2).then_inc(S["f0_down"], 1)
            else:
                pe.wait_ge(*done(f"f{k}_gated", at(i, 2 * nu, v + 1 + RH)))
                mm(bank(4 + u % 2), w2_(k, s, u // 2), hidg[:, v % RH, :], False, False).then_inc(S[f"f{k}_down"], 1)

        def ffn_units_pe(pe, k, i, experts):
            n = NU[k] * experts
            for v in range(n + 2):
                if v < n:
                    ffn_up(pe, k, i, v // NU[k], v)
                if v >= 2:
                    ffn_down(pe, k, i, (v - 2) // NU[k], v - 2)

        def ffn_pe(pe, k, bias):
            E = FFN_EXPERTS[k]
            pe.sem_inc(S[f"f{k}_down"], RH)
            pe.wait_ge(*done("gatesT", k + 1))
            for c in range(2):
                mm(bank(4 + c), bias, gT[0:E, c * HALF:(c + 1) * HALF], True, False)
            with pe.Fori(0, E // 2) as i:
                ffn_units_pe(pe, k, i, 2)
            if E % 2:
                ffn_units_pe(pe, k, E // 2, 1)

        def ffn_unit_act(act, k, i, s, v):
            u, nu = v % NU[k], NU[k]
            act.wait_ge(*done(f"f{k}_up", at(i, 2 * nu, v + 1)))
            if k == 0:
                act.wait_ge(*done("f0_down", at(i, 2 * nu, v + 1)))
                nc.scalar.activation(hid[:, v % RH, :], bank(v % 4), ACT.Relu,
                                     bias=wslot[:, s, 1024 + u // 2:1025 + u // 2]).then_inc(S["f0_act"], 1)
                return
            act.wait_ge(*done(f"f{k}_gated", at(i, 2 * nu, v + 1)))
            if k == 1:
                nc.scalar.activation(hid[:, v % RH, :], bank(2 * (v % 2)), ACT.Silu).then_inc(S["f1_act"], 1)
            elif k == 2:
                b1 = wslot[:, s, 1024 + u // 2:1025 + u // 2]
                nc.scalar.activation(hid[:, v % RH, :], bank(v % 4), ACT.Exp, bias=b1)
                nc.scalar.activation(hid2[:, v % RH, :], bank(v % 4), ACT.Relu, bias=b1).then_inc(S["f2_act"], 1)
            else:
                nc.scalar.activation(hid[:, v % RH, :], bank(v % 4), ACT.Gelu,
                                     bias=wslot[:, s, 1024 + u // 2:1025 + u // 2]).then_inc(S["f3_act"], 1)

        def ffn_act(act, k):
            E = FFN_EXPERTS[k]
            act.sem_inc(S[f"f{k}_act"], RP[k])
            with act.Fori(0, E // 2) as i:
                for v in range(2 * NU[k]):
                    ffn_unit_act(act, k, i, v // NU[k], v)
            if E % 2:
                for v in range(NU[k]):
                    ffn_unit_act(act, k, E // 2, 0, v)

        def ffn_unit_dve(dve, o, k, i, s, v):
            V = nc.vector
            u, nu = v % NU[k], NU[k]
            if u == 0:
                dve.wait_ge(*done(f"f{k}_g{s}", i * 16 + 16))
            dve.wait_ge(*done(f"f{k}_act", at(i, 2 * nu, v + 1 + RP[k])))
            dve.wait_ge(*done(f"f{k}_down", at(i, 2 * nu, v + 1)))
            g = gslot[:, s, (u % 2) * HALF:(u % 2 + 1) * HALF]
            hv = hid[:, v % RH, :]
            if k == 1:
                o.step(V.tensor_tensor(hv, hv, bank(2 * (v % 2) + 1), ALU.mult))
                V.tensor_tensor(hidg[:, v % RH, :], hv, g, ALU.mult).then_inc(S["f1_gated"], 1)
            elif k == 2:
                o.step(V.scalar_tensor_tensor(out=hv, in0=hv, scalar=1.0, in1=hid2[:, v % RH, :], op0=ALU.min, op1=ALU.add))
                V.scalar_tensor_tensor(out=hidg[:, v % RH, :], in0=hv, scalar=-1.0, in1=g, op0=ALU.add,
                                       op1=ALU.mult).then_inc(S["f2_gated"], 1)
            else:
                V.tensor_tensor(hidg[:, v % RH, :], hv, g, ALU.mult).then_inc(S[f"f{k}_gated"], 1)

        def ffn_dve(dve, o, k):
            E = FFN_EXPERTS[k]
            dve.sem_inc(S[f"f{k}_gated"], RH)
            steps = {1: 2 * NU[1], 2: 2 * NU[2]}.get(k, 0)
            with dve.Fori(0, E // 2) as i:
                o.loop(i, steps)
                for v in range(2 * NU[k]):
                    ffn_unit_dve(dve, o, k, i, v // NU[k], v)
                o.end(E // 2)
            if E % 2:
                for v in range(NU[k]):
                    ffn_unit_dve(dve, o, k, E // 2, 0, v)
            dve.wait_ge(*done(f"f{k}_down", NU[k] * E + RH))

        def f0_mean_pe(pe, i, s):
            for c in range(2):
                pe.wait_ge(*done("f0_z", at(i, 4, 2 * s + c + 1 + 2)))
                mm(bank(6 + c), W("mean"), h(z0, c)).then_inc(S["f0_mean"], 1)

        def f0_var_pe(pe, i, s):
            for c in range(2):
                pe.wait_ge(*done("f0_sq", at(i, 4, 2 * s + c + 1)))
                mm(bank(6 + c), W("mean"), h(zs, c)).then_inc(S["f0_var"], 1)

        def f0_pe(pe):
            pe.sem_inc(S["f0_down"], RH)
            pe.wait_ge(*done("gatesT", 1))
            n = NU[0]
            with pe.Fori(0, 4) as i:
                for v in range(2 * n + 2):
                    if v < 2 * n:
                        ffn_up(pe, 0, i, v // n, v)
                    if v >= 2:
                        ffn_down(pe, 0, i, (v - 2) // n, v - 2)
                    if v == n + 3:
                        f0_mean_pe(pe, i, 0)
                    if v == n + 5:
                        f0_var_pe(pe, i, 0)
                f0_mean_pe(pe, i, 1)
                f0_var_pe(pe, i, 1)
            pe.wait_ge(*done("f0_z", 18))
            for c in range(2):
                mm(bank(4 + c), W("f0_beta"), gT[0:8, c * HALF:(c + 1) * HALF]).then_inc(S["f0_beta"], 1)

        def f0_sq_act(act, i, s):
            for c in range(2):
                act.wait_ge(*done("f0_zc", at(i, 4, 2 * s + c + 1)))
                nc.scalar.activation(h(zs, c), h(zc, c), ACT.Square).then_inc(S["f0_sq"], 1)

        def f0_std_act(act, i, s):
            for c in range(2):
                act.wait_ge(*done("f0_var", at(i, 4, 2 * s + c + 1)))
                nc.scalar.activation(h(zs, c), bank(6 + c), ACT.Sqrt, bias=eps6[:, 0:1]).then_inc(S["f0_std"], 1)

        def f0_act(act):
            act.sem_inc(S["f0_act"], RP[0])
            n = NU[0]
            with act.Fori(0, 4) as i:
                for v in range(2 * n):
                    ffn_unit_act(act, 0, i, v // n, v)
                    if v == n + 3:
                        f0_sq_act(act, i, 0)
                    if v == n + 5:
                        f0_std_act(act, i, 0)
                f0_sq_act(act, i, 1)
                f0_std_act(act, i, 1)

        def f0_dve(dve, o):
            V = nc.vector
            dve.sem_inc(S["f0_z"], 2)
            o.step(V.memset(acc, 0.0))
            n = NU[0]
            with dve.Fori(0, 4) as i:
                o.loop(i, 12)
                for s in range(2):
                    dve.wait_ge(*done(f"f0_g{s}", i * 16 + 16))
                    for c in range(2):
                        dve.wait_ge(*done("f0_down", at(i, 2 * n, n * s + n - 1 + c + RH)))
                        V.scalar_tensor_tensor(out=h(z0, c), in0=bank(4 + c), scalar=wslot[:, s, 1028:1029],
                                               in1=h(xT, c), op0=ALU.add, op1=ALU.add).then_inc(S["f0_z"], 1)
                    for c in range(2):
                        dve.wait_ge(*done("f0_mean", at(i, 4, 2 * s + c + 1)))
                        V.tensor_tensor(h(zc, c), h(z0, c), bank(6 + c), ALU.subtract).then_inc(S["f0_zc"], 1)
                    for c in range(2):
                        dve.wait_ge(*done("f0_std", at(i, 4, 2 * s + c + 1)))
                        o.step(V.reciprocal(h(zs, c), h(zs, c)))
                        o.step(V.tensor_tensor(h(zc, c), h(zc, c), h(zs, c), ALU.mult))
                        o.step(V.scalar_tensor_tensor(out=h(zc, c), in0=h(zc, c), scalar=wslot[:, s, 1029:1030],
                                                      in1=gslot[:, s, c * HALF:(c + 1) * HALF], op0=ALU.mult, op1=ALU.mult))
                        V.tensor_tensor(h(acc, c), h(acc, c), h(zc, c), ALU.add).then_inc(S["f0_sum"], 1)
                o.end(4)
            dve.wait_ge(*done("f0_sum", 16))
            for c in range(2):
                dve.wait_ge(*done("f0_beta", c + 1))
                o.step(V.tensor_tensor(h(hT, c), h(hT, c), h(acc, c), ALU.add))
                o.tell_step(V.tensor_tensor(h(hT, c), h(hT, c), bank(4 + c), ALU.add), "h_ready")

        def softmax2(o, act_sem, k, v1_, v2_, g1, g2, d):
            V = nc.vector
            o.tell_step(V.tensor_tensor(d, v2_, v1_, ALU.subtract), f"g{k}_shift")
            o.eng.wait_ge(*done(f"g{k}_exp", 1))
            o.step(V.tensor_scalar(g1, d, 1.0, None, ALU.add))
            o.step(V.reciprocal(g1, g1))
            o.step(V.tensor_tensor(g2, d, g1, ALU.mult))

        def mix2(o, e, m1, m2, g1, g2, dst, k):
            V = nc.vector
            o.step(V.tensor_tensor(m1, m1, gbc(g1, e), ALU.mult))
            o.step(V.tensor_tensor(m2, m2, gbc(g2, e), ALU.mult))
            o.tell_step(V.tensor_tensor(dst, m1, m2, ALU.add), "gates")

        def g0_dve(dve, o):
            V = nc.vector
            dve.wait_ge(*done("logits", 1))
            lg, m1, m2, dst = gview(1, 8), gview(2, 8), gview(3, 8), gview(0, 8)
            o.step(V.tensor_copy(lg, PS[:, 1024:1024 + 64].rearrange("p (t e) -> p t e", e=8)))
            top(o, lg, gcol(4), m1, gcol(5), 8, True)
            top(o, lg, gcol(6), m2, gcol(5), 8, False)
            softmax2(o, None, 0, gcol(4), gcol(6), gcol(7), gcol(8), gcol(9))
            mix2(o, 8, m1, m2, gcol(7), gcol(8), dst, 0)

        def g_exp_act(act, k):
            act.wait_ge(*done(f"g{k}_shift", 1))
            nc.scalar.activation(gcol(9), gcol(9), ACT.Exp).then_inc(S[f"g{k}_exp"], 1)

        def g1_dve(dve, o):
            V = nc.vector
            dve.wait_ge(*done("logits", 2))
            lg, lb, m1, m2, mx = (gview(x, 8) for x in (1, 2, 3, 4, 5))
            o.step(V.tensor_copy(lg, PS[:, 1024:1024 + 64].rearrange("p (t e) -> p t e", e=8)))
            o.step(V.tensor_tensor(lb, lg, W("f1_bias").unsqueeze(1).to_broadcast([128, 8, 8]), ALU.add))
            top(o, lb, gcol(6), m1, gcol(7), 8, True)
            top(o, lb, gcol(6), m2, gcol(7), 8, False)
            v12 = gtmp[:, 8, 0:16]
            top(o, lg, gtmp[:, 8, 0:8], mx, gcol(7), 8, True)
            o.tell_step(V.tensor_reduce(gtmp[:, 8, 8:16], lg, AX_X, ALU.max), "g1_top")
            dve.wait_ge(*done("g1_sig", 1))
            o.step(V.tensor_tensor(gcol(9), gtmp[:, 8, 0:8], gtmp[:, 8, 8:16], ALU.add))
            o.step(V.reciprocal(gcol(9), gcol(9)))
            o.step(V.tensor_tensor(gcol(10), gtmp[:, 8, 0:8], gcol(9), ALU.mult))
            o.step(V.tensor_tensor(gcol(11), gtmp[:, 8, 8:16], gcol(9), ALU.mult))
            dst = gview(0, 9)
            o.step(V.memset(dst, 1.0))
            mix2(o, 8, m1, m2, gcol(10), gcol(11), dst[:, :, 0:8], 1)

        def g1_act(act):
            act.wait_ge(*done("g1_top", 1))
            nc.scalar.activation(gtmp[:, 8, 0:16], gtmp[:, 8, 0:16], ACT.Sigmoid).then_inc(S["g1_sig"], 1)

        def ffn_add_dve(dve, o, k):
            for c in range(2):
                o.tell_step(nc.vector.tensor_tensor(h(hT, c), h(hT, c), bank(4 + c), ALU.add), "h_ready")

        def a1_pe(pe):
            pe.wait_ge(*done("pack2", 16))
            pe.wait_ge(*done("ln_out", 6))
            for x, name in enumerate(("a1_wq", "a1_wk", "a1_wf")):
                for k in range(2):
                    last = mm(bank(2 * x + k, rows=64), W(name), h(xT, k))
                last.then_inc(S["a1_qkf"], 1)
            for t in range(NT):
                last = mm(PS[:, 3072 + t * 128:3072 + (t + 1) * 128], tile(xT, t), W("a1_wv"))
            last.then_inc(S["a1_v"], 1)
            pe.wait_ge(*done("a1_qk", 2))
            for k in range(2):
                last = mm(bank(k, rows=32), W("a1_c1w"), h(xT, k))
            last.then_inc(S["a1_c1"], 1)
            for k in range(2):
                last = mm(bank(2 + k), W("a1_eq"), h(xT, k))
            last.then_inc(S["a1_qh"], 1)
            pe.wait_ge(*done("a1_sig", 1))
            for k in range(2):
                last = mm(bank(4 + k), W("a1_sin"), h(xT, k))
            last.then_inc(S["a1_qs"], 1)
            pe.wait_ge(*done("a1_vcopy", 1))
            mm(PS[:, 3072:3072 + 32], W("a1_ek"), W("a1_slots"))
            mm(PS[:, 3584:3584 + 128], W("a1_slots4"), W("a1_ev")).then_inc(S["a1_kv"], 1)
            pe.wait_ge(*done("a1_kvm", 2))
            pe.wait_ge(*done("a1_qhcopy", 1))
            for t in range(NT):
                last = mm(PS[:, 1024 + t * 128:1024 + (t + 1) * 128], tile(qhT, t), khm)
            last.then_inc(S["a1_se"], 1)
            pe.wait_ge(*done("a1_qscopy", 1))
            for t in range(NT):
                last = mm(PS[:, 2048 + t * 64:2048 + (t + 1) * 64], tile(qsT, t), W("a1_knowT"))
            last.then_inc(S["a1_ss"], 1)
            pe.wait_ge(*done("a1_silu", 1))
            for t in range(NT):
                last = mm(PS[:, 2560 + t * 3:2560 + (t + 1) * 3], tile(c1, t), W("a1_c2w"))
            last.then_inc(S["a1_sc"], 1)
            pe.wait_ge(*done("a1_hat", 2))
            for t in range(NT):
                last = mm(PS[:, t * 128:(t + 1) * 128], tile(khat, t), tile(qhat, t))
            last.then_inc(S["a1_sl"], 1)
            pe.wait_ge(*done("a1_slm", 1))
            for t in range(NT):
                mm(PS[:, 3072 + t * 128:3072 + (t + 1) * 128], tile(vN, t), tile(slm, t))
            for k in range(2):
                last = mm(bank(k), W("ones"), h(slm, k))
            last.then_inc(S["a1_num"], 1)
            pe.wait_ge(*done("a1_pe", 1))
            for t in range(NT):
                last = nc.tensor.transpose(PS[:, 1024 + t * 128:1024 + (t + 1) * 128], tile(pE, t), W("ident"))
            last.then_inc(S["a1_peT"], 1)
            pe.wait_ge(*done("a1_ps", 1))
            for t in range(NT):
                last = nc.tensor.transpose(PS[0:64, 2048 + t * 128:2048 + (t + 1) * 128], pS[:, t * 64:(t + 1) * 64],
                                           W("ident"))
            last.then_inc(S["a1_psT"], 1)
            pe.wait_ge(*done("a1_peTcopy", 1))
            for k in range(2):
                last = mm(bank(2 + k), vhm, h(peT, k))
            last.then_inc(S["a1_oh"], 1)
            ln_pe(pe, 3, wn, ("a1_w", 1, 2))
            pe.wait_ge(*done("a1_ohcopy", 1))
            for k in range(2):
                last = mm(bank(2 + k), W("a1_eo"), h(ohT, k))
            last.then_inc(S["a1_eo"], 1)
            pe.wait_ge(*done("a1_psTcopy", 1))
            for k in range(2):
                last = mm(bank(k), W("a1_know"), h(psT, k))
            last.then_inc(S["a1_ret"], 1)
            for k in range(2):
                last = mm(bank(4 + k), W("a1_sgw"), h(xT, k))
            last.then_inc(S["a1_sg"], 1)
            for k in range(2):
                pe.wait_ge(*done("ln_out", 7 + k))
                last = mm(bank(6 + k), W("a1_wo"), h(wln, k))
            last.then_inc(S["a1_wo"], 1)
            pe.wait_ge(*done("a1_gate", 1))
            pe.wait_ge(*done("a1_pc", 1))
            for t in range(NT):
                last = nc.tensor.transpose(PS[0:3, 2048 + t * 128:2048 + (t + 1) * 128], pC[:, t * 3:(t + 1) * 3],
                                           W("ident"))
            last.then_inc(S["a1_pcT"], 1)
            pe.wait_ge(*done("a1_sin_", 2))
            for k in range(2):
                last = mm(bank(k), W("a1_so"), h(sIn, k))
            last.then_inc(S["a1_so"], 1)
            pe.wait_ge(*done("a1_pcTcopy", 1))
            for b in range(3):
                if b:
                    pe.wait_ge(*done("a1_mixed", b))
                for k in range(2):
                    last = mm(bank(4 + k), W("sel3", b * 128, (b + 1) * 128), wT[:, k * HALF:(k + 1) * HALF])
                last.then_inc(S["a1_bw"], 1)

        minq, mink = big(0, rows=64), big(1, rows=64)
        qhat, khat = big(2, rows=64), big(3, rows=64)
        slm, wn, vN, qhT, qsT, pE = big(4), big(5), big(10), big(11), big(12), big(13)
        logf, eneg, epos = big(6, rows=64), big(7, rows=64), big(8, rows=64)
        c1 = big(9, rows=32)
        pS = big(14)[:, 0:512]
        pC = big(14)[:, 512:536]
        pst = big(14)[:, 640:768]
        peT = big(15)
        psT, ohT, wln = bigb(0, rows=64), bigb(1), bigb(3)
        khm, vhm = bigb(4)[:, 0:128], bigb(4)[:, 128:256]
        wT = bigb(2, rows=3)
        reset = bigb(5)
        gS, sIn, rec = big(0), big(1), big(6)

        def a1_act(act, o):
            A = nc.scalar
            act.wait_ge(*done("pack2", 16))
            act.wait_ge(*done("a1_qkf", 3))
            A.activation(logf, PS[0:64, 2048:3072], ACT.Sigmoid, bias=W("a1_bf")).then_inc(S["a1_sig"], 1)
            act.wait_ge(*done("a1_v", 1))
            A.activation(vN, PS[:, 3072:4096], ACT.Copy).then_inc(S["a1_vcopy"], 1)
            for x, m in enumerate((minq, mink)):
                act.wait_ge(*done("a1_min", x + 1))
                A.activation(m, m, ACT.Exp).then_inc(S["a1_exp2"], 1)
            act.wait_ge(*done("a1_qh", 1))
            A.activation(qhT, PS[:, 1024:2048], ACT.Copy).then_inc(S["a1_qhcopy"], 1)
            act.wait_ge(*done("a1_c1", 1))
            A.activation(c1, PS[0:32, 0:1024], ACT.Silu, bias=W("a1_c1b")).then_inc(S["a1_silu"], 1)
            act.wait_ge(*done("a1_qs", 1))
            A.activation(qsT, PS[:, 2048:3072], ACT.Copy).then_inc(S["a1_qscopy"], 1)
            act.wait_ge(*done("a1_sgmax", 1))
            A.activation(logf, logf, ACT.Ln).then_inc(S["a1_ln"], 1)
            act.wait_ge(*done("a1_cum", 1))
            A.activation(eneg, logf, ACT.Exp, scale=-1.0).then_inc(S["a1_en"], 1)
            A.activation(epos, logf, ACT.Exp).then_inc(S["a1_ep"], 1)
            act.wait_ge(*done("a1_eshift", 1))
            A.activation(pE, pE, ACT.Exp, scale=32.0 ** -0.5).then_inc(S["a1_eexp"], 1)
            act.wait_ge(*done("a1_sshift", 1))
            A.activation(pS, pS, ACT.Exp, scale=128.0 ** -0.5).then_inc(S["a1_sexp"], 1)
            act.wait_ge(*done("a1_cshift", 1))
            A.activation(pC, pC, ACT.Exp).then_inc(S["a1_cexp"], 1)
            act.wait_ge(*done("a1_peT", 1))
            A.activation(peT, PS[:, 1024:2048], ACT.Copy).then_inc(S["a1_peTcopy"], 1)
            act.wait_ge(*done("a1_psT", 1))
            A.activation(psT, PS[0:64, 2048:3072], ACT.Copy).then_inc(S["a1_psTcopy"], 1)
            act.wait_ge(*done("a1_oh", 1))
            A.activation(ohT, PS[:, 1024:2048], ACT.Copy).then_inc(S["a1_ohcopy"], 1)
            ln_act(act, 3, eps5)
            act.wait_ge(*done("a1_sg", 1))
            A.activation(gS, PS[:, 2048:3072], ACT.Sigmoid, bias=W("a1_sgb")).then_inc(S["a1_gate"], 1)
            act.wait_ge(*done("a1_pcT", 1))
            A.activation(wT, PS[0:3, 2048:3072], ACT.Copy).then_inc(S["a1_pcTcopy"], 1)

        def a1_pool(pool):
            pool.wait_ge(*done("h_ready", 4))
            nc.gpsimd.memset(reset, 1.0).then_inc(S["reset"], 1)
            pool.wait_ge(*done("reset", 1))
            nc.gpsimd.memset(reset.rearrange("p (b t) -> p b t", t=T)[:, :, 0], 0.0).then_inc(S["reset"], 1)

        def soft_shift(o, dst, src, top_, grp, width, name, extra=None):
            V = nc.vector
            d3 = dst.rearrange("p (g w) -> p g w", w=width)
            s3 = src.rearrange("p (g w) -> p g w", w=width)
            if extra is not None:
                o.step(V.tensor_tensor(d3, s3, extra, ALU.add))
                s3 = d3
            o.step(V.tensor_reduce(top_, s3, AX_X, ALU.max))
            o.tell_step(V.tensor_tensor(d3, s3, top_.unsqueeze(2).to_broadcast([128, grp, width]), ALU.subtract), name)

        def soft_norm(o, x, sum_, grp, width, name):
            V = nc.vector
            x3 = x.rearrange("p (g w) -> p g w", w=width)
            o.step(V.tensor_reduce(sum_, x3, AX_X, ALU.add))
            o.step(V.reciprocal(sum_, sum_))
            o.tell_step(V.tensor_tensor(x3, x3, sum_.unsqueeze(2).to_broadcast([128, grp, width]), ALU.mult), name)

        def a1_dve(dve, o):
            V = nc.vector
            dve.wait_ge(*done("pack2", 16))
            for x, m in enumerate((minq, mink)):
                dve.wait_ge(*done("a1_qkf", x + 1))
                o.tell(V.tensor_scalar(m, PS[0:64, x * 1024:(x + 1) * 1024], 0.0, None, ALU.min), "a1_min")
            dve.wait_ge(*done("a1_sig", 1))
            o.tell(V.tensor_scalar(logf, logf, 1e-6, None, ALU.max), "a1_sgmax")
            for x, (m, dst) in enumerate(((minq, qhat), (mink, khat))):
                dve.wait_ge(*done("a1_exp2", x + 1))
                o.tell_step(V.scalar_tensor_tensor(out=dst, in0=PS[0:64, x * 1024:(x + 1) * 1024], scalar=0.0, in1=m,
                                                   op0=ALU.max, op1=ALU.add), "a1_qk")
            dve.wait_ge(*done("a1_kv", 1))
            hv = W("heads4")
            o.tell(V.tensor_tensor(khm.rearrange("p (h s) -> p h s", s=32),
                                   PS[:, 3072:3104].unsqueeze(1).to_broadcast([128, 4, 32]),
                                   hv.rearrange("p (h s) -> p h s", s=32), ALU.mult), "a1_kvm")
            o.tell(V.tensor_tensor(vhm, PS[:, 3584:3712], hv, ALU.mult), "a1_kvm")
            dve.wait_ge(*done("a1_ln", 1))
            dve.wait_ge(*done("reset", 2))
            o.step(V.tensor_tensor_scan(eneg, reset[0:64, :], logf, 0.0, ALU.mult, ALU.add))
            o.tell_step(V.tensor_scalar(logf, eneg, -20.0, 20.0, ALU.max, ALU.min), "a1_cum")
            dve.wait_ge(*done("a1_ep", 1))
            o.tell(V.scalar_tensor_tensor(out=qhat, in0=qhat, scalar=0.125, in1=epos, op0=ALU.mult, op1=ALU.mult), "a1_hat")
            o.tell(V.tensor_tensor(khat, khat, eneg, ALU.mult), "a1_hat")
            dve.wait_ge(*done("a1_se", 1))
            soft_shift(o, pE, PS[:, 1024:2048], pst[:, 0:32], 32, 32, "a1_eshift")
            dve.wait_ge(*done("a1_ss", 1))
            soft_shift(o, pS, PS[:, 2048:2560], pst[:, 32:40], 8, 64, "a1_sshift")
            dve.wait_ge(*done("a1_sc", 1))
            soft_shift(o, pC, PS[:, 2560:2584], pst[:, 40:48], 8, 3, "a1_cshift",
                       extra=W("a1_c2b").unsqueeze(1).to_broadcast([128, 8, 3]))
            dve.wait_ge(*done("a1_sl", 1))
            o.tell(V.tensor_tensor(slm.rearrange("p (t l) -> p t l", l=128), PS[:, 0:1024].rearrange("p (t l) -> p t l", l=128),
                                   W("causal_sl").unsqueeze(1).to_broadcast([128, 8, 128]), ALU.mult), "a1_slm")
            dve.wait_ge(*done("a1_eexp", 1))
            soft_norm(o, pE, pst[:, 0:32], 32, 32, "a1_pe")
            dve.wait_ge(*done("a1_sexp", 1))
            soft_norm(o, pS, pst[:, 32:40], 8, 64, "a1_ps")
            dve.wait_ge(*done("a1_cexp", 1))
            soft_norm(o, pC, pst[:, 40:48], 8, 3, "a1_pc")
            dve.wait_ge(*done("a1_num", 1))
            for k in range(2):
                o.step(V.tensor_scalar(h(rec, k), bank(k), 1e-6, None, ALU.add))
                o.step(V.reciprocal(h(rec, k), h(rec, k)))
                o.tell_step(V.tensor_tensor(h(wn, k), bank(6 + k), h(rec, k), ALU.mult), "a1_w")
            ln_dve(dve, o, 3, wn, wln, W("a1_g"), W("a1_b"))
            dve.wait_ge(*done("a1_ret", 1))
            dve.wait_ge(*done("a1_gate", 1))
            for k in range(2):
                o.step(V.tensor_tensor(h(sIn, k), bank(k), h(xT, k), ALU.subtract))
                o.step(V.tensor_tensor(h(sIn, k), h(sIn, k), h(gS, k), ALU.mult))
                o.tell_step(V.tensor_tensor(h(sIn, k), h(sIn, k), h(xT, k), ALU.add), "a1_sin_")
            for b, (ready, where_) in enumerate((("a1_wo", 6), ("a1_eo", 2), ("a1_so", 0))):
                dve.wait_ge(*done(ready, 1))
                o.step(V.tensor_copy(rec, PS[:, where_ * 512:(where_ + 2) * 512]))
                dve.wait_ge(*done("a1_bw", b + 1))
                o.tell_step(V.tensor_tensor(rec, rec, PS[:, 2048:3072], ALU.mult), "a1_mixed")
                for k in range(2):
                    ins = V.tensor_tensor(h(hT, k), h(hT, k), h(rec, k), ALU.add)
                    if b == 2:
                        o.tell_step(ins, "h_ready")
                    else:
                        o.step(ins)

        xcv = [big(0), big(1)]
        zg = [big(2), big(3)]
        dt = [big(4), big(5)]
        dtx = [big(6), big(7)]
        dA = [big(8), big(9)]
        dB = [big(10), big(11)]
        hs = [big(12), big(13)]
        hc = [big(14), big(15)]
        bcs = [[bigb(0), bigb(1)], [bigb(2), bigb(3)]]
        bcT = bigb(4, rows=32)
        dtl = gslot[0:8, 0, :]
        negA = sb("negA", [128, 32])
        ym = [big(8), big(9)]
        xm, q2, k2, v2, at2, atT, o2 = big(10), big(11), big(12), big(13), big(14), big(15), big(0)

        def bt(x):
            return x.rearrange("p (b t) -> p b t", t=T)

        def a2_pe(pe):
            pe.wait_ge(*done("pack3", 16))
            pe.wait_ge(*done("ln_out", 12))
            for x in range(4):
                for k in range(2):
                    last = mm(bank(2 * x + k), W("a2_in", x * 128, (x + 1) * 128), h(xT, k))
                last.then_inc(S["a2_xz"], 1)
            pe.wait_ge(*done("a2_xc", 2))
            for r0, r1, b0 in ((0, 8, 0), (8, 40, 2)):
                for k in range(2):
                    for c in range(2):
                        last = mm(bank(b0 + k, rows=r1 - r0), W("a2_xp", c * 40 + r0, c * 40 + r1), h(xcv[c], k), c == 0, c == 1)
                last.then_inc(S["a2_xp"], 1)
            pe.wait_ge(*done("a2_dtl", 1))
            for c in range(2):
                for k in range(2):
                    last = mm(bank(4 + 2 * c + k), W("a2_dtw", c * 128, (c + 1) * 128), h(dtl, k))
                last.then_inc(S["a2_dt"], 1)
            pe.wait_ge(*done("a2_bcT", 1))
            for b in range(4):
                mm(bank(b), W("f1_zero"), xT[0:9, 0:HALF], True, False)
            with pe.Fori(0, 8) as i:
                for s in range(2):
                    for c in range(2):
                        pe.wait_ge(*done("a2_hc", i * 4 + (2 * s + c + 1)))
                        for k in range(2):
                            last = mm(bank(2 * c + k), W("ident"), h(hc[c], k), False, False)
                        last.then_inc(S["a2_ysum"], 1)
            pe.wait_ge(*done("a2_ym", 2))
            for k in range(2):
                for c in range(2):
                    last = mm(bank(4 + k), W("a2_out", c * 128, (c + 1) * 128), h(ym[c], k), c == 0, c == 1)
            last.then_inc(S["a2_out"], 1)
            pe.wait_ge(*done("a2_xm", 1))
            for x, name in enumerate(("a2_wq", "a2_wk")):
                for k in range(2):
                    last = mm(bank(2 * x + k), W(name), h(xm, k))
                last.then_inc(S["a2_qk"], 1)
            for t in range(NT):
                last = mm(PS[:, 3072 + t * 128:3072 + (t + 1) * 128], tile(xm, t), W("a2_wv"))
            last.then_inc(S["a2_v"], 1)
            pe.wait_ge(*done("a2_qkcopy", 2))
            for t in range(NT):
                last = mm(PS[:, 2048 + t * 128:2048 + (t + 1) * 128], tile(q2, t), tile(k2, t))
            last.then_inc(S["a2_s"], 1)
            pe.wait_ge(*done("a2_att", 1))
            for t in range(NT):
                last = nc.tensor.transpose(PS[:, t * 128:(t + 1) * 128], tile(at2, t), W("ident"))
            last.then_inc(S["a2_atT"], 1)
            pe.wait_ge(*done("a2_atTcopy", 1))
            pe.wait_ge(*done("a2_vcopy", 1))
            for t in range(NT):
                last = mm(PS[:, 1024 + t * 128:1024 + (t + 1) * 128], tile(v2, t), tile(atT, t))
            last.then_inc(S["a2_o"], 1)
            pe.wait_ge(*done("a2_ocopy", 1))
            for k in range(2):
                mm(bank(4 + k), W("a2_fc"), h(o2, k)).then_inc(S["a2_fc"], 1)

        def a2_sp(sp):
            sp.wait_ge(*done("a2_bcT", 1))
            sp.dma_start(bc_dram, bcT).then_inc(S["a2_bcout"], 16)
            sp.wait_ge(*done("a2_bcout", 16))

            def load(s, b, c):
                sp.dma_start(bcs[s][0], b.to_broadcast([128, N])).then_inc(S[f"a2_bc{s}"], 16)
                sp.dma_start(bcs[s][1], c.to_broadcast([128, N])).then_inc(S[f"a2_bc{s}"], 16)

            for s in range(2):
                load(s, bc_dram[s:s + 1], bc_dram[16 + s:17 + s])
            with sp.Fori(1, 8) as i:
                for s in range(2):
                    sp.wait_ge(*done("a2_hc", i * 4 + (2 * s + 2 - 4)))
                    load(s, bc_dram[bass.ds(i * 2 + s, 1)], bc_dram[bass.ds(i * 2 + (s + 16), 1)])

        def a2_pool(pool):
            pool.wait_ge(*done("h_ready", 10))
            for c in range(2):
                nc.gpsimd.memset(bt(dA[c])[:, :, 0], 0.0).then_inc(S["a2_dA0"], 1)
            with pool.Fori(0, 8) as i:
                for s in range(2):
                    pool.wait_ge(*done(f"a2_bc{s}", i * 32 + 32))
                    for c in range(2):
                        if s == 0:
                            pool.wait_ge(*done("a2_dtx", 2))
                        pool.wait_ge(*done("a2_scan", i * 4 + (2 * s + c + 1)))
                        nc.gpsimd.tensor_tensor(dB[c], dtx[c], bcs[s][0], ALU.mult).then_inc(S["a2_dB"], 1)

        def a2_act(act, o):
            A = nc.scalar
            act.wait_ge(*done("pack3", 16))
            for c in range(2):
                act.wait_ge(*done("a2_xz", 3 + c))
                A.activation(zg[c], PS[:, (4 + 2 * c) * 512:(6 + 2 * c) * 512], ACT.Silu).then_inc(S["a2_zg"], 1)
            for c in range(2):
                act.wait_ge(*done("a2_conv", c + 1))
                A.activation(xcv[c], xcv[c], ACT.Silu, bias=W("a2_cb", c, c + 1)).then_inc(S["a2_xc"], 1)
            act.wait_ge(*done("a2_xp", 1))
            A.activation(dtl, PS[0:8, 0:1024], ACT.Copy).then_inc(S["a2_dtl"], 1)
            act.wait_ge(*done("a2_xp", 2))
            A.activation(bcT, PS[0:32, 1024:2048], ACT.Copy).then_inc(S["a2_bcT"], 1)
            A.activation(negA[:, :], W("a2_alog"), ACT.Exp).then_inc(S["a2_A"], 1)
            for c in range(2):
                act.wait_ge(*done("a2_nabs", c + 1))
                A.activation(hs[c], hs[c], ACT.Exp).then_inc(S["a2_e"], 1)
            for c in range(2):
                act.wait_ge(*done("a2_e", c + 1))
                A.activation(hs[c], hs[c], ACT.Ln, bias=W("ones", 0, 1)).then_inc(S["a2_l"], 1)
            act.wait_ge(*done("a2_negA", 1))
            act.wait_ge(*done("a2_dtx", 2))
            act.wait_ge(*done("a2_dA0", 2))
            with act.Fori(0, 8) as i:
                for s in range(2):
                    for c in range(2):
                        act.wait_ge(*done("a2_scan", i * 4 + (2 * s + c + 1)))
                        A.activation(bt(dA[c])[:, :, 1:], bt(dt[c])[:, :, 1:], ACT.Exp,
                                     scale=negA[:, bass.ds(i * 2 + (c * 16 + s), 1)]).then_inc(S["a2_dA"], 1)
            act.wait_ge(*done("a2_out", 1))
            A.activation(xm, PS[:, 2048:3072], ACT.Copy).then_inc(S["a2_xm"], 1)
            for x, dst in enumerate((q2, k2)):
                act.wait_ge(*done("a2_qk", x + 1))
                A.activation(dst, PS[:, x * 1024:(x + 1) * 1024], ACT.Copy).then_inc(S["a2_qkcopy"], 1)
            act.wait_ge(*done("a2_v", 1))
            A.activation(v2, PS[:, 3072:4096], ACT.Copy).then_inc(S["a2_vcopy"], 1)
            act.wait_ge(*done("a2_shift", 1))
            A.activation(at2, at2, ACT.Exp).then_inc(S["a2_aexp"], 1)
            act.wait_ge(*done("a2_atT", 1))
            A.activation(atT, PS[:, 0:1024], ACT.Copy).then_inc(S["a2_atTcopy"], 1)
            act.wait_ge(*done("a2_o", 1))
            A.activation(o2, PS[:, 1024:2048], ACT.Copy).then_inc(S["a2_ocopy"], 1)

        def a2_dve(dve, o):
            V = nc.vector
            dve.wait_ge(*done("pack3", 16))
            for c in range(2):
                dve.wait_ge(*done("a2_xz", c + 1))
                xi = bt(PS[:, c * 1024:(c + 1) * 1024])
                y = bt(xcv[c])
                o.step(V.tensor_scalar(y, xi, W("a2_cw", 4 * c + 3, 4 * c + 4), None, ALU.mult))
                for d in (1, 2, 3):
                    ins = V.scalar_tensor_tensor(out=y[:, :, d:], in0=xi[:, :, 0:T - d],
                                                 scalar=W("a2_cw", 4 * c + 3 - d, 4 * c + 4 - d), in1=y[:, :, d:],
                                                 op0=ALU.mult, op1=ALU.add)
                    if d < 3:
                        o.step(ins)
                    else:
                        o.tell_step(ins, "a2_conv")
            dve.wait_ge(*done("a2_A", 1))
            o.tell(V.tensor_scalar(negA[:, :], negA[:, :], -1.0, None, ALU.mult), "a2_negA")
            for c in range(2):
                dve.wait_ge(*done("a2_dt", c + 1))
                o.step(V.tensor_scalar(dt[c], PS[:, (4 + 2 * c) * 512:(6 + 2 * c) * 512], W("a2_dtb", c, c + 1), None, ALU.add))
                o.tell_step(V.scalar_tensor_tensor(out=hs[c], in0=dt[c], scalar=-1.0, in1=dt[c], op0=ALU.mult, op1=ALU.min),
                            "a2_nabs")
            dve.wait_ge(*done("a2_xc", 2))
            for c in range(2):
                dve.wait_ge(*done("a2_l", c + 1))
                o.step(V.scalar_tensor_tensor(out=dt[c], in0=dt[c], scalar=0.0, in1=hs[c], op0=ALU.max, op1=ALU.add))
                o.tell_step(V.tensor_tensor(dtx[c], dt[c], xcv[c], ALU.mult), "a2_dtx")
            dve.sem_inc(S["a2_scan"], 2)
            with dve.Fori(0, 8) as i:
                for s in range(2):
                    for c in range(2):
                        n = 2 * s + c
                        dve.wait_ge(*done("a2_dA", i * 4 + (n + 1)))
                        dve.wait_ge(*done("a2_dB", i * 4 + (n + 1)))
                        V.tensor_tensor_scan(hs[c], dA[c], dB[c], 0.0, ALU.mult, ALU.add).then_inc(S["a2_scan"], 1)
                        dve.wait_ge(*done("a2_scan", i * 4 + (n + 3)))
                        dve.wait_ge(*done("a2_ysum", i * 4 + (n + 1)))
                        V.tensor_tensor(hc[c], hs[c], bcs[s][1], ALU.mult).then_inc(S["a2_hc"], 1)
            dve.wait_ge(*done("a2_ysum", 34))
            for c in range(2):
                o.step(V.scalar_tensor_tensor(out=ym[c], in0=xcv[c], scalar=W("a2_d", c, c + 1),
                                              in1=PS[:, c * 1024:(c + 1) * 1024], op0=ALU.mult, op1=ALU.add))
                o.tell_step(V.tensor_tensor(ym[c], ym[c], zg[c], ALU.mult), "a2_ym")
            dve.wait_ge(*done("a2_s", 1))
            a3d = at2.rearrange("p (t l) -> p t l", l=128)
            o.step(V.scalar_tensor_tensor(out=a3d, in0=PS[:, 2048:3072].rearrange("p (t l) -> p t l", l=128),
                                          scalar=128.0 ** -0.5, in1=W("causal_add").unsqueeze(1).to_broadcast([128, 8, 128]),
                                          op0=ALU.mult, op1=ALU.add))
            soft_shift(o, at2, at2, small[:, 32:40], 8, 128, "a2_shift")
            dve.wait_ge(*done("a2_aexp", 1))
            soft_norm(o, at2, small[:, 32:40], 8, 128, "a2_att")
            for k in range(2):
                dve.wait_ge(*done("a2_fc", k + 1))
                o.tell_step(V.scalar_tensor_tensor(out=h(hT, k), in0=bank(4 + k), scalar=W("a2_fcb"), in1=h(hT, k),
                                                   op0=ALU.add, op1=ALU.add), "h_ready")

        xpad = BIG[:, 10 * N:10 * N + 64 * 24].rearrange("p (b t) -> p b t", t=24)
        rpad = BIG[:, 12 * N:12 * N + 64 * 24].rearrange("p (b t) -> p b t", t=24)
        lnz = big(7)
        lno = big(9)

        def f2_pool(pool):
            pool.wait_ge(*done("h_ready", 12))
            nc.gpsimd.memset(xpad, 0.0).then_inc(S["f2_pad0"], 1)
            nc.gpsimd.memset(rpad, 0.0).then_inc(S["f2_pad0"], 1)

        def f2_pe(pe):
            pe.wait_ge(*done("f2_xpad", 1))
            for k in range(2):
                for j in range(3):
                    last = mm(bank(k).rearrange("p (b t) -> p b t", t=T), W("f2_rc1", j * 128, (j + 1) * 128),
                              xpad[:, 32 * k:32 * k + 32, 3 + j:19 + j], j == 0, j == 2)
            last.then_inc(S["f2_rc"], 1)
            pe.wait_ge(*done("f2_rpad", 1))
            for k in range(2):
                for j in range(3):
                    last = mm(bank(2 + k, rows=10).rearrange("p (b t) -> p b t", t=T), W("f2_rc2", j * 10, (j + 1) * 10),
                              rpad[:, 32 * k:32 * k + 32, 3 + j:19 + j], j == 0, j == 2)
            last.then_inc(S["f2_lt"], 1)
            pe.wait_ge(*done("f2_ltcopy", 1))
            for t in range(NT):
                last = nc.tensor.transpose(PS[:, 1024 + t * 10:1024 + (t + 1) * 10], gT[0:10, t * 128:(t + 1) * 128],
                                           W("ident")[0:10, 0:10])
            last.then_inc(S["logits"], 1)
            ring = [0, 1, 6, 7]

            def sh_down(u):
                pe.wait_ge(*done("f2_shact", u + 1))
                mm(bank(4 + u % 2), W("f2_sh2", (u // 2) * 128, (u // 2) * 128 + 128), hid[:, u % RH, :], u < 2,
                   False).then_inc(S["f2_shdown"], 1)

            for u in range(8):
                if u >= 4:
                    pe.wait_ge(*done("f2_shact", u - 3))
                for j in range(9):
                    c0 = j * 512 + (u // 2) * 128
                    last = mm(bank(ring[u % 4]).rearrange("p (b t) -> p b t", t=T), W("f2_sh1", c0, c0 + 128),
                              xpad[:, 32 * (u % 2):32 * (u % 2) + 32, j:j + T], j == 0, j == 8)
                last.then_inc(S["f2_shup"], 1)
                if u >= 1:
                    sh_down(u - 1)
            sh_down(7)
            gates_pe(pe, 2)

        def f2_loop_pe(pe):
            pe.sem_inc(S["f2_down"], RH)
            pe.wait_ge(*done("gatesT", 3))
            for c in range(2):
                mm(bank(4 + c), W("f2_eb2"), gT[0:10, c * HALF:(c + 1) * HALF], False, False)
            with pe.Fori(0, 5) as i:
                ffn_units_pe(pe, 2, i, 2)

        def f2_act(act, o):
            A = nc.scalar
            act.wait_ge(*done("f2_pad0", 2))
            act.wait_ge(*done("ln_out", 14))
            A.activation(xpad[:, :, 4:20], bt(xT[:, :]), ACT.Copy).then_inc(S["f2_xpad"], 1)
            act.wait_ge(*done("f2_rc", 1))
            A.activation(rpad[:, :, 4:20], bt(PS[:, 0:1024]), ACT.Gelu, bias=W("f2_rcb1")).then_inc(S["f2_rpad"], 1)
            act.wait_ge(*done("f2_lt", 1))
            A.activation(gT[0:10, :], PS[0:10, 1024:2048], ACT.Copy).then_inc(S["f2_ltcopy"], 1)
            for u in range(8):
                act.wait_ge(*done("f2_shup", u + 1))
                if u >= RH:
                    act.wait_ge(*done("f2_shdown", u - RH + 1))
                A.activation(hid[:, u % RH, :], bank([0, 1, 6, 7][u % 4]), ACT.Silu,
                             bias=W("f2_shb1", u // 2, u // 2 + 1)).then_inc(S["f2_shact"], 1)
            g_exp_act(act, 2)
            gates_act(act, 2)
            ffn_act(act, 2)

        def f2_dve(dve, o):
            V = nc.vector
            dve.wait_ge(*done("logits", 3))
            lg, m1, m2, dst = gview(1, 10), gview(2, 10), gview(3, 10), gview(0, 10)
            o.step(V.tensor_tensor(lg, PS[:, 1024:1024 + 80].rearrange("p (t e) -> p t e", e=10),
                                   W("f2_rcb2").unsqueeze(1).to_broadcast([128, 8, 10]), ALU.add))
            top(o, lg, gcol(4), m1, gcol(5), 10, True)
            top(o, lg, gcol(6), m2, gcol(5), 10, False)
            softmax2(o, None, 2, gcol(4), gcol(6), gcol(7), gcol(8), gcol(9))
            mix2(o, 10, m1, m2, gcol(7), gcol(8), dst, 2)
            ffn_dve(dve, o, 2)
            for k in range(2):
                o.tell_step(V.scalar_tensor_tensor(out=h(lnz, k), in0=bank(4 + k), scalar=W("f2_shb2"), in1=h(xT, k),
                                                   op0=ALU.add, op1=ALU.add), "f2_z")
            ln_dve(dve, o, 7, lnz, lno, W("f2_g"), W("f2_b"))
            for k in range(2):
                o.tell_step(V.tensor_tensor(h(hT, k), h(hT, k), h(lno, k), ALU.add), "h_ready")

        x3 = big(0)
        sk3, sv3, se3, sa3 = (big(1 + j, rows=64) for j in range(4))
        vT3 = [big(5 + j) for j in range(4)]
        sh3 = big(9, rows=64)
        vh3 = big(5, 4).rearrange("p (t c) -> p t c", c=512)
        kT3 = big(10, 4).rearrange("p (g n) -> p g n", n=N)
        qT3 = bigb(0, 4).rearrange("p (g n) -> p g n", n=N)
        kw = big(14).rearrange("p (r c) -> p r c", r=2)
        qw = big(15).rearrange("p (r c) -> p r c", r=2)
        sqk = bigb(4).rearrange("p (r c) -> p r c", r=2)
        st3 = sb("st3", [128, 2, 32])
        la3 = sb("la3", [128, 5, 64])
        yT3 = big(0, 4).rearrange("p (g n) -> p g n", n=N)
        dec = big(4).rearrange("p (x c) -> p x c", x=2)
        kz3 = xT[:, :].rearrange("p (x c) -> p x c", x=2)
        mt3 = [big(14).rearrange("p (x c) -> p x c", x=2), big(15).rearrange("p (x c) -> p x c", x=2)]
        pt3 = [bigb(4).rearrange("p (x c) -> p x c", x=2), bigb(5).rearrange("p (x c) -> p x c", x=2)]
        nu3 = [xc[:, 0:768].rearrange("p (b c) -> p b c", b=4), big(9)[:, 0:768].rearrange("p (b c) -> p b c", b=4)]
        mw3 = sq[:, :].rearrange("p (x c) -> p x c", x=2)
        LEVELS = 4
        NREADY = [1, 3, 5, 6]

        def nu_ps(x):
            return PS[:, 3 * x * 512:(3 * x + 2) * 512].rearrange("p (b c) -> p b c", b=4)

        def h4(x):
            return x.rearrange("p (b d) -> p b d", b=4)

        def h8(x):
            return x.rearrange("p (h d) -> p h d", h=8)

        def a3_pe(pe):
            pe.wait_ge(*done("pack4", 16))
            pe.wait_ge(*done("a3_x", 1))
            for j, name in enumerate(("a3_k2", "a3_v2", "a3_e2", "a3_a2")):
                for k in range(2):
                    last = mm(bank(2 * j + k, rows=64), W(name), h(x3, k))
                last.then_inc(S["a3_s"], 1)
            pe.wait_ge(*done("a3_silu", 4))
            for f in range(4):
                if f >= 2:
                    pe.wait_ge(*done("a3_vT", f - 1))
                for k in range(2):
                    last = mm(bank(2 * (f % 2) + k), W("a3_v1", f * 128, (f + 1) * 128), h(sv3, k))
                last.then_inc(S["a3_vps"], 1)
            pe.wait_ge(*done("a3_vT", 4))
            for k in range(2):
                for f in range(4):
                    last = mm(bank(4 + k, rows=64), W("a3_h2", f * 64, (f + 1) * 64), h(vT3[f], k), f == 0, f == 3)
            last.then_inc(S["a3_h"], 1)
            for t in range(NT):
                mm(PS[:, 3072 + t * 8:3072 + (t + 1) * 8], tile(se3, t), W("a3_e1"))
                last = mm(PS[:, 3136 + t * 8:3136 + (t + 1) * 8], tile(sa3, t), W("a3_a1"))
            last.then_inc(S["a3_ea"], 1)
            pe.wait_ge(*done("a3_hsilu", 1))
            pe.wait_ge(*done("a3_la", 1))
            mm(PS[:, 3584:3648], W("incl01"), la3[:, 0, :]).then_inc(S["a3_cum"], 1)
            pe.wait_ge(*done("a3_negc", 1))

            def turn(t):
                j = t % 2
                pe.wait_ge(*done("a3_kn", t + 1))
                if t:
                    pe.wait_ge(*done("a3_kqT", 2 * t))
                for g in range(4):
                    last = nc.tensor.transpose(PS[:, 3072 + g * 128:3072 + (g + 1) * 128], kw[:, j, g * 128:(g + 1) * 128],
                                               W("ident"))
                last.then_inc(S["a3_turn"], 1)
                pe.wait_ge(*done("a3_qn", t + 1))
                for g in range(4):
                    last = nc.tensor.transpose(PS[:, 3584 + g * 128:3584 + (g + 1) * 128], qw[:, j, g * 128:(g + 1) * 128],
                                               W("ident"))
                last.then_inc(S["a3_turn"], 1)

            for t in range(NT):
                j = t % 2
                if t >= 2:
                    pe.wait_ge(*done("a3_kraw", t - 1))
                    pe.wait_ge(*done("a3_qraw", t - 1))
                    pe.wait_ge(*done("a3_vh", t - 1))
                mm(bank(j), tile(sk3, t), W("a3_k1")).then_inc(S["a3_kqv"], 1)
                mm(bank(2 + j), tile(x3, t), W("a3_wq")).then_inc(S["a3_kqv"], 1)
                mm(bank(4 + j), tile(sv3, t), W("a3_v1"), True, False)
                mm(bank(4 + j), tile(sh3, t), W("a3_h1"), False, True).then_inc(S["a3_kqv"], 1)
                if t >= 1:
                    turn(t - 1)
            turn(NT - 1)
            pe.wait_ge(*done("a3_kqT", 2 * NT))
            pe.wait_ge(*done("a3_vh", NT))

            def decay_sums(t, x):
                c = 2 * t + x
                if c:
                    pe.wait_ge(*done("a3_m", c))
                    pe.wait_ge(*done("a3_p", c))
                for k, (src, right, sem) in enumerate(((0, "strict01", "a3_cex"), (1, "ident", "a3_eb"))):
                    for b in range(4):
                        col = t * 8 + 2 * b + x
                        last = mm(tile(bank(6 + k), b), la3[:, src, col:col + 1].to_broadcast([128, 128]), W(right))
                    last.then_inc(S[sem], 1)

            def key_products(t, x):
                pe.wait_ge(*done("a3_me", 2 * t + x + 1))
                pe.wait_ge(*done("a3_kz", 2 * t + x + 1))
                for k, src in enumerate((kT3, qT3)):
                    for b in range(4):
                        last = mm(tile(bank(6 + k), b), kz3[:, x, b * 128:(b + 1) * 128], src[:, b, t * 128:(t + 1) * 128])
                last.then_inc(S["a3_gqps"], 1)

            def system_turn(t, x):
                pe.wait_ge(*done("a3_m", 2 * t + x + 1))
                for b in range(4):
                    last = nc.tensor.transpose(tile(bank(3 * x + 2), b), tile(mt3[t % 2][:, x], b), W("ident"))
                last.then_inc(S[f"a3_tr{x}"], 1)

            def level(t, x, lv):
                pe.wait_ge(*done(f"a3_n{x}", 6 * t + NREADY[lv]))
                pe.wait_ge(*done(f"a3_u{x}", 5 * t + lv + 1))
                if t and x and lv == 0:
                    pe.wait_ge(*done("a3_yT", t))
                m = (mt3[t % 2] if lv == 0 else mw3)[:, x]
                c0 = 0 if lv < 2 else 64
                for b in range(4):
                    last = mm(nu_ps(x)[:, b, c0:192], tile(m, b), nu3[x][:, b, c0:192])
                if lv < LEVELS - 1:
                    for b in range(4):
                        last = mm(tile(bank(3 * x + 2), b), nu3[x][:, b, 0:128], tile(m, b))
                last.then_inc(S[f"a3_lv{x}"], 1)

            def outputs(t, x):
                pe.wait_ge(*done(f"a3_u{x}", 5 * t + 5))
                if x == 0:
                    pe.wait_ge(*done("a3_u1", 5 * t + 5))
                for b in range(4):
                    last = mm(PS[x * 64:x * 64 + 64, 3 * 512 + b * 128:3 * 512 + (b + 1) * 128], nu3[x][:, b, 128:192],
                              tile(pt3[t % 2][:, x], b))
                last.then_inc(S["a3_y"], 1)

            for x in range(2):
                decay_sums(0, x)
                key_products(0, x)
            for x in range(2):
                system_turn(0, x)
            for t in range(NT):
                more = t < NT - 1
                level(t, 0, 0)
                level(t, 1, 0)
                if more:
                    decay_sums(t + 1, 0)
                level(t, 0, 1)
                if more:
                    key_products(t + 1, 0)
                level(t, 1, 1)
                if more:
                    decay_sums(t + 1, 1)
                level(t, 0, 2)
                level(t, 1, 2)
                if more:
                    key_products(t + 1, 1)
                level(t, 0, 3)
                level(t, 1, 3)
                for x in range(2):
                    if more:
                        system_turn(t + 1, x)
                    outputs(t, x)
            pe.wait_ge(*done("a3_yT", NT))
            for k in range(2):
                for g in range(4):
                    last = mm(bank(4 + k), W("a3_ow", g * 128, (g + 1) * 128), yT3[:, g, k * HALF:(k + 1) * HALF], g == 0, g == 3)
                last.then_inc(S["a3_o"], 1)

        def a3_act(act, o):
            A = nc.scalar
            act.wait_ge(*done("pack4", 16))
            for j, dst in enumerate((sk3, sv3, se3, sa3)):
                act.wait_ge(*done("a3_s", j + 1))
                A.activation(dst, PS[0:64, 2 * j * 512:(2 * j + 2) * 512], ACT.Silu).then_inc(S["a3_silu"], 1)
            for f in range(4):
                act.wait_ge(*done("a3_vps", f + 1))
                A.activation(vT3[f], PS[:, (f % 2) * 1024:(f % 2 + 1) * 1024], ACT.Copy).then_inc(S["a3_vT"], 1)
            act.wait_ge(*done("a3_h", 1))
            A.activation(sh3, PS[0:64, 2048:3072], ACT.Silu).then_inc(S["a3_hsilu"], 1)
            act.wait_ge(*done("a3_nabs", 1))
            A.activation(la3[:, 2:4, :], la3[:, 2:4, :], ACT.Exp).then_inc(S["a3_e"], 1)
            act.wait_ge(*done("a3_e", 1))
            A.activation(la3[:, 2:4, :], la3[:, 2:4, :], ACT.Ln, bias=W("a3_one")).then_inc(S["a3_l"], 1)
            for t in range(NT):
                j = t % 2
                act.wait_ge(*done("a3_kqv", 3 * t + 3))
                A.activation(vh3[:, t, :], bank(4 + j), ACT.Copy).then_inc(S["a3_vh"], 1)
                act.wait_ge(*done("a3_mv", t + 1))
                A.activation(st3[:, j, 16:18], st3[:, j, 12:16].rearrange("p (x y) -> p x y", y=2)[:, :, 1], ACT.Sqrt,
                             bias=eps5[:, 0:1]).then_inc(S["a3_sd"], 1)
                act.wait_ge(*done("a3_kk", t + 1))
                A.activation(sqk[:, j, :], kw[:, j, :], ACT.Square).then_inc(S["a3_sq"], 1)
                act.wait_ge(*done("a3_n2", t + 1))
                A.activation(st3[:, j, 18:26], st3[:, j, 18:26], ACT.Sqrt).then_inc(S["a3_nrm"], 1)
                for x, dst in enumerate((kT3, qT3)):
                    act.wait_ge(*done("a3_turn", 2 * t + x + 1))
                    A.activation(dst[:, :, t * 128:(t + 1) * 128], bank(6 + x).rearrange("p (g c) -> p g c", g=4),
                                 ACT.Copy).then_inc(S["a3_kqT"], 1)

            def decays(t, x):
                act.wait_ge(*done("a3_dm", 2 * t + x + 1))
                for b in range(4):
                    hd = 2 * b + x
                    c = tile(dec[:, x], b)
                    last = A.activation(c, c, ACT.Exp, bias=la3[:, 4, t * 8 + hd:t * 8 + hd + 1])
                last.then_inc(S["a3_dec"], 1)

            def powers(t, x, lv):
                act.wait_ge(*done(f"a3_lv{x}", 4 * t + lv + 1))
                A.activation(mw3[:, x], bank(3 * x + 2), ACT.Copy).then_inc(S[f"a3_n{x}"], 1)
                if lv < 2:
                    act.wait_ge(*done(f"a3_u{x}", 5 * t + lv + 2))
                    A.activation(nu3[x][:, :, 0:128], nu_ps(x)[:, :, 0:128], ACT.Copy).then_inc(S[f"a3_n{x}"], 1)

            def system(t, x):
                act.wait_ge(*done(f"a3_tr{x}", t + 1))
                A.activation(nu3[x][:, :, 0:128], h4(bank(3 * x + 2)), ACT.Copy).then_inc(S[f"a3_n{x}"], 1)

            decays(0, 0)
            decays(0, 1)
            system(0, 0)
            system(0, 1)
            for t in range(NT):
                more = t < NT - 1
                powers(t, 0, 0)
                powers(t, 1, 0)
                if more:
                    decays(t + 1, 0)
                powers(t, 0, 1)
                powers(t, 1, 1)
                if more:
                    decays(t + 1, 1)
                powers(t, 0, 2)
                powers(t, 1, 2)
                if more:
                    system(t + 1, 0)
                    system(t + 1, 1)
                act.wait_ge(*done("a3_y", 2 * t + 2))
                A.activation(yT3[:, :, t * 128:(t + 1) * 128], bank(3).rearrange("p (g c) -> p g c", g=4),
                             ACT.Copy).then_inc(S["a3_yT"], 1)

        def a3_pool(pool):
            pool.wait_ge(*done("a3_kqv", 3 * NT))
            nc.gpsimd.memset(xT[:, :], 0.0).then_inc(S["a3_kzero"], 1)
            pool.wait_ge(*done("a3_kzero", 1))
            pool.wait_ge(*done("a3_kqT", 2 * NT))
            for t in range(NT):
                for x in range(2):
                    if t:
                        pool.wait_ge(*done("a3_gqps", 2 * t + x - 1))
                    r = slice(64 * x, 64 * x + 64)
                    nc.gpsimd.tensor_copy(h4(kz3[r, x]), kT3[r, :, t * 128:(t + 1) * 128]).then_inc(S["a3_kz"], 1)

        def a3_dve(dve, o):
            V = nc.vector
            dve.wait_ge(*done("pack4", 16))
            x, y = bt(xT[:, :]), bt(x3)
            o.step(V.tensor_scalar(y, x, W("a3_cw", 3, 4), W("a3_cb"), ALU.mult, ALU.add))
            for d in (1, 2, 3):
                o.step(V.scalar_tensor_tensor(out=y[:, :, d:], in0=x[:, :, 0:T - d], scalar=W("a3_cw", 3 - d, 4 - d),
                                              in1=y[:, :, d:], op0=ALU.mult, op1=ALU.add))
            o.tell_step(V.tensor_tensor(x3, x3, xT[:, :], ALU.add), "a3_x")
            dve.wait_ge(*done("a3_ea", 1))
            o.step(V.tensor_copy(la3[:, 1, :], PS[:, 3072:3136]))
            o.step(V.tensor_scalar(la3[:, 0, :], PS[:, 3136:3200], -1.0, None, ALU.mult))
            o.tell_step(V.scalar_tensor_tensor(out=la3[:, 2:4, :], in0=la3[:, 0:2, :], scalar=-1.0, in1=la3[:, 0:2, :],
                                               op0=ALU.mult, op1=ALU.min), "a3_nabs")
            dve.wait_ge(*done("a3_l", 1))
            o.step(V.scalar_tensor_tensor(out=la3[:, 0:2, :], in0=la3[:, 0:2, :], scalar=0.0, in1=la3[:, 2:4, :],
                                          op0=ALU.max, op1=ALU.add))
            o.step(V.tensor_scalar(la3[:, 1, :], la3[:, 1, :], 0.1, None, ALU.mult))
            o.tell_step(V.tensor_scalar(la3[:, 0, :], la3[:, 0, :], -1.0, None, ALU.mult), "a3_la")
            dve.wait_ge(*done("a3_cum", 1))
            o.tell_step(V.tensor_scalar(la3[:, 4, :], PS[:, 3584:3648], -1.0, None, ALU.mult), "a3_negc")
            for t in range(NT):
                j = t % 2
                for x_, b in ((0, j), (1, 2 + j)):
                    dve.wait_ge(*done("a3_kqv", 3 * t + 1 + x_))
                    if t >= 2 and x_ == 0:
                        dve.wait_ge(*done("a3_turn", 2 * t - 2))
                    o.step(V.bn_stats(st3[:, j, 6 * x_:6 * x_ + 6], bank(b)))
                    ins = V.bn_aggr(st3[:, j, 12 + 2 * x_:14 + 2 * x_], st3[:, j, 6 * x_:6 * x_ + 6])
                    if x_:
                        o.tell_step(ins, "a3_mv")
                    else:
                        o.step(ins)
                dve.wait_ge(*done("a3_sd", t + 1))
                o.step(V.reciprocal(st3[:, j, 16:18], st3[:, j, 16:18]))
                for x_, (w_, g_, b_, raw, fin) in enumerate(((kw, "a3_kg", "a3_kb", "a3_kraw", "a3_kk"),
                                                             (qw, "a3_qg", "a3_qb", "a3_qraw", "a3_qn"))):
                    if x_ and t >= 2:
                        dve.wait_ge(*done("a3_turn", 2 * t - 2))
                    o.tell_step(V.tensor_scalar(w_[:, j, :], bank(2 * x_ + j), st3[:, j, 12 + 2 * x_:13 + 2 * x_],
                                                st3[:, j, 16 + x_:17 + x_], ALU.subtract, ALU.mult), raw)
                    o.step(V.tensor_tensor(w_[:, j, :], w_[:, j, :], W(g_), ALU.mult))
                    o.tell_step(V.tensor_tensor(w_[:, j, :], w_[:, j, :], W(b_), ALU.add), fin)
                dve.wait_ge(*done("a3_sq", t + 1))
                o.tell_step(V.tensor_reduce(st3[:, j, 18:26], h8(sqk[:, j, :]), AX_X, ALU.add), "a3_n2")
                dve.wait_ge(*done("a3_nrm", t + 1))
                o.step(V.tensor_scalar(st3[:, j, 18:26], st3[:, j, 18:26], 1e-12, None, ALU.max))
                o.step(V.reciprocal(st3[:, j, 18:26], st3[:, j, 18:26]))
                o.tell_step(V.tensor_tensor(h8(kw[:, j, :]), h8(kw[:, j, :]),
                                            st3[:, j, 18:26].unsqueeze(2).to_broadcast([128, 8, 64]), ALU.mult), "a3_kn")
            dve.wait_ge(*done("a3_turn", 2 * NT))
            mask = W("strict_add").unsqueeze(1).to_broadcast([128, 4, 128])

            def scaled_decays(t, x):
                c = 2 * t + x
                dve.wait_ge(*done("a3_cex", c + 1))
                o.tell(V.tensor_tensor(h4(dec[:, x]), h4(bank(6)), mask, ALU.add), "a3_dm")
                dve.wait_ge(*done("a3_dec", c + 1))
                dve.wait_ge(*done("a3_eb", c + 1))
                o.tell_step(V.tensor_tensor(mt3[t % 2][:, x], dec[:, x], bank(7), ALU.mult), "a3_me")

            def systems(t, x):
                m = mt3[t % 2][:, x]
                dve.wait_ge(*done("a3_gqps", 2 * t + x + 1))
                o.tell(V.scalar_tensor_tensor(out=m, in0=m, scalar=2.0, in1=bank(6), op0=ALU.mult, op1=ALU.mult), "a3_m")
                o.tell(V.tensor_tensor(pt3[t % 2][:, x], dec[:, x], bank(7), ALU.mult), "a3_p")

            def values(t, x):
                if t:
                    dve.wait_ge(*done("a3_y", 2 * t - 1 + x))
                e = la3[:, 1, t * 8:(t + 1) * 8].rearrange("p (b x) -> p x b", x=2)[:, x]
                v = vh3[:, t, :].rearrange("p (b x d) -> p x b d", x=2, d=64)[:, x]
                o.tell_step(V.tensor_tensor(nu3[x][:, :, 128:192], v, e.unsqueeze(2).to_broadcast([128, 4, 64]),
                                            ALU.mult), f"a3_u{x}")

            def update(t, x, lv):
                dve.wait_ge(*done(f"a3_lv{x}", 4 * t + lv + 1))
                u = nu3[x][:, :, 128:192]
                o.tell_step(V.tensor_tensor(u, u, nu_ps(x)[:, :, 128:192], ALU.subtract if lv == 0 else ALU.add), f"a3_u{x}")

            for x in range(2):
                values(0, x)
                scaled_decays(0, x)
                systems(0, x)
            for t in range(NT):
                more = t < NT - 1
                update(t, 0, 0)
                update(t, 1, 0)
                if more:
                    scaled_decays(t + 1, 0)
                update(t, 0, 1)
                if more:
                    systems(t + 1, 0)
                update(t, 1, 1)
                if more:
                    scaled_decays(t + 1, 1)
                update(t, 0, 2)
                update(t, 1, 2)
                if more:
                    systems(t + 1, 1)
                update(t, 0, 3)
                update(t, 1, 3)
                if more:
                    values(t + 1, 0)
                    values(t + 1, 1)
            for k in range(2):
                dve.wait_ge(*done("a3_o", k + 1))
                o.tell_step(V.scalar_tensor_tensor(out=h(hT, k), in0=bank(4 + k), scalar=W("a3_ob"), in1=h(hT, k),
                                                   op0=ALU.add, op1=ALU.add), "h_ready")

        def g3_act(act):
            act.wait_ge(*done("g3_shift", 1))
            nc.scalar.activation(gview(1, 16), gview(1, 16), ACT.Exp).then_inc(S["g3_exp"], 1)
            act.wait_ge(*done("g3_shift", 2))
            nc.scalar.activation(gtmp[:, 8, 0:32], gtmp[:, 8, 0:32], ACT.Exp).then_inc(S["g3_exp"], 1)

        def g3_dve(dve, o):
            V = nc.vector
            dve.wait_ge(*done("logits", 4))
            sc = gview(1, 16)
            lg = PS[:, 1024:1152].rearrange("p (t e) -> p t e", e=16)
            o.step(V.tensor_reduce(gcol(6), lg, AX_X, ALU.max))
            o.tell_step(V.tensor_tensor(sc, lg, gbc(gcol(6), 16), ALU.subtract), "g3_shift")
            dve.wait_ge(*done("g3_exp", 1))
            o.step(V.tensor_reduce(gcol(6), sc, AX_X, ALU.add))
            o.step(V.reciprocal(gcol(6), gcol(6)))
            o.step(V.tensor_tensor(sc, sc, gbc(gcol(6), 16), ALU.mult))
            vals = gtmp[:, 8, 0:32]
            for r in range(4):
                top(o, sc, gtmp[:, 8, 8 * r:8 * r + 8], gview(2 + r, 16), gcol(7), 16, r < 3)
            v3_ = vals.rearrange("p (r t) -> p r t", r=4)
            o.step(V.tensor_copy(gcol(6), gtmp[:, 8, 0:8]))
            o.tell_step(V.tensor_tensor(v3_, v3_, gcol(6).unsqueeze(1).to_broadcast([128, 4, 8]), ALU.subtract), "g3_shift")
            dve.wait_ge(*done("g3_exp", 2))
            o.step(V.tensor_reduce(gcol(6), vals.rearrange("p (r t) -> p t r", r=4), AX_X, ALU.add))
            o.step(V.reciprocal(gcol(6), gcol(6)))
            o.step(V.tensor_tensor(v3_, v3_, gcol(6).unsqueeze(1).to_broadcast([128, 4, 8]), ALU.mult))
            dst = gview(0, 18)
            o.step(V.memset(dst, 0.5))
            for r in range(4):
                m = gview(2 + r, 16)
                o.step(V.tensor_tensor(m, m, gbc(gtmp[:, 8, 8 * r:8 * r + 8], 16), ALU.mult))
            o.step(V.tensor_tensor(gview(2, 16), gview(2, 16), gview(3, 16), ALU.add))
            o.step(V.tensor_tensor(gview(4, 16), gview(4, 16), gview(5, 16), ALU.add))
            o.tell_step(V.tensor_tensor(dst[:, :, 0:16], gview(2, 16), gview(4, 16), ALU.add), "gates")

        block = ctx.enter_context(nc.Block())

        @block.sync
        def _(sp):
            tok_sp(sp)
            if STAGES >= 2:
                a0_sp(sp)
                for k in range(2, 5):
                    sp.dma_start(WP[k][:, :], a[f"pack{k}"]).then_inc(S[f"pack{k}"], 16)
            if STAGES >= 3:
                ffn_sp(sp, 0)
            if STAGES >= 5:
                ffn_sp(sp, 1)
            if STAGES >= 6:
                a2_sp(sp)
            if STAGES >= 7:
                ffn_sp(sp, 2)
            if STAGES >= 9:
                ffn_sp(sp, 3)
            for k in range(2):
                sp.wait_ge(*done("h_ready", 2 * STAGES))
                sp.dma_start(out[:, k * HALF:(k + 1) * HALF], h(hT, k)).then_inc(S["stored"], 16)
            sp.wait_ge(*done("stored", 32))

        @block.gpsimd
        def _(pool):
            a0_pool(pool)
            if STAGES >= 2:
                a0_pool2(pool)
            if STAGES >= 4:
                a1_pool(pool)
            if STAGES >= 6:
                a2_pool(pool)
            if STAGES >= 7:
                f2_pool(pool)
            if STAGES >= 8:
                a3_pool(pool)

        @block.tensor
        def _(pe):
            tok_pe(pe)
            if STAGES >= 2:
                ln_pe(pe, 0, hT, ("h_ready", 2, 2))
                pe.sem_inc(S["a0_pv"], 2)
                a0_pe(pe)
            if STAGES >= 3:
                ln_pe(pe, 1, hT, ("h_ready", 3, 4))
                router_pe(pe, 0, xT, "f0_router", ("ln_out", 4))
                gates_pe(pe, 0)
                f0_pe(pe)
            if STAGES >= 4:
                ln_pe(pe, 2, hT, ("h_ready", 5, 6))
                a1_pe(pe)
            if STAGES >= 5:
                ln_pe(pe, 4, hT, ("h_ready", 7, 8))
                router_pe(pe, 1, xT, "f1_gate", ("ln_out", 10))
                gates_pe(pe, 1)
                ffn_pe(pe, 1, W("f1_zero"))
            if STAGES >= 6:
                ln_pe(pe, 5, hT, ("h_ready", 9, 10))
                pe.sem_inc(S["a2_ysum"], 2)
                a2_pe(pe)
            if STAGES >= 7:
                ln_pe(pe, 6, hT, ("h_ready", 11, 12))
                f2_pe(pe)
                f2_loop_pe(pe)
                ln_pe(pe, 7, lnz, ("f2_z", 1, 2))
            if STAGES >= 8:
                ln_pe(pe, 8, hT, ("h_ready", 13, 14))
                a3_pe(pe)
            if STAGES >= 9:
                ln_pe(pe, 9, hT, ("h_ready", 15, 16))
                router_pe(pe, 3, xT, "f3_gate", ("ln_out", 20))
                gates_pe(pe, 3)
                ffn_pe(pe, 3, W("f3_b2"))

        @block.scalar
        def _(act):
            o = Order(act, S["act_step"], S)
            act.wait_ge(*done("eps", 3))
            if STAGES >= 2:
                ln_act(act, 0, eps5)
                a0_act(act, o)
            if STAGES >= 3:
                ln_act(act, 1, eps5)
                g_exp_act(act, 0)
                gates_act(act, 0)
                f0_act(act)
            if STAGES >= 4:
                ln_act(act, 2, eps5)
                a1_act(act, o)
            if STAGES >= 5:
                ln_act(act, 4, eps5)
                g1_act(act)
                gates_act(act, 1)
                ffn_act(act, 1)
            if STAGES >= 6:
                ln_act(act, 5, eps5)
                a2_act(act, o)
            if STAGES >= 7:
                ln_act(act, 6, eps5)
                f2_act(act, o)
                ln_act(act, 7, eps5)
            if STAGES >= 8:
                ln_act(act, 8, eps5)
                a3_act(act, o)
            if STAGES >= 9:
                ln_act(act, 9, eps5)
                g3_act(act)
                gates_act(act, 3)
                ffn_act(act, 3)

        @block.vector
        def _(dve):
            o = Order(dve, S["dve_step"], S)
            tok_dve(dve, o)
            if STAGES >= 2:
                ln_dve(dve, o, 0, hT, xT)
                dve.sem_inc(S["a0_ctx"], 2)
                dve.sem_inc(S["a0_raw0"], 64)
                dve.sem_inc(S["a0_raw1"], 64)
                a0_dve(dve, o)
            if STAGES >= 3:
                ln_dve(dve, o, 1, hT, xT)
                g0_dve(dve, o)
                f0_dve(dve, o)
            if STAGES >= 4:
                ln_dve(dve, o, 2, hT, xT)
                a1_dve(dve, o)
            if STAGES >= 5:
                ln_dve(dve, o, 4, hT, xT)
                g1_dve(dve, o)
                ffn_dve(dve, o, 1)
                ffn_add_dve(dve, o, 1)
            if STAGES >= 6:
                ln_dve(dve, o, 5, hT, xT)
                a2_dve(dve, o)
            if STAGES >= 7:
                ln_dve(dve, o, 6, hT, xT)
                f2_dve(dve, o)
            if STAGES >= 8:
                ln_dve(dve, o, 8, hT, xT)
                a3_dve(dve, o)
            if STAGES >= 9:
                ln_dve(dve, o, 9, hT, xT)
                g3_dve(dve, o)
                ffn_dve(dve, o, 3)
                ffn_add_dve(dve, o, 3)


def kernel(**inputs):
    import concourse.bacc as bacc
    from concourse.bass_utils import run_bass_kernel_spmd

    w = {k: np.asarray(v) for k, v in inputs.items()}
    f = np.float32

    def rows(x, cols=None):
        x = np.asarray(x).reshape(1, -1)
        return np.broadcast_to(x, (128, x.shape[1]))

    def col(x):
        return np.asarray(x).reshape(-1, 128).T

    i = np.arange(128)
    same = (i[:, None] // T) == (i[None, :] // T)
    parts = {
        "ident": np.eye(128, dtype=f), "mean": np.full((128, 128), 1.0 / 128, f), "tok_bias": w["L0_tok_bias"].T,
        "a0_nat": np.concatenate([w[f"L0_attn_W_{n}"].T for n in ("qf", "kf", "vf", "qt", "kt", "vt")], axis=1),
        "a0_natb": rows(np.concatenate([w[f"L0_attn_b_{n}"] for n in ("qf", "kf", "vf", "qt", "kt", "vt")])),
        "a0_vt": w["L0_attn_W_vt"].T, "a0_vtb": col(w["L0_attn_b_vt"]),
        "f0_router": w["L0_ffn_router_w"], "f0_beta": w["L0_ffn_beta"],
        "rank": rows(np.arange(16, 0, -1).astype(f)),
        "causal_sl": (same & (i[:, None] <= i[None, :])).astype(f), "ones": np.ones((128, 128), f),
        "a1_wq": w["L1_attn_Wq"], "a1_wk": w["L1_attn_Wk"], "a1_wf": w["L1_attn_Wf"],
        "a1_bf": w["L1_attn_bf"].reshape(64, 1), "a1_wv": w["L1_attn_Wv"], "a1_wo": w["L1_attn_Wo"],
        "a1_g": col(w["L1_attn_ln_g"]), "a1_b": col(w["L1_attn_ln_b"]),
        "a1_slots": w["L1_attn_eslots"][0].T, "a1_slots4": np.tile(w["L1_attn_eslots"][0].T, (1, 4)),
        "a1_eq": w["L1_attn_Eq"], "a1_ek": w["L1_attn_Ek"], "a1_ev": w["L1_attn_Ev"], "a1_eo": w["L1_attn_Eo"],
        "heads4": ((i[:, None] // 32) == (i[None, :] // 32)).astype(f),
        "a1_sin": w["L1_attn_Sin"], "a1_knowT": w["L1_attn_know"][0].T, "a1_know": w["L1_attn_know"][0],
        "a1_sgw": w["L1_attn_Sg_w"], "a1_sgb": col(w["L1_attn_Sg_b"]), "a1_so": w["L1_attn_So"],
        "a1_c1w": w["L1_attn_C1w"], "a1_c1b": w["L1_attn_C1b"].reshape(32, 1), "a1_c2w": w["L1_attn_C2w"],
        "a1_c2b": rows(w["L1_attn_C2b"]), "sel3": np.repeat(np.eye(3, dtype=f), 128, axis=1),
        "f1_gate": w["L1_ffn_gate_w"].T, "f1_bias": rows(w["L1_ffn_biases"]),
        "f1_zero": np.zeros((9, 128), f),
        "a2_in": w["L2_attn_in_proj_w"].T, "a2_cw": w["L2_attn_conv_w"].reshape(2, 128, 4).transpose(1, 0, 2).reshape(128, 8),
        "a2_cb": col(w["L2_attn_conv_b"]),
        "a2_xp": w["L2_attn_x_proj_w"].T.reshape(2, 128, 40).transpose(1, 0, 2).reshape(128, 80),
        "a2_dtw": w["L2_attn_dt_proj_w"].T, "a2_dtb": col(w["L2_attn_dt_proj_b"]),
        "a2_alog": w["L2_attn_A_log"].reshape(2, 128, 16).transpose(1, 0, 2).reshape(128, 32),
        "a2_d": col(w["L2_attn_D_param"]),
        "a2_out": w["L2_attn_out_proj_w"].T.reshape(2, 128, 128).transpose(1, 0, 2).reshape(128, 256),
        "a2_wq": w["L2_attn_wq"].T, "a2_wk": w["L2_attn_wk"].T, "a2_wv": w["L2_attn_wv"].T,
        "a2_fc": w["L2_attn_fc_w"].T, "a2_fcb": col(w["L2_attn_fc_b"]),
        "causal_add": np.where(same & (i[None, :] <= i[:, None]), 0, NEG).astype(f),
        "f2_rc1": w["L2_ffn_rc_w1"].transpose(1, 2, 0).reshape(128, 384), "f2_rcb1": col(w["L2_ffn_rc_b1"]),
        "f2_rc2": w["L2_ffn_rc_w2"].transpose(1, 2, 0).reshape(128, 30), "f2_rcb2": rows(w["L2_ffn_rc_b2"]),
        "f2_sh1": w["L2_ffn_sh_w1"].transpose(1, 2, 0).reshape(128, 9 * 512), "f2_shb1": col(w["L2_ffn_sh_b1"]),
        "f2_sh2": w["L2_ffn_sh_w2"][:, :, 0].T.reshape(4, 128, 128).transpose(1, 0, 2).reshape(128, 512),
        "f2_shb2": col(w["L2_ffn_sh_b2"]), "f2_eb2": w["L2_ffn_e_b2"], "f2_g": col(w["L2_ffn_ln_g"]),
        "f2_b": col(w["L2_ffn_ln_b"]),
        "a3_cw": w["L3_attn_conv_w"][:, 0, :], "a3_cb": col(w["L3_attn_conv_b"]), "a3_wq": w["L3_attn_Wq"].T,
        "a3_k2": w["L3_attn_Mk_W2"].T, "a3_k1": w["L3_attn_Mk_W1"].T, "a3_v2": w["L3_attn_Mv_W2"].T,
        "a3_v1": w["L3_attn_Mv_W1"].T, "a3_e2": w["L3_attn_Meta_W2"].T, "a3_e1": w["L3_attn_Meta_W1"].T,
        "a3_a2": w["L3_attn_Malpha_W2"].T, "a3_a1": w["L3_attn_Malpha_W1"].T,
        "a3_h2": w["L3_attn_Mvh_W2"].T.reshape(4, 128, 64).transpose(1, 0, 2).reshape(128, 256),
        "a3_h1": w["L3_attn_Mvh_W1"].T, "a3_kg": rows(w["L3_attn_normk_g"]), "a3_kb": rows(w["L3_attn_normk_b"]),
        "a3_qg": rows(w["L3_attn_normq_g"]), "a3_qb": rows(w["L3_attn_normq_b"]),
        "a3_ow": w["L3_attn_out_W"].T.reshape(4, 128, 128).transpose(1, 0, 2).reshape(128, 512),
        "a3_ob": col(w["L3_attn_out_b"]),
        "strict_add": np.where(same & (i[:, None] < i[None, :]), 0, NEG).astype(f),
        "strict01": (same & (i[:, None] < i[None, :])).astype(f),
        "incl01": (same & (i[:, None] <= i[None, :])).astype(f),
        "a3_one": np.ones((128, 1), f), "f3_gate": w["L3_ffn_gate_w"].T, "f3_b2": np.concatenate([w["L3_ffn_re_b2"], w["L3_ffn_se_b2"]]),
    }
    arrays = {}
    for k, p in enumerate(pack_columns()):
        pack = np.zeros((128, sum(c for _, _, c in p)), f)
        at = 0
        for name, r, c in p:
            assert parts[name].shape == (r, c), (name, parts[name].shape, r, c)
            pack[:r, at:at + c] = parts[name]
            at += c
        arrays[f"pack{k}"] = pack

    def up(x):
        return x

    def down(x):
        e, ff, d = x.shape
        return x.reshape(e, ff // 128, 128, d).transpose(0, 2, 1, 3).reshape(e, 128, ff)

    def cols(x):
        return x.reshape(x.shape[0], -1, 128).transpose(0, 2, 1)

    arrays["ffn0"] = np.concatenate([w["L0_ffn_w1"], down(w["L0_ffn_w2"]), cols(w["L0_ffn_b1"]), cols(w["L0_ffn_b2"]),
                                     cols(w["L0_ffn_gamma"]), cols(w["L0_ffn_beta"])], axis=2)
    arrays["ffn1"] = np.concatenate([
        np.concatenate([w["L1_ffn_w1"], w["L1_ffn_sw1"][None]]), np.concatenate([w["L1_ffn_w3"], w["L1_ffn_sw3"][None]]),
        down(np.concatenate([w["L1_ffn_w2"], w["L1_ffn_sw2"][None]]))], axis=2)
    arrays["ffn2"] = np.concatenate([w["L2_ffn_e_w1"], down(w["L2_ffn_e_w2"]), cols(w["L2_ffn_e_b1"])], axis=2)
    arrays["ffn3"] = np.concatenate([
        np.concatenate([w["L3_ffn_re_w1"], w["L3_ffn_se_w1"]]), down(np.concatenate([w["L3_ffn_re_w2"], w["L3_ffn_se_w2"]])),
        cols(np.concatenate([w["L3_ffn_re_b1"], w["L3_ffn_se_b1"]]))], axis=2)
    arrays["tok_w"] = w["L0_tok_weight"]
    arrays["tok_m"] = w["L0_tok_mask"]
    arrays["tok_x"] = w["x"].T.reshape(GP, GC * B)

    nc = bacc.Bacc("TRN2", target_bir_lowering=False, num_devices=1)
    arrays = {k: np.ascontiguousarray(v) for k, v in arrays.items()}
    a = {k: nc.dram_tensor(k, v.shape, F32, kind="ExternalInput").ap() for k, v in arrays.items()}
    out = nc.dram_tensor("out_dram", (128, N), F32, kind="ExternalOutput").ap()
    build(nc, a, out)
    r = run_bass_kernel_spmd(nc, [arrays], core_ids=[0])
    return np.ascontiguousarray(r.results[0]["out_dram"].T).reshape(B, T, D)
```

```python
from contextlib import ExitStack

import numpy as np

import concourse.bass as bass
from concourse import mybir

F32 = mybir.dt.float32
BF16 = mybir.dt.bfloat16
F32R = mybir.dt.float32r
ALU = mybir.AluOpType
ACT = mybir.ActivationFunctionType
AX_X = mybir.AxisListType.X

STAGES = 9
D = 128
B, T = 64, 16
N = B * T
HALF = 512
NT = N // 128
G, GP = 5000, 125
GC = G // GP
NEG = -1.0e30
LATE_PIECES = 15
LN_ROOT = (4, 5)


def pack_columns():
    first = [("ident", 128, 128), ("mean", 128, 128), ("tok_bias", 128, 16)]
    l0 = [("a0_nat", 128, 768), ("a0_natb", 128, 768), ("a0_vt", 128, 128), ("a0_vtb", 128, 1),
          ("f0_router", 128, 8), ("f0_beta", 8, 128), ("f0_cols", 128, 56), ("rank", 128, 16)]
    l1 = [("causal_sl", 128, 128), ("ones", 128, 128), ("a1_wq", 128, 64), ("a1_wk", 128, 64), ("a1_wf", 128, 64),
          ("a1_bf", 64, 1), ("a1_wv", 128, 128), ("a1_wo", 128, 128), ("a1_g", 128, 1), ("a1_b", 128, 1),
          ("a1_slots", 128, 32), ("a1_slots4", 128, 128), ("a1_eq", 128, 128), ("a1_ek", 128, 128),
          ("a1_ev", 128, 128), ("a1_eo", 128, 128), ("heads4", 128, 128), ("a1_sin", 128, 128),
          ("a1_knowT", 128, 64), ("a1_know", 64, 128), ("a1_sgw", 128, 128), ("a1_sgb", 128, 1),
          ("a1_so", 128, 128), ("a1_c1w", 128, 32), ("a1_c1b", 32, 1), ("a1_c2w", 32, 3), ("a1_c2b", 128, 3),
          ("sel3", 3, 384), ("f1_gate", 128, 8), ("f1_bias", 128, 8), ("f1_zero", 9, 128)]
    l2 = [("a2_in", 128, 512), ("a2_cw", 128, 8), ("a2_cb", 128, 2), ("a2_xp", 128, 80), ("a2_dtw", 8, 256),
          ("a2_dtb", 128, 2), ("a2_alog", 128, 32), ("a2_d", 128, 2), ("a2_out", 128, 256), ("a2_wq", 128, 128),
          ("a2_wk", 128, 128), ("a2_wv", 128, 128), ("a2_fc", 128, 128), ("a2_fcb", 128, 1), ("causal_add", 128, 128),
          ("f2_rc1", 128, 384), ("f2_rcb1", 128, 1), ("f2_rc2", 128, 30), ("f2_rcb2", 128, 10),
          ("f2_sh1", 128, 9 * 512), ("f2_shb1", 128, 4), ("f2_sh2", 128, 512), ("f2_shb2", 128, 1),
          ("f2_eb2", 10, 128), ("f2_g", 128, 1), ("f2_b", 128, 1)]
    l3 = [("a3_cw", 128, 4), ("a3_cb", 128, 1), ("a3_wq", 128, 512), ("a3_k2", 128, 64), ("a3_k1", 64, 512),
          ("a3_v2", 128, 64), ("a3_v1", 64, 512), ("a3_e2", 128, 64), ("a3_e1", 64, 8), ("a3_a2", 128, 64),
          ("a3_a1", 64, 8), ("a3_h2", 128, 256), ("a3_h1", 64, 512), ("a3_kg", 128, 512), ("a3_kb", 128, 512),
          ("a3_qg", 128, 512), ("a3_qb", 128, 512), ("a3_ow", 128, 512), ("a3_ob", 128, 1),
          ("strict_add", 128, 128), ("strict01", 128, 128), ("incl01", 128, 128),
          ("a3_one", 128, 1), ("f3_gate", 128, 16), ("f3_b2", 18, 128)]
    late = l1 + l2 + l3
    width = sum(c for _, _, c in late)
    return [first, l0, late + [("pad", 128, -width % LATE_PIECES)]]


FFN_COLUMNS = [512 + 512 + 4 + 3, 768, 512 + 512 + 4, 512 + 512 + 4]
FFN_EXPERTS = [8, 9, 10, 18]


LINES = {
    "a0_tensor": [
        ("tok_turned", 2), ("a0_vps", 2), ("a0_proj", 8), ("a0_ctxT", 2),
    ],
    "a1_tensor": [
        ("a1_qkf", 3), ("a1_v", 1), ("a1_c1", 1), ("a1_qh", 1), ("a1_qs", 1), ("a1_kv", 1), ("a1_se", 1),
        ("a1_ss", 1), ("a1_sc", 1), ("a1_sl", 1), ("a1_num", 1), ("a1_peT", 1), ("a1_psT", 1), ("a1_oh", 1),
        ("a1_eo", 1), ("a1_ret", 1), ("a1_sg", 1), ("a1_wo", 1), ("a1_pcT", 1), ("a1_so", 1), ("a1_bw", 3),
    ],
    "a2_tensor": [
        ("a2_xz", 4), ("a2_xp", 2), ("a2_dt", 2), ("a2_out", 1), ("a2_qk", 2), ("a2_v", 1), ("a2_s", 1),
        ("a2_atT", 1), ("a2_o", 1), ("a2_fc", 2),
    ],
    "a3_tensor": [
        ("a3_s", 4), ("a3_vps", 4), ("a3_h", 1), ("a3_ea", 1), ("a3_cum", 1), ("a3_o", 2),
    ],
    "a0_scalar": [
        ("a0_v", 2), ("a0_split", 9), ("a0_fexp", 1),
    ],
    "gates_scalar": [
        ("g0_exp", 1), ("g1_sig", 1), ("g2_exp", 1), ("g3_exp", 2),
    ],
    "a1_scalar": [
        ("a1_sig", 1), ("a1_vcopy", 1), ("a1_exp2", 2), ("a1_qhcopy", 1), ("a1_silu", 1), ("a1_qscopy", 1),
        ("a1_ln", 1), ("a1_en", 1), ("a1_ep", 1), ("a1_eexp", 1), ("a1_sexp", 1), ("a1_cexp", 1),
        ("a1_peTcopy", 1), ("a1_psTcopy", 1), ("a1_ohcopy", 1), ("a1_gate", 1), ("a1_pcTcopy", 1),
    ],
    "a2_scalar": [
        ("a2_zg", 2), ("a2_xc", 2), ("a2_dtl", 1), ("a2_bcT", 1), ("a2_A", 1), ("a2_e", 2), ("a2_l", 2),
        ("a2_xm", 1), ("a2_qkcopy", 2), ("a2_vcopy", 1), ("a2_aexp", 1), ("a2_atTcopy", 1), ("a2_ocopy", 1),
    ],
    "a3_scalar": [
        ("a3_silu", 4), ("a3_vT", 4), ("a3_hsilu", 1), ("a3_e", 1), ("a3_l", 1),
    ],
    "a0_vector": [
        ("tok_zero", 1), ("tok_rows", 2), ("a0_nat", 8), ("a0_max", 1), ("a0_rest", 6), ("a0_fshift", 1),
        ("a0_ctxf", 1), ("a0_ctxsum", 2),
    ],
    "gates_vector": [
        ("g0_shift", 1), ("g1_top", 1), ("g2_shift", 1), ("g3_shift", 2),
    ],
    "a1_vector": [
        ("a1_min", 2), ("a1_sgmax", 1), ("a1_qk", 2), ("a1_kvm", 2), ("a1_cum", 1), ("a1_hat", 2),
        ("a1_eshift", 1), ("a1_sshift", 1), ("a1_cshift", 1), ("a1_slm", 1), ("a1_pe", 1), ("a1_ps", 1),
        ("a1_pc", 1), ("a1_w", 2), ("a1_sin_", 2), ("a1_mixed", 3),
    ],
    "a2_vector": [
        ("a2_conv", 2), ("a2_negA", 1), ("a2_nabs", 2), ("a2_dtx", 2), ("a2_ym", 2), ("a2_shift", 1),
        ("a2_att", 1),
    ],
    "a3_vector": [
        ("a3_x", 1), ("a3_nabs", 1), ("a3_la", 1), ("a3_negc", 1),
    ],
}


SHARED = {
    "mixtures_scalar": [("f0_sq", 16), ("f3_hh", 144)],
    "mixtures_scalar2": [("f0_log", 16), ("f3_xh", 2)],
    "mixtures_scalar3": [("a0_exp", 130), ("f0_xh", 2)],
    "mixtures_vector": [("f0_hl", 64), ("f3_hl", 144)],
    "mixtures_vector2": [("f0_zc", 16), ("f3_xl", 2)],
    "mixtures_vector3": [("tok_masked", 20), ("f0_xl", 2)],
    "pool_a": [("a0_zero", 4), ("f0_w1h", 8), ("f3_w1h", 18)],
    "pool_b": [("a0_ones", 2), ("f0_w2h", 8), ("f3_w2h", 18)],
    "pool_c": [("a0_v1s", 32), ("f0_w1s", 8), ("f3_w1s", 18)],
    "pool_d": [("a0_v1ones", 2), ("f0_w2s", 8), ("f3_w2s", 18)],
}


class Sems(dict):

    def __init__(self, make):
        super().__init__()
        self.make, self.log = make, []
        self.lines = dict(list(LINES.items()) + list(SHARED.items()))
        self.line = {name: line for line, results in self.lines.items() for name, _ in results}

    def __missing__(self, name):
        line = self.line.get(name)
        self[name] = self[line] if line else self.make(name)
        return self[name]

    def base(self, name):
        base = 0
        for other, times in self.lines.get(self.line.get(name), ()):
            if other == name:
                return base
            base += times
        return 0


class Order:

    def __init__(self, eng, sem, sems):
        self.eng, self.sem, self.sems, self.n = eng, sem, sems, 0
        self.told = {}
        self.i = None

    def loop(self, i, per):
        self.i, self.per, self.base, self.n = i, per, self.n, 0

    def end(self, times):
        assert self.n == self.per, (self.n, self.per)
        self.n, self.i = self.base + times * self.per, None

    def step(self, ins):
        self.n += 1
        ins.then_inc(self.sem, 1)
        if self.i is None:
            self.eng.wait_ge(self.sem, self.n)
        else:
            self.eng.wait_ge(self.sem, self.i * self.per + (self.base + self.n))

    def tell(self, ins, name):
        ins.then_inc(self.sems[name], 1)
        self.told[name] = self.told.get(name, 0) + 1

    def tell_step(self, ins, name):
        self.tell(ins, name)
        self.eng.wait_ge(self.sems[name], self.told[name] + self.sems.base(name))


def build(nc, a, out):
    ctx = ExitStack()
    with ctx:
        S = Sems(lambda name: ctx.enter_context(nc.semaphore("s_" + name)))

        def done(name, n):
            return S[name], n + S.base(name)

        def sb(name, shape, dt=F32):
            return ctx.enter_context(nc.sbuf_tensor(name, shape, dt))

        PS = ctx.enter_context(nc.psum_tensor("banks", [128, 8 * 512], F32))

        def bank(b, n=1, rows=128):
            return PS[0:rows, b * 512:(b + n) * 512]

        packs = pack_columns()
        width = [sum(c for _, _, c in p) for p in packs]
        WP = [sb(f"weights{k}", [128, w]) for k, w in enumerate(width)]
        where = {}
        for k, p in enumerate(packs):
            at = 0
            for name, rows, cols in p:
                where[name] = (k, rows, at, cols)
                at += cols

        def W(name, c0=0, c1=None):
            k, rows, at, cols = where[name]
            return WP[k][0:rows, at + c0:at + (cols if c1 is None else c1)]

        hT = sb("hT", [128, N])
        xT = sb("xT", [128, N])
        xc = sb("ln_xc", [128, N])
        sq = sb("ln_sq", [128, N])
        eps5 = sb("eps5", [128, 1])
        eps6 = sb("eps6", [128, 1])
        one = sb("one", [128, 1])
        with nc.sbuf_tensor("before_split", [128, 6 * N], F32), nc.sbuf_tensor("split", [128, 10 * N], F32R) as SPLIT:
            pass
        BIG = sb("big", [128, 16 * N])
        POOLB = sb("bigb", [128, 6 * N])

        def big(k, n=1, rows=128):
            return BIG[0:rows, k * N:(k + n) * N]

        def bigb(k, n=1, rows=128):
            return POOLB[0:rows, k * N:(k + n) * N]

        wslot = sb("wslot", [128, 2, max(FFN_COLUMNS)])
        gslot = sb("gslot", [128, 2, N])

        spl_dram = nc.dram_tensor("spl_dram", [9, N, 128], BF16).ap()
        raw_dram = nc.dram_tensor("raw_dram", [N // 16, 4, 5 * 512], F32).ap()
        gates_dram = nc.dram_tensor("gates_dram", [4, 18, N], F32).ap()
        bc_dram = nc.dram_tensor("bc_dram", [32, N], F32).ap()

        def h(x, k):
            return x[:, k * HALF:(k + 1) * HALF]

        def mm(o, l, r, start=True, stop=True):
            return nc.tensor.matmul(o, l, r, start=start, stop=stop, skip_group_check=True)

        def tile(x, t):
            return x[:, t * 128:(t + 1) * 128]

        TQ, TSLOTS = 2, 4
        TGROUPS = GC // TQ
        tokw = BIG[0:GP, 0:TSLOTS * 16 * TQ * 128].rearrange("p (s e q d) -> p s e q d", s=TSLOTS, e=16, q=TQ)
        tokm = POOLB[0:GP, 0:TSLOTS * TQ * 128].rearrange("p (s q d) -> p s q d", s=TSLOTS, q=TQ)
        tokx = POOLB[0:GP, N:N + TSLOTS * TQ * B].rearrange("p (s q b) -> p s q b", s=TSLOTS, q=TQ)
        wtok = a["tok_w"].rearrange("e (p c) d -> p e (c d)", p=GP)
        mtok = a["tok_m"].rearrange("(p c) d -> p (c d)", p=GP)

        def tok_load(sp, s, at, xat):
            sp.dma_start(tokx[:, s].rearrange("p q b -> p (q b)"), a["tok_x"][:, xat]).then_inc(S[f"tok_loaded{s}"], 16)
            sp.dma_start(tokw[:, s].rearrange("p e q d -> p e (q d)"),
                         wtok[:, :, at]).then_inc(S[f"tok_loaded{s}"], 16)
            sp.dma_start(tokm[:, s].rearrange("p q d -> p (q d)"), mtok[:, at]).then_inc(S[f"tok_loaded{s}"], 16)

        def tok_sp(sp):
            sp.dma_start(WP[0][:, :], a["pack0"]).then_inc(S["pack0"], 16)
            for s in range(TSLOTS):
                tok_load(sp, s, slice(s * TQ * 128, (s + 1) * TQ * 128),
                         slice(s * TQ * B, (s + 1) * TQ * B))
            with sp.Fori(1, TGROUPS // TSLOTS) as i:
                for s in range(TSLOTS):
                    sp.wait_ge(*done("tok_used", i * TSLOTS + (s + 1 - TSLOTS)))
                    tok_load(sp, s, bass.ds(i * (TSLOTS * TQ * 128) + s * TQ * 128, TQ * 128),
                             bass.ds(i * (TSLOTS * TQ * B) + s * TQ * B, TQ * B))

        def tok_dve(dve, o):
            nc.vector.memset(h(sq, 0), 0.0).then_inc(S["tok_zero"], 1)
            with dve.Fori(0, TGROUPS // TSLOTS) as i:
                for s in range(TSLOTS):
                    dve.wait_ge(*done(f"tok_loaded{s}", i * 48 + 48))
                    m = tokm[:, s].unsqueeze(1).to_broadcast([GP, 16, TQ, 128])
                    nc.vector.tensor_tensor(
                        tokw[:, s].rearrange("p e q d -> p e (q d)"), tokw[:, s].rearrange("p e q d -> p e (q d)"),
                        m.rearrange("p e q d -> p e (q d)"), ALU.mult).then_inc(S["tok_masked"], 1)
            dve.wait_ge(*done("tok_used", TGROUPS))
            for k in range(2):
                nc.vector.tensor_copy(h(xc, k), bank(k)).then_inc(S["tok_rows"], 1)
            hv = hT[:, :].rearrange("p (b g k e) -> p k e g b", g=2, k=2, e=4)
            bias = W("tok_bias").rearrange("p (g k e) -> p k e g", g=2, k=2)
            dve.wait_ge(*done("pack0", 16))
            for k in range(2):
                dve.wait_ge(*done("tok_turned", k + 1))
                o.tell_step(nc.vector.tensor_tensor(
                    hv[:, k], bank(2 + k).rearrange("p (e g b) -> p e g b", e=4, g=2),
                    bias[:, k].unsqueeze(3).to_broadcast([128, 4, 2, 64]), ALU.add), "h_ready")

        def tok_pe(pe):
            pe.wait_ge(*done("tok_zero", 1))
            for k in range(2):
                mm(bank(k), sq[:, 0:128], sq[:, 0:HALF], True, False)
            with pe.Fori(0, TGROUPS // TSLOTS) as i:
                for s in range(TSLOTS):
                    pe.wait_ge(*done("tok_masked", i * TSLOTS + (s + 1)))
                    for q in range(TQ):
                        for k in range(2):
                            for g in range(2):
                                e = 8 * g + 4 * k
                                last = nc.tensor.matmul(PS[64 * g:64 * g + 64, k * 512:(k + 1) * 512], tokx[:, s, q],
                                                        tokw[:, s, e:e + 4, q, :], start=False, stop=False,
                                                        skip_group_check=True, tile_position=(0, 64 * g))
                    last.then_inc(S["tok_used"], 1)
            pe.wait_ge(*done("pack0", 16))
            for k in range(2):
                pe.wait_ge(*done("tok_rows", k + 1))
                for e in range(4):
                    last = nc.tensor.transpose(PS[:, (2 + k) * 512 + e * 128:(2 + k) * 512 + (e + 1) * 128],
                                               xc[:, k * HALF + e * 128:k * HALF + (e + 1) * 128], W("ident"))
                last.then_inc(S["tok_turned"], 1)

        def ln_pe(pe, c, src, ready, rows=None):
            for k in range(2):
                pe.wait_ge(*done(ready[0], ready[1 + k]))
                mm(bank(6 + k), W("mean"), h(src, k)).then_inc(S["ln_mean"], 1)
            for k in range(2):
                pe.wait_ge(*done("ln_sq", 2 * c + k + 1))
                mm(bank(6 + k), W("mean"), h(sq, k)).then_inc(S["ln_var"], 1)

        def log_exp_tables(act):
            act.preload_act_table_set("natural_log_exp_and_others")

        def ln_act(act, c, eps):
            if c in LN_ROOT:
                act.preload_act_table_set("sqrt_and_others")
            else:
                log_exp_tables(act)
            for k in range(2):
                act.wait_ge(*done("ln_xc", 2 * c + k + 1))
                nc.scalar.activation(h(sq, k), h(xc, k), ACT.Square).then_inc(S["ln_sq"], 1)
            for k in range(2):
                act.wait_ge(*done("ln_var", 2 * c + k + 1))
                if c in LN_ROOT:
                    nc.scalar.activation(h(sq, k), bank(6 + k), ACT.Sqrt, bias=eps[:, 0:1]).then_inc(S["ln_log"], 1)
                    continue
                nc.scalar.activation(h(sq, k), bank(6 + k), ACT.Ln, bias=eps[:, 0:1]).then_inc(S["ln_log"], 1)
            if c in LN_ROOT:
                act.sem_inc(S["ln_rstd"], 2)
                return
            for k in range(2):
                act.wait_ge(*done("ln_log", 2 * c + k + 1))
                nc.scalar.activation(h(sq, k), h(sq, k), ACT.Exp, scale=-0.5).then_inc(S["ln_rstd"], 1)

        def ln_dve(dve, o, c, src, dst, gain=None, shift=None):
            for k in range(2):
                dve.wait_ge(*done("ln_mean", 2 * c + k + 1))
                o.tell_step(nc.vector.tensor_tensor(h(xc, k), h(src, k), bank(6 + k), ALU.subtract), "ln_xc")
            for k in range(2):
                if c in LN_ROOT:
                    dve.wait_ge(*done("ln_log", 2 * c + k + 1))
                    o.step(nc.vector.reciprocal(h(sq, k), h(sq, k)))
                else:
                    dve.wait_ge(*done("ln_rstd", 2 * c + k + 1))
                if gain is not None:
                    o.step(nc.vector.tensor_tensor(h(xc, k), h(xc, k), h(sq, k), ALU.mult))
                    o.tell_step(nc.vector.tensor_scalar(h(dst, k), h(xc, k), gain, shift, ALU.mult, ALU.add), "ln_out")
                else:
                    o.tell_step(nc.vector.tensor_tensor(h(dst, k), h(xc, k), h(sq, k), ALU.mult), "ln_out")

        nat = BIG[:, 0:8 * 768].rearrange("p (t c) -> p t c", c=768)
        neg_max = big(6)
        rest = big(7)
        a0_left = [big(7), big(15), big(14)]
        spl = BIG[:, 8 * N:8 * N + 9 * 512].bitcast(BF16).rearrange("p (x t d) -> p x t d", x=9, d=128)
        expf = big(13)
        ctxf = big(14)
        num0 = big(0).rearrange("p (t d) -> p t d", d=128)
        den0 = big(1).rearrange("p (t d) -> p t d", d=128)
        small = sb("small", [128, 96])
        QC, MC = 5, 32
        v1 = bigb(0, 2)
        v1q = v1[:, 0:N // 4 * QC].rearrange("p (q f) -> p q f", f=QC)
        VW = N // 4 * QC + MC - QC
        AG = 32
        SW = AG // 4 * QC + MC - QC
        v1s = sb("v1s", [128, 2, SW])
        krows32 = [bigb(2, 2), wslot[:, :, :].rearrange("p s c -> p (s c)")[:, 0:2 * N]]
        qrows32 = [bigb(4, 2), gslot[:, :, :].rearrange("p s c -> p (s c)")]
        krows = [x.bitcast(BF16) for x in krows32]
        qrows = [x.bitcast(BF16) for x in qrows32]
        Ex = [[big(8), big(9)], [big(10), big(11)]]
        stg = big(2, 2).rearrange("p (s c) -> p s c", s=4)
        AGROUPS = N // AG
        ATIMES = AGROUPS // 2

        def a0_rows_load(sp, s, at):
            sl = S[f"a0_rows{s}"]
            k = spl_dram[3:6].rearrange("a n d -> a (n d)")[:, at]
            q = spl_dram[0:3].rearrange("a n d -> a (n d)")[:, at]
            m = spl_dram[6:9].rearrange("a n d -> a (n d)")[:, at]
            sp.dma_start(krows[s][3:12, :], k.unsqueeze(0).to_broadcast([3, 3, AG * 128])).then_inc(sl, 16)
            sp.dma_start(qrows[s][3:12, :], q.unsqueeze(1).to_broadcast([3, 3, AG * 128])).then_inc(sl, 16)
            sp.dma_start(qrows[s][0:3, :], m).then_inc(sl, 16)

        def a0_sp(sp):
            sp.dma_start(WP[1][:, :], a["pack1"]).then_inc(S["pack1"], 16)
            for x in range(3):
                sp.wait_ge(*done("a0_split", x + 7))
                sp.dma_start(spl_dram[3 * x:3 * x + 3].rearrange("x (t p) d -> p x t d", p=128),
                             spl[:, 3 * x:3 * x + 3]).then_inc(S["a0_spl_out"], 16)
            sp.wait_ge(*done("a0_spl_out", 48))
            sp.wait_ge(*done("a0_ones", 2))
            for s in range(2):
                a0_rows_load(sp, s, slice(s * AG * 128, (s + 1) * AG * 128))

            def raw_store(i, c):
                sp.wait_ge(*done("a0_ctx", i * 4 + (c + 4)))
                for g in range(4):
                    sp.dma_start(raw_dram[bass.ds(i * 4 + c, 2), g].rearrange("b (m c) -> m b c", m=QC),
                                 stg[32 * g:32 * g + QC, c:c + 2, :]).then_inc(S[f"a0_raw{c // 2}"], 16)

            piece = width[2] // LATE_PIECES
            with sp.Fori(0, ATIMES - 1) as i:
                sp.dma_start(WP[2][:, bass.ds(i * piece, piece)], a["pack2"][:, bass.ds(i * piece, piece)]
                             ).then_inc(S["pack2"], 16)
                for s in range(2):
                    sp.wait_ge(*done("a0_arg", i * 8 + 4 * (s + 1)))
                    a0_rows_load(sp, s, bass.ds(i * (2 * AG * 128) + (s + 2) * AG * 128, AG * 128))
                    raw_store(i, 2 * s)
            for s in range(2):
                raw_store(ATIMES - 1, 2 * s)
            for s in range(2):
                sp.wait_ge(*done(f"a0_raw{s}", 64 * ATIMES + 64))
            for t in range(NT):
                q = raw_dram[t * 8:(t + 1) * 8].rearrange("b g c -> (b g) c")
                for dst, c0, y in ((num0, 0, 640), (den0, 4 * 512, 128)):
                    sp.dma_start(dst[:, t, :], q[:, c0:c0 + 4 * y].rearrange("q (r y) -> q r y", r=4)[:, :, 0:128]
                                 ).then_inc(S[f"a0_nums{t // 4}"], 16)

        def a0_pool(pool):
            nc.gpsimd.memset(eps5[:, :], 1e-5).then_inc(S["eps"], 1)
            nc.gpsimd.memset(eps6[:, :], 1e-6).then_inc(S["eps"], 1)
            nc.gpsimd.memset(one[:, :], 1.0).then_inc(S["eps"], 1)
            pool.wait_ge(*done("eps", 3))
            for x in krows32 + qrows32:
                nc.gpsimd.memset(x, 0.0).then_inc(S["a0_zero"], 1)
            pool.wait_ge(*done("a0_zero", 4))
            for s in range(2):
                nc.gpsimd.memset(krows[s][0:3, :], 1.0).then_inc(S["a0_ones"], 1)

        def a0_pool2(pool):
            pool.wait_ge(*done("tok_used", TGROUPS))
            nc.gpsimd.memset(v1q[:, :, 4], 1.0).then_inc(S["a0_v1ones"], 1)
            nc.gpsimd.memset(v1[:, N // 4 * QC:VW], 0.0).then_inc(S["a0_v1ones"], 1)
            pool.wait_ge(*done("a0_v", 2))
            pool.wait_ge(*done("a0_v1ones", 2))
            for s in range(2):
                nc.gpsimd.tensor_copy(v1s[:, s], v1[:, s * (SW - MC + QC):s * (SW - MC + QC) + SW]).then_inc(S["a0_v1s"], 1)
            with pool.Fori(1, ATIMES) as i:
                for s in range(2):
                    pool.wait_ge(*done("a0_pv", i * 4 + 2 * s))
                    nc.gpsimd.tensor_copy(v1s[:, s], v1[:, bass.ds(i * (2 * (SW - MC + QC)) + s * (SW - MC + QC), SW)]
                                          ).then_inc(S["a0_v1s"], 1)

        def a0_pe(pe):
            pe.wait_ge(*done("pack1", 16))
            for k in range(2):
                pe.wait_ge(*done("ln_out", k + 1))
                mm(bank(4 + k), W("a0_vt"), h(xT, k)).then_inc(S["a0_vps"], 1)
            for t in range(NT):
                if t >= 2:
                    pe.wait_ge(*done("a0_nat", t - 1))
                b = 2 * (t % 2)
                mm(bank(b), tile(xT, t), W("a0_nat", 0, 512))
                mm(PS[:, (b + 1) * 512:(b + 1) * 512 + 256], tile(xT, t), W("a0_nat", 512, 768)).then_inc(S["a0_proj"], 1)
            pe.wait_ge(*done("a0_nat", 8))
            pe.wait_ge(*done("a0_v", 2))

            def args(i, c):
                s = c // 2 % 2
                if c % 2 == 0:
                    pe.wait_ge(*done(f"a0_rows{s}", (i + c // 4) * 48 + 48))
                for f in range(2):
                    pe.wait_ge(*done("a0_exp", i * 8 + (2 * c + f + 1)))
                    for n in range(8):
                        t = (c % 2) * 16 + f * 8 + n
                        last = mm(PS[:, f * 1024 + n * 128:f * 1024 + (n + 1) * 128],
                                  krows[s][:, t * 128:(t + 1) * 128], qrows[s][:, t * 128:(t + 1) * 128])
                    last.then_inc(S["a0_arg"], 1)

            def weigh(i, c):
                s = c // 2
                if c % 2 == 0:
                    pe.wait_ge(*done("a0_v1s", i * 2 + (s + 1)))
                pe.wait_ge(*done("a0_ctx", i * 4 + (c + 1)))
                pe.wait_ge(*done("a0_exp", i * 8 + (2 * c + 4)))
                for g in range(4):
                    v = v1s[:, s, ((c % 2) * 4 + g) * QC:((c % 2) * 4 + g) * QC + MC]
                    last = nc.tensor.matmul(PS[32 * g:32 * g + 32, (4 + c % 2) * 512:(5 + c % 2) * 512], v,
                                            Ex[c % 2][g // 2][:, (g % 2) * 512:(g % 2 + 1) * 512], start=True, stop=True,
                                            skip_group_check=True, tile_position=(0, 32 * g))
                last.then_inc(S["a0_pv"], 1)

            args(0, 0)
            with pe.Fori(0, ATIMES - 1) as i:
                for c in range(4):
                    args(i, c + 1)
                    weigh(i, c)
            for c in range(4):
                if c < 3:
                    args(ATIMES - 1, c + 1)
                weigh(ATIMES - 1, c)
            for t in range(NT):
                pe.wait_ge(*done("a0_ctxsum", t // 4 + 1))
                last = nc.tensor.transpose(PS[:, t * 128:(t + 1) * 128], ctxf[:, t * 128:(t + 1) * 128], W("ident"))
                if t % 4 == 3:
                    last.then_inc(S["a0_ctxT"], 1)

        def a0_act(act, o):
            act.wait_ge(*done("tok_used", TGROUPS))
            for k in range(2):
                act.wait_ge(*done("a0_vps", k + 1))
                nc.scalar.activation(v1q[:, k * 128:(k + 1) * 128, 0:4], bank(4 + k).rearrange("p (q f) -> p q f", f=4),
                                     ACT.Identity, bias=W("a0_vtb")).then_inc(S["a0_v"], 1)
            act.sem_inc(S["a0_exp"], 2)
            split = (nat[:, :, 384:512], nat[:, :, 512:640], neg_max.rearrange("p (t d) -> p t d", d=128))
            for k in range(3):
                for x in range(3):
                    if k:
                        act.wait_ge(*done("a0_rest", 3 * (k - 1) + x + 1))
                    elif x == 0:
                        act.wait_ge(*done("a0_nat", 8))
                    elif x == 2:
                        act.wait_ge(*done("a0_max", 1))
                    src = a0_left[x].rearrange("p (t d) -> p t d", d=128) if k else split[x]
                    nc.scalar.activation(spl[:, 3 * x + k], src, ACT.Copy).then_inc(S["a0_split"], 1)
            act.wait_ge(*done("a0_fshift", 1))
            nc.scalar.activation(expf, expf, ACT.Exp).then_inc(S["a0_fexp"], 1)
            with act.Fori(0, ATIMES) as i:
                for c in range(4):
                    for f in range(2):
                        act.wait_ge(*done("a0_arg", i * 8 + (2 * c + f + 1)))
                        if f == 0:
                            act.wait_ge(*done("a0_pv", i * 4 + (c + 1)))
                        nc.scalar.activation(Ex[c % 2][f], PS[:, f * 1024:(f + 1) * 1024], ACT.Exp).then_inc(S["a0_exp"], 1)

        def a0_dve(dve, o):
            V = nc.vector
            for t in range(NT):
                dve.wait_ge(*done("a0_proj", t + 1))
                b = 2 * (t % 2)
                o.tell_step(V.tensor_tensor(nat[:, t, :], PS[:, b * 512:b * 512 + 768], W("a0_natb"), ALU.add), "a0_nat")
            qf, kf, vf, qt, kt = (nat[:, :, x * 128:(x + 1) * 128] for x in range(5))
            kmax, kmin = small[:, 0:8], small[:, 8:16]
            v3 = lambda x: x.rearrange("p (t d) -> p t d", d=128)
            bc = lambda x: x.unsqueeze(2).to_broadcast([128, 8, 128])
            o.step(V.tensor_reduce(kmax, kt, AX_X, ALU.max))
            o.step(V.tensor_reduce(kmin, kt, AX_X, ALU.min))
            o.step(V.tensor_scalar(small[:, 0:16], small[:, 0:16], -1.0, None, ALU.mult))
            o.step(V.tensor_tensor(v3(neg_max), qt, bc(kmax), ALU.mult))
            o.step(V.tensor_tensor(v3(rest), qt, bc(kmin), ALU.mult))
            o.tell_step(V.tensor_tensor(neg_max, neg_max, rest, ALU.min), "a0_max")
            left = [v3(x) for x in a0_left]
            for k in range(2):
                for x, src in enumerate((qt, kt, v3(neg_max))):
                    dve.wait_ge(*done("a0_split", 3 * k + x + 1))
                    o.tell(V.tensor_tensor(left[x], left[x] if k else src, spl[:, 3 * x + k], ALU.subtract), "a0_rest")
            fmax, fsum = small[:, 16:24], small[:, 24:32]
            o.step(V.tensor_tensor(v3(expf), qf, kf, ALU.mult))
            o.step(V.tensor_reduce(fmax, v3(expf), AX_X, ALU.max))
            o.tell_step(V.tensor_tensor(v3(expf), v3(expf), bc(fmax), ALU.subtract), "a0_fshift")
            dve.wait_ge(*done("a0_fexp", 1))
            o.step(V.tensor_reduce(fsum, v3(expf), AX_X, ALU.add))
            o.step(V.reciprocal(fsum, fsum))
            o.step(V.tensor_tensor(v3(ctxf), v3(expf), vf, ALU.mult))
            o.tell_step(V.tensor_tensor(v3(ctxf), v3(ctxf), bc(fsum), ALU.mult), "a0_ctxf")
            with dve.Fori(0, ATIMES) as i:
                for c in range(4):
                    dve.wait_ge(*done("a0_pv", i * 4 + (c + 3)))
                    if c % 2 == 0:
                        dve.wait_ge(*done(f"a0_raw{c // 2}", i * 64 + 64))
                    V.tensor_copy(stg[:, c, :], bank(4 + c % 2)).then_inc(S["a0_ctx"], 1)
            for k in range(2):
                dve.wait_ge(*done(f"a0_nums{k}", 128))
                o.step(V.reciprocal(h(big(1), k), h(big(1), k)))
                o.step(V.tensor_tensor(h(big(0), k), h(big(0), k), h(big(1), k), ALU.mult))
                o.tell_step(V.tensor_tensor(h(ctxf, k), h(ctxf, k), h(big(0), k), ALU.add), "a0_ctxsum")
            for k in range(2):
                dve.wait_ge(*done("a0_ctxT", k + 1))
                o.tell_step(V.tensor_tensor(h(hT, k), h(hT, k), bank(k), ALU.add), "h_ready")

        gT = sb("gT", [18, N])
        gtmp = sb("gtmp", [128, 14, 8 * 18])
        RH = 4
        hid = big(0, 2).rearrange("p (r c) -> p r c", r=RH)
        hidg = big(2, 2).rearrange("p (r c) -> p r c", r=RH)
        hid2 = big(4, 2).rearrange("p (r c) -> p r c", r=RH)
        FC = [4, 2, 4, 4]
        RP = [4, 2, 4, 4]
        NU = [2 * c for c in FC]

        def gview(j, e):
            return gtmp[:, j, 0:8 * e].rearrange("p (t e) -> p t e", e=e)

        def gcol(j):
            return gtmp[:, j, 0:8]

        def gbc(x, e):
            return x.unsqueeze(2).to_broadcast([128, 8, e])

        def top(o, score, value, mark, idx, e, more):
            V = nc.vector
            rank = W("rank", 0, e).unsqueeze(1).to_broadcast([128, 8, e])
            o.step(V.tensor_reduce(value, score, AX_X, ALU.max))
            o.step(V.tensor_tensor(mark, score, gbc(value, e), ALU.is_equal))
            o.step(V.tensor_tensor(mark, mark, rank, ALU.mult))
            o.step(V.tensor_reduce(idx, mark, AX_X, ALU.max))
            o.step(V.tensor_tensor(mark, mark, gbc(idx, e), ALU.is_equal))
            if more:
                o.step(V.scalar_tensor_tensor(out=score, in0=mark, scalar=NEG, in1=score, op0=ALU.mult, op1=ALU.add))

        def router_pe(pe, k, lhs, wname, ready):
            e = FFN_EXPERTS[k] - {1: 1, 3: 2}.get(k, 0)
            pe.wait_ge(*done(ready[0], ready[1]))
            for t in range(NT):
                last = mm(PS[:, 1024 + t * e:1024 + (t + 1) * e], tile(lhs, t), W(wname))
            last.then_inc(S["logits"], 1)

        def gates_pe(pe, k):
            e = FFN_EXPERTS[k]
            pe.wait_ge(*done("gates", k + 1))
            for t in range(NT):
                last = nc.tensor.transpose(PS[0:e, 1024 + t * 128:1024 + (t + 1) * 128], gview(0, e)[:, t, :], W("ident"))
            last.then_inc(S["gatesT_ps"], 1)

        def gates_act(act, k):
            e = FFN_EXPERTS[k]
            act.wait_ge(*done("gatesT_ps", k + 1))
            nc.scalar.activation(gT[0:e, :], PS[0:e, 1024:2048], ACT.Copy).then_inc(S["gatesT"], 1)

        def ffn_load(sp, k, s, e):
            sp.dma_start(wslot[:, s, 0:FFN_COLUMNS[k]], a[f"ffn{k}"][e].rearrange("o p c -> (o p) c")).then_inc(S[f"f{k}_w{s}"], 16)

        def gate_load(sp, k, s, e):
            sp.dma_start(gslot[:, s, :], gates_dram[k][e].to_broadcast([128, N])).then_inc(S[f"f{k}_g{s}"], 16)

        def ffn_sp(sp, k):
            E = FFN_EXPERTS[k]
            if k == 1:
                sp.wait_ge(*done("h_ready", 6))
            if k:
                sp.wait_ge(*done(f"f{k - 1}_down", NU[k - 1] * FFN_EXPERTS[k - 1] + RH))
            for s in range(2):
                ffn_load(sp, k, s, slice(s, s + 1))
            sp.wait_ge(*done("gatesT", k + 1))
            sp.dma_start(gates_dram[k, 0:E], gT[0:E, :]).then_inc(S["gates_out"], 16)
            sp.wait_ge(*done("gates_out", 16 * (k + 1)))
            if k:
                sp.wait_ge(*done("h_ready", 4 * k + 2))
            for s in range(2):
                gate_load(sp, k, s, slice(s, s + 1))
            if k == 0:
                for e in range(2, E + 1):
                    if e < E:
                        sp.wait_ge(*done("f0_w2s", e - 1))
                        ffn_load(sp, k, e % 2, slice(e, e + 1))
                    if e > 2:
                        sp.wait_ge(*done("f0_sum", 2 * e - 4))
                        gate_load(sp, k, (e - 1) % 2, slice(e - 1, e))
                return
            with sp.Fori(1, E // 2) as i:
                for s in range(2):
                    sp.wait_ge(*done(f"f{k}_down", i * (2 * NU[k]) + (NU[k] * (s - 1) + RH)))
                    ffn_load(sp, k, s, bass.ds(i * 2 + s, 1))
                    gate_load(sp, k, s, bass.ds(i * 2 + s, 1))
            if E % 2:
                sp.wait_ge(*done(f"f{k}_down", NU[k] * (E - 2) + RH))
                ffn_load(sp, k, 0, slice(E - 1, E))
                gate_load(sp, k, 0, slice(E - 1, E))

        def at(i, per, x):
            return i * per + x

        def w1_(k, s, f):
            return wslot[:, s, f * 128:(f + 1) * 128]

        def w2_(k, s, f):
            c = 512 + f * 128
            return wslot[:, s, c:c + 128]

        def ffn_up(pe, k, i, s, v):
            u, nu = v % NU[k], NU[k]
            if u == 0:
                pe.wait_ge(*done(f"f{k}_w{s}", i * 16 + 16))
            if k == 1:
                pe.wait_ge(*done("f1_gated", at(i, 2 * nu, v + 1 + RH - RP[1])))
                b = 2 * (v % 2)
                mm(bank(b), w1_(k, s, u // 2), h(xT, u % 2))
                mm(bank(b + 1), wslot[:, s, 256 + (u // 2) * 128:256 + (u // 2) * 128 + 128],
                   h(xT, u % 2)).then_inc(S["f1_up"], 1)
            else:
                pe.wait_ge(*done(f"f{k}_act", at(i, 2 * nu, v + 1)))
                mm(bank(v % 4), w1_(k, s, u // 2), h(xT, u % 2)).then_inc(S[f"f{k}_up"], 1)

        def ffn_down(pe, k, i, s, v):
            u, nu = v % NU[k], NU[k]
            pe.wait_ge(*done(f"f{k}_gated", at(i, 2 * nu, v + 1 + RH)))
            mm(bank(4 + u % 2), w2_(k, s, u // 2), hidg[:, v % RH, :], False, False).then_inc(S[f"f{k}_down"], 1)

        def ffn_units_pe(pe, k):
            ahead, per, E = 2, 2 * NU[k], FFN_EXPERTS[k]
            turns = (E - 1) // 2
            for v in range(ahead):
                ffn_up(pe, k, 0, 0, v)
            with pe.Fori(0, turns) as i:
                for v in range(per):
                    w = (v + ahead) % per
                    ffn_up(pe, k, i + 1 if v + ahead >= per else i, w // NU[k], w)
                    ffn_down(pe, k, i, v // NU[k], v)
            left = NU[k] * (E - 2 * turns)
            for v in range(left):
                if v + ahead < left:
                    ffn_up(pe, k, turns, (v + ahead) // NU[k], v + ahead)
                ffn_down(pe, k, turns, v // NU[k], v)

        def ffn_pe(pe, k, bias):
            E = FFN_EXPERTS[k]
            pe.sem_inc(S[f"f{k}_down"], RH)
            pe.wait_ge(*done("gatesT", k + 1))
            for c in range(2):
                mm(bank(4 + c), bias, gT[0:E, c * HALF:(c + 1) * HALF], True, False)
            ffn_units_pe(pe, k)

        def ffn_unit_act(act, k, i, s, v):
            u, nu = v % NU[k], NU[k]
            act.wait_ge(*done(f"f{k}_up", at(i, 2 * nu, v + 1)))
            act.wait_ge(*done(f"f{k}_gated", at(i, 2 * nu, v + 1)))
            if k == 1:
                nc.scalar.activation(hid[:, v % RH, :], bank(2 * (v % 2)), ACT.Silu).then_inc(S["f1_act"], 1)
            elif k == 2:
                b1 = wslot[:, s, 1024 + u // 2:1025 + u // 2]
                nc.scalar.activation(hid[:, v % RH, :], bank(v % 4), ACT.Exp, bias=b1)
                nc.scalar.activation(hid2[:, v % RH, :], bank(v % 4), ACT.Relu, bias=b1).then_inc(S["f2_act"], 1)
            else:
                nc.scalar.activation(hid[:, v % RH, :], bank(v % 4), ACT.Gelu,
                                     bias=wslot[:, s, 1024 + u // 2:1025 + u // 2]).then_inc(S["f3_act"], 1)

        def ffn_act(act, k):
            E = FFN_EXPERTS[k]
            act.sem_inc(S[f"f{k}_act"], RP[k])
            if k == 1:
                act.preload_act_table(ACT.Silu)
            with act.Fori(0, E // 2) as i:
                for v in range(2 * NU[k]):
                    ffn_unit_act(act, k, i, v // NU[k], v)
            if E % 2:
                for v in range(NU[k]):
                    ffn_unit_act(act, k, E // 2, 0, v)

        def ffn_unit_dve(dve, o, k, i, s, v):
            V = nc.vector
            u, nu = v % NU[k], NU[k]
            if u == 0:
                dve.wait_ge(*done(f"f{k}_g{s}", i * 16 + 16))
            dve.wait_ge(*done(f"f{k}_act", at(i, 2 * nu, v + 1 + RP[k])))
            dve.wait_ge(*done(f"f{k}_down", at(i, 2 * nu, v + 1)))
            g = gslot[:, s, (u % 2) * HALF:(u % 2 + 1) * HALF]
            hv = hid[:, v % RH, :]
            if k == 1:
                o.step(V.tensor_tensor(hv, hv, bank(2 * (v % 2) + 1), ALU.mult))
                V.tensor_tensor(hidg[:, v % RH, :], hv, g, ALU.mult).then_inc(S["f1_gated"], 1)
            elif k == 2:
                o.step(V.scalar_tensor_tensor(out=hv, in0=hv, scalar=1.0, in1=hid2[:, v % RH, :], op0=ALU.min, op1=ALU.add))
                V.scalar_tensor_tensor(out=hidg[:, v % RH, :], in0=hv, scalar=-1.0, in1=g, op0=ALU.add,
                                       op1=ALU.mult).then_inc(S["f2_gated"], 1)
            else:
                V.tensor_tensor(hidg[:, v % RH, :], hv, g, ALU.mult).then_inc(S[f"f{k}_gated"], 1)

        def ffn_dve(dve, o, k):
            E = FFN_EXPERTS[k]
            dve.sem_inc(S[f"f{k}_gated"], RH)
            steps = {1: 2 * NU[1], 2: 2 * NU[2]}.get(k, 0)
            with dve.Fori(0, E // 2) as i:
                o.loop(i, steps)
                for v in range(2 * NU[k]):
                    ffn_unit_dve(dve, o, k, i, v // NU[k], v)
                o.end(E // 2)
            if E % 2:
                for v in range(NU[k]):
                    ffn_unit_dve(dve, o, k, E // 2, 0, v)
            dve.wait_ge(*done(f"f{k}_down", NU[k] * E + RH))

        def part(k, n=1):
            return SPLIT[:, k * N:(k + n) * N]

        xh3, xl3 = part(0), part(1)
        wh3 = [part(2), part(3)]
        wl3 = [part(4), part(5)]
        hh3 = part(6, 2).rearrange("p (r c) -> p r c", r=RH)
        hl3 = part(8, 2).rearrange("p (r c) -> p r c", r=RH)
        LAG = 3

        def split_weights(pool, k, i, s, first=False):
            pool.wait_ge(*done(f"f{k}_w{s}", i * 16 + 16))
            for part_, c0 in (("1", 0), ("2", 512)):
                c = slice(c0, c0 + 512)
                if not first:
                    if part_ == "1":
                        pool.wait_ge(*done(f"f{k}_up", i * 16 + 8 * (s - 1)))
                    else:
                        pool.wait_ge(*done(f"f{k}_down", i * 16 + (8 * (s - 1) + RH)))
                nc.gpsimd.tensor_tensor(wh3[s][:, c], wslot[:, s, c], one[:, 0:1].to_broadcast([128, 512]),
                                        ALU.mult).then_inc(S[f"f{k}_w{part_}h"], 1)
                pool.wait_ge(*done(f"f{k}_w{part_}h", i * 2 + (s + 1)))
                nc.gpsimd.tensor_tensor(wl3[s][:, c], wslot[:, s, c], wh3[s][:, c].bitcast(F32),
                                        ALU.subtract).then_inc(S[f"f{k}_w{part_}s"], 1)

        def split_pool(pool, k, times, ready):
            pool.wait_ge(*done("h_ready", ready))
            for s in range(2):
                split_weights(pool, k, 0, s, True)
            with pool.Fori(1, times) as i:
                for s in range(2):
                    split_weights(pool, k, i, s)

        def mm3(o, wh, wl, xh, xl, start=False):
            mm(o, wh, xl, start, False)
            mm(o, wl, xh, False, False)
            return mm(o, wh, xh, False, False)

        def f3_pe(pe):
            pe.sem_inc(S["f3_down"], RH)

            def up(i, v):
                s, u = v // 8, v % 8
                if u == 0:
                    pe.wait_ge(*done("f3_w1s", i * 2 + (s + 1)))
                pe.wait_ge(*done("f3_act", i * 16 + (v + 1)))
                c = slice((u // 2) * 128, (u // 2 + 1) * 128)
                mm3(bank(v % 4), wh3[s][:, c], wl3[s][:, c], h(xh3, u % 2), h(xl3, u % 2),
                    True).then_inc(S["f3_up"], 1)

            def down(i, v):
                s, u = v // 8, v % 8
                if u == 0:
                    pe.wait_ge(*done("f3_w2s", i * 2 + (s + 1)))
                pe.wait_ge(*done("f3_hl", i * 16 + (v + 1)))
                c = slice(512 + (u // 2) * 128, 512 + (u // 2 + 1) * 128)
                mm3(bank(4 + u % 2), wh3[s][:, c], wl3[s][:, c],
                    hh3[:, v % RH, :], hl3[:, v % RH, :]).then_inc(S["f3_down"], 1)

            pe.wait_ge(*done("f3_xl", 2))
            pe.wait_ge(*done("gatesT", 4))
            for v in range(LAG):
                up(0, v)
            for c in range(2):
                mm(bank(4 + c), W("f3_b2"), gT[0:18, c * HALF:(c + 1) * HALF], True, False)
            with pe.Fori(0, 8) as i:
                for v in range(16):
                    up(i if v + LAG < 16 else i + 1, (v + LAG) % 16)
                    down(i, v)
            for v in range(16):
                if v + LAG < 16:
                    up(8, v + LAG)
                down(8, v)

        def f3_act(act):
            act.sem_inc(S["f3_act"], RP[3])

            def high(i, v):
                act.wait_ge(*done("f3_gated", i * 16 + (v + 1 + RH)))
                act.wait_ge(*done("f3_down", i * 16 + (v + 1)))
                nc.scalar.activation(hh3[:, v % RH, :], hidg[:, v % RH, :], ACT.Copy).then_inc(S["f3_hh"], 1)

            nc.scalar.preload_act_table(ACT.Gelu)
            ffn_unit_act(act, 3, 0, 0, 0)
            with act.Fori(0, 8) as i:
                for v in range(16):
                    w = (v + 1) % 16
                    ffn_unit_act(act, 3, i if w else i + 1, w // 8, w)
                    high(i, v)
            for v in range(16):
                if v < 15:
                    ffn_unit_act(act, 3, 8, (v + 1) // 8, v + 1)
                high(8, v)

        def f3_dve(dve, o):
            dve.sem_inc(S["f3_gated"], RH)

            def low(i, v):
                dve.wait_ge(*done("f3_hh", i * 16 + (v + 1)))
                nc.vector.tensor_tensor(hl3[:, v % RH, :], hidg[:, v % RH, :], hh3[:, v % RH, :].bitcast(F32),
                                        ALU.subtract).then_inc(S["f3_hl"], 1)

            def gated(i, v):
                s, u = v // 8, v % 8
                if u == 0:
                    dve.wait_ge(*done(f"f3_g{s}", i * 16 + 16))
                dve.wait_ge(*done("f3_act", i * 16 + (v + 1 + RP[3])))
                nc.vector.tensor_tensor(hidg[:, v % RH, :], hid[:, v % RH, :],
                                        gslot[:, s, (u % 2) * HALF:(u % 2 + 1) * HALF],
                                        ALU.mult).then_inc(S["f3_gated"], 1)

            gated(0, 0)
            with dve.Fori(0, 8) as i:
                for v in range(16):
                    w = (v + 1) % 16
                    gated(i if w else i + 1, w)
                    low(i, v)
            for v in range(16):
                if v < 15:
                    gated(8, v + 1)
                low(8, v)
            dve.wait_ge(*done("f3_down", 18 * 8 + RH))

        def split_x_act(act, k, ln):
            for c in range(2):
                act.wait_ge(*done("ln_out", 2 * ln + c + 1))
                nc.scalar.activation(h(xh3, c), h(xT, c), ACT.Copy).then_inc(S[f"f{k}_xh"], 1)

        def split_x_dve(dve, k):
            for c in range(2):
                dve.wait_ge(*done(f"f{k}_xh", c + 1))
                nc.vector.tensor_tensor(h(xl3, c), h(xT, c), h(xh3, c).bitcast(F32), ALU.subtract).then_inc(S[f"f{k}_xl"], 1)

        acc, z0, zc, zs = bigb(0), bigb(1), bigb(2), bigb(3)
        UNITS = 8 * 8

        def f0_col(e, c):
            return W("f0_cols", 7 * e + c, 7 * e + c + 1)

        def f0_mean_pe(pe, e):
            for c in range(2):
                pe.wait_ge(*done("f0_z", 2 * e + c + 1 + 2))
                if e:
                    pe.wait_ge(*done("f0_log", 2 * e + c - 1))
                mm(bank(6 + c), W("mean"), h(z0, c)).then_inc(S["f0_mean"], 1)

        def f0_var_pe(pe, e):
            for c in range(2):
                pe.wait_ge(*done("f0_sq", 2 * e + c + 1))
                mm(bank(6 + c), W("mean"), h(zs, c)).then_inc(S["f0_var"], 1)

        def f0_pe(pe):
            pe.sem_inc(S["f0_down"], RH)

            def up(v):
                e, u = v // 8, v % 8
                if u == 0:
                    pe.wait_ge(*done("f0_w1s", e + 1))
                pe.wait_ge(*done("f0_act", v + 1))
                c = slice((u // 2) * 128, (u // 2 + 1) * 128)
                mm3(bank(v % 4), wh3[e % 2][:, c], wl3[e % 2][:, c], h(xh3, u % 2), h(xl3, u % 2),
                    True).then_inc(S["f0_up"], 1)

            def down(v):
                e, u = v // 8, v % 8
                if u == 0:
                    pe.wait_ge(*done("f0_w2s", e + 1))
                if u < 2:
                    pe.wait_ge(*done("f0_z", 2 * e + u + 1))
                pe.wait_ge(*done("f0_hl", v + 1))
                c = slice(512 + (u // 2) * 128, 512 + (u // 2 + 1) * 128)
                mm3(bank(4 + u % 2), wh3[e % 2][:, c], wl3[e % 2][:, c], hh3[:, v % RH, :], hl3[:, v % RH, :],
                    u < 2).then_inc(S["f0_down"], 1)

            pe.wait_ge(*done("f0_xl", 2))
            pe.wait_ge(*done("gatesT", 1))
            for v in range(UNITS + LAG):
                if v < UNITS:
                    up(v)
                if v >= LAG:
                    d = v - LAG
                    down(d)
                    if d > 8 and d % 8 == 1:
                        f0_mean_pe(pe, d // 8 - 1)
                    if d > 8 and d % 8 == 6:
                        f0_var_pe(pe, d // 8 - 1)
            f0_mean_pe(pe, 7)
            f0_var_pe(pe, 7)
            pe.wait_ge(*done("f0_z", 18))
            for c in range(2):
                mm(bank(4 + c), W("f0_beta"), gT[0:8, c * HALF:(c + 1) * HALF]).then_inc(S["f0_beta"], 1)

        def f0_sq_act(act, e):
            for c in range(2):
                act.wait_ge(*done("f0_zc", 2 * e + c + 1))
                nc.scalar.activation(h(zs, c), h(zc, c), ACT.Square).then_inc(S["f0_sq"], 1)

        def f0_rstd_act(act, e):
            for c in range(2):
                act.wait_ge(*done("f0_var", 2 * e + c + 1))
                nc.scalar.activation(h(zs, c), bank(6 + c), ACT.Ln, bias=eps6[:, 0:1]).then_inc(S["f0_log"], 1)
            for c in range(2):
                act.wait_ge(*done("f0_log", 2 * e + c + 1))
                nc.scalar.activation(h(zs, c), h(zs, c), ACT.Exp, scale=-0.5).then_inc(S["f0_rstd"], 1)

        def f0_act(act):
            act.sem_inc(S["f0_act"], RP[0])
            log_exp_tables(act)
            for v in range(UNITS):
                e, u = v // 8, v % 8
                act.wait_ge(*done("f0_up", v + 1))
                if v >= RH:
                    act.wait_ge(*done("f0_hl", v - RH + 1))
                act.wait_ge(*done("f0_down", v + 1))
                last = nc.scalar.activation(hid[:, v % RH, :], bank(v % 4), ACT.Relu, bias=f0_col(e, u // 2))
                if v % 2:
                    last = nc.scalar.activation(hh3[:, v % RH, :], bank(v % 4), ACT.Relu, bias=f0_col(e, u // 2))
                last.then_inc(S["f0_act"], 1)
                if u == 0 and e >= 2:
                    f0_sq_act(act, e - 2)
                if u == 2 and e >= 2:
                    f0_rstd_act(act, e - 2)
            for e in (6, 7):
                f0_sq_act(act, e)
                f0_rstd_act(act, e)

        def f0_dve(dve, o):
            V = nc.vector
            dve.sem_inc(S["f0_z"], 2)
            o.step(V.memset(acc, 0.0))

            def sums(e):
                for c in range(2):
                    dve.wait_ge(*done("f0_down", 8 * e + 7 + c + RH))
                    if e:
                        dve.wait_ge(*done("f0_zc", 2 * e + c - 1))
                    V.scalar_tensor_tensor(out=h(z0, c), in0=bank(4 + c), scalar=f0_col(e, 4), in1=h(xT, c),
                                           op0=ALU.add, op1=ALU.add).then_inc(S["f0_z"], 1)

            def centre(e):
                for c in range(2):
                    dve.wait_ge(*done("f0_mean", 2 * e + c + 1))
                    if e:
                        dve.wait_ge(*done("f0_sum", 2 * e + c - 1))
                    V.tensor_tensor(h(zc, c), h(z0, c), bank(6 + c), ALU.subtract).then_inc(S["f0_zc"], 1)

            def finish(e, halves=(0, 1)):
                dve.wait_ge(*done(f"f0_g{e % 2}", 16 * (e // 2) + 16))
                for c in halves:
                    dve.wait_ge(*done("f0_rstd", 2 * e + c + 1))
                    o.step(V.tensor_tensor(h(zc, c), h(zc, c), h(zs, c), ALU.mult))
                    o.step(V.scalar_tensor_tensor(out=h(zc, c), in0=h(zc, c), scalar=f0_col(e, 5),
                                                  in1=gslot[:, e % 2, c * HALF:(c + 1) * HALF], op0=ALU.mult, op1=ALU.mult))
                    V.tensor_tensor(h(acc, c), h(acc, c), h(zc, c), ALU.add).then_inc(S["f0_sum"], 1)

            for v in range(UNITS):
                e, u = v // 8, v % 8
                dve.wait_ge(*done("f0_act", v + 1 + RP[0]))
                dve.wait_ge(*done("f0_down", v + 1))
                if v % 2 == 0:
                    o.step(V.tensor_copy(hh3[:, v % RH, :], hid[:, v % RH, :]))
                V.tensor_tensor(hl3[:, v % RH, :], hid[:, v % RH, :], hh3[:, v % RH, :].bitcast(F32),
                                ALU.subtract).then_inc(S["f0_hl"], 1)
                if u == 2 and e >= 1:
                    sums(e - 1)
                if u in (4, 5) and e >= 2:
                    finish(e - 2, (u - 4,))
                if u == 6 and e >= 1:
                    centre(e - 1)
            sums(7)
            finish(6)
            centre(7)
            finish(7)
            dve.wait_ge(*done("f0_sum", 16))
            for c in range(2):
                dve.wait_ge(*done("f0_beta", c + 1))
                o.step(V.tensor_tensor(h(hT, c), h(hT, c), h(acc, c), ALU.add))
                o.tell_step(V.tensor_tensor(h(hT, c), h(hT, c), bank(4 + c), ALU.add), "h_ready")

        def softmax2(o, act_sem, k, v1_, v2_, g1, g2, d):
            V = nc.vector
            o.tell_step(V.tensor_tensor(d, v2_, v1_, ALU.subtract), f"g{k}_shift")
            o.eng.wait_ge(*done(f"g{k}_exp", 1))
            o.step(V.tensor_scalar(g1, d, 1.0, None, ALU.add))
            o.step(V.reciprocal(g1, g1))
            o.step(V.tensor_tensor(g2, d, g1, ALU.mult))

        def mix2(o, e, m1, m2, g1, g2, dst, k):
            V = nc.vector
            o.step(V.tensor_tensor(m1, m1, gbc(g1, e), ALU.mult))
            o.step(V.tensor_tensor(m2, m2, gbc(g2, e), ALU.mult))
            o.tell_step(V.tensor_tensor(dst, m1, m2, ALU.add), "gates")

        def g0_dve(dve, o):
            V = nc.vector
            dve.wait_ge(*done("logits", 1))
            lg, m1, m2, dst = gview(1, 8), gview(2, 8), gview(3, 8), gview(0, 8)
            o.step(V.tensor_copy(lg, PS[:, 1024:1024 + 64].rearrange("p (t e) -> p t e", e=8)))
            top(o, lg, gcol(4), m1, gcol(5), 8, True)
            top(o, lg, gcol(6), m2, gcol(5), 8, False)
            softmax2(o, None, 0, gcol(4), gcol(6), gcol(7), gcol(8), gcol(9))
            mix2(o, 8, m1, m2, gcol(7), gcol(8), dst, 0)

        def g_exp_act(act, k):
            act.wait_ge(*done(f"g{k}_shift", 1))
            nc.scalar.activation(gcol(9), gcol(9), ACT.Exp).then_inc(S[f"g{k}_exp"], 1)

        def g1_dve(dve, o):
            V = nc.vector
            dve.wait_ge(*done("logits", 2))
            lg, lb, m1, m2, mx = (gview(x, 8) for x in (1, 2, 3, 4, 5))
            o.step(V.tensor_copy(lg, PS[:, 1024:1024 + 64].rearrange("p (t e) -> p t e", e=8)))
            o.step(V.tensor_tensor(lb, lg, W("f1_bias").unsqueeze(1).to_broadcast([128, 8, 8]), ALU.add))
            top(o, lb, gcol(6), m1, gcol(7), 8, True)
            top(o, lb, gcol(6), m2, gcol(7), 8, False)
            v12 = gtmp[:, 8, 0:16]
            top(o, lg, gtmp[:, 8, 0:8], mx, gcol(7), 8, True)
            o.tell_step(V.tensor_reduce(gtmp[:, 8, 8:16], lg, AX_X, ALU.max), "g1_top")
            dve.wait_ge(*done("g1_sig", 1))
            o.step(V.tensor_tensor(gcol(9), gtmp[:, 8, 0:8], gtmp[:, 8, 8:16], ALU.add))
            o.step(V.reciprocal(gcol(9), gcol(9)))
            o.step(V.tensor_tensor(gcol(10), gtmp[:, 8, 0:8], gcol(9), ALU.mult))
            o.step(V.tensor_tensor(gcol(11), gtmp[:, 8, 8:16], gcol(9), ALU.mult))
            dst = gview(0, 9)
            o.step(V.memset(dst, 1.0))
            mix2(o, 8, m1, m2, gcol(10), gcol(11), dst[:, :, 0:8], 1)

        def g1_act(act):
            act.wait_ge(*done("g1_top", 1))
            nc.scalar.activation(gtmp[:, 8, 0:16], gtmp[:, 8, 0:16], ACT.Sigmoid).then_inc(S["g1_sig"], 1)

        def ffn_add_dve(dve, o, k):
            for c in range(2):
                o.tell_step(nc.vector.tensor_tensor(h(hT, c), h(hT, c), bank(4 + c), ALU.add), "h_ready")

        def a1_pe(pe):
            pe.wait_ge(*done("pack2", 16 * LATE_PIECES))
            pe.wait_ge(*done("ln_out", 6))
            for x, name in enumerate(("a1_wq", "a1_wk", "a1_wf")):
                for k in range(2):
                    last = mm(bank(2 * x + k, rows=64), W(name), h(xT, k))
                last.then_inc(S["a1_qkf"], 1)
            for t in range(NT):
                last = mm(PS[:, 3072 + t * 128:3072 + (t + 1) * 128], tile(xT, t), W("a1_wv"))
            last.then_inc(S["a1_v"], 1)
            pe.wait_ge(*done("a1_qk", 2))
            for k in range(2):
                last = mm(bank(k, rows=32), W("a1_c1w"), h(xT, k))
            last.then_inc(S["a1_c1"], 1)
            for k in range(2):
                last = mm(bank(2 + k), W("a1_eq"), h(xT, k))
            last.then_inc(S["a1_qh"], 1)
            pe.wait_ge(*done("a1_sig", 1))
            for k in range(2):
                last = mm(bank(4 + k), W("a1_sin"), h(xT, k))
            last.then_inc(S["a1_qs"], 1)
            pe.wait_ge(*done("a1_vcopy", 1))
            mm(PS[:, 3072:3072 + 32], W("a1_ek"), W("a1_slots"))
            mm(PS[:, 3584:3584 + 128], W("a1_slots4"), W("a1_ev")).then_inc(S["a1_kv"], 1)
            pe.wait_ge(*done("a1_kvm", 2))
            pe.wait_ge(*done("a1_qhcopy", 1))
            for t in range(NT):
                last = mm(PS[:, 1024 + t * 128:1024 + (t + 1) * 128], tile(qhT, t), khm)
            last.then_inc(S["a1_se"], 1)
            pe.wait_ge(*done("a1_qscopy", 1))
            for t in range(NT):
                last = mm(PS[:, 2048 + t * 64:2048 + (t + 1) * 64], tile(qsT, t), W("a1_knowT"))
            last.then_inc(S["a1_ss"], 1)
            pe.wait_ge(*done("a1_silu", 1))
            for t in range(NT):
                last = mm(PS[:, 2560 + t * 3:2560 + (t + 1) * 3], tile(c1, t), W("a1_c2w"))
            last.then_inc(S["a1_sc"], 1)
            pe.wait_ge(*done("a1_hat", 2))
            for t in range(NT):
                last = mm(PS[:, t * 128:(t + 1) * 128], tile(khat, t), tile(qhat, t))
            last.then_inc(S["a1_sl"], 1)
            pe.wait_ge(*done("a1_slm", 1))
            for t in range(NT):
                mm(PS[:, 3072 + t * 128:3072 + (t + 1) * 128], tile(vN, t), tile(slm, t))
            for k in range(2):
                last = mm(bank(k), W("ones"), h(slm, k))
            last.then_inc(S["a1_num"], 1)
            pe.wait_ge(*done("a1_pe", 1))
            for t in range(NT):
                last = nc.tensor.transpose(PS[:, 1024 + t * 128:1024 + (t + 1) * 128], tile(pE, t), W("ident"))
            last.then_inc(S["a1_peT"], 1)
            pe.wait_ge(*done("a1_ps", 1))
            for t in range(NT):
                last = nc.tensor.transpose(PS[0:64, 2048 + t * 128:2048 + (t + 1) * 128], pS[:, t * 64:(t + 1) * 64],
                                           W("ident"))
            last.then_inc(S["a1_psT"], 1)
            pe.wait_ge(*done("a1_peTcopy", 1))
            for k in range(2):
                last = mm(bank(2 + k), vhm, h(peT, k))
            last.then_inc(S["a1_oh"], 1)
            ln_pe(pe, 3, wn, ("a1_w", 1, 2))
            pe.wait_ge(*done("a1_ohcopy", 1))
            for k in range(2):
                last = mm(bank(2 + k), W("a1_eo"), h(ohT, k))
            last.then_inc(S["a1_eo"], 1)
            pe.wait_ge(*done("a1_psTcopy", 1))
            for k in range(2):
                last = mm(bank(k), W("a1_know"), h(psT, k))
            last.then_inc(S["a1_ret"], 1)
            for k in range(2):
                last = mm(bank(4 + k), W("a1_sgw"), h(xT, k))
            last.then_inc(S["a1_sg"], 1)
            for k in range(2):
                pe.wait_ge(*done("ln_out", 7 + k))
                last = mm(bank(6 + k), W("a1_wo"), h(wln, k))
            last.then_inc(S["a1_wo"], 1)
            pe.wait_ge(*done("a1_gate", 1))
            pe.wait_ge(*done("a1_pc", 1))
            for t in range(NT):
                last = nc.tensor.transpose(PS[0:3, 2048 + t * 128:2048 + (t + 1) * 128], pC[:, t * 3:(t + 1) * 3],
                                           W("ident"))
            last.then_inc(S["a1_pcT"], 1)
            pe.wait_ge(*done("a1_sin_", 2))
            for k in range(2):
                last = mm(bank(k), W("a1_so"), h(sIn, k))
            last.then_inc(S["a1_so"], 1)
            pe.wait_ge(*done("a1_pcTcopy", 1))
            for b in range(3):
                if b:
                    pe.wait_ge(*done("a1_mixed", b))
                for k in range(2):
                    last = mm(bank(4 + k), W("sel3", b * 128, (b + 1) * 128), wT[:, k * HALF:(k + 1) * HALF])
                last.then_inc(S["a1_bw"], 1)

        minq, mink = big(0, rows=64), big(1, rows=64)
        qhat, khat = big(2, rows=64), big(3, rows=64)
        slm, wn, vN, qhT, qsT, pE = big(4), big(5), big(10), big(11), big(12), big(13)
        logf, eneg, epos = big(6, rows=64), big(7, rows=64), big(8, rows=64)
        c1 = big(9, rows=32)
        pS = big(14)[:, 0:512]
        pC = big(14)[:, 512:536]
        pst = big(14)[:, 640:768]
        peT = big(15)
        psT, ohT, wln = bigb(0, rows=64), bigb(1), bigb(3)
        khm, vhm = bigb(4)[:, 0:128], bigb(4)[:, 128:256]
        wT = bigb(2, rows=3)
        reset = bigb(5)
        gS, sIn, rec = big(0), big(1), big(6)

        def a1_act(act, o):
            A = nc.scalar
            act.wait_ge(*done("pack2", 16 * LATE_PIECES))
            A.preload_act_table(ACT.Sigmoid)
            act.wait_ge(*done("a1_qkf", 3))
            A.activation(logf, PS[0:64, 2048:3072], ACT.Sigmoid, bias=W("a1_bf")).then_inc(S["a1_sig"], 1)
            act.wait_ge(*done("a1_v", 1))
            A.activation(vN, PS[:, 3072:4096], ACT.Copy).then_inc(S["a1_vcopy"], 1)
            for x, m in enumerate((minq, mink)):
                act.wait_ge(*done("a1_min", x + 1))
                A.activation(m, m, ACT.Exp).then_inc(S["a1_exp2"], 1)
            act.wait_ge(*done("a1_qh", 1))
            A.activation(qhT, PS[:, 1024:2048], ACT.Copy).then_inc(S["a1_qhcopy"], 1)
            act.wait_ge(*done("a1_c1", 1))
            A.activation(c1, PS[0:32, 0:1024], ACT.Silu, bias=W("a1_c1b")).then_inc(S["a1_silu"], 1)
            act.wait_ge(*done("a1_qs", 1))
            A.activation(qsT, PS[:, 2048:3072], ACT.Copy).then_inc(S["a1_qscopy"], 1)
            log_exp_tables(act)
            act.wait_ge(*done("a1_sgmax", 1))
            A.activation(logf, logf, ACT.Ln).then_inc(S["a1_ln"], 1)
            act.wait_ge(*done("a1_cum", 1))
            A.activation(eneg, logf, ACT.Exp, scale=-1.0).then_inc(S["a1_en"], 1)
            A.activation(epos, logf, ACT.Exp).then_inc(S["a1_ep"], 1)
            act.wait_ge(*done("a1_eshift", 1))
            A.activation(pE, pE, ACT.Exp, scale=32.0 ** -0.5).then_inc(S["a1_eexp"], 1)
            act.wait_ge(*done("a1_sshift", 1))
            A.activation(pS, pS, ACT.Exp, scale=128.0 ** -0.5).then_inc(S["a1_sexp"], 1)
            act.wait_ge(*done("a1_cshift", 1))
            A.activation(pC, pC, ACT.Exp).then_inc(S["a1_cexp"], 1)
            act.wait_ge(*done("a1_peT", 1))
            A.activation(peT, PS[:, 1024:2048], ACT.Copy).then_inc(S["a1_peTcopy"], 1)
            act.wait_ge(*done("a1_psT", 1))
            A.activation(psT, PS[0:64, 2048:3072], ACT.Copy).then_inc(S["a1_psTcopy"], 1)
            act.wait_ge(*done("a1_oh", 1))
            A.activation(ohT, PS[:, 1024:2048], ACT.Copy).then_inc(S["a1_ohcopy"], 1)
            ln_act(act, 3, eps5)
            A.preload_act_table(ACT.Sigmoid)
            act.wait_ge(*done("a1_sg", 1))
            A.activation(gS, PS[:, 2048:3072], ACT.Sigmoid, bias=W("a1_sgb")).then_inc(S["a1_gate"], 1)
            act.wait_ge(*done("a1_pcT", 1))
            A.activation(wT, PS[0:3, 2048:3072], ACT.Copy).then_inc(S["a1_pcTcopy"], 1)

        def a1_pool(pool):
            pool.wait_ge(*done("h_ready", 4))
            nc.gpsimd.memset(reset, 1.0).then_inc(S["reset"], 1)
            pool.wait_ge(*done("reset", 1))
            nc.gpsimd.memset(reset.rearrange("p (b t) -> p b t", t=T)[:, :, 0], 0.0).then_inc(S["reset"], 1)

        def soft_shift(o, dst, src, top_, grp, width, name, extra=None):
            V = nc.vector
            d3 = dst.rearrange("p (g w) -> p g w", w=width)
            s3 = src.rearrange("p (g w) -> p g w", w=width)
            if extra is not None:
                o.step(V.tensor_tensor(d3, s3, extra, ALU.add))
                s3 = d3
            o.step(V.tensor_reduce(top_, s3, AX_X, ALU.max))
            o.tell_step(V.tensor_tensor(d3, s3, top_.unsqueeze(2).to_broadcast([128, grp, width]), ALU.subtract), name)

        def soft_norm(o, x, sum_, grp, width, name):
            V = nc.vector
            x3 = x.rearrange("p (g w) -> p g w", w=width)
            o.step(V.tensor_reduce(sum_, x3, AX_X, ALU.add))
            o.step(V.reciprocal(sum_, sum_))
            o.tell_step(V.tensor_tensor(x3, x3, sum_.unsqueeze(2).to_broadcast([128, grp, width]), ALU.mult), name)

        def a1_dve(dve, o):
            V = nc.vector
            dve.wait_ge(*done("pack2", 16 * LATE_PIECES))
            for x, m in enumerate((minq, mink)):
                dve.wait_ge(*done("a1_qkf", x + 1))
                o.tell(V.tensor_scalar(m, PS[0:64, x * 1024:(x + 1) * 1024], 0.0, None, ALU.min), "a1_min")
            dve.wait_ge(*done("a1_sig", 1))
            o.tell(V.tensor_scalar(logf, logf, 1e-6, None, ALU.max), "a1_sgmax")
            for x, (m, dst) in enumerate(((minq, qhat), (mink, khat))):
                dve.wait_ge(*done("a1_exp2", x + 1))
                o.tell_step(V.scalar_tensor_tensor(out=dst, in0=PS[0:64, x * 1024:(x + 1) * 1024], scalar=0.0, in1=m,
                                                   op0=ALU.max, op1=ALU.add), "a1_qk")
            dve.wait_ge(*done("a1_kv", 1))
            hv = W("heads4")
            o.tell(V.tensor_tensor(khm.rearrange("p (h s) -> p h s", s=32),
                                   PS[:, 3072:3104].unsqueeze(1).to_broadcast([128, 4, 32]),
                                   hv.rearrange("p (h s) -> p h s", s=32), ALU.mult), "a1_kvm")
            o.tell(V.tensor_tensor(vhm, PS[:, 3584:3712], hv, ALU.mult), "a1_kvm")
            dve.wait_ge(*done("a1_ln", 1))
            dve.wait_ge(*done("reset", 2))
            o.step(V.tensor_tensor_scan(eneg, reset[0:64, :], logf, 0.0, ALU.mult, ALU.add))
            o.tell_step(V.tensor_scalar(logf, eneg, -20.0, 20.0, ALU.max, ALU.min), "a1_cum")
            dve.wait_ge(*done("a1_ep", 1))
            o.tell(V.scalar_tensor_tensor(out=qhat, in0=qhat, scalar=0.125, in1=epos, op0=ALU.mult, op1=ALU.mult), "a1_hat")
            o.tell(V.tensor_tensor(khat, khat, eneg, ALU.mult), "a1_hat")
            dve.wait_ge(*done("a1_se", 1))
            soft_shift(o, pE, PS[:, 1024:2048], pst[:, 0:32], 32, 32, "a1_eshift")
            dve.wait_ge(*done("a1_ss", 1))
            soft_shift(o, pS, PS[:, 2048:2560], pst[:, 32:40], 8, 64, "a1_sshift")
            dve.wait_ge(*done("a1_sc", 1))
            soft_shift(o, pC, PS[:, 2560:2584], pst[:, 40:48], 8, 3, "a1_cshift",
                       extra=W("a1_c2b").unsqueeze(1).to_broadcast([128, 8, 3]))
            dve.wait_ge(*done("a1_sl", 1))
            o.tell(V.tensor_tensor(slm.rearrange("p (t l) -> p t l", l=128), PS[:, 0:1024].rearrange("p (t l) -> p t l", l=128),
                                   W("causal_sl").unsqueeze(1).to_broadcast([128, 8, 128]), ALU.mult), "a1_slm")
            dve.wait_ge(*done("a1_eexp", 1))
            soft_norm(o, pE, pst[:, 0:32], 32, 32, "a1_pe")
            dve.wait_ge(*done("a1_sexp", 1))
            soft_norm(o, pS, pst[:, 32:40], 8, 64, "a1_ps")
            dve.wait_ge(*done("a1_cexp", 1))
            soft_norm(o, pC, pst[:, 40:48], 8, 3, "a1_pc")
            dve.wait_ge(*done("a1_num", 1))
            for k in range(2):
                o.step(V.tensor_scalar(h(rec, k), bank(k), 1e-6, None, ALU.add))
                o.step(V.reciprocal(h(rec, k), h(rec, k)))
                o.tell_step(V.tensor_tensor(h(wn, k), bank(6 + k), h(rec, k), ALU.mult), "a1_w")
            ln_dve(dve, o, 3, wn, wln, W("a1_g"), W("a1_b"))
            dve.wait_ge(*done("a1_ret", 1))
            dve.wait_ge(*done("a1_gate", 1))
            for k in range(2):
                o.step(V.tensor_tensor(h(sIn, k), bank(k), h(xT, k), ALU.subtract))
                o.step(V.tensor_tensor(h(sIn, k), h(sIn, k), h(gS, k), ALU.mult))
                o.tell_step(V.tensor_tensor(h(sIn, k), h(sIn, k), h(xT, k), ALU.add), "a1_sin_")
            for b, (ready, where_) in enumerate((("a1_wo", 6), ("a1_eo", 2), ("a1_so", 0))):
                dve.wait_ge(*done(ready, 1))
                o.step(V.tensor_copy(rec, PS[:, where_ * 512:(where_ + 2) * 512]))
                dve.wait_ge(*done("a1_bw", b + 1))
                o.tell_step(V.tensor_tensor(rec, rec, PS[:, 2048:3072], ALU.mult), "a1_mixed")
                for k in range(2):
                    ins = V.tensor_tensor(h(hT, k), h(hT, k), h(rec, k), ALU.add)
                    if b == 2:
                        o.tell_step(ins, "h_ready")
                    else:
                        o.step(ins)

        xcv = [big(0), big(1)]
        zg = [big(2), big(3)]
        dt = [big(4), big(5)]
        dtx = [big(6), big(7)]
        dA = [big(8), big(9)]
        dB = [big(10), big(11)]
        hs = [big(12), big(13)]
        hc = [big(14), big(15)]
        bcs = [[bigb(0), bigb(1)], [bigb(2), bigb(3)]]
        bcT = bigb(4, rows=32)
        dtl = gslot[0:8, 0, :]
        negA = sb("negA", [128, 32])
        ym = [big(8), big(9)]
        xm, q2, k2, v2, at2, atT, o2 = big(10), big(11), big(12), big(13), big(14), big(15), big(0)

        def bt(x):
            return x.rearrange("p (b t) -> p b t", t=T)

        def a2_pe(pe):
            pe.wait_ge(*done("pack2", 16 * LATE_PIECES))
            pe.wait_ge(*done("ln_out", 12))
            for x in range(4):
                for k in range(2):
                    last = mm(bank(2 * x + k), W("a2_in", x * 128, (x + 1) * 128), h(xT, k))
                last.then_inc(S["a2_xz"], 1)
            pe.wait_ge(*done("a2_xc", 2))
            for r0, r1, b0 in ((0, 8, 0), (8, 40, 2)):
                for k in range(2):
                    for c in range(2):
                        last = mm(bank(b0 + k, rows=r1 - r0), W("a2_xp", c * 40 + r0, c * 40 + r1), h(xcv[c], k), c == 0, c == 1)
                last.then_inc(S["a2_xp"], 1)
            pe.wait_ge(*done("a2_dtl", 1))
            for c in range(2):
                for k in range(2):
                    last = mm(bank(4 + 2 * c + k), W("a2_dtw", c * 128, (c + 1) * 128), h(dtl, k))
                last.then_inc(S["a2_dt"], 1)
            pe.wait_ge(*done("a2_bcT", 1))
            for b in range(4):
                mm(bank(b), W("f1_zero"), xT[0:9, 0:HALF], True, False)
            with pe.Fori(0, 8) as i:
                for s in range(2):
                    for c in range(2):
                        pe.wait_ge(*done("a2_hc", i * 4 + (2 * s + c + 1)))
                        for k in range(2):
                            last = mm(bank(2 * c + k), W("ident"), h(hc[c], k), False, False)
                        last.then_inc(S["a2_ysum"], 1)
            pe.wait_ge(*done("a2_ym", 2))
            for k in range(2):
                for c in range(2):
                    last = mm(bank(4 + k), W("a2_out", c * 128, (c + 1) * 128), h(ym[c], k), c == 0, c == 1)
            last.then_inc(S["a2_out"], 1)
            pe.wait_ge(*done("a2_xm", 1))
            for x, name in enumerate(("a2_wq", "a2_wk")):
                for k in range(2):
                    last = mm(bank(2 * x + k), W(name), h(xm, k))
                last.then_inc(S["a2_qk"], 1)
            for t in range(NT):
                last = mm(PS[:, 3072 + t * 128:3072 + (t + 1) * 128], tile(xm, t), W("a2_wv"))
            last.then_inc(S["a2_v"], 1)
            pe.wait_ge(*done("a2_qkcopy", 2))
            for t in range(NT):
                last = mm(PS[:, 2048 + t * 128:2048 + (t + 1) * 128], tile(q2, t), tile(k2, t))
            last.then_inc(S["a2_s"], 1)
            pe.wait_ge(*done("a2_att", 1))
            for t in range(NT):
                last = nc.tensor.transpose(PS[:, t * 128:(t + 1) * 128], tile(at2, t), W("ident"))
            last.then_inc(S["a2_atT"], 1)
            pe.wait_ge(*done("a2_atTcopy", 1))
            pe.wait_ge(*done("a2_vcopy", 1))
            for t in range(NT):
                last = mm(PS[:, 1024 + t * 128:1024 + (t + 1) * 128], tile(v2, t), tile(atT, t))
            last.then_inc(S["a2_o"], 1)
            pe.wait_ge(*done("a2_ocopy", 1))
            for k in range(2):
                mm(bank(4 + k), W("a2_fc"), h(o2, k)).then_inc(S["a2_fc"], 1)

        def a2_sp(sp):
            sp.wait_ge(*done("a2_bcT", 1))
            sp.dma_start(bc_dram, bcT).then_inc(S["a2_bcout"], 16)
            sp.wait_ge(*done("a2_bcout", 16))

            def load(s, b, c):
                sp.dma_start(bcs[s][0], b.to_broadcast([128, N])).then_inc(S[f"a2_bc{s}"], 16)
                sp.dma_start(bcs[s][1], c.to_broadcast([128, N])).then_inc(S[f"a2_bc{s}"], 16)

            for s in range(2):
                load(s, bc_dram[s:s + 1], bc_dram[16 + s:17 + s])
            with sp.Fori(1, 8) as i:
                for s in range(2):
                    sp.wait_ge(*done("a2_hc", i * 4 + (2 * s + 2 - 4)))
                    load(s, bc_dram[bass.ds(i * 2 + s, 1)], bc_dram[bass.ds(i * 2 + (s + 16), 1)])

        def a2_pool(pool):
            pool.wait_ge(*done("h_ready", 10))
            for c in range(2):
                nc.gpsimd.memset(bt(dA[c])[:, :, 0], 0.0).then_inc(S["a2_dA0"], 1)
            with pool.Fori(0, 8) as i:
                for s in range(2):
                    pool.wait_ge(*done(f"a2_bc{s}", i * 32 + 32))
                    for c in range(2):
                        if s == 0:
                            pool.wait_ge(*done("a2_dtx", 2))
                        pool.wait_ge(*done("a2_scan", i * 4 + (2 * s + c + 1)))
                        nc.gpsimd.tensor_tensor(dB[c], dtx[c], bcs[s][0], ALU.mult).then_inc(S["a2_dB"], 1)

        def a2_act(act, o):
            A = nc.scalar
            act.wait_ge(*done("pack2", 16 * LATE_PIECES))
            A.preload_act_table(ACT.Silu)
            for c in range(2):
                act.wait_ge(*done("a2_xz", 3 + c))
                A.activation(zg[c], PS[:, (4 + 2 * c) * 512:(6 + 2 * c) * 512], ACT.Silu).then_inc(S["a2_zg"], 1)
            for c in range(2):
                act.wait_ge(*done("a2_conv", c + 1))
                A.activation(xcv[c], xcv[c], ACT.Silu, bias=W("a2_cb", c, c + 1)).then_inc(S["a2_xc"], 1)
            act.wait_ge(*done("a2_xp", 1))
            A.activation(dtl, PS[0:8, 0:1024], ACT.Copy).then_inc(S["a2_dtl"], 1)
            act.wait_ge(*done("a2_xp", 2))
            A.activation(bcT, PS[0:32, 1024:2048], ACT.Copy).then_inc(S["a2_bcT"], 1)
            log_exp_tables(act)
            A.activation(negA[:, :], W("a2_alog"), ACT.Exp).then_inc(S["a2_A"], 1)
            for c in range(2):
                act.wait_ge(*done("a2_nabs", c + 1))
                A.activation(hs[c], hs[c], ACT.Exp).then_inc(S["a2_e"], 1)
            for c in range(2):
                act.wait_ge(*done("a2_e", c + 1))
                A.activation(hs[c], hs[c], ACT.Ln, bias=W("ones", 0, 1)).then_inc(S["a2_l"], 1)
            act.wait_ge(*done("a2_negA", 1))
            act.wait_ge(*done("a2_dtx", 2))
            act.wait_ge(*done("a2_dA0", 2))
            with act.Fori(0, 8) as i:
                for s in range(2):
                    for c in range(2):
                        act.wait_ge(*done("a2_scan", i * 4 + (2 * s + c + 1)))
                        A.activation(bt(dA[c])[:, :, 1:], bt(dt[c])[:, :, 1:], ACT.Exp,
                                     scale=negA[:, bass.ds(i * 2 + (c * 16 + s), 1)]).then_inc(S["a2_dA"], 1)
            act.wait_ge(*done("a2_out", 1))
            A.activation(xm, PS[:, 2048:3072], ACT.Copy).then_inc(S["a2_xm"], 1)
            for x, dst in enumerate((q2, k2)):
                act.wait_ge(*done("a2_qk", x + 1))
                A.activation(dst, PS[:, x * 1024:(x + 1) * 1024], ACT.Copy).then_inc(S["a2_qkcopy"], 1)
            act.wait_ge(*done("a2_v", 1))
            A.activation(v2, PS[:, 3072:4096], ACT.Copy).then_inc(S["a2_vcopy"], 1)
            act.wait_ge(*done("a2_shift", 1))
            A.activation(at2, at2, ACT.Exp).then_inc(S["a2_aexp"], 1)
            act.wait_ge(*done("a2_atT", 1))
            A.activation(atT, PS[:, 0:1024], ACT.Copy).then_inc(S["a2_atTcopy"], 1)
            act.wait_ge(*done("a2_o", 1))
            A.activation(o2, PS[:, 1024:2048], ACT.Copy).then_inc(S["a2_ocopy"], 1)

        def a2_dve(dve, o):
            V = nc.vector
            dve.wait_ge(*done("pack2", 16 * LATE_PIECES))
            for c in range(2):
                dve.wait_ge(*done("a2_xz", c + 1))
                xi = bt(PS[:, c * 1024:(c + 1) * 1024])
                y = bt(xcv[c])
                o.step(V.tensor_scalar(y, xi, W("a2_cw", 4 * c + 3, 4 * c + 4), None, ALU.mult))
                for d in (1, 2, 3):
                    ins = V.scalar_tensor_tensor(out=y[:, :, d:], in0=xi[:, :, 0:T - d],
                                                 scalar=W("a2_cw", 4 * c + 3 - d, 4 * c + 4 - d), in1=y[:, :, d:],
                                                 op0=ALU.mult, op1=ALU.add)
                    if d < 3:
                        o.step(ins)
                    else:
                        o.tell_step(ins, "a2_conv")
            dve.wait_ge(*done("a2_A", 1))
            o.tell(V.tensor_scalar(negA[:, :], negA[:, :], -1.0, None, ALU.mult), "a2_negA")
            for c in range(2):
                dve.wait_ge(*done("a2_dt", c + 1))
                o.step(V.tensor_scalar(dt[c], PS[:, (4 + 2 * c) * 512:(6 + 2 * c) * 512], W("a2_dtb", c, c + 1), None, ALU.add))
                o.tell_step(V.scalar_tensor_tensor(out=hs[c], in0=dt[c], scalar=-1.0, in1=dt[c], op0=ALU.mult, op1=ALU.min),
                            "a2_nabs")
            dve.wait_ge(*done("a2_xc", 2))
            for c in range(2):
                dve.wait_ge(*done("a2_l", c + 1))
                o.step(V.scalar_tensor_tensor(out=dt[c], in0=dt[c], scalar=0.0, in1=hs[c], op0=ALU.max, op1=ALU.add))
                o.tell_step(V.tensor_tensor(dtx[c], dt[c], xcv[c], ALU.mult), "a2_dtx")
            dve.sem_inc(S["a2_scan"], 2)
            with dve.Fori(0, 8) as i:
                for s in range(2):
                    for c in range(2):
                        n = 2 * s + c
                        dve.wait_ge(*done("a2_dA", i * 4 + (n + 1)))
                        dve.wait_ge(*done("a2_dB", i * 4 + (n + 1)))
                        V.tensor_tensor_scan(hs[c], dA[c], dB[c], 0.0, ALU.mult, ALU.add).then_inc(S["a2_scan"], 1)
                        dve.wait_ge(*done("a2_scan", i * 4 + (n + 3)))
                        dve.wait_ge(*done("a2_ysum", i * 4 + (n + 1)))
                        V.tensor_tensor(hc[c], hs[c], bcs[s][1], ALU.mult).then_inc(S["a2_hc"], 1)
            dve.wait_ge(*done("a2_ysum", 34))
            for c in range(2):
                o.step(V.scalar_tensor_tensor(out=ym[c], in0=xcv[c], scalar=W("a2_d", c, c + 1),
                                              in1=PS[:, c * 1024:(c + 1) * 1024], op0=ALU.mult, op1=ALU.add))
                o.tell_step(V.tensor_tensor(ym[c], ym[c], zg[c], ALU.mult), "a2_ym")
            dve.wait_ge(*done("a2_s", 1))
            a3d = at2.rearrange("p (t l) -> p t l", l=128)
            o.step(V.scalar_tensor_tensor(out=a3d, in0=PS[:, 2048:3072].rearrange("p (t l) -> p t l", l=128),
                                          scalar=128.0 ** -0.5, in1=W("causal_add").unsqueeze(1).to_broadcast([128, 8, 128]),
                                          op0=ALU.mult, op1=ALU.add))
            soft_shift(o, at2, at2, small[:, 32:40], 8, 128, "a2_shift")
            dve.wait_ge(*done("a2_aexp", 1))
            soft_norm(o, at2, small[:, 32:40], 8, 128, "a2_att")
            for k in range(2):
                dve.wait_ge(*done("a2_fc", k + 1))
                o.tell_step(V.scalar_tensor_tensor(out=h(hT, k), in0=bank(4 + k), scalar=W("a2_fcb"), in1=h(hT, k),
                                                   op0=ALU.add, op1=ALU.add), "h_ready")

        xpad = BIG[:, 10 * N:10 * N + 64 * 24].rearrange("p (b t) -> p b t", t=24)
        rpad = BIG[:, 12 * N:12 * N + 64 * 24].rearrange("p (b t) -> p b t", t=24)
        lnz = big(7)
        lno = big(9)

        def f2_pool(pool):
            pool.wait_ge(*done("h_ready", 12))
            nc.gpsimd.memset(xpad, 0.0).then_inc(S["f2_pad0"], 1)
            nc.gpsimd.memset(rpad, 0.0).then_inc(S["f2_pad0"], 1)

        def f2_pe(pe):
            pe.wait_ge(*done("f2_xpad", 1))
            for k in range(2):
                for j in range(3):
                    last = mm(bank(k).rearrange("p (b t) -> p b t", t=T), W("f2_rc1", j * 128, (j + 1) * 128),
                              xpad[:, 32 * k:32 * k + 32, 3 + j:19 + j], j == 0, j == 2)
            last.then_inc(S["f2_rc"], 1)
            pe.wait_ge(*done("f2_rpad", 1))
            for k in range(2):
                for j in range(3):
                    last = mm(bank(2 + k, rows=10).rearrange("p (b t) -> p b t", t=T), W("f2_rc2", j * 10, (j + 1) * 10),
                              rpad[:, 32 * k:32 * k + 32, 3 + j:19 + j], j == 0, j == 2)
            last.then_inc(S["f2_lt"], 1)
            pe.wait_ge(*done("f2_ltcopy", 1))
            for t in range(NT):
                last = nc.tensor.transpose(PS[:, 1024 + t * 10:1024 + (t + 1) * 10], gT[0:10, t * 128:(t + 1) * 128],
                                           W("ident")[0:10, 0:10])
            last.then_inc(S["logits"], 1)
            ring = [0, 1, 6, 7]

            def sh_down(u):
                pe.wait_ge(*done("f2_shact", u + 1))
                mm(bank(4 + u % 2), W("f2_sh2", (u // 2) * 128, (u // 2) * 128 + 128), hid[:, u % RH, :], u < 2,
                   False).then_inc(S["f2_shdown"], 1)

            for u in range(8):
                if u >= 4:
                    pe.wait_ge(*done("f2_shact", u - 3))
                for j in range(9):
                    c0 = j * 512 + (u // 2) * 128
                    last = mm(bank(ring[u % 4]).rearrange("p (b t) -> p b t", t=T), W("f2_sh1", c0, c0 + 128),
                              xpad[:, 32 * (u % 2):32 * (u % 2) + 32, j:j + T], j == 0, j == 8)
                last.then_inc(S["f2_shup"], 1)
                if u >= 1:
                    sh_down(u - 1)
            sh_down(7)
            gates_pe(pe, 2)

        def f2_loop_pe(pe):
            pe.sem_inc(S["f2_down"], RH)
            pe.wait_ge(*done("gatesT", 3))
            for c in range(2):
                mm(bank(4 + c), W("f2_eb2"), gT[0:10, c * HALF:(c + 1) * HALF], False, False)
            ffn_units_pe(pe, 2)

        def f2_act(act, o):
            A = nc.scalar
            A.preload_act_table(ACT.Gelu)
            act.wait_ge(*done("f2_pad0", 2))
            act.wait_ge(*done("ln_out", 14))
            A.activation(xpad[:, :, 4:20], bt(xT[:, :]), ACT.Copy).then_inc(S["f2_xpad"], 1)
            act.wait_ge(*done("f2_rc", 1))
            A.activation(rpad[:, :, 4:20], bt(PS[:, 0:1024]), ACT.Gelu, bias=W("f2_rcb1")).then_inc(S["f2_rpad"], 1)
            A.preload_act_table(ACT.Silu)
            act.wait_ge(*done("f2_lt", 1))
            A.activation(gT[0:10, :], PS[0:10, 1024:2048], ACT.Copy).then_inc(S["f2_ltcopy"], 1)
            for u in range(8):
                act.wait_ge(*done("f2_shup", u + 1))
                if u >= RH:
                    act.wait_ge(*done("f2_shdown", u - RH + 1))
                A.activation(hid[:, u % RH, :], bank([0, 1, 6, 7][u % 4]), ACT.Silu,
                             bias=W("f2_shb1", u // 2, u // 2 + 1)).then_inc(S["f2_shact"], 1)
            g_exp_act(act, 2)
            gates_act(act, 2)
            ffn_act(act, 2)

        def f2_dve(dve, o):
            V = nc.vector
            dve.wait_ge(*done("logits", 3))
            lg, m1, m2, dst = gview(1, 10), gview(2, 10), gview(3, 10), gview(0, 10)
            o.step(V.tensor_tensor(lg, PS[:, 1024:1024 + 80].rearrange("p (t e) -> p t e", e=10),
                                   W("f2_rcb2").unsqueeze(1).to_broadcast([128, 8, 10]), ALU.add))
            top(o, lg, gcol(4), m1, gcol(5), 10, True)
            top(o, lg, gcol(6), m2, gcol(5), 10, False)
            softmax2(o, None, 2, gcol(4), gcol(6), gcol(7), gcol(8), gcol(9))
            mix2(o, 10, m1, m2, gcol(7), gcol(8), dst, 2)
            ffn_dve(dve, o, 2)
            for k in range(2):
                o.tell_step(V.scalar_tensor_tensor(out=h(lnz, k), in0=bank(4 + k), scalar=W("f2_shb2"), in1=h(xT, k),
                                                   op0=ALU.add, op1=ALU.add), "f2_z")
            ln_dve(dve, o, 7, lnz, lno, W("f2_g"), W("f2_b"))
            for k in range(2):
                o.tell_step(V.tensor_tensor(h(hT, k), h(hT, k), h(lno, k), ALU.add), "h_ready")

        x3 = big(0)
        sk3, sv3, se3, sa3 = (big(1 + j, rows=64) for j in range(4))
        vT3 = [big(5 + j) for j in range(4)]
        sh3 = big(9, rows=64)
        vh3 = big(5, 4).rearrange("p (t c) -> p t c", c=512)
        kT3 = big(10, 4).rearrange("p (g n) -> p g n", n=N)
        qT3 = bigb(0, 4).rearrange("p (g n) -> p g n", n=N)
        kw = big(14).rearrange("p (r c) -> p r c", r=2)
        qw = big(15).rearrange("p (r c) -> p r c", r=2)
        sqk = bigb(4).rearrange("p (r c) -> p r c", r=2)
        st3 = sb("st3", [128, 2, 32])
        la3 = sb("la3", [128, 5, 64])
        yT3 = big(0, 4).rearrange("p (g n) -> p g n", n=N)
        dec = big(4).rearrange("p (x c) -> p x c", x=2)
        kz3 = xT[:, :].rearrange("p (x c) -> p x c", x=2)
        mt3 = [big(14).rearrange("p (x c) -> p x c", x=2), big(15).rearrange("p (x c) -> p x c", x=2)]
        pt3 = [bigb(4).rearrange("p (x c) -> p x c", x=2), bigb(5).rearrange("p (x c) -> p x c", x=2)]
        nu3 = [xc[:, 0:768].rearrange("p (b c) -> p b c", b=4), big(9)[:, 0:768].rearrange("p (b c) -> p b c", b=4)]
        mw3 = sq[:, :].rearrange("p (x c) -> p x c", x=2)
        LEVELS = 4
        NREADY = [1, 3, 5, 6]

        def nu_ps(x):
            return PS[:, 3 * x * 512:(3 * x + 2) * 512].rearrange("p (b c) -> p b c", b=4)

        def h4(x):
            return x.rearrange("p (b d) -> p b d", b=4)

        def h8(x):
            return x.rearrange("p (h d) -> p h d", h=8)

        def a3_pe(pe):
            pe.wait_ge(*done("pack2", 16 * LATE_PIECES))
            pe.wait_ge(*done("a3_x", 1))
            for j, name in enumerate(("a3_k2", "a3_v2", "a3_e2", "a3_a2")):
                for k in range(2):
                    last = mm(bank(2 * j + k, rows=64), W(name), h(x3, k))
                last.then_inc(S["a3_s"], 1)
            pe.wait_ge(*done("a3_silu", 4))
            for f in range(4):
                if f >= 2:
                    pe.wait_ge(*done("a3_vT", f - 1))
                for k in range(2):
                    last = mm(bank(2 * (f % 2) + k), W("a3_v1", f * 128, (f + 1) * 128), h(sv3, k))
                last.then_inc(S["a3_vps"], 1)
            pe.wait_ge(*done("a3_vT", 4))
            for k in range(2):
                for f in range(4):
                    last = mm(bank(4 + k, rows=64), W("a3_h2", f * 64, (f + 1) * 64), h(vT3[f], k), f == 0, f == 3)
            last.then_inc(S["a3_h"], 1)
            for t in range(NT):
                mm(PS[:, 3072 + t * 8:3072 + (t + 1) * 8], tile(se3, t), W("a3_e1"))
                last = mm(PS[:, 3136 + t * 8:3136 + (t + 1) * 8], tile(sa3, t), W("a3_a1"))
            last.then_inc(S["a3_ea"], 1)
            pe.wait_ge(*done("a3_hsilu", 1))
            pe.wait_ge(*done("a3_la", 1))
            mm(PS[:, 3584:3648], W("incl01"), la3[:, 0, :]).then_inc(S["a3_cum"], 1)
            pe.wait_ge(*done("a3_negc", 1))

            def turn(t):
                j = t % 2
                pe.wait_ge(*done("a3_kn", t + 1))
                if t:
                    pe.wait_ge(*done("a3_kqT", 2 * t))
                for g in range(4):
                    last = nc.tensor.transpose(PS[:, 3072 + g * 128:3072 + (g + 1) * 128], kw[:, j, g * 128:(g + 1) * 128],
                                               W("ident"))
                last.then_inc(S["a3_turn"], 1)
                pe.wait_ge(*done("a3_qn", t + 1))
                for g in range(4):
                    last = nc.tensor.transpose(PS[:, 3584 + g * 128:3584 + (g + 1) * 128], qw[:, j, g * 128:(g + 1) * 128],
                                               W("ident"))
                last.then_inc(S["a3_turn"], 1)

            for t in range(NT):
                j = t % 2
                if t >= 2:
                    pe.wait_ge(*done("a3_kraw", t - 1))
                    pe.wait_ge(*done("a3_qraw", t - 1))
                    pe.wait_ge(*done("a3_vh", t - 1))
                mm(bank(j), tile(sk3, t), W("a3_k1")).then_inc(S["a3_kqv"], 1)
                mm(bank(2 + j), tile(x3, t), W("a3_wq")).then_inc(S["a3_kqv"], 1)
                mm(bank(4 + j), tile(sv3, t), W("a3_v1"), True, False)
                mm(bank(4 + j), tile(sh3, t), W("a3_h1"), False, True).then_inc(S["a3_kqv"], 1)
                if t >= 1:
                    turn(t - 1)
            turn(NT - 1)
            pe.wait_ge(*done("a3_kqT", 2 * NT))
            pe.wait_ge(*done("a3_vh", NT))

            def decay_sums(t, x):
                c = 2 * t + x
                if c:
                    pe.wait_ge(*done("a3_m", c))
                    pe.wait_ge(*done("a3_p", c))
                for k, (src, right, sem) in enumerate(((0, "strict01", "a3_cex"), (1, "ident", "a3_eb"))):
                    for b in range(4):
                        col = t * 8 + 2 * b + x
                        last = mm(tile(bank(6 + k), b), la3[:, src, col:col + 1].to_broadcast([128, 128]), W(right))
                    last.then_inc(S[sem], 1)

            def key_products(t, x):
                pe.wait_ge(*done("a3_me", 2 * t + x + 1))
                pe.wait_ge(*done("a3_kz", 2 * t + x + 1))
                for k, src in enumerate((kT3, qT3)):
                    for b in range(4):
                        last = mm(tile(bank(6 + k), b), kz3[:, x, b * 128:(b + 1) * 128], src[:, b, t * 128:(t + 1) * 128])
                last.then_inc(S["a3_gqps"], 1)

            def system_turn(t, x):
                pe.wait_ge(*done("a3_m", 2 * t + x + 1))
                for b in range(4):
                    last = nc.tensor.transpose(tile(bank(3 * x + 2), b), tile(mt3[t % 2][:, x], b), W("ident"))
                last.then_inc(S[f"a3_tr{x}"], 1)

            def level(t, x, lv):
                pe.wait_ge(*done(f"a3_n{x}", 6 * t + NREADY[lv]))
                pe.wait_ge(*done(f"a3_u{x}", 5 * t + lv + 1))
                if t and x and lv == 0:
                    pe.wait_ge(*done("a3_yT", t))
                m = (mt3[t % 2] if lv == 0 else mw3)[:, x]
                c0 = 0 if lv < 2 else 64
                for b in range(4):
                    last = mm(nu_ps(x)[:, b, c0:192], tile(m, b), nu3[x][:, b, c0:192])
                if lv < LEVELS - 1:
                    for b in range(4):
                        last = mm(tile(bank(3 * x + 2), b), nu3[x][:, b, 0:128], tile(m, b))
                last.then_inc(S[f"a3_lv{x}"], 1)

            def outputs(t, x):
                pe.wait_ge(*done(f"a3_u{x}", 5 * t + 5))
                if x == 0:
                    pe.wait_ge(*done("a3_u1", 5 * t + 5))
                for b in range(4):
                    last = mm(PS[x * 64:x * 64 + 64, 3 * 512 + b * 128:3 * 512 + (b + 1) * 128], nu3[x][:, b, 128:192],
                              tile(pt3[t % 2][:, x], b))
                last.then_inc(S["a3_y"], 1)

            for x in range(2):
                decay_sums(0, x)
                key_products(0, x)
            for x in range(2):
                system_turn(0, x)
            for t in range(NT):
                more = t < NT - 1
                level(t, 0, 0)
                level(t, 1, 0)
                if more:
                    decay_sums(t + 1, 0)
                level(t, 0, 1)
                if more:
                    key_products(t + 1, 0)
                level(t, 1, 1)
                if more:
                    decay_sums(t + 1, 1)
                level(t, 0, 2)
                level(t, 1, 2)
                if more:
                    key_products(t + 1, 1)
                level(t, 0, 3)
                level(t, 1, 3)
                for x in range(2):
                    if more:
                        system_turn(t + 1, x)
                    outputs(t, x)
            pe.wait_ge(*done("a3_yT", NT))
            for k in range(2):
                for g in range(4):
                    last = mm(bank(4 + k), W("a3_ow", g * 128, (g + 1) * 128), yT3[:, g, k * HALF:(k + 1) * HALF], g == 0, g == 3)
                last.then_inc(S["a3_o"], 1)

        def a3_act(act, o):
            A = nc.scalar
            act.wait_ge(*done("pack2", 16 * LATE_PIECES))
            A.preload_act_table(ACT.Silu)
            for j, dst in enumerate((sk3, sv3, se3, sa3)):
                act.wait_ge(*done("a3_s", j + 1))
                A.activation(dst, PS[0:64, 2 * j * 512:(2 * j + 2) * 512], ACT.Silu).then_inc(S["a3_silu"], 1)
            for f in range(4):
                act.wait_ge(*done("a3_vps", f + 1))
                A.activation(vT3[f], PS[:, (f % 2) * 1024:(f % 2 + 1) * 1024], ACT.Copy).then_inc(S["a3_vT"], 1)
            act.wait_ge(*done("a3_h", 1))
            A.activation(sh3, PS[0:64, 2048:3072], ACT.Silu).then_inc(S["a3_hsilu"], 1)
            log_exp_tables(act)
            act.wait_ge(*done("a3_nabs", 1))
            A.activation(la3[:, 2:4, :], la3[:, 2:4, :], ACT.Exp).then_inc(S["a3_e"], 1)
            act.wait_ge(*done("a3_e", 1))
            A.activation(la3[:, 2:4, :], la3[:, 2:4, :], ACT.Ln, bias=W("a3_one")).then_inc(S["a3_l"], 1)
            A.preload_act_table(ACT.Sqrt)
            for t in range(NT):
                j = t % 2
                act.wait_ge(*done("a3_kqv", 3 * t + 3))
                A.activation(vh3[:, t, :], bank(4 + j), ACT.Copy).then_inc(S["a3_vh"], 1)
                act.wait_ge(*done("a3_mv", t + 1))
                A.activation(st3[:, j, 16:18], st3[:, j, 12:16].rearrange("p (x y) -> p x y", y=2)[:, :, 1], ACT.Sqrt,
                             bias=eps5[:, 0:1]).then_inc(S["a3_sd"], 1)
                act.wait_ge(*done("a3_kk", t + 1))
                A.activation(sqk[:, j, :], kw[:, j, :], ACT.Square).then_inc(S["a3_sq"], 1)
                act.wait_ge(*done("a3_n2", t + 1))
                A.activation(st3[:, j, 18:26], st3[:, j, 18:26], ACT.Sqrt).then_inc(S["a3_nrm"], 1)
                for x, dst in enumerate((kT3, qT3)):
                    act.wait_ge(*done("a3_turn", 2 * t + x + 1))
                    A.activation(dst[:, :, t * 128:(t + 1) * 128], bank(6 + x).rearrange("p (g c) -> p g c", g=4),
                                 ACT.Copy).then_inc(S["a3_kqT"], 1)

            def decays(t, x):
                act.wait_ge(*done("a3_dm", 2 * t + x + 1))
                for b in range(4):
                    hd = 2 * b + x
                    c = tile(dec[:, x], b)
                    last = A.activation(c, c, ACT.Exp, bias=la3[:, 4, t * 8 + hd:t * 8 + hd + 1])
                last.then_inc(S["a3_dec"], 1)

            def powers(t, x, lv):
                act.wait_ge(*done(f"a3_lv{x}", 4 * t + lv + 1))
                A.activation(mw3[:, x], bank(3 * x + 2), ACT.Copy).then_inc(S[f"a3_n{x}"], 1)
                if lv < 2:
                    act.wait_ge(*done(f"a3_u{x}", 5 * t + lv + 2))
                    A.activation(nu3[x][:, :, 0:128], nu_ps(x)[:, :, 0:128], ACT.Copy).then_inc(S[f"a3_n{x}"], 1)

            def system(t, x):
                act.wait_ge(*done(f"a3_tr{x}", t + 1))
                A.activation(nu3[x][:, :, 0:128], h4(bank(3 * x + 2)), ACT.Copy).then_inc(S[f"a3_n{x}"], 1)

            A.preload_act_table(ACT.Exp)
            decays(0, 0)
            decays(0, 1)
            system(0, 0)
            system(0, 1)
            for t in range(NT):
                more = t < NT - 1
                powers(t, 0, 0)
                powers(t, 1, 0)
                if more:
                    decays(t + 1, 0)
                powers(t, 0, 1)
                powers(t, 1, 1)
                if more:
                    decays(t + 1, 1)
                powers(t, 0, 2)
                powers(t, 1, 2)
                if more:
                    system(t + 1, 0)
                    system(t + 1, 1)
                act.wait_ge(*done("a3_y", 2 * t + 2))
                A.activation(yT3[:, :, t * 128:(t + 1) * 128], bank(3).rearrange("p (g c) -> p g c", g=4),
                             ACT.Copy).then_inc(S["a3_yT"], 1)

        def a3_pool(pool):
            pool.wait_ge(*done("a3_kqv", 3 * NT))
            nc.gpsimd.memset(xT[:, :], 0.0).then_inc(S["a3_kzero"], 1)
            pool.wait_ge(*done("a3_kzero", 1))
            pool.wait_ge(*done("a3_kqT", 2 * NT))
            for t in range(NT):
                for x in range(2):
                    if t:
                        pool.wait_ge(*done("a3_gqps", 2 * t + x - 1))
                    r = slice(64 * x, 64 * x + 64)
                    nc.gpsimd.tensor_copy(h4(kz3[r, x]), kT3[r, :, t * 128:(t + 1) * 128]).then_inc(S["a3_kz"], 1)

        def a3_dve(dve, o):
            V = nc.vector
            dve.wait_ge(*done("pack2", 16 * LATE_PIECES))
            x, y = bt(xT[:, :]), bt(x3)
            o.step(V.tensor_scalar(y, x, W("a3_cw", 3, 4), W("a3_cb"), ALU.mult, ALU.add))
            for d in (1, 2, 3):
                o.step(V.scalar_tensor_tensor(out=y[:, :, d:], in0=x[:, :, 0:T - d], scalar=W("a3_cw", 3 - d, 4 - d),
                                              in1=y[:, :, d:], op0=ALU.mult, op1=ALU.add))
            o.tell_step(V.tensor_tensor(x3, x3, xT[:, :], ALU.add), "a3_x")
            dve.wait_ge(*done("a3_ea", 1))
            o.step(V.tensor_copy(la3[:, 1, :], PS[:, 3072:3136]))
            o.step(V.tensor_scalar(la3[:, 0, :], PS[:, 3136:3200], -1.0, None, ALU.mult))
            o.tell_step(V.scalar_tensor_tensor(out=la3[:, 2:4, :], in0=la3[:, 0:2, :], scalar=-1.0, in1=la3[:, 0:2, :],
                                               op0=ALU.mult, op1=ALU.min), "a3_nabs")
            dve.wait_ge(*done("a3_l", 1))
            o.step(V.scalar_tensor_tensor(out=la3[:, 0:2, :], in0=la3[:, 0:2, :], scalar=0.0, in1=la3[:, 2:4, :],
                                          op0=ALU.max, op1=ALU.add))
            o.step(V.tensor_scalar(la3[:, 1, :], la3[:, 1, :], 0.1, None, ALU.mult))
            o.tell_step(V.tensor_scalar(la3[:, 0, :], la3[:, 0, :], -1.0, None, ALU.mult), "a3_la")
            dve.wait_ge(*done("a3_cum", 1))
            o.tell_step(V.tensor_scalar(la3[:, 4, :], PS[:, 3584:3648], -1.0, None, ALU.mult), "a3_negc")
            for t in range(NT):
                j = t % 2
                for x_, b in ((0, j), (1, 2 + j)):
                    dve.wait_ge(*done("a3_kqv", 3 * t + 1 + x_))
                    if t >= 2 and x_ == 0:
                        dve.wait_ge(*done("a3_turn", 2 * t - 2))
                    o.step(V.bn_stats(st3[:, j, 6 * x_:6 * x_ + 6], bank(b)))
                    ins = V.bn_aggr(st3[:, j, 12 + 2 * x_:14 + 2 * x_], st3[:, j, 6 * x_:6 * x_ + 6])
                    if x_:
                        o.tell_step(ins, "a3_mv")
                    else:
                        o.step(ins)
                dve.wait_ge(*done("a3_sd", t + 1))
                o.step(V.reciprocal(st3[:, j, 16:18], st3[:, j, 16:18]))
                for x_, (w_, g_, b_, raw, fin) in enumerate(((kw, "a3_kg", "a3_kb", "a3_kraw", "a3_kk"),
                                                             (qw, "a3_qg", "a3_qb", "a3_qraw", "a3_qn"))):
                    if x_ and t >= 2:
                        dve.wait_ge(*done("a3_turn", 2 * t - 2))
                    o.tell_step(V.tensor_scalar(w_[:, j, :], bank(2 * x_ + j), st3[:, j, 12 + 2 * x_:13 + 2 * x_],
                                                st3[:, j, 16 + x_:17 + x_], ALU.subtract, ALU.mult), raw)
                    o.step(V.tensor_tensor(w_[:, j, :], w_[:, j, :], W(g_), ALU.mult))
                    o.tell_step(V.tensor_tensor(w_[:, j, :], w_[:, j, :], W(b_), ALU.add), fin)
                dve.wait_ge(*done("a3_sq", t + 1))
                o.tell_step(V.tensor_reduce(st3[:, j, 18:26], h8(sqk[:, j, :]), AX_X, ALU.add), "a3_n2")
                dve.wait_ge(*done("a3_nrm", t + 1))
                o.step(V.tensor_scalar(st3[:, j, 18:26], st3[:, j, 18:26], 1e-12, None, ALU.max))
                o.step(V.reciprocal(st3[:, j, 18:26], st3[:, j, 18:26]))
                o.tell_step(V.tensor_tensor(h8(kw[:, j, :]), h8(kw[:, j, :]),
                                            st3[:, j, 18:26].unsqueeze(2).to_broadcast([128, 8, 64]), ALU.mult), "a3_kn")
            dve.wait_ge(*done("a3_turn", 2 * NT))
            mask = W("strict_add").unsqueeze(1).to_broadcast([128, 4, 128])

            def scaled_decays(t, x):
                c = 2 * t + x
                dve.wait_ge(*done("a3_cex", c + 1))
                o.tell(V.tensor_tensor(h4(dec[:, x]), h4(bank(6)), mask, ALU.add), "a3_dm")
                dve.wait_ge(*done("a3_dec", c + 1))
                dve.wait_ge(*done("a3_eb", c + 1))
                o.tell_step(V.tensor_tensor(mt3[t % 2][:, x], dec[:, x], bank(7), ALU.mult), "a3_me")

            def systems(t, x):
                m = mt3[t % 2][:, x]
                dve.wait_ge(*done("a3_gqps", 2 * t + x + 1))
                o.tell(V.scalar_tensor_tensor(out=m, in0=m, scalar=2.0, in1=bank(6), op0=ALU.mult, op1=ALU.mult), "a3_m")
                o.tell(V.tensor_tensor(pt3[t % 2][:, x], dec[:, x], bank(7), ALU.mult), "a3_p")

            def values(t, x):
                if t:
                    dve.wait_ge(*done("a3_y", 2 * t - 1 + x))
                e = la3[:, 1, t * 8:(t + 1) * 8].rearrange("p (b x) -> p x b", x=2)[:, x]
                v = vh3[:, t, :].rearrange("p (b x d) -> p x b d", x=2, d=64)[:, x]
                o.tell_step(V.tensor_tensor(nu3[x][:, :, 128:192], v, e.unsqueeze(2).to_broadcast([128, 4, 64]),
                                            ALU.mult), f"a3_u{x}")

            def update(t, x, lv):
                dve.wait_ge(*done(f"a3_lv{x}", 4 * t + lv + 1))
                u = nu3[x][:, :, 128:192]
                o.tell_step(V.tensor_tensor(u, u, nu_ps(x)[:, :, 128:192], ALU.subtract if lv == 0 else ALU.add), f"a3_u{x}")

            for x in range(2):
                values(0, x)
                scaled_decays(0, x)
                systems(0, x)
            for t in range(NT):
                more = t < NT - 1
                update(t, 0, 0)
                update(t, 1, 0)
                if more:
                    scaled_decays(t + 1, 0)
                update(t, 0, 1)
                if more:
                    systems(t + 1, 0)
                update(t, 1, 1)
                if more:
                    scaled_decays(t + 1, 1)
                update(t, 0, 2)
                update(t, 1, 2)
                if more:
                    systems(t + 1, 1)
                update(t, 0, 3)
                update(t, 1, 3)
                if more:
                    values(t + 1, 0)
                    values(t + 1, 1)
            for k in range(2):
                dve.wait_ge(*done("a3_o", k + 1))
                o.tell_step(V.scalar_tensor_tensor(out=h(hT, k), in0=bank(4 + k), scalar=W("a3_ob"), in1=h(hT, k),
                                                   op0=ALU.add, op1=ALU.add), "h_ready")

        def g3_act(act):
            act.wait_ge(*done("g3_shift", 1))
            nc.scalar.activation(gview(1, 16), gview(1, 16), ACT.Exp).then_inc(S["g3_exp"], 1)
            act.wait_ge(*done("g3_shift", 2))
            nc.scalar.activation(gtmp[:, 8, 0:32], gtmp[:, 8, 0:32], ACT.Exp).then_inc(S["g3_exp"], 1)

        def g3_dve(dve, o):
            V = nc.vector
            dve.wait_ge(*done("logits", 4))
            sc = gview(1, 16)
            lg = PS[:, 1024:1152].rearrange("p (t e) -> p t e", e=16)
            o.step(V.tensor_reduce(gcol(6), lg, AX_X, ALU.max))
            o.tell_step(V.tensor_tensor(sc, lg, gbc(gcol(6), 16), ALU.subtract), "g3_shift")
            dve.wait_ge(*done("g3_exp", 1))
            o.step(V.tensor_reduce(gcol(6), sc, AX_X, ALU.add))
            o.step(V.reciprocal(gcol(6), gcol(6)))
            o.step(V.tensor_tensor(sc, sc, gbc(gcol(6), 16), ALU.mult))
            vals = gtmp[:, 8, 0:32]
            for r in range(4):
                top(o, sc, gtmp[:, 8, 8 * r:8 * r + 8], gview(2 + r, 16), gcol(7), 16, r < 3)
            v3_ = vals.rearrange("p (r t) -> p r t", r=4)
            o.step(V.tensor_copy(gcol(6), gtmp[:, 8, 0:8]))
            o.tell_step(V.tensor_tensor(v3_, v3_, gcol(6).unsqueeze(1).to_broadcast([128, 4, 8]), ALU.subtract), "g3_shift")
            dve.wait_ge(*done("g3_exp", 2))
            o.step(V.tensor_reduce(gcol(6), vals.rearrange("p (r t) -> p t r", r=4), AX_X, ALU.add))
            o.step(V.reciprocal(gcol(6), gcol(6)))
            o.step(V.tensor_tensor(v3_, v3_, gcol(6).unsqueeze(1).to_broadcast([128, 4, 8]), ALU.mult))
            dst = gview(0, 18)
            o.step(V.memset(dst, 0.5))
            for r in range(4):
                m = gview(2 + r, 16)
                o.step(V.tensor_tensor(m, m, gbc(gtmp[:, 8, 8 * r:8 * r + 8], 16), ALU.mult))
            o.step(V.tensor_tensor(gview(2, 16), gview(2, 16), gview(3, 16), ALU.add))
            o.step(V.tensor_tensor(gview(4, 16), gview(4, 16), gview(5, 16), ALU.add))
            o.tell_step(V.tensor_tensor(dst[:, :, 0:16], gview(2, 16), gview(4, 16), ALU.add), "gates")

        block = ctx.enter_context(nc.Block())

        @block.sync
        def _(sp):
            tok_sp(sp)
            if STAGES >= 2:
                a0_sp(sp)
            if STAGES >= 3:
                ffn_sp(sp, 0)
            if STAGES >= 5:
                ffn_sp(sp, 1)
            if STAGES >= 6:
                a2_sp(sp)
            if STAGES >= 7:
                ffn_sp(sp, 2)
            if STAGES >= 9:
                ffn_sp(sp, 3)
            for k in range(2):
                sp.wait_ge(*done("h_ready", 2 * STAGES))
                sp.dma_start(out[:, k * HALF:(k + 1) * HALF], h(hT, k)).then_inc(S["stored"], 16)
            sp.wait_ge(*done("stored", 32))

        @block.gpsimd
        def _(pool):
            a0_pool(pool)
            if STAGES >= 2:
                a0_pool2(pool)
            if STAGES >= 3:
                split_pool(pool, 0, 4, 4)
            if STAGES >= 4:
                a1_pool(pool)
            if STAGES >= 6:
                a2_pool(pool)
            if STAGES >= 7:
                f2_pool(pool)
            if STAGES >= 8:
                a3_pool(pool)
            if STAGES >= 9:
                split_pool(pool, 3, 9, 16)

        @block.tensor
        def _(pe):
            tok_pe(pe)
            if STAGES >= 2:
                ln_pe(pe, 0, hT, ("h_ready", 2, 2))
                pe.sem_inc(S["a0_pv"], 2)
                a0_pe(pe)
            if STAGES >= 3:
                ln_pe(pe, 1, hT, ("h_ready", 3, 4))
                router_pe(pe, 0, xT, "f0_router", ("ln_out", 4))
                gates_pe(pe, 0)
                f0_pe(pe)
            if STAGES >= 4:
                ln_pe(pe, 2, hT, ("h_ready", 5, 6))
                a1_pe(pe)
            if STAGES >= 5:
                ln_pe(pe, 4, hT, ("h_ready", 7, 8))
                router_pe(pe, 1, xT, "f1_gate", ("ln_out", 10))
                gates_pe(pe, 1)
                ffn_pe(pe, 1, W("f1_zero"))
            if STAGES >= 6:
                ln_pe(pe, 5, hT, ("h_ready", 9, 10))
                pe.sem_inc(S["a2_ysum"], 2)
                a2_pe(pe)
            if STAGES >= 7:
                ln_pe(pe, 6, hT, ("h_ready", 11, 12))
                f2_pe(pe)
                f2_loop_pe(pe)
                ln_pe(pe, 7, lnz, ("f2_z", 1, 2))
            if STAGES >= 8:
                ln_pe(pe, 8, hT, ("h_ready", 13, 14))
                a3_pe(pe)
            if STAGES >= 9:
                ln_pe(pe, 9, hT, ("h_ready", 15, 16))
                router_pe(pe, 3, xT, "f3_gate", ("ln_out", 20))
                gates_pe(pe, 3)
                f3_pe(pe)

        @block.scalar
        def _(act):
            o = Order(act, S["act_step"], S)
            act.wait_ge(*done("eps", 3))
            if STAGES >= 2:
                ln_act(act, 0, eps5)
                a0_act(act, o)
            if STAGES >= 3:
                ln_act(act, 1, eps5)
                split_x_act(act, 0, 1)
                g_exp_act(act, 0)
                gates_act(act, 0)
                f0_act(act)
            if STAGES >= 4:
                ln_act(act, 2, eps5)
                a1_act(act, o)
            if STAGES >= 5:
                ln_act(act, 4, eps5)
                g1_act(act)
                gates_act(act, 1)
                ffn_act(act, 1)
            if STAGES >= 6:
                ln_act(act, 5, eps5)
                a2_act(act, o)
            if STAGES >= 7:
                ln_act(act, 6, eps5)
                f2_act(act, o)
                ln_act(act, 7, eps5)
            if STAGES >= 8:
                ln_act(act, 8, eps5)
                a3_act(act, o)
            if STAGES >= 9:
                ln_act(act, 9, eps5)
                split_x_act(act, 3, 9)
                g3_act(act)
                gates_act(act, 3)
                f3_act(act)

        @block.vector
        def _(dve):
            o = Order(dve, S["dve_step"], S)
            tok_dve(dve, o)
            if STAGES >= 2:
                ln_dve(dve, o, 0, hT, xT)
                dve.sem_inc(S["a0_ctx"], 2)
                dve.sem_inc(S["a0_raw0"], 64)
                dve.sem_inc(S["a0_raw1"], 64)
                a0_dve(dve, o)
            if STAGES >= 3:
                ln_dve(dve, o, 1, hT, xT)
                split_x_dve(dve, 0)
                g0_dve(dve, o)
                f0_dve(dve, o)
            if STAGES >= 4:
                ln_dve(dve, o, 2, hT, xT)
                a1_dve(dve, o)
            if STAGES >= 5:
                ln_dve(dve, o, 4, hT, xT)
                g1_dve(dve, o)
                ffn_dve(dve, o, 1)
                ffn_add_dve(dve, o, 1)
            if STAGES >= 6:
                ln_dve(dve, o, 5, hT, xT)
                a2_dve(dve, o)
            if STAGES >= 7:
                ln_dve(dve, o, 6, hT, xT)
                f2_dve(dve, o)
            if STAGES >= 8:
                ln_dve(dve, o, 8, hT, xT)
                a3_dve(dve, o)
            if STAGES >= 9:
                ln_dve(dve, o, 9, hT, xT)
                split_x_dve(dve, 3)
                g3_dve(dve, o)
                f3_dve(dve, o)
                ffn_add_dve(dve, o, 3)


def kernel(**inputs):
    import concourse.bacc as bacc
    from concourse.bass_utils import run_bass_kernel_spmd

    w = {k: np.asarray(v) for k, v in inputs.items()}
    f = np.float32

    def rows(x, cols=None):
        x = np.asarray(x).reshape(1, -1)
        return np.broadcast_to(x, (128, x.shape[1]))

    def col(x):
        return np.asarray(x).reshape(-1, 128).T

    i = np.arange(128)
    same = (i[:, None] // T) == (i[None, :] // T)
    parts = {
        "ident": np.eye(128, dtype=f), "mean": np.full((128, 128), 1.0 / 128, f), "tok_bias": w["L0_tok_bias"].T,
        "a0_nat": np.concatenate([w[f"L0_attn_W_{n}"].T for n in ("qf", "kf", "vf", "qt", "kt", "vt")], axis=1),
        "a0_natb": rows(np.concatenate([w[f"L0_attn_b_{n}"] for n in ("qf", "kf", "vf", "qt", "kt", "vt")])),
        "a0_vt": w["L0_attn_W_vt"].T, "a0_vtb": col(w["L0_attn_b_vt"]),
        "f0_router": w["L0_ffn_router_w"], "f0_beta": w["L0_ffn_beta"],
        "f0_cols": np.concatenate([np.concatenate([w[f"L0_ffn_{n}"][e].reshape(-1, 128).T for n in ("b1", "b2", "gamma", "beta")],
                                                  axis=1) for e in range(8)], axis=1),
        "rank": rows(np.arange(16, 0, -1).astype(f)),
        "causal_sl": (same & (i[:, None] <= i[None, :])).astype(f), "ones": np.ones((128, 128), f),
        "a1_wq": w["L1_attn_Wq"], "a1_wk": w["L1_attn_Wk"], "a1_wf": w["L1_attn_Wf"],
        "a1_bf": w["L1_attn_bf"].reshape(64, 1), "a1_wv": w["L1_attn_Wv"], "a1_wo": w["L1_attn_Wo"],
        "a1_g": col(w["L1_attn_ln_g"]), "a1_b": col(w["L1_attn_ln_b"]),
        "a1_slots": w["L1_attn_eslots"][0].T, "a1_slots4": np.tile(w["L1_attn_eslots"][0].T, (1, 4)),
        "a1_eq": w["L1_attn_Eq"], "a1_ek": w["L1_attn_Ek"], "a1_ev": w["L1_attn_Ev"], "a1_eo": w["L1_attn_Eo"],
        "heads4": ((i[:, None] // 32) == (i[None, :] // 32)).astype(f),
        "a1_sin": w["L1_attn_Sin"], "a1_knowT": w["L1_attn_know"][0].T, "a1_know": w["L1_attn_know"][0],
        "a1_sgw": w["L1_attn_Sg_w"], "a1_sgb": col(w["L1_attn_Sg_b"]), "a1_so": w["L1_attn_So"],
        "a1_c1w": w["L1_attn_C1w"], "a1_c1b": w["L1_attn_C1b"].reshape(32, 1), "a1_c2w": w["L1_attn_C2w"],
        "a1_c2b": rows(w["L1_attn_C2b"]), "sel3": np.repeat(np.eye(3, dtype=f), 128, axis=1),
        "f1_gate": w["L1_ffn_gate_w"].T, "f1_bias": rows(w["L1_ffn_biases"]),
        "f1_zero": np.zeros((9, 128), f),
        "a2_in": w["L2_attn_in_proj_w"].T, "a2_cw": w["L2_attn_conv_w"].reshape(2, 128, 4).transpose(1, 0, 2).reshape(128, 8),
        "a2_cb": col(w["L2_attn_conv_b"]),
        "a2_xp": w["L2_attn_x_proj_w"].T.reshape(2, 128, 40).transpose(1, 0, 2).reshape(128, 80),
        "a2_dtw": w["L2_attn_dt_proj_w"].T, "a2_dtb": col(w["L2_attn_dt_proj_b"]),
        "a2_alog": w["L2_attn_A_log"].reshape(2, 128, 16).transpose(1, 0, 2).reshape(128, 32),
        "a2_d": col(w["L2_attn_D_param"]),
        "a2_out": w["L2_attn_out_proj_w"].T.reshape(2, 128, 128).transpose(1, 0, 2).reshape(128, 256),
        "a2_wq": w["L2_attn_wq"].T, "a2_wk": w["L2_attn_wk"].T, "a2_wv": w["L2_attn_wv"].T,
        "a2_fc": w["L2_attn_fc_w"].T, "a2_fcb": col(w["L2_attn_fc_b"]),
        "causal_add": np.where(same & (i[None, :] <= i[:, None]), 0, NEG).astype(f),
        "f2_rc1": w["L2_ffn_rc_w1"].transpose(1, 2, 0).reshape(128, 384), "f2_rcb1": col(w["L2_ffn_rc_b1"]),
        "f2_rc2": w["L2_ffn_rc_w2"].transpose(1, 2, 0).reshape(128, 30), "f2_rcb2": rows(w["L2_ffn_rc_b2"]),
        "f2_sh1": w["L2_ffn_sh_w1"].transpose(1, 2, 0).reshape(128, 9 * 512), "f2_shb1": col(w["L2_ffn_sh_b1"]),
        "f2_sh2": w["L2_ffn_sh_w2"][:, :, 0].T.reshape(4, 128, 128).transpose(1, 0, 2).reshape(128, 512),
        "f2_shb2": col(w["L2_ffn_sh_b2"]), "f2_eb2": w["L2_ffn_e_b2"], "f2_g": col(w["L2_ffn_ln_g"]),
        "f2_b": col(w["L2_ffn_ln_b"]),
        "a3_cw": w["L3_attn_conv_w"][:, 0, :], "a3_cb": col(w["L3_attn_conv_b"]), "a3_wq": w["L3_attn_Wq"].T,
        "a3_k2": w["L3_attn_Mk_W2"].T, "a3_k1": w["L3_attn_Mk_W1"].T, "a3_v2": w["L3_attn_Mv_W2"].T,
        "a3_v1": w["L3_attn_Mv_W1"].T, "a3_e2": w["L3_attn_Meta_W2"].T, "a3_e1": w["L3_attn_Meta_W1"].T,
        "a3_a2": w["L3_attn_Malpha_W2"].T, "a3_a1": w["L3_attn_Malpha_W1"].T,
        "a3_h2": w["L3_attn_Mvh_W2"].T.reshape(4, 128, 64).transpose(1, 0, 2).reshape(128, 256),
        "a3_h1": w["L3_attn_Mvh_W1"].T, "a3_kg": rows(w["L3_attn_normk_g"]), "a3_kb": rows(w["L3_attn_normk_b"]),
        "a3_qg": rows(w["L3_attn_normq_g"]), "a3_qb": rows(w["L3_attn_normq_b"]),
        "a3_ow": w["L3_attn_out_W"].T.reshape(4, 128, 128).transpose(1, 0, 2).reshape(128, 512),
        "a3_ob": col(w["L3_attn_out_b"]),
        "strict_add": np.where(same & (i[:, None] < i[None, :]), 0, NEG).astype(f),
        "strict01": (same & (i[:, None] < i[None, :])).astype(f),
        "incl01": (same & (i[:, None] <= i[None, :])).astype(f),
        "a3_one": np.ones((128, 1), f), "f3_gate": w["L3_ffn_gate_w"].T, "f3_b2": np.concatenate([w["L3_ffn_re_b2"], w["L3_ffn_se_b2"]]),
    }
    arrays = {}
    for k, p in enumerate(pack_columns()):
        pack = np.zeros((128, sum(c for _, _, c in p)), f)
        at = 0
        for name, r, c in p:
            if name != "pad":
                assert parts[name].shape == (r, c), (name, parts[name].shape, r, c)
                pack[:r, at:at + c] = parts[name]
            at += c
        arrays[f"pack{k}"] = pack

    def up(x):
        return x

    def down(x):
        e, ff, d = x.shape
        return x.reshape(e, ff // 128, 128, d).transpose(0, 2, 1, 3).reshape(e, 128, ff)

    def cols(x):
        return x.reshape(x.shape[0], -1, 128).transpose(0, 2, 1)

    arrays["ffn0"] = np.concatenate([w["L0_ffn_w1"], down(w["L0_ffn_w2"]), cols(w["L0_ffn_b1"]), cols(w["L0_ffn_b2"]),
                                     cols(w["L0_ffn_gamma"]), cols(w["L0_ffn_beta"])], axis=2)
    arrays["ffn1"] = np.concatenate([
        np.concatenate([w["L1_ffn_w1"], w["L1_ffn_sw1"][None]]), np.concatenate([w["L1_ffn_w3"], w["L1_ffn_sw3"][None]]),
        down(np.concatenate([w["L1_ffn_w2"], w["L1_ffn_sw2"][None]]))], axis=2)
    arrays["ffn2"] = np.concatenate([w["L2_ffn_e_w1"], down(w["L2_ffn_e_w2"]), cols(w["L2_ffn_e_b1"])], axis=2)
    arrays["ffn3"] = np.concatenate([
        np.concatenate([w["L3_ffn_re_w1"], w["L3_ffn_se_w1"]]), down(np.concatenate([w["L3_ffn_re_w2"], w["L3_ffn_se_w2"]])),
        cols(np.concatenate([w["L3_ffn_re_b1"], w["L3_ffn_se_b1"]]))], axis=2)
    arrays["tok_w"] = w["L0_tok_weight"]
    arrays["tok_m"] = w["L0_tok_mask"]
    arrays["tok_x"] = w["x"].T.reshape(GP, GC * B)

    nc = bacc.Bacc("TRN2", target_bir_lowering=False, num_devices=1)
    arrays = {k: np.ascontiguousarray(v) for k, v in arrays.items()}
    a = {k: nc.dram_tensor(k, v.shape, F32, kind="ExternalInput").ap() for k, v in arrays.items()}
    out = nc.dram_tensor("out_dram", (128, N), F32, kind="ExternalOutput").ap()
    build(nc, a, out)
    r = run_bass_kernel_spmd(nc, [arrays], core_ids=[0])
    return np.ascontiguousarray(r.results[0]["out_dram"].T).reshape(B, T, D)
```
